# Optimizing a Trainium2 kernel written in Bass

```python
import numpy as np
import jax
import jax.numpy as jnp

def _softmax(x, axis=-1):
    return jax.nn.softmax(x, axis=axis)

def _gelu(x):
    return jax.nn.gelu(x, approximate=True)

def _silu(x):
    return jax.nn.silu(x)

def _sigmoid(x):
    return jax.nn.sigmoid(x)

def _layernorm(x, axis=-1, eps=1e-05):
    m = jnp.mean(x, axis=axis, keepdims=True)
    v = jnp.var(x, axis=axis, keepdims=True)
    return (x - m) / jnp.sqrt(v + eps)

def _scatter_add(tgt, idx, src, axis=0):
    return tgt.at[idx].add(src)

def _segment_sum(src, seg, n):
    return jax.ops.segment_sum(src, seg, n)
kernel_name = 'mk_flamingo_gated_d4_seqx_r4_8953b5'

def setup_inputs(seed: int=0):
    np.random.seed(seed)
    _w = jnp.asarray

    def _rec_inputs():
        import jax
        import jax.numpy as jnp
        _rk = jax.random.key(seed)
        x = 0.0002417 + 0.9998 * jax.random.normal(jax.random.fold_in(_rk, 1), (16, 256, 256), jnp.float32)
        _lenS = 256 - jax.random.randint(jax.random.fold_in(_rk, 7), (16,), 0, max(1, 256 // 4) + 1, jnp.int32)
        _lenS2 = 256 - jax.random.randint(jax.random.fold_in(_rk, 8), (16,), 0, max(1, 256 // 4) + 1, jnp.int32)
        _ctx_1024P = jax.random.normal(jax.random.fold_in(_rk, 11), (16, 16, 256), jnp.float32)
        _ctx_1024c = jax.random.dirichlet(jax.random.fold_in(_rk, 511), 0.3 * jnp.ones((16,), jnp.float32), (16, 256))
        _ctx_1024t = jnp.einsum('bsk,bkd->bsd', _ctx_1024c, _ctx_1024P)
        _ctx_1024t = _ctx_1024t * jax.lax.rsqrt(jnp.mean(jnp.square(_ctx_1024t)) + 1e-12) * 0.953939
        ctx_1024 = 7.22013e-05 + 1.00017 * (_ctx_1024t + 0.3 * jax.random.normal(jax.random.fold_in(_rk, 611), (16, 256, 256), jnp.float32))
        _validS = jnp.arange(256)[None, :] < _lenS[:, None]
        _validS2 = jnp.arange(256)[None, :] < _lenS2[:, None]
        _causal = jnp.tril(jnp.ones((256, 256), dtype=bool))
        mask_1x1xSxS2_fk1 = jnp.where(jnp.broadcast_to(_validS2[0:1, None, None, :], (1, 1, 256, 256)), 1.0, 0.0).astype(jnp.float32)
        _g = jax.random.normal(jax.random.fold_in(_rk, 9001), (2, 4), jnp.float32)
        _g = jnp.sign(_g) * jnp.maximum(jnp.abs(_g), 1.0) + (_g == 0) * 1.0
        g_xattn = _g[0]
        g_ffn = _g[1]
        return (x, ctx_1024, mask_1x1xSxS2_fk1, g_xattn, g_ffn)
    x, ctx_1024, mask_1x1xSxS2_fk1, g_xattn, g_ffn = _rec_inputs()

    def _L0_xattn_setup():
        import jax, jax.numpy as jnp
        import numpy as np
        B, S, D, H = (4, 512, 256, 16)
        DEPTH = D // H

        def _split_heads(x):
            b, s, _ = x.shape
            return x.reshape(b, s, H, DEPTH).transpose(0, 2, 1, 3)
        key = jax.random.key(seed)
        ks = jax.random.split(key, 11)
        scale = 1.0 / np.sqrt(D)
        inp = {'v': jax.random.normal(ks[0], (B, S, D), jnp.float32), 'k': jax.random.normal(ks[1], (B, S, D), jnp.float32), 'q': jax.random.normal(ks[2], (B, S, D), jnp.float32), 'mask': jnp.triu(jnp.ones((S, S), jnp.float32), k=1)[None, None, :, :], 'wq': jax.random.normal(ks[3], (D, D), jnp.float32) * scale, 'bq': jnp.zeros((D,), jnp.float32), 'wk': jax.random.normal(ks[4], (D, D), jnp.float32) * scale, 'bk': jnp.zeros((D,), jnp.float32), 'wv': jax.random.normal(ks[5], (D, D), jnp.float32) * scale, 'bv': jnp.zeros((D,), jnp.float32), 'wo': jax.random.normal(ks[6], (D, D), jnp.float32) * scale, 'bo': jnp.zeros((D,), jnp.float32)}
        return inp
    _L0_xattn_all = _L0_xattn_setup()
    _L0_xattn_in = {k: v for k, v in _L0_xattn_all.items() if k in ('wq', 'bq', 'wk', 'bk', 'wv', 'bv', 'wo', 'bo')}
    del _L0_xattn_all

    def _L0_ffn_setup():
        import jax, jax.numpy as jnp
        import numpy as np
        import math
        D = 256
        H = 16
        E = 8
        TOPK = 2
        LAT = D // 2
        KPH = LAT // H
        HD = D // H

        def _forward(hs, q_w, q_b, k_w, k_b, v_w, v_b, o_w, o_b, router_w, router_b, w1, b1, w2, b2):
            B, S, _ = hs.shape
            Q = (hs @ q_w + q_b).reshape(B, S, H, HD).transpose(0, 2, 1, 3)
            K = (hs @ k_w + k_b).reshape(B, S, H, KPH).transpose(0, 2, 1, 3)
            V = (hs @ v_w + v_b).reshape(B, S, H, KPH).transpose(0, 2, 1, 3)
            scores = jnp.einsum('bhsk,bhtk->bhst', Q[..., :KPH], K) / math.sqrt(KPH)
            attn = jax.nn.softmax(scores, axis=-1)
            ao = jnp.einsum('bhst,bhtv->bhsv', attn, V)
            ao = ao.transpose(0, 2, 1, 3).reshape(B, S, H * KPH)
            ao = jnp.concatenate([ao, jnp.zeros((B, S, D - LAT), ao.dtype)], axis=-1)
            mla_out = ao @ o_w + o_b
            probs = jax.nn.softmax(mla_out @ router_w + router_b, axis=-1)
            topw, topi = jax.lax.top_k(probs, TOPK)
            topw = topw / (topw.sum(-1, keepdims=True) + 1e-08)
            combine = jnp.sum(jax.nn.one_hot(topi, E, dtype=probs.dtype) * topw[..., None], axis=-2)
            h1 = jnp.einsum('bsd,edf->ebsf', mla_out, w1) + b1[:, None, None, :]
            h1 = jax.nn.gelu(h1, approximate=False)
            h2 = jnp.einsum('ebsf,efd->ebsd', h1, w2) + b2[:, None, None, :]
            moe_out = jnp.einsum('bse,ebsd->bsd', combine, h2)
            return hs + 0.3 * moe_out
        key = jax.random.key(seed)
        ks = jax.random.split(key, 16)
        s = 0.02
        inp = {'hidden_states': jax.random.normal(ks[0], (2, 512, D), jnp.float32), 'q_w': jax.random.normal(ks[1], (D, D), jnp.float32) * s, 'q_b': jnp.zeros((D,), jnp.float32), 'k_w': jax.random.normal(ks[2], (D, LAT), jnp.float32) * s, 'k_b': jnp.zeros((LAT,), jnp.float32), 'v_w': jax.random.normal(ks[3], (D, LAT), jnp.float32) * s, 'v_b': jnp.zeros((LAT,), jnp.float32), 'o_w': jax.random.normal(ks[4], (D, D), jnp.float32) * s, 'o_b': jnp.zeros((D,), jnp.float32), 'router_w': jax.random.normal(ks[5], (D, E), jnp.float32) * s, 'router_b': jnp.zeros((E,), jnp.float32), 'w1': jax.random.normal(ks[6], (E, D, 2 * D), jnp.float32) * s, 'b1': jnp.zeros((E, 2 * D), jnp.float32), 'w2': jax.random.normal(ks[7], (E, 2 * D, D), jnp.float32) * s, 'b2': jnp.zeros((E, D), jnp.float32)}
        return inp
    _L0_ffn_all = _L0_ffn_setup()
    _L0_ffn_in = {k: v for k, v in _L0_ffn_all.items() if k in ('q_w', 'q_b', 'k_w', 'k_b', 'v_w', 'v_b', 'o_w', 'o_b', 'router_w', 'router_b', 'w1', 'b1', 'w2', 'b2')}
    del _L0_ffn_all

    def _L1_xattn_setup():
        import jax, jax.numpy as jnp
        import numpy as np
        DIM = 256
        NUM_HEADS = 16
        DIM_HEAD = 64
        INNER = NUM_HEADS * DIM_HEAD
        SCALE = DIM_HEAD ** (-0.5)

        def _layernorm(x, gamma, beta, eps=1e-05):
            mu = jnp.mean(x, axis=-1, keepdims=True)
            var = jnp.mean(jnp.square(x - mu), axis=-1, keepdims=True)
            return (x - mu) * jax.lax.rsqrt(var + eps) * gamma + beta
        key = jax.random.key(seed)
        ks = jax.random.split(key, 8)
        B, SQ, SK = (2, 512, 1024)
        x = jax.random.normal(ks[0], (B, SQ, DIM), dtype=jnp.float32)
        context = jax.random.normal(ks[1], (B, SK, DIM), dtype=jnp.float32)
        ln_gamma = jnp.ones((DIM,), jnp.float32)
        ln_beta = jnp.zeros((DIM,), jnp.float32)
        w_q = jax.random.normal(ks[2], (DIM, INNER), dtype=jnp.float32) / np.sqrt(DIM)
        w_kv = jax.random.normal(ks[3], (DIM, 2 * INNER), dtype=jnp.float32) / np.sqrt(DIM)
        w_out = jax.random.normal(ks[4], (INNER, DIM), dtype=jnp.float32) / np.sqrt(INNER)
        b_out = jnp.zeros((DIM,), jnp.float32)
        gate = jnp.array([0.5], jnp.float32)
        return {'x': x, 'context': context, 'ln_gamma': ln_gamma, 'ln_beta': ln_beta, 'w_q': w_q, 'w_kv': w_kv, 'w_out': w_out, 'b_out': b_out, 'gate': gate}
    _L1_xattn_all = _L1_xattn_setup()
    _L1_xattn_in = {k: v for k, v in _L1_xattn_all.items() if k in ('ln_gamma', 'ln_beta', 'w_q', 'w_kv', 'w_out', 'b_out', 'gate')}
    del _L1_xattn_all

    def _L1_ffn_setup():
        import jax, jax.numpy as jnp
        import numpy as np
        B, S, D = (1, 512, 256)
        E, K, F = (64, 8, 192)
        SF = 192
        C = 128
        ROUTED_SCALE = 1.0

        def _moe_forward(x, router_w, w_gate, w_up, w_down, ws_gate_up, ws_down):
            T = x.shape[0]
            logits = x.astype(jnp.float32) @ router_w.T
            probs = jax.nn.softmax(logits, axis=-1)
            topk_w, topk_ids = jax.lax.top_k(probs, K)
            topk_w = topk_w / jnp.sum(topk_w, axis=-1, keepdims=True)
            topk_w = topk_w.astype(x.dtype)
            N = T * K
            flat_e = topk_ids.reshape(-1)
            flat_w = topk_w.reshape(-1)
            tok = jnp.arange(N) // K
            onehot = flat_e[:, None] == jnp.arange(E)[None, :]
            pos = jnp.cumsum(onehot, axis=0)[jnp.arange(N), flat_e] - 1
            valid = pos < C
            idx = jnp.where(valid, flat_e * C + pos, E * C)
            x_buf = jnp.zeros((E * C + 1, x.shape[1]), x.dtype).at[idx].set(x[tok])
            xb = x_buf[:E * C].reshape(E, C, -1)
            g = jnp.einsum('ecd,edf->ecf', xb, w_gate)
            u = jnp.einsum('ecd,edf->ecf', xb, w_up)
            h = jax.nn.silu(g) * u
            y = jnp.einsum('ecf,efd->ecd', h, w_down).reshape(E * C, -1)
            safe = jnp.where(valid, idx, 0)
            contrib = y[safe] * (flat_w * valid.astype(flat_w.dtype))[:, None]
            routed = jax.ops.segment_sum(contrib, tok, num_segments=T)
            routed = routed * ROUTED_SCALE
            gu = x @ ws_gate_up
            sg, su = (gu[:, :SF], gu[:, SF:])
            shared = jax.nn.silu(sg) * su @ ws_down
            return routed + shared
        key = jax.random.key(seed)
        ks = jax.random.split(key, 7)
        w = 0.02
        return {'hidden_states': jax.random.normal(ks[0], (B, S, D), jnp.float32), 'router_w': jax.random.normal(ks[1], (E, D), jnp.float32) * w, 'w_gate': jax.random.normal(ks[2], (E, D, F), jnp.float32) * w, 'w_up': jax.random.normal(ks[3], (E, D, F), jnp.float32) * w, 'w_down': jax.random.normal(ks[4], (E, F, D), jnp.float32) * w, 'ws_gate_up': jax.random.normal(ks[5], (D, 2 * SF), jnp.float32) * w, 'ws_down': jax.random.normal(ks[6], (SF, D), jnp.float32) * w}
    _L1_ffn_all = _L1_ffn_setup()
    _L1_ffn_in = {k: v for k, v in _L1_ffn_all.items() if k in ('router_w', 'w_gate', 'w_up', 'w_down', 'ws_gate_up', 'ws_down')}
    del _L1_ffn_all

    def _L2_xattn_setup():
        import jax, jax.numpy as jnp
        import numpy as np
        D_MODEL = 256
        NUM_HEADS = 16
        HEAD_DIM = D_MODEL // NUM_HEADS
        MAX_SEQ = 128

        def rope_tables(seq_len, dim):
            inv_freq = 1.0 / 10000.0 ** (jnp.arange(0, dim, 2, dtype=jnp.float32) / dim)
            t = jnp.arange(seq_len, dtype=jnp.float32)
            freqs = jnp.einsum('i,j->ij', t, inv_freq)
            emb = jnp.concatenate([freqs, freqs], axis=-1)
            return (jnp.cos(emb), jnp.sin(emb))

        def rotate_half(x):
            x1, x2 = jnp.split(x, 2, axis=-1)
            return jnp.concatenate([-x2, x1], axis=-1)
        key = jax.random.key(seed)
        ks = jax.random.split(key, 12)
        B, S, D = (16, 128, D_MODEL)
        s = 1.0 / np.sqrt(D)
        inp = {'query': jax.random.normal(ks[0], (B, S, D), jnp.float32), 'key': jax.random.normal(ks[1], (B, S, D), jnp.float32), 'value': jax.random.normal(ks[2], (B, S, D), jnp.float32), 'Wq': jax.random.normal(ks[3], (D, D), jnp.float32) * s, 'bq': jnp.zeros((D,), jnp.float32), 'Wk': jax.random.normal(ks[4], (D, D), jnp.float32) * s, 'bk': jnp.zeros((D,), jnp.float32), 'Wv': jax.random.normal(ks[5], (D, D), jnp.float32) * s, 'bv': jnp.zeros((D,), jnp.float32), 'Wo': jax.random.normal(ks[6], (D, D), jnp.float32) * s, 'bo': jnp.zeros((D,), jnp.float32)}
        return inp
    _L2_xattn_all = _L2_xattn_setup()
    _L2_xattn_in = {k: v for k, v in _L2_xattn_all.items() if k in ('Wq', 'bq', 'Wk', 'bk', 'Wv', 'bv', 'Wo', 'bo')}
    del _L2_xattn_all

    def _L2_ffn_setup():
        import jax, jax.numpy as jnp
        import numpy as np
        HIDDEN = 256
        INTER = 1024
        key = jax.random.key(seed)
        k1, k2, k3, k4, k5 = jax.random.split(key, 5)
        hidden_states = jax.random.normal(k1, (4, 512, HIDDEN), dtype=jnp.float32)
        W1 = jax.random.normal(k2, (HIDDEN, INTER), dtype=jnp.float32) * (1.0 / np.sqrt(HIDDEN))
        b1 = jax.random.normal(k3, (INTER,), dtype=jnp.float32) * 0.02
        W2 = jax.random.normal(k4, (INTER, HIDDEN), dtype=jnp.float32) * (1.0 / np.sqrt(INTER))
        b2 = jax.random.normal(k5, (HIDDEN,), dtype=jnp.float32) * 0.02
        return {'hidden_states': hidden_states, 'W1': W1, 'b1': b1, 'W2': W2, 'b2': b2}
    _L2_ffn_all = _L2_ffn_setup()
    _L2_ffn_in = {k: v for k, v in _L2_ffn_all.items() if k in ('W1', 'b1', 'W2', 'b2')}
    del _L2_ffn_all

    def _L3_xattn_setup():
        import jax, jax.numpy as jnp
        import numpy as np
        DIM = 256
        HEAD_DIM = 64
        NUM_HEADS = 8
        INNER = HEAD_DIM * NUM_HEADS
        ROT_DIM = HEAD_DIM
        ROPE_BASE = 10000.0
        EPS = 1e-05

        def layer_norm(x, g, b):
            mu = jnp.mean(x, axis=-1, keepdims=True)
            var = jnp.var(x, axis=-1, keepdims=True)
            return (x - mu) * jax.lax.rsqrt(var + EPS) * g + b

        def rope_rotate_k(k):
            n = k.shape[1]
            half = ROT_DIM // 2
            inv_freq = 1.0 / ROPE_BASE ** (jnp.arange(0, ROT_DIM, 2, dtype=jnp.float32) / ROT_DIM)
            theta = jnp.arange(n, dtype=jnp.float32)[:, None] * inv_freq[None, :]
            angles = jnp.concatenate([theta, theta], axis=-1)
            cos = jnp.cos(angles)[None, :, None, :].astype(k.dtype)
            sin = jnp.sin(angles)[None, :, None, :].astype(k.dtype)
            k_rope, k_pass = (k[..., :ROT_DIM], k[..., ROT_DIM:])
            neg_half = jnp.concatenate([-k_rope[..., half:], k_rope[..., :half]], axis=-1)
            k_rope = k_rope * cos + neg_half * sin
            return jnp.concatenate([k_rope, k_pass], axis=-1)
        key = jax.random.key(seed)
        ks = jax.random.split(key, 5)
        b, n, m = (8, 2048, 64)
        s = 1.0 / np.sqrt(DIM)
        return {'x': jax.random.normal(ks[0], (b, n, DIM), jnp.float32), 'latents': jax.random.normal(ks[1], (b, m, DIM), jnp.float32), 'gamma_x': jnp.ones((DIM,), jnp.float32), 'beta_x': jnp.zeros((DIM,), jnp.float32), 'gamma_l': jnp.ones((DIM,), jnp.float32), 'beta_l': jnp.zeros((DIM,), jnp.float32), 'Wq': jax.random.normal(ks[2], (DIM, INNER), jnp.float32) * s, 'Wkv': jax.random.normal(ks[3], (DIM, 2 * INNER), jnp.float32) * s, 'Wo': jax.random.normal(ks[4], (INNER, DIM), jnp.float32) * (1.0 / np.sqrt(INNER))}
    _L3_xattn_all = _L3_xattn_setup()
    _L3_xattn_in = {k: v for k, v in _L3_xattn_all.items() if k in ('gamma_x', 'beta_x', 'gamma_l', 'beta_l', 'Wq', 'Wkv', 'Wo')}
    del _L3_xattn_all

    def _L3_ffn_setup():
        import jax, jax.numpy as jnp
        import numpy as np
        BLOCK = 32
        W_BITS = 4
        ACT_BITS = 16

        def act_qdq(x):
            qmax = 2.0 ** (ACT_BITS - 1) - 1.0
            scale = jnp.maximum(jnp.max(jnp.abs(x)) / qmax, 1e-12)
            return jnp.clip(jnp.round(x / scale), -qmax - 1.0, qmax) * scale

        def fixed_qdq_u16(x):
            scale = 1.0 / 65536.0
            return jnp.clip(jnp.round(x / scale), 0.0, 65535.0) * scale

        def lpbq_dequant(w):
            O, I = w.shape
            qmax = 2.0 ** (W_BITS - 1) - 1.0
            wb = w.reshape(O, I // BLOCK, BLOCK)
            s = jnp.maximum(jnp.max(jnp.abs(wb), axis=-1, keepdims=True) / qmax, 1e-12)
            wq = jnp.clip(jnp.round(wb / s), -qmax - 1.0, qmax) * s
            return wq.reshape(O, I)
        key = jax.random.key(seed)
        k1, k2, k3, k4 = jax.random.split(key, 4)
        B, S, H, I = (2, 1024, 256, 768)
        x = jax.random.normal(k1, (B, S, H), jnp.float32)
        w_gate = jax.random.normal(k2, (I, H), jnp.float32) * 0.02
        w_up = jax.random.normal(k3, (I, H), jnp.float32) * 0.02
        w_down = jax.random.normal(k4, (H, I), jnp.float32) * 0.02
        return {'x': x, 'w_gate': w_gate, 'w_up': w_up, 'w_down': w_down}
    _L3_ffn_all = _L3_ffn_setup()
    _L3_ffn_in = {k: v for k, v in _L3_ffn_all.items() if k in ('w_gate', 'w_up', 'w_down')}
    del _L3_ffn_all
    return {'x': x, 'ctx_1024': ctx_1024, 'mask_1x1xSxS2_fk1': mask_1x1xSxS2_fk1, 'g_xattn': g_xattn, 'g_ffn': g_ffn, 'L0_xattn_wq': _L0_xattn_in['wq'], 'L0_xattn_bq': _L0_xattn_in['bq'], 'L0_xattn_wk': _L0_xattn_in['wk'], 'L0_xattn_bk': _L0_xattn_in['bk'], 'L0_xattn_wv': _L0_xattn_in['wv'], 'L0_xattn_bv': _L0_xattn_in['bv'], 'L0_xattn_wo': _L0_xattn_in['wo'], 'L0_xattn_bo': _L0_xattn_in['bo'], 'L0_ffn_q_w': _L0_ffn_in['q_w'], 'L0_ffn_q_b': _L0_ffn_in['q_b'], 'L0_ffn_k_w': _L0_ffn_in['k_w'], 'L0_ffn_k_b': _L0_ffn_in['k_b'], 'L0_ffn_v_w': _L0_ffn_in['v_w'], 'L0_ffn_v_b': _L0_ffn_in['v_b'], 'L0_ffn_o_w': _L0_ffn_in['o_w'], 'L0_ffn_o_b': _L0_ffn_in['o_b'], 'L0_ffn_router_w': _L0_ffn_in['router_w'], 'L0_ffn_router_b': _L0_ffn_in['router_b'], 'L0_ffn_w1': _L0_ffn_in['w1'], 'L0_ffn_b1': _L0_ffn_in['b1'], 'L0_ffn_w2': _L0_ffn_in['w2'], 'L0_ffn_b2': _L0_ffn_in['b2'], 'L1_xattn_ln_gamma': _L1_xattn_in['ln_gamma'], 'L1_xattn_ln_beta': _L1_xattn_in['ln_beta'], 'L1_xattn_w_q': _L1_xattn_in['w_q'], 'L1_xattn_w_kv': _L1_xattn_in['w_kv'], 'L1_xattn_w_out': _L1_xattn_in['w_out'], 'L1_xattn_b_out': _L1_xattn_in['b_out'], 'L1_xattn_gate': _L1_xattn_in['gate'], 'L1_ffn_router_w': _L1_ffn_in['router_w'], 'L1_ffn_w_gate': _L1_ffn_in['w_gate'], 'L1_ffn_w_up': _L1_ffn_in['w_up'], 'L1_ffn_w_down': _L1_ffn_in['w_down'], 'L1_ffn_ws_gate_up': _L1_ffn_in['ws_gate_up'], 'L1_ffn_ws_down': _L1_ffn_in['ws_down'], 'L2_xattn_Wq': _L2_xattn_in['Wq'], 'L2_xattn_bq': _L2_xattn_in['bq'], 'L2_xattn_Wk': _L2_xattn_in['Wk'], 'L2_xattn_bk': _L2_xattn_in['bk'], 'L2_xattn_Wv': _L2_xattn_in['Wv'], 'L2_xattn_bv': _L2_xattn_in['bv'], 'L2_xattn_Wo': _L2_xattn_in['Wo'], 'L2_xattn_bo': _L2_xattn_in['bo'], 'L2_ffn_W1': _L2_ffn_in['W1'], 'L2_ffn_b1': _L2_ffn_in['b1'], 'L2_ffn_W2': _L2_ffn_in['W2'], 'L2_ffn_b2': _L2_ffn_in['b2'], 'L3_xattn_gamma_x': _L3_xattn_in['gamma_x'], 'L3_xattn_beta_x': _L3_xattn_in['beta_x'], 'L3_xattn_gamma_l': _L3_xattn_in['gamma_l'], 'L3_xattn_beta_l': _L3_xattn_in['beta_l'], 'L3_xattn_Wq': _L3_xattn_in['Wq'], 'L3_xattn_Wkv': _L3_xattn_in['Wkv'], 'L3_xattn_Wo': _L3_xattn_in['Wo'], 'L3_ffn_w_gate': _L3_ffn_in['w_gate'], 'L3_ffn_w_up': _L3_ffn_in['w_up'], 'L3_ffn_w_down': _L3_ffn_in['w_down']}

def reference(x, ctx_1024, mask_1x1xSxS2_fk1, g_xattn, g_ffn, L0_xattn_wq, L0_xattn_bq, L0_xattn_wk, L0_xattn_bk, L0_xattn_wv, L0_xattn_bv, L0_xattn_wo, L0_xattn_bo, L0_ffn_q_w, L0_ffn_q_b, L0_ffn_k_w, L0_ffn_k_b, L0_ffn_v_w, L0_ffn_v_b, L0_ffn_o_w, L0_ffn_o_b, L0_ffn_router_w, L0_ffn_router_b, L0_ffn_w1, L0_ffn_b1, L0_ffn_w2, L0_ffn_b2, L1_xattn_ln_gamma, L1_xattn_ln_beta, L1_xattn_w_q, L1_xattn_w_kv, L1_xattn_w_out, L1_xattn_b_out, L1_xattn_gate, L1_ffn_router_w, L1_ffn_w_gate, L1_ffn_w_up, L1_ffn_w_down, L1_ffn_ws_gate_up, L1_ffn_ws_down, L2_xattn_Wq, L2_xattn_bq, L2_xattn_Wk, L2_xattn_bk, L2_xattn_Wv, L2_xattn_bv, L2_xattn_Wo, L2_xattn_bo, L2_ffn_W1, L2_ffn_b1, L2_ffn_W2, L2_ffn_b2, L3_xattn_gamma_x, L3_xattn_beta_x, L3_xattn_gamma_l, L3_xattn_beta_l, L3_xattn_Wq, L3_xattn_Wkv, L3_xattn_Wo, L3_ffn_w_gate, L3_ffn_w_up, L3_ffn_w_down):
    import jax
    import jax.numpy as jnp

    def _L0_xattn_ref(v, k, q, mask, wq, bq, wk, bk, wv, bv, wo, bo):
        import jax, jax.numpy as jnp
        import numpy as np
        B, S, D, H = (4, 512, 256, 16)
        DEPTH = D // H

        def _split_heads(x):
            b, s, _ = x.shape
            return x.reshape(b, s, H, DEPTH).transpose(0, 2, 1, 3)
        qh = _split_heads(q @ wq + bq)
        kh = _split_heads(k @ wk + bk)
        vh = _split_heads(v @ wv + bv)
        logits = jnp.einsum('bhqd,bhkd->bhqk', qh, kh) / jnp.sqrt(jnp.asarray(DEPTH, jnp.float32))
        logits = logits + mask * -1000000000.0
        attn = jax.nn.softmax(logits, axis=-1)
        out = jnp.einsum('bhqk,bhkd->bhqd', attn, vh)
        out = out.transpose(0, 2, 1, 3).reshape(q.shape[0], -1, D)
        return out @ wo + bo

    def _L0_ffn_ref(hidden_states, q_w, q_b, k_w, k_b, v_w, v_b, o_w, o_b, router_w, router_b, w1, b1, w2, b2):
        import jax, jax.numpy as jnp
        import numpy as np
        import math
        D = 256
        H = 16
        E = 8
        TOPK = 2
        LAT = D // 2
        KPH = LAT // H
        HD = D // H

        def _forward(hs, q_w, q_b, k_w, k_b, v_w, v_b, o_w, o_b, router_w, router_b, w1, b1, w2, b2):
            B, S, _ = hs.shape
            Q = (hs @ q_w + q_b).reshape(B, S, H, HD).transpose(0, 2, 1, 3)
            K = (hs @ k_w + k_b).reshape(B, S, H, KPH).transpose(0, 2, 1, 3)
            V = (hs @ v_w + v_b).reshape(B, S, H, KPH).transpose(0, 2, 1, 3)
            scores = jnp.einsum('bhsk,bhtk->bhst', Q[..., :KPH], K) / math.sqrt(KPH)
            attn = jax.nn.softmax(scores, axis=-1)
            ao = jnp.einsum('bhst,bhtv->bhsv', attn, V)
            ao = ao.transpose(0, 2, 1, 3).reshape(B, S, H * KPH)
            ao = jnp.concatenate([ao, jnp.zeros((B, S, D - LAT), ao.dtype)], axis=-1)
            mla_out = ao @ o_w + o_b
            probs = jax.nn.softmax(mla_out @ router_w + router_b, axis=-1)
            topw, topi = jax.lax.top_k(probs, TOPK)
            topw = topw / (topw.sum(-1, keepdims=True) + 1e-08)
            combine = jnp.sum(jax.nn.one_hot(topi, E, dtype=probs.dtype) * topw[..., None], axis=-2)
            h1 = jnp.einsum('bsd,edf->ebsf', mla_out, w1) + b1[:, None, None, :]
            h1 = jax.nn.gelu(h1, approximate=False)
            h2 = jnp.einsum('ebsf,efd->ebsd', h1, w2) + b2[:, None, None, :]
            moe_out = jnp.einsum('bse,ebsd->bsd', combine, h2)
            return hs + 0.3 * moe_out
        return _forward(hidden_states, q_w, q_b, k_w, k_b, v_w, v_b, o_w, o_b, router_w, router_b, w1, b1, w2, b2)

    def _L1_xattn_ref(x, context, ln_gamma, ln_beta, w_q, w_kv, w_out, b_out, gate):
        import jax, jax.numpy as jnp
        import numpy as np
        DIM = 256
        NUM_HEADS = 16
        DIM_HEAD = 64
        INNER = NUM_HEADS * DIM_HEAD
        SCALE = DIM_HEAD ** (-0.5)

        def _layernorm(x, gamma, beta, eps=1e-05):
            mu = jnp.mean(x, axis=-1, keepdims=True)
            var = jnp.mean(jnp.square(x - mu), axis=-1, keepdims=True)
            return (x - mu) * jax.lax.rsqrt(var + eps) * gamma + beta
        B, SQ, _ = x.shape
        SK = context.shape[1]
        xn = _layernorm(x, ln_gamma, ln_beta)
        q = (xn @ w_q).reshape(B, SQ, NUM_HEADS, DIM_HEAD)
        kv = context @ w_kv
        k, v = jnp.split(kv, 2, axis=-1)
        k = k.reshape(B, SK, NUM_HEADS, DIM_HEAD)
        v = v.reshape(B, SK, NUM_HEADS, DIM_HEAD)
        scores = jnp.einsum('bqhd,bkhd->bhqk', q * SCALE, k)
        attn = jax.nn.softmax(scores, axis=-1)
        out = jnp.einsum('bhqk,bkhd->bqhd', attn, v).reshape(B, SQ, INNER)
        out = out @ w_out + b_out
        return out * jnp.tanh(gate[0])

    def _L1_ffn_ref(hidden_states, router_w, w_gate, w_up, w_down, ws_gate_up, ws_down):
        import jax, jax.numpy as jnp
        import numpy as np
        B, S, D = (1, 512, 256)
        E, K, F = (64, 8, 192)
        SF = 192
        C = 128
        ROUTED_SCALE = 1.0

        def _moe_forward(x, router_w, w_gate, w_up, w_down, ws_gate_up, ws_down):
            T = x.shape[0]
            logits = x.astype(jnp.float32) @ router_w.T
            probs = jax.nn.softmax(logits, axis=-1)
            topk_w, topk_ids = jax.lax.top_k(probs, K)
            topk_w = topk_w / jnp.sum(topk_w, axis=-1, keepdims=True)
            topk_w = topk_w.astype(x.dtype)
            N = T * K
            flat_e = topk_ids.reshape(-1)
            flat_w = topk_w.reshape(-1)
            tok = jnp.arange(N) // K
            onehot = flat_e[:, None] == jnp.arange(E)[None, :]
            pos = jnp.cumsum(onehot, axis=0)[jnp.arange(N), flat_e] - 1
            valid = pos < C
            idx = jnp.where(valid, flat_e * C + pos, E * C)
            x_buf = jnp.zeros((E * C + 1, x.shape[1]), x.dtype).at[idx].set(x[tok])
            xb = x_buf[:E * C].reshape(E, C, -1)
            g = jnp.einsum('ecd,edf->ecf', xb, w_gate)
            u = jnp.einsum('ecd,edf->ecf', xb, w_up)
            h = jax.nn.silu(g) * u
            y = jnp.einsum('ecf,efd->ecd', h, w_down).reshape(E * C, -1)
            safe = jnp.where(valid, idx, 0)
            contrib = y[safe] * (flat_w * valid.astype(flat_w.dtype))[:, None]
            routed = jax.ops.segment_sum(contrib, tok, num_segments=T)
            routed = routed * ROUTED_SCALE
            gu = x @ ws_gate_up
            sg, su = (gu[:, :SF], gu[:, SF:])
            shared = jax.nn.silu(sg) * su @ ws_down
            return routed + shared
        b, s, d = hidden_states.shape
        x = hidden_states.reshape(-1, d)
        out = _moe_forward(x, router_w, w_gate, w_up, w_down, ws_gate_up, ws_down)
        return out.reshape(b, s, d)

    def _L2_xattn_ref(query, key, value, Wq, bq, Wk, bk, Wv, bv, Wo, bo):
        import jax, jax.numpy as jnp
        import numpy as np
        D_MODEL = 256
        NUM_HEADS = 16
        HEAD_DIM = D_MODEL // NUM_HEADS
        MAX_SEQ = 128

        def rope_tables(seq_len, dim):
            inv_freq = 1.0 / 10000.0 ** (jnp.arange(0, dim, 2, dtype=jnp.float32) / dim)
            t = jnp.arange(seq_len, dtype=jnp.float32)
            freqs = jnp.einsum('i,j->ij', t, inv_freq)
            emb = jnp.concatenate([freqs, freqs], axis=-1)
            return (jnp.cos(emb), jnp.sin(emb))

        def rotate_half(x):
            x1, x2 = jnp.split(x, 2, axis=-1)
            return jnp.concatenate([-x2, x1], axis=-1)
        B, S, D = query.shape
        H, Hd = (NUM_HEADS, HEAD_DIM)
        scale = Hd ** (-0.5)

        def proj(x, W, b):
            y = jnp.einsum('bsd,ed->bse', x, W) + b
            return y.reshape(B, S, H, Hd).transpose(0, 2, 1, 3)
        q = proj(query, Wq, bq)
        k = proj(key, Wk, bk)
        v = proj(value, Wv, bv)
        cos, sin = rope_tables(S, Hd)
        cos = cos[None, None]
        sin = sin[None, None]
        q = q * cos + rotate_half(q) * sin
        k = k * cos + rotate_half(k) * sin
        attn = jnp.einsum('bhqd,bhkd->bhqk', q, k) * scale
        attn_w = jax.nn.softmax(attn, axis=-1)
        out = jnp.einsum('bhqk,bhkd->bhqd', attn_w, v)
        out = out.transpose(0, 2, 1, 3).reshape(B, S, D)
        out = jnp.einsum('bsd,ed->bse', out, Wo) + bo
        return out

    def _L2_ffn_ref(hidden_states, W1, b1, W2, b2):
        import jax, jax.numpy as jnp
        import numpy as np
        HIDDEN = 256
        INTER = 1024
        h = jax.nn.relu(jnp.einsum('bsh,hi->bsi', hidden_states, W1) + b1)
        return jnp.einsum('bsi,ih->bsh', h, W2) + b2

    def _L3_xattn_ref(x, latents, gamma_x, beta_x, gamma_l, beta_l, Wq, Wkv, Wo):
        import jax, jax.numpy as jnp
        import numpy as np
        DIM = 256
        HEAD_DIM = 64
        NUM_HEADS = 8
        INNER = HEAD_DIM * NUM_HEADS
        ROT_DIM = HEAD_DIM
        ROPE_BASE = 10000.0
        EPS = 1e-05

        def layer_norm(x, g, b):
            mu = jnp.mean(x, axis=-1, keepdims=True)
            var = jnp.var(x, axis=-1, keepdims=True)
            return (x - mu) * jax.lax.rsqrt(var + EPS) * g + b

        def rope_rotate_k(k):
            n = k.shape[1]
            half = ROT_DIM // 2
            inv_freq = 1.0 / ROPE_BASE ** (jnp.arange(0, ROT_DIM, 2, dtype=jnp.float32) / ROT_DIM)
            theta = jnp.arange(n, dtype=jnp.float32)[:, None] * inv_freq[None, :]
            angles = jnp.concatenate([theta, theta], axis=-1)
            cos = jnp.cos(angles)[None, :, None, :].astype(k.dtype)
            sin = jnp.sin(angles)[None, :, None, :].astype(k.dtype)
            k_rope, k_pass = (k[..., :ROT_DIM], k[..., ROT_DIM:])
            neg_half = jnp.concatenate([-k_rope[..., half:], k_rope[..., :half]], axis=-1)
            k_rope = k_rope * cos + neg_half * sin
            return jnp.concatenate([k_rope, k_pass], axis=-1)
        b, n, _ = x.shape
        m = latents.shape[1]
        h, d = (NUM_HEADS, HEAD_DIM)
        scale = d ** (-0.5)
        xn = layer_norm(x, gamma_x, beta_x)
        ln = layer_norm(latents, gamma_l, beta_l)
        q = (ln @ Wq).reshape(b, m, h, d)
        kv_x = xn @ Wkv
        k_x, v_x = (kv_x[..., :INNER], kv_x[..., INNER:])
        kv_l = ln @ Wkv
        k_l, v_l = (kv_l[..., :INNER], kv_l[..., INNER:])
        k_x = k_x.reshape(b, n, h, d)
        v_x = v_x.reshape(b, n, h, d)
        k_x = rope_rotate_k(k_x)
        q = jnp.transpose(q, (0, 2, 1, 3)) * scale
        k_x = jnp.transpose(k_x, (0, 2, 1, 3))
        v_x = jnp.transpose(v_x, (0, 2, 1, 3))
        k_l = jnp.transpose(k_l.reshape(b, m, h, d), (0, 2, 1, 3))
        v_l = jnp.transpose(v_l.reshape(b, m, h, d), (0, 2, 1, 3))
        k = jnp.concatenate([k_x, k_l], axis=2)
        v = jnp.concatenate([v_x, v_l], axis=2)
        sim = jnp.einsum('bhid,bhjd->bhij', q, k)
        attn = jax.nn.softmax(sim, axis=-1)
        out = jnp.einsum('bhij,bhjd->bhid', attn, v)
        out = jnp.transpose(out, (0, 2, 1, 3)).reshape(b, m, INNER)
        return out @ Wo

    def _L3_ffn_ref(x, w_gate, w_up, w_down):
        import jax, jax.numpy as jnp
        import numpy as np
        BLOCK = 32
        W_BITS = 4
        ACT_BITS = 16

        def act_qdq(x):
            qmax = 2.0 ** (ACT_BITS - 1) - 1.0
            scale = jnp.maximum(jnp.max(jnp.abs(x)) / qmax, 1e-12)
            return jnp.clip(jnp.round(x / scale), -qmax - 1.0, qmax) * scale

        def fixed_qdq_u16(x):
            scale = 1.0 / 65536.0
            return jnp.clip(jnp.round(x / scale), 0.0, 65535.0) * scale

        def lpbq_dequant(w):
            O, I = w.shape
            qmax = 2.0 ** (W_BITS - 1) - 1.0
            wb = w.reshape(O, I // BLOCK, BLOCK)
            s = jnp.maximum(jnp.max(jnp.abs(wb), axis=-1, keepdims=True) / qmax, 1e-12)
            wq = jnp.clip(jnp.round(wb / s), -qmax - 1.0, qmax) * s
            return wq.reshape(O, I)
        x = act_qdq(x)
        up = act_qdq(x @ lpbq_dequant(w_up).T)
        gate = act_qdq(x @ lpbq_dequant(w_gate).T)
        sig = fixed_qdq_u16(jax.nn.sigmoid(gate))
        gate = act_qdq(gate * sig)
        o = act_qdq(gate * up)
        return o @ lpbq_dequant(w_down).T
    x = x + jnp.tanh(g_xattn[0]) * _L0_xattn_ref(ctx_1024, ctx_1024, _layernorm(x, axis=-1), mask_1x1xSxS2_fk1, L0_xattn_wq, L0_xattn_bq, L0_xattn_wk, L0_xattn_bk, L0_xattn_wv, L0_xattn_bv, L0_xattn_wo, L0_xattn_bo)
    x = x + jnp.tanh(g_ffn[0]) * _L0_ffn_ref(_layernorm(x, axis=-1), L0_ffn_q_w, L0_ffn_q_b, L0_ffn_k_w, L0_ffn_k_b, L0_ffn_v_w, L0_ffn_v_b, L0_ffn_o_w, L0_ffn_o_b, L0_ffn_router_w, L0_ffn_router_b, L0_ffn_w1, L0_ffn_b1, L0_ffn_w2, L0_ffn_b2)
    x = x + jnp.tanh(g_xattn[1]) * _L1_xattn_ref(_layernorm(x, axis=-1), ctx_1024, L1_xattn_ln_gamma, L1_xattn_ln_beta, L1_xattn_w_q, L1_xattn_w_kv, L1_xattn_w_out, L1_xattn_b_out, L1_xattn_gate)
    x = x + jnp.tanh(g_ffn[1]) * _L1_ffn_ref(_layernorm(x, axis=-1), L1_ffn_router_w, L1_ffn_w_gate, L1_ffn_w_up, L1_ffn_w_down, L1_ffn_ws_gate_up, L1_ffn_ws_down)
    x = x + jnp.tanh(g_xattn[2]) * _L2_xattn_ref(_layernorm(x, axis=-1), ctx_1024, ctx_1024, L2_xattn_Wq, L2_xattn_bq, L2_xattn_Wk, L2_xattn_bk, L2_xattn_Wv, L2_xattn_bv, L2_xattn_Wo, L2_xattn_bo)
    x = x + jnp.tanh(g_ffn[2]) * _L2_ffn_ref(_layernorm(x, axis=-1), L2_ffn_W1, L2_ffn_b1, L2_ffn_W2, L2_ffn_b2)
    x = x + jnp.tanh(g_xattn[3]) * _L3_xattn_ref(ctx_1024, _layernorm(x, axis=-1), L3_xattn_gamma_x, L3_xattn_beta_x, L3_xattn_gamma_l, L3_xattn_beta_l, L3_xattn_Wq, L3_xattn_Wkv, L3_xattn_Wo)
    x = x + jnp.tanh(g_ffn[3]) * _L3_ffn_ref(_layernorm(x, axis=-1), L3_ffn_w_gate, L3_ffn_w_up, L3_ffn_w_down)
    return x

_drawn_inputs = setup_inputs


def setup_inputs(seed=0):
    import zlib

    import numpy as np

    out = dict(_drawn_inputs(seed))
    spreads = {'L0_xattn_bq': (0.0, 0.622),
     'L0_xattn_bk': (0.0, 2.0),
     'L0_xattn_bv': (0.0, 0.1),
     'L0_xattn_bo': (0.0, 0.1),
     'L0_ffn_q_b': (0.0, 0.8),
     'L0_ffn_k_b': (0.0, 2.0),
     'L0_ffn_v_b': (0.0, 0.8),
     'L0_ffn_o_b': (0.0, 0.279),
     'L0_ffn_router_b': (0.0, 0.1),
     'L0_ffn_b1': (0.0, 0.8),
     'L0_ffn_b2': (0.0, 0.27),
     'L1_xattn_ln_gamma': (1.0, 0.6),
     'L1_xattn_ln_beta': (0.0, 1.339),
     'L1_xattn_b_out': (0.0, 0.1),
     'L2_xattn_bq': (0.0, 2.0),
     'L2_xattn_bk': (0.0, 2.0),
     'L2_xattn_bv': (0.0, 0.728),
     'L2_xattn_bo': (0.0, 0.69),
     'L3_xattn_gamma_x': (1.0, 0.6),
     'L3_xattn_beta_x': (0.0, 0.8),
     'L3_xattn_gamma_l': (1.0, 0.6),
     'L3_xattn_beta_l': (0.0, 0.8)}
    factors = {'g_ffn': 8.0,
     'L0_ffn_q_w': 8.0,
     'L0_ffn_k_w': 8.0,
     'L0_ffn_v_w': 8.0,
     'L0_ffn_o_w': 8.0,
     'L0_ffn_router_w': 2.733,
     'L0_ffn_w1': 8.0,
     'L0_ffn_w2': 7.694,
     'L1_ffn_router_w': 8.0,
     'L1_ffn_w_gate': 8.0,
     'L1_ffn_w_up': 8.0,
     'L1_ffn_w_down': 8.0,
     'L2_ffn_b1': 27.682,
     'L2_ffn_b2': 19.253,
     'L1_ffn_ws_gate_up': 8.0,
     'L1_ffn_ws_down': 8.0,
     'L2_xattn_Wq': 2.821,
     'L2_xattn_Wk': 2.708,
     'L3_xattn_Wq': 3.033,
     'L3_ffn_w_gate': 8.0,
     'L3_ffn_w_up': 8.0,
     'L3_ffn_w_down': 8.0}
    for name, (base, spread) in spreads.items():
        noise = np.random.default_rng([zlib.crc32(name.encode()), seed]).standard_normal(out[name].shape)
        drawn = base * np.exp(spread * noise) if base else spread * noise
        out[name] = jnp.asarray(drawn.astype(out[name].dtype))
    for name, factor in factors.items():
        out[name] = (out[name] * factor).astype(out[name].dtype)
    return out
```

```python
from contextlib import ExitStack

import numpy as np

import concourse.bass as bass
from concourse import mybir

F32 = mybir.dt.float32
I16 = mybir.dt.int16
U32 = mybir.dt.uint32
ALU = mybir.AluOpType
ACT = mybir.ActivationFunctionType
AX = mybir.AxisListType

BATCH, SEQ, D = 16, 256, 256
TOKENS = BATCH * SEQ
P = 128
TILES = TOKENS // P
QT = SEQ // P
KT = D // P
EPS = 1e-5
BIG = 1.0e9


def wait(eng, sem, value):
    if isinstance(value, int) and value <= 0:
        return
    eng.wait_ge(sem, value)


def zero_semaphores(nc, sems):
    with nc.Block() as block:
        @block.gpsimd
        def _(pool):
            for s in sems:
                pool.sem_clear(s)


def attention_stage(nc, keep, S, cfg):
    UN = 16
    H, VD, G = cfg["heads"], cfg["vd"], cfg["group"]
    wide = cfg["wide"]
    NP, NE, NL = cfg["n_pro"], cfg["n_epi"], cfg["n_norm"]
    narrow = cfg["narrow"]
    VW = 32 if narrow else VD + 1
    UG = G * (2 if wide else 1)
    NG = UN // UG
    pT_on_act = cfg["pT_on_act"]

    with ExitStack() as ctx:
        def sb(name, shape, dt=F32):
            return ctx.enter_context(nc.sbuf_tensor(cfg["name"] + name, shape, dt))

        def psum(name, shape):
            return ctx.enter_context(nc.psum_tensor(cfg["name"] + name, shape, F32))

        score = [psum(f"score{i}", [P, 512]) for i in range(4)]
        ptp = psum("ptp", [P, 512])
        pvp = [psum(f"pvp{i}", [P, 512]) for i in range(2)]
        work = psum("work", [P, 512])

        bufs = {}
        bufs["sb"], bufs["pro"], bufs["epi"] = sb, work, work
        prob = [sb(f"prob{i}", [P, 512]) for i in range(2)]
        pT = [sb(f"pT{i}", [P, 4, P]) for i in range(2)]
        nmax = sb("nmax", [P, 4, 2])
        if narrow:
            raw = [sb(f"raw{i}", [P, SEQ]) for i in range(2)]
        rden = sb("rden", [P, 2, 2, G])
        o = [sb(f"o{i}", [P, QT, H * VD]) for i in range(2)]
        st = sb("st", [P, NL, QT, 6])
        mv = sb("mv", [P, NL, QT, 2])
        rstd = sb("rstd", [P, NL, QT])
        bufs.update(o=o, nmax=nmax)
        fns = cfg["make"](nc, keep, bufs, S, ctx)
        qT_of, kT_of, v_of = fns["q"], fns["k"], fns["v"]

        def for_batches(eng, head, body, tail):
            head()
            body(0, 0, 0, True, False)
            with eng.Fori(0, (BATCH - 2) // 2) as i:
                body(2 * i + 1, i + 0, 1, False, False)
                body(2 * i + 2, i + 1, 0, False, False)
            body(BATCH - 1, BATCH // 2 - 1, 1, False, True)
            tail()

        with nc.Block() as block:
            @block.sync
            def _(sp):
                for dst, src in fns["weights"]:
                    sp.dma_start(dst, src).then_inc(S["weights"], 16)
                if "stream" in cfg:
                    for c in range(2):
                        for dst, src in cfg["stream"](bufs, c, c):
                            sp.dma_start(dst, src).then_inc(S["stream"][c], 16)
                    with sp.Fori(0, BATCH // 2 - 1) as i:
                        for par in range(2):
                            sp.wait_ge(S["pro_filled"], NP * (2 * i + par + 1))
                            for dst, src in cfg["stream"](bufs, 2 * i + par + 2, par):
                                sp.dma_start(dst, src).then_inc(S["stream"][par], 16)

                if fns.get("sync_more"):
                    fns["sync_more"](sp)

            @block.gpsimd
            def _(pool):
                def rstds(c, half, par):
                    for n in range(NL):
                        pool.wait_ge(S["var"], NL * c + n + 1)
                        nc.gpsimd.tensor_tensor(rstd[:, n, :], mv[:, n, :, 1], keep["eps"][:, 0:QT],
                                                ALU.add).then_inc(S["vareps"], 1)
                        pool.wait_ge(S["vareps"], NL * c + n + 1)
                        nc.gpsimd.tensor_tensor(rstd[:, n, :], rstd[:, n, :], keep["mhalf"][:, 0:QT],
                                                ALU.pow).then_inc(S["rstd"], 1)
                    if fns.get("pool"):
                        fns["pool"](pool, c, half, par)
                rstds(0, 0, 0)
                with pool.Fori(1, BATCH) as c:
                    rstds(c, None, None)
                if fns.get("pool_tail"):
                    fns["pool_tail"](pool)

            @block.vector
            def _(dve):
                def norm(n, c, half, par):
                    src, dst = fns["norm"](n, c, half, par)
                    fns["norm_wait"](dve, n, c, half, par)
                    for t in range(QT):
                        ins = nc.vector.bn_stats(st[:, n, t, :], src(t))
                    ins.then_inc(S["stats"], 1)
                    dve.wait_ge(S["stats"], NL * c + n + 1)
                    nc.vector.memset(keep["scratch"][:, 0:1], 0.0)
                    for t in range(QT):
                        ins = nc.vector.bn_aggr(mv[:, n, t, :], st[:, n, t, :])
                    ins.then_inc(S["var"], 1)

                def normed(n, c, half, par):
                    src, dst = fns["norm"](n, c, half, par)
                    dve.wait_ge(S["rstd"], NL * c + n + 1)
                    if fns["norm_job"][n] is not None:
                        wait(dve, S["pro_filled"], NP * (c - 1) + fns["norm_job"][n] + 1)
                    for t in range(QT):
                        ins = nc.vector.tensor_scalar(dst(t), src(t), mv[:, n, t, 0:1],
                                                      rstd[:, n, t:t + 1], ALU.subtract, ALU.mult)
                    ins.then_inc(S["normed"], 1)

                def row_max(c, h, par):
                    p = h % 4
                    dve.wait_ge(S["scores"], UN * c + h + 1)
                    fns["row_max"](dve, nmax, score[p], c, h, p).then_inc(S["row_max"], 1)

                def copy_pT(c, h):
                    p = h % 2
                    dve.wait_ge(S["pT"], UN * c + h + 1)
                    wait(dve, S["pv"], UN * c + h - 1)
                    nc.vector.tensor_copy(pT[p][:, :, :].rearrange("p a b -> p (a b)"),
                                          ptp[:, :]).then_inc(S["pT_copied"], 1)

                def normalise(c, g, par):
                    p = g % 2
                    bank = pvp[1 if narrow else p][:, 0:QT * G * VW].rearrange("p (t g v) -> p t g v", t=QT, g=G)
                    if narrow:
                        dve.wait_ge(S["back"], NG * c + g + 1)
                    else:
                        dve.wait_ge(S["pv"], UN * c + UG * (g + 1))
                    nc.vector.reciprocal(rden[:, p, :, :], bank[:, :, :, VD]).then_inc(S["rden"], 1)
                    dve.wait_ge(S["rden"], NG * c + g + 1)
                    if g == 0:
                        wait(dve, S["epi_filled"], NE * (c - 1))
                    for t in range(QT):
                        r = rden[:, p, t, :].unsqueeze(2).to_broadcast([P, G, VD])
                        dst = o[par][:, t, g * G * VD:(g + 1) * G * VD].rearrange("p (g v) -> p g v", g=G)
                        ins = nc.vector.tensor_tensor(dst, bank[:, t, :, 0:VD], r, ALU.mult)
                    ins.then_inc(S["o_ready"], 1)

                def copy_raw(c, g):
                    dve.wait_ge(S["pv"], UN * c + UG * (g + 1))
                    wait(dve, S["back"], NG * c + g - 1)
                    nc.vector.tensor_copy(raw[g % 2][:, :], pvp[0][:, 0:SEQ]).then_inc(S["raw"], 1)

                def pro_copy(j, c, half, par):
                    if fns["pro_engine"](j) == "dve":
                        dve.wait_ge(S["pro_filled"], NP * c + j + 1)
                        if j in fns["pro_frees"]:
                            wait(dve, S["pv"], UN * (c - 1))
                        fns["pro_copy"](dve, j, c, half, par).then_inc(S["pro_copied"], 1)

                def epi_copy(j, c, half, par):
                    if fns["epi_engine"](j) == "dve":
                        dve.wait_ge(S["epi_filled"], NE * c + j + 1)
                        fns["epi_copy"](dve, j, c, half, par).then_inc(S["epi_copied"], 1)

                def prologue(c, half, par):
                    for n in range(NL):
                        norm(n, c, half, par)
                        normed(n, c, half, par)
                    for j in range(NP):
                        pro_copy(j, c, half, par)

                def head():
                    dve.wait_ge(S["weights"], 16 * len(fns["weights"]))
                    fns["setup"](dve)
                    prologue(0, 0, 0)
                    row_max(0, 0, 0)
                    row_max(0, 1, 0)

                def body(c, half, par, first, last):
                    nxt = (c + 1, half + par, 1 - par)

                    def jobs(at):
                        if not first:
                            for j in fns["epi_at"](at):
                                epi_copy(j, c - 1, None, 1 - par)
                        if not last:
                            for j in fns["pro_at"](at):
                                pro_copy(j, *nxt)

                    for h in range(UN):
                        if h + 2 < UN:
                            row_max(c, h + 2, par)
                        elif not last:
                            row_max(c + 1, h + 2 - UN, 1 - par)
                        if narrow and h > UG and h % UG == 1:
                            normalise(c, h // UG - 1, par)
                        if narrow and h == 1 and not first:
                            normalise(c - 1, NG - 1, 1 - par)
                        jobs(h)
                        if not pT_on_act:
                            copy_pT(c, h)
                        if h >= 1 and h % UG == 0:
                            (copy_raw(c, h // UG - 1) if narrow else normalise(c, h // UG - 1, par))
                        if h == 0 and not first:
                            (copy_raw(c - 1, NG - 1) if narrow else normalise(c - 1, NG - 1, 1 - par))
                        jobs(h + 0.5)
                        if not last:
                            for n in range(NL):
                                if h == 2 * n:
                                    norm(n, *nxt)
                                if h == 2 * n + 1:
                                    normed(n, *nxt)

                def tail():
                    if narrow:
                        copy_raw(BATCH - 1, NG - 1)
                    normalise(BATCH - 1, NG - 1, 1)
                    for j in range(NE):
                        epi_copy(j, BATCH - 1, BATCH // 2 - 1, 1)

                for_batches(dve, head, body, tail)

            @block.scalar
            def _(act):
                def exp(c, h):
                    p = h % 2
                    act.wait_ge(S["row_max"], UN * c + h + 1)
                    wait(act, S["pT"], UN * c + h - 1)
                    fns["exp"](act, prob[p], nmax, score[h % 4], h, h % 4).then_inc(S["exp"], 1)

                def copy_pT(c, h):
                    p = h % 2
                    act.wait_ge(S["pT"], UN * c + h + 1)
                    wait(act, S["pv"], UN * c + h - 1)
                    nc.scalar.copy(pT[p][:, :, :].rearrange("p a b -> p (a b)"),
                                   ptp[:, :]).then_inc(S["pT_copied"], 1)

                def pro_copy(j, c, half, par):
                    if fns["pro_engine"](j) == "act":
                        act.wait_ge(S["pro_filled"], NP * c + j + 1)
                        if j in fns["pro_frees"]:
                            wait(act, S["pv"], UN * (c - 1))
                        fns["pro_copy"](act, j, c, half, par).then_inc(S["pro_copied"], 1)

                def epi_copy(j, c, half, par):
                    if fns["epi_engine"](j) == "act":
                        act.wait_ge(S["epi_filled"], NE * c + j + 1)
                        fns["epi_copy"](act, j, c, half, par).then_inc(S["epi_copied"], 1)
                    if fns.get("epi_act"):
                        fns["epi_act"](act, j, c)

                def head():
                    act.wait_ge(S["weights"], 16 * len(fns["weights"]))
                    fns["act_setup"](act)
                    for j in range(NP):
                        pro_copy(j, 0, 0, 0)
                    exp(0, 0)

                def body(c, half, par, first, last):
                    nxt = (c + 1, half + par, 1 - par)

                    def jobs(at):
                        if not first:
                            for j in fns["epi_at"](at):
                                epi_copy(j, c - 1, None, 1 - par)
                        if not last:
                            for j in fns["pro_at"](at):
                                pro_copy(j, *nxt)

                    for h in range(UN):
                        if h + 1 < UN:
                            exp(c, h + 1)
                        elif not last:
                            exp(c + 1, 0)
                        jobs(h)
                        if pT_on_act:
                            copy_pT(c, h)
                        jobs(h + 0.5)

                def tail():
                    for j in range(NE):
                        epi_copy(j, BATCH - 1, BATCH // 2 - 1, 1)

                for_batches(act, head, body, tail)

            @block.tensor
            def _(pe):
                def scores(c, h, par):
                    p = h % 4
                    wait(pe, S["exp"], UN * c + h - 3)
                    if h == 0:
                        pe.wait_ge(S["pro_copied"], NP * (c + 1))
                    if wide:
                        head, t = h // 2, h % 2
                        mm = nc.tensor.matmul(score[p][:, :], qT_of(par, head, t), kT_of(par, head),
                                              start=True, stop=True)
                    else:
                        for t in range(QT):
                            mm = nc.tensor.matmul(score[p][:, t * SEQ:(t + 1) * SEQ], qT_of(par, h, t),
                                                  kT_of(par, h), start=True, stop=True)
                    mm.then_inc(S["scores"], 1)

                def transpose_probs(c, h):
                    p = h % 2
                    pe.wait_ge(S["exp"], UN * c + h + 1)
                    wait(pe, S["pT_copied"], UN * c + h)
                    for k in range(4):
                        to = (k % 2) * 2 + k // 2 if narrow else k
                        mm = nc.tensor.transpose(ptp[:, to * P:(to + 1) * P],
                                                 prob[p][:, k * P:(k + 1) * P], keep["ident"][:, :])
                    mm.then_inc(S["pT"], 1)

                def pv(c, h, par):
                    p = h % 2
                    g = h // UG
                    pe.wait_ge(S["pT_copied"], UN * c + h + 1)
                    if narrow:
                        if h % UG == 0:
                            wait(pe, S["raw"], NG * c + g)
                        r = 32 * (h % G)
                        for k in range(2):
                            mm = nc.tensor.matmul(pvp[0][r:r + 32, 0:SEQ], v_of(par, h, k),
                                                  pT[p][:, 2 * k:2 * k + 2, :], start=(k == 0), stop=(k == 1))
                        mm.then_inc(S["pv"], 1)
                        return
                    if h % UG == 0:
                        wait(pe, S["o_ready"], NG * c + g - 1)
                    bank = pvp[g % 2]
                    W = VD + 1
                    if wide:
                        head, t = h // 2, h % 2
                        at = (t * G + head % G) * W
                        for k in range(4):
                            mm = nc.tensor.matmul(bank[:, at:at + W], pT[p][:, k, :], v_of(par, head, k),
                                                  start=(k == 0), stop=(k == 3))
                    else:
                        for t in range(QT):
                            at = (t * G + h % G) * W
                            for k in range(2):
                                mm = nc.tensor.matmul(bank[:, at:at + W], pT[p][:, 2 * t + k, :],
                                                      v_of(par, h, k), start=(k == 0), stop=(k == 1))
                    mm.then_inc(S["pv"], 1)

                def turn_back(c, g):
                    pe.wait_ge(S["raw"], NG * c + g + 1)
                    wait(pe, S["o_ready"], NG * c + g)
                    for t in range(QT):
                        mm = nc.tensor.transpose(pvp[1][:, t * P:(t + 1) * P], raw[g % 2][:, t * P:(t + 1) * P],
                                                 keep["ident"][:, :])
                    mm.then_inc(S["back"], 1)

                def pro_fill(j, c, half, par):
                    wait(pe, S["pro_copied"], NP * c + j)
                    if j == 0:
                        wait(pe, S["epi_copied"], NE * (c - 1))
                    if j in fns["norm_job"]:
                        pe.wait_ge(S["normed"], NL * c + fns["norm_job"].index(j) + 1)
                    fns["pro_fill"](pe, j, c, half, par).then_inc(S["pro_filled"], 1)

                def epi_fill(j, c, par):
                    wait(pe, S["epi_copied"], NE * c + j)
                    if j == 0:
                        pe.wait_ge(S["o_ready"], NG * (c + 1))
                    fns["epi_fill"](pe, j, c, par).then_inc(S["epi_filled"], 1)

                def head():
                    pe.wait_ge(S["weights"], 16 * len(fns["weights"]))
                    for j in range(NP):
                        pro_fill(j, 0, 0, 0)
                    scores(0, 0, 0)
                    scores(0, 1, 0)

                def body(c, half, par, first, last):
                    nxt = (c + 1, half + par, 1 - par)

                    def jobs(at):
                        if not first:
                            for j in fns["epi_at"](at):
                                epi_fill(j, c - 1, 1 - par)
                        if not last:
                            for j in fns["pro_at"](at):
                                pro_fill(j, *nxt)

                    for h in range(UN):
                        if h + 2 < UN:
                            scores(c, h + 2, par)
                        elif not last:
                            scores(c + 1, h + 2 - UN, 1 - par)
                        if h > 0:
                            pv(c, h - 1, par)
                        elif not first:
                            pv(c - 1, UN - 1, 1 - par)
                        if narrow and h > UG and h % UG == 1:
                            turn_back(c, h // UG - 1)
                        if narrow and h == 1 and not first:
                            turn_back(c - 1, NG - 1)
                        jobs(h)
                        transpose_probs(c, h)
                        jobs(h + 0.5)

                def tail():
                    pv(BATCH - 1, UN - 1, 1)
                    if narrow:
                        turn_back(BATCH - 1, NG - 1)
                    for j in range(NE):
                        epi_fill(j, BATCH - 1, 1)

                for_batches(pe, head, body, tail)
    zero_semaphores(nc, S["all"])


def spread(slots):
    return lambda h: [j for j, s in enumerate(slots) if s == h]


def plain_max(nc, dve, nmax, bank, p):
    return nc.vector.tensor_reduce(nmax[:, p, :], bank[:, :].rearrange("p (t k) -> p t k", t=QT), AX.X,
                                   ALU.max, negate=True)


def plain_exp(nc, act, prob, nmax, bank, p, scale=1.0):
    for t in range(QT):
        ins = nc.scalar.activation(prob[:, t * SEQ:(t + 1) * SEQ], bank[:, t * SEQ:(t + 1) * SEQ], ACT.Exp,
                                   bias=nmax[:, p, t:t + 1], scale=scale)
    return ins


def project(nc, bank, w, rhs, tiles, n=SEQ):
    for i, m in enumerate(tiles):
        for k in range(KT):
            mm = nc.tensor.matmul(bank[:, i * n:(i + 1) * n], w[:, k, m * P:(m + 1) * P], rhs[:, k, :],
                                  start=(k == 0), stop=(k == KT - 1))
    return mm


def project_rows(nc, bank, lhsT, w, cols, n):
    for t in range(QT):
        for k in range(KT):
            mm = nc.tensor.matmul(bank[:, t * n:(t + 1) * n], lhsT[:, k, t * P:(t + 1) * P],
                                  w[:, k, cols:cols + n], start=(k == 0), stop=(k == KT - 1))
    return mm


def turn(nc, keep, bank, rows, features=slice(0, D)):
    base = features.start
    for k in range(KT):
        for t in range(QT):
            mm = nc.tensor.transpose(bank[:, k * SEQ + t * P:k * SEQ + (t + 1) * P],
                                     rows[:, t, base + k * P:base + (k + 1) * P], keep["ident"][:, :])
    return mm


def output_rows(nc, bank, oT, w, bias, keep, parts):
    for t in range(QT):
        for k in range(parts):
            mm = nc.tensor.matmul(bank[:, t * D:(t + 1) * D], oT[:, k, t * P:(t + 1) * P], w[:, k, :],
                                  start=(k == 0), stop=(bias is None and k == parts - 1))
        if bias is not None:
            mm = nc.tensor.matmul(bank[:, t * D:(t + 1) * D], keep["ones"][0:1, :], bias,
                                  start=False, stop=True)
    return mm


def flat(ap):
    return ap.rearrange("p a b -> p (a b)")


def add_output(nc, dve, keep, bank, gate, c):
    xs = keep["x"][:, bass.ds(c * QT, QT), :]
    return nc.vector.scalar_tensor_tensor(out=flat(xs), in0=bank[:, :], scalar=gate, in1=flat(xs),
                                          op0=ALU.mult, op1=ALU.add)


def x_norm(keep, h):
    def norm(n, c, half, par):
        return (lambda t: keep["x"][:, bass.ds(c * QT + t, 1), :].rearrange("p a b -> p (a b)"),
                lambda t: h[:, t, :])
    return norm


def cross_small(nc, keep, S, dram, rope):
    H, VD, G = 16, 16, 4
    scale = 0.25 if rope else -0.25
    L = "L2" if rope else "L0"
    n_pro = 6 if rope else 4
    qj, kj, vj = (1, 3, 5) if rope else (1, 2, 3)

    def make(nc, keep, bufs, S, ctx):
        sb = bufs["sb"]
        wq, wk, wv, wo = [sb(n, [P, KT, D]) for n in ("wq", "wk", "wv", "wo")]
        bq, bk = sb("bq", [P, 2]), sb("bk", [P, 2])
        bqv = sb("bqv", [P, 2, 2])
        bv, bo = sb("bv", [P, D]), sb("bo", [1, D])
        pick = sb("pick", [P, 2])
        h = sb("h", [P, QT, D])
        hT = sb("hT", [P, KT, SEQ])
        cT = [sb(f"cT{i}", [P, KT, SEQ]) for i in range(2)]
        qT = [sb(f"qT{i}", [P, 2, KT, SEQ]) for i in range(2)]
        kT = [sb(f"kT{i}", [P, KT, SEQ]) for i in range(2)]
        v = [sb(f"v{i}", [P, QT, H, 32]) for i in range(2)]
        oT = sb("oT", [P, KT, SEQ])
        bufs["cT"] = cT
        pro, epi, o = bufs["pro"], bufs["epi"], bufs["o"]
        weights = [(w[:, :, :], dram[L + n].rearrange("(k p) m -> p k m", p=P))
                   for w, n in ((wq, "wq"), (wk, "wk"), (wv, "wv"), (wo, "wo"))]
        weights += [(bq[:, :], dram[L + "bq"]), (bk[:, :], dram[L + "bk"]), (bv[:, :], dram[L + "bv"]),
                    (bo[:, :], dram[L + "bo"]), (pick[:, :], dram["pick2"])]
        if rope:
            wqr, wkr = sb("wqr", [P, KT, D]), sb("wkr", [P, KT, D])
            bqr, bkr = sb("bqr", [P, 2]), sb("bkr", [P, 2])
            cos, sin = sb("cos", [P, SEQ]), sb("sin", [P, SEQ])
            turned, mixed = sb("turned", [P, KT, SEQ]), sb("mixed", [P, KT, SEQ])
            weights += [(w[:, :, :], dram[L + n].rearrange("(k p) m -> p k m", p=P))
                        for w, n in ((wqr, "wqr"), (wkr, "wkr"))]
            weights += [(bqr[:, :], dram[L + "bqr"]), (bkr[:, :], dram[L + "bkr"]),
                        (cos[:, :], dram["cos16"]), (sin[:, :], dram["sin16"])]
        else:
            mask = sb("mask", [P, QT, SEQ])
            masked = [sb(f"masked{i}", [P, QT, SEQ]) for i in range(4)]
            weights += [(mask[:, :, :], dram["mask"].rearrange("(t p) k -> p t k", p=P))]

        def setup(dve):
            for i in range(2):
                nc.vector.memset(v[i][:, :, :, VD:VD + 1], 1.0)
                nc.vector.memset(v[i][:, :, :, VD + 1:32], 0.0)
            if not rope:
                nc.vector.tensor_scalar(flat(mask[:, :, :]), flat(mask[:, :, :]), BIG, None, ALU.mult)
            ins = nc.vector.tensor_scalar(pick[:, :], pick[:, :], scale, None, ALU.mult)
            ins.then_inc(S["setup"], 1)
            dve.wait_ge(S["setup"], 1)
            for var in range(2):
                ins = nc.vector.tensor_scalar(bqv[:, var, :], bq[:, :], pick[:, var:var + 1], None, ALU.mult)
            ins.then_inc(S["setup"], 1)
            dve.wait_ge(S["setup"], 2)

        def pro_fill(pe, j, c, half, par):
            if j == 0:
                return turn(nc, keep, pro, h)
            if j in (qj, qj + 1) and j < kj:
                return project(nc, pro, wq if j == qj else wqr, hT, range(KT))
            if j == kj:
                pe.wait_ge(S["stream"][par], 16 * (half + 1))
            if j < vj:
                return project(nc, pro, wk if j == kj else wkr, cT[par], range(KT))
            return project_rows(nc, pro, cT[par], wv, 0, D)

        def pro_copy(eng, j, c, half, par):
            if j == 0:
                return nc.scalar.copy(flat(hT[:, :, :]), pro[:, :])
            if j == vj:
                return nc.vector.tensor_tensor(
                    v[par][:, :, :, 0:VD], pro[:, :].rearrange("p (t h v) -> p t h v", t=QT, h=H),
                    bv[:, :].rearrange("p (h v) -> p h v", h=H).unsqueeze(1).to_broadcast([P, QT, H, VD]),
                    ALU.add)
            if not rope:
                for k in range(KT):
                    if j == qj:
                        for var in range(2):
                            ins = nc.vector.tensor_scalar(
                                qT[par][:, var, k, :], pro[:, k * SEQ:(k + 1) * SEQ], pick[:, var:var + 1],
                                bqv[:, var, k:k + 1], ALU.mult, ALU.add)
                    else:
                        ins = nc.vector.tensor_scalar(kT[par][:, k, :], pro[:, k * SEQ:(k + 1) * SEQ],
                                                      bk[:, k:k + 1], None, ALU.add)
                return ins
            b, table, to = ((bq, cos, mixed), (bqr, sin, turned), (bk, cos, mixed), (bkr, sin, turned))[j - 1]
            for k in range(KT):
                ins = nc.vector.scalar_tensor_tensor(out=to[:, k, :], in0=pro[:, k * SEQ:(k + 1) * SEQ],
                                                     scalar=b[:, k:k + 1], in1=table[:, :],
                                                     op0=ALU.add, op1=ALU.mult)
            if j in (1, 3):
                return ins
            ins.then_inc(S["rope"], 1)
            eng.wait_ge(S["rope"], 3 * c + (1 if j == 2 else 3))
            if j == 4:
                return nc.vector.tensor_tensor(flat(kT[par][:, :, :]), flat(mixed[:, :, :]),
                                               flat(turned[:, :, :]), ALU.add)
            nc.vector.tensor_tensor(flat(mixed[:, :, :]), flat(mixed[:, :, :]), flat(turned[:, :, :]),
                                    ALU.add).then_inc(S["rope"], 1)
            eng.wait_ge(S["rope"], 3 * c + 2)
            for var in range(2):
                ins = nc.vector.tensor_scalar(qT[par][:, var, :, :], mixed[:, :, :], pick[:, var:var + 1],
                                              None, ALU.mult)
            return ins

        def epi_fill(pe, j, c, par):
            if j == 0:
                return turn(nc, keep, epi, o[par])
            return output_rows(nc, epi, oT, wo, bo[0:1, :], keep, KT)

        def epi_copy(eng, j, c, half, par):
            if j == 0:
                return nc.scalar.copy(flat(oT[:, :, :]), epi[:, :])
            return add_output(nc, eng, keep, epi, keep["gate"][:, (4 if rope else 0):(5 if rope else 1)], c)

        def row_max(dve, nmax, bank, c, h, p):
            if rope:
                return plain_max(nc, dve, nmax, bank, p)
            for t in range(QT):
                ins = nc.vector.tensor_tensor(masked[p][:, t, :], bank[:, t * SEQ:(t + 1) * SEQ], mask[:, t, :],
                                              ALU.add)
            ins.then_inc(S["masked"], 1)
            dve.wait_ge(S["masked"], 16 * c + h + 1)
            return nc.vector.tensor_reduce(nmax[:, p, :], masked[p][:, :, :], AX.X, ALU.min)

        def exp(act, prob, nmax, bank, h, p):
            if rope:
                return plain_exp(nc, act, prob, nmax, bank, p)
            return plain_exp(nc, act, prob, nmax, flat(masked[p][:, :, :]), p, scale=-1.0)

        def q_of(par, h, t):
            r = 32 * ((h % 8) // 2)
            return qT[par][r:r + 32, h % 2, h // 8, t * P:(t + 1) * P]

        def k_of(par, h):
            r = 32 * ((h % 8) // 2)
            return kT[par][r:r + 32, h // 8, :]

        return dict(weights=weights, setup=setup, act_setup=lambda act: None,
                    norm=x_norm(keep, h), norm_job=[0], norm_wait=lambda *a: None,
                    q=q_of, k=k_of, v=lambda par, h, k: v[par][:, k, h, :],
                    pro_fill=pro_fill, pro_copy=pro_copy, pro_frees=(qj if not rope else 2, kj if not rope else 4, vj),
                    pro_engine=lambda j: "act" if j == 0 else "dve",
                    epi_fill=epi_fill, epi_copy=epi_copy, epi_engine=lambda j: "act" if j == 0 else "dve",
                    pro_at=spread([3, 5, 6, 8, 9, 11] if rope else [4, 6, 8, 10]), epi_at=spread([2, 3]),
                    row_max=row_max, exp=exp)

    attention_stage(nc, keep, S, dict(
        name=L, heads=H, vd=VD, group=G, wide=False, narrow=True, n_pro=n_pro, n_epi=2, n_norm=1, pT_on_act=True,
        stream=lambda bufs, c, par: [(bufs["cT"][par][:, :, :],
                                      dram["ctxT"][bass.ds(c, 1), :, :, :].rearrange("a p k s -> (a p) k s"))],
        make=make))


def latent_attention(nc, keep, S, dram):
    H, VD, G, L, E = 16, 8, 4, "L0f", 8
    LAT = H * VD
    scale = float(np.float32(1.0) / np.sqrt(np.float32(VD)))
    R = 13

    def make(nc, keep, bufs, S, ctx):
        sb = bufs["sb"]
        wq, wk, wv = [sb(n, [P, KT, LAT]) for n in ("wq", "wk", "wv")]
        wo, router, b2 = sb("wo", [P, D]), sb("router", [P, KT, E]), sb("b2", [E, D])
        bq, bk, bo, br = sb("bq", [P, 1]), sb("bk", [P, 1]), sb("bo", [P, KT]), sb("br", [1, E])
        bqv, bv, pick = sb("bqv", [P, 4]), sb("bv", [P, LAT]), sb("pick", [P, 4])
        iota = sb("iota", [P, E])
        h, hT = sb("h", [P, QT, D]), sb("hT", [P, KT, SEQ])
        qT = [sb(f"qT{i}", [P, 4, SEQ]) for i in range(2)]
        kT = [sb(f"kT{i}", [P, SEQ]) for i in range(2)]
        v = [sb(f"v{i}", [P, QT, H, 32]) for i in range(2)]
        oT, mT = sb("oT", [P, SEQ]), sb("mT", [P, KT, SEQ])
        nm, tot, rtot = sb("nm", [P, QT]), sb("tot", [P, QT]), sb("rtot", [P, QT])
        e, top, idx = sb("e", [P, QT, E]), sb("top", [P, QT, 8]), sb("idx", [P, QT, 8], U32)
        idf, comb, hit = sb("idf", [P, QT, 8]), sb("comb", [P, QT, E]), sb("hit", [P, QT, E])
        combT = sb("combT", [E, SEQ])
        work, o = bufs["pro"], bufs["o"]

        weights = [(w[:, :, :], dram[L + n].rearrange("(k p) m -> p k m", p=P))
                   for w, n in ((wq, "wq"), (wk, "wk"), (wv, "wv"), (router, "router"))]
        weights += [(w[:, :], dram[L + n]) for w, n in ((wo, "wo"), (b2, "b2"), (bq, "bq"), (bk, "bk"), (bo, "bo"),
                                                        (br, "br"), (bv, "bv"))]
        weights += [(pick[:, :], dram["pick4"]), (iota[:, :], dram["iota"][:, 0:E])]

        def setup(dve):
            for i in range(2):
                nc.vector.memset(v[i][:, :, :, VD:VD + 1], 1.0)
                nc.vector.memset(v[i][:, :, :, VD + 1:32], 0.0)
            nc.vector.tensor_scalar(pick[:, :], pick[:, :], scale, None, ALU.mult).then_inc(S["setup"], 1)
            dve.wait_ge(S["setup"], 1)
            nc.vector.tensor_scalar(bqv[:, :], pick[:, :], bq[:, 0:1], None, ALU.mult).then_inc(S["setup"], 1)
            dve.wait_ge(S["setup"], 2)

        def norm_wait(dve, n, c, half, par):
            wait(dve, S["hs_saved"], 16 * c)
            nc.vector.memset(keep["scratch"][:, 1:2], 0.0)

        def pro_fill(pe, j, c, half, par):
            if j == 0:
                return turn(nc, keep, work, h)
            if j == 1:
                for i, w in enumerate((wq, wk)):
                    for k in range(KT):
                        mm = nc.tensor.matmul(work[:, i * SEQ:(i + 1) * SEQ], w[:, k, :], hT[:, k, :],
                                              start=(k == 0), stop=(k == KT - 1))
                return mm
            return project_rows(nc, work, hT, wv, 0, LAT)

        def pro_copy(eng, j, c, half, par):
            if j == 0:
                return nc.scalar.copy(flat(hT[:, :, :]), work[:, :])
            if j == 1:
                for i in range(4):
                    nc.vector.tensor_scalar(qT[par][:, i, :], work[:, 0:SEQ], pick[:, i:i + 1], bqv[:, i:i + 1],
                                            ALU.mult, ALU.add)
                return nc.vector.tensor_scalar(kT[par][:, :], work[:, SEQ:2 * SEQ], bk[:, 0:1], None, ALU.add)
            return nc.vector.tensor_tensor(
                v[par][:, :, :, 0:VD], work[:, 0:QT * LAT].rearrange("p (t h v) -> p t h v", t=QT, h=H),
                bv[:, :].rearrange("p (h v) -> p h v", h=H).unsqueeze(1).to_broadcast([P, QT, H, VD]), ALU.add)

        def epi_fill(pe, j, c, par):
            if j == 0:
                for t in range(QT):
                    mm = nc.tensor.transpose(work[:, t * P:(t + 1) * P], o[par][:, t, :], keep["ident"][:, :])
                return mm
            if j == 1:
                for m in range(KT):
                    mm = nc.tensor.matmul(work[:, m * SEQ:(m + 1) * SEQ], wo[:, m * P:(m + 1) * P], oT[:, :],
                                          start=True, stop=True)
                return mm
            for t in range(QT):
                if j == 2:
                    for k in range(KT):
                        nc.tensor.matmul(work[:, t * E:(t + 1) * E], mT[:, k, t * P:(t + 1) * P], router[:, k, :],
                                         start=(k == 0), stop=False)
                    mm = nc.tensor.matmul(work[:, t * E:(t + 1) * E], keep["ones"][0:1, :], br[0:1, :],
                                          start=False, stop=True)
                if j == 3:
                    mm = nc.tensor.transpose(work[0:E, t * P:(t + 1) * P], comb[:, t, :], keep["ident"][:, :])
                if j == 4:
                    mm = nc.tensor.matmul(work[:, t * D:(t + 1) * D], combT[:, t * P:(t + 1) * P], b2[:, :],
                                          start=True, stop=True)
            return mm

        def route(dve, c):
            n = [0]

            def linked(ins):
                n[0] += 1
                ins.then_inc(S["route"], 1)
                dve.wait_ge(S["route"], R * c + n[0])

            def take_wait():
                nc.vector.memset(keep["scratch"][:, 2:3], 0.0)

            logits = work[:, 0:QT * E].rearrange("p (t e) -> p t e", t=QT)
            nc.vector.tensor_reduce(nm[:, :], logits, AX.X, ALU.max, negate=True).then_inc(S["route_max"], 1)
            dve.wait_ge(S["route_exp"], c + 1)
            linked(nc.vector.tensor_reduce(tot[:, :], e[:, :, :], AX.X, ALU.add))
            linked(nc.vector.reciprocal(rtot[:, :], tot[:, :]))
            linked(nc.vector.tensor_tensor(e[:, :, :], e[:, :, :],
                                           rtot[:, :].unsqueeze(2).to_broadcast([P, QT, E]), ALU.mult))
            take_wait()
            for t in range(QT):
                ins = nc.vector.max(top[:, t, :], e[:, t, :])
            linked(ins)
            take_wait()
            for t in range(QT):
                ins = nc.vector.max_index(idx[:, t, :], top[:, t, :], e[:, t, :])
            linked(ins)
            linked(nc.vector.tensor_copy(idf[:, :, :], idx[:, :, :]))
            linked(nc.vector.tensor_tensor(tot[:, :], top[:, :, 0], top[:, :, 1], ALU.add))
            linked(nc.vector.tensor_scalar(tot[:, :], tot[:, :], 1e-8, None, ALU.add))
            linked(nc.vector.reciprocal(rtot[:, :], tot[:, :]))
            linked(nc.vector.tensor_tensor(top[:, :, 0:2], top[:, :, 0:2],
                                           rtot[:, :].unsqueeze(2).to_broadcast([P, QT, 2]), ALU.mult))
            for t in range(QT):
                nc.vector.tensor_scalar(comb[:, t, :], iota[:, :], idf[:, t, 0:1], top[:, t, 0:1],
                                        ALU.is_equal, ALU.mult)
                ins = nc.vector.tensor_scalar(hit[:, t, :], iota[:, :], idf[:, t, 1:2], top[:, t, 1:2],
                                              ALU.is_equal, ALU.mult)
            linked(ins)
            linked(nc.vector.tensor_tensor(comb[:, :, :], comb[:, :, :], hit[:, :, :], ALU.add))
            linked(nc.vector.tensor_scalar(keep["comb"][:, bass.ds(c * QT, QT), :], comb[:, :, :], 1.0, None,
                                           ALU.mult))
            assert n[0] == R
            return nc.vector.memset(keep["scratch"][:, 3:4], 0.0)

        def epi_copy(eng, j, c, half, par):
            if j == 0:
                return nc.scalar.copy(oT[:, :], work[:, 0:SEQ])
            if j == 1:
                wait(eng, S["mT_saved"], 16 * c)
                for m in range(KT):
                    ins = nc.vector.tensor_scalar(mT[:, m, :], work[:, m * SEQ:(m + 1) * SEQ], bo[:, m:m + 1], None,
                                                  ALU.add)
                return ins
            if j == 2:
                return route(eng, c)
            if j == 3:
                return nc.vector.tensor_copy(combT[:, :], work[0:E, 0:SEQ])
            eng.wait_ge(S["hs_saved"], 16 * (c + 1))
            hs = flat(keep["hs"][:, bass.ds(c * QT, QT), :])
            return nc.vector.scalar_tensor_tensor(out=hs, in0=work[:, :], scalar=0.3, in1=hs, op0=ALU.mult,
                                                  op1=ALU.add)

        def epi_act(act, j, c):
            if j == 2:
                act.wait_ge(S["route_max"], c + 1)
                for t in range(QT):
                    ins = nc.scalar.activation(e[:, t, :], work[:, t * E:(t + 1) * E], ACT.Exp,
                                               bias=nm[:, t:t + 1])
                ins.then_inc(S["route_exp"], 1)

        def save(sp, c):
            sp.wait_ge(S["normed"], c + 1)
            sp.dma_start(keep["hs"][:, bass.ds(c * QT, QT), :], h[:, :, :]).then_inc(S["hs_saved"], 16)

        def save_m(eng, c):
            eng.wait_ge(S["epi_copied"], 5 * c + 2)
            eng.dma_start(keep["mT"][:, :, bass.ds(c * SEQ, SEQ)], mT[:, :, :]).then_inc(S["mT_saved"], 16)

        def sync_more(sp):
            save(sp, 0)
            with sp.Fori(1, BATCH) as c:
                save(sp, c)
                save_m(sp, c - 1)
            save_m(sp, BATCH - 1)
            sp.wait_ge(S["mT_saved"], 16 * BATCH)

        def q_of(par, hh, t):
            r = 32 * (hh // 4)
            return qT[par][r:r + 32, hh % 4, t * P:(t + 1) * P]

        def k_of(par, hh):
            r = 32 * (hh // 4)
            return kT[par][r:r + 32, :]

        return dict(weights=weights, setup=setup, act_setup=lambda act: None, norm=x_norm(keep, h), norm_job=[0],
                    norm_wait=norm_wait, q=q_of, k=k_of, v=lambda par, hh, k: v[par][:, k, hh, :],
                    pro_fill=pro_fill, pro_copy=pro_copy, pro_frees=(1, 2),
                    pro_engine=lambda j: "act" if j == 0 else "dve",
                    epi_fill=epi_fill, epi_copy=epi_copy, epi_act=epi_act,
                    epi_engine=lambda j: "act" if j == 0 else "dve",
                    pro_at=spread([8, 10, 12]), epi_at=spread([2, 3, 4, 6, 7]), sync_more=sync_more,
                    row_max=lambda dve, nmax, bank, c, hh, p: plain_max(nc, dve, nmax, bank, p),
                    exp=lambda act, prob, nmax, bank, hh, p: plain_exp(nc, act, prob, nmax, bank, p))

    attention_stage(nc, keep, S, dict(name=L, heads=H, vd=VD, group=G, wide=False, narrow=True, n_pro=3, n_epi=5,
                                      n_norm=1, pT_on_act=True, make=make))


def experts_of_two(nc, keep, S, dram):
    E, F, N = 8, 512, 512
    FT, BT, BLOCKS = F // P, N // P, TOKENS // N
    L = "L0f"
    with ExitStack() as ctx:
        def sb(name, shape, dt=F32):
            return ctx.enter_context(nc.sbuf_tensor("moe0" + name, shape, dt))
        w1, w2 = sb("w1", [P, E, KT, F]), sb("w2", [P, E, FT, D])
        b1 = sb("b1", [P, E, FT])
        hT = [sb(f"hT{i}", [P, FT, N]) for i in range(2)]
        share, acc = sb("share", [P, BT, E]), sb("acc", [P, BT, D])
        hp = [ctx.enter_context(nc.psum_tensor(f"moe0h{i}", [P, N], F32)) for i in range(FT)]
        yp = [ctx.enter_context(nc.psum_tensor(f"moe0y{i}", [P, 2, D], F32)) for i in range(4)]

        with nc.Block() as block:
            @block.sync
            def _(sp):
                sp.dma_start(b1[:, :, :], dram[L + "b1"]).then_inc(S["weights"], 16)
                for e in range(E):
                    sp.dma_start(w1[:, e, :, :], dram[L + "w1"][e].rearrange("(k p) f -> p k f", p=P)
                                 ).then_inc(S["weights"], 16)
                    sp.dma_start(w2[:, e, :, :], dram[L + "w2"][e].rearrange("(k p) f -> p k f", p=P)
                                 ).then_inc(S["weights"], 16)

            @block.tensor
            def _(pe):
                pe.wait_ge(S["weights"], 16 * (2 * E + 1))

                def hidden(b, e):
                    for m in range(FT):
                        wait(pe, S["act"], FT * (E * b + e - 1) + m + 1)
                        for k in range(KT):
                            mm = nc.tensor.matmul(hp[m][:, :], w1[:, e, k, m * P:(m + 1) * P],
                                                  keep["mT"][:, k, bass.ds(b * N, N)],
                                                  start=(k == 0), stop=(k == KT - 1))
                        mm.then_inc(S["hidden"], 1)

                def outputs(b, e):
                    pe.wait_ge(S["act"], FT * (E * b + e + 1))
                    for t in range(BT):
                        if t % 2 == 0:
                            wait(pe, S["added"], BT * (E * b + e - 2) + t + 2)
                        for k in range(FT):
                            mm = nc.tensor.matmul(yp[2 * (e % 2) + t // 2][:, t % 2, :],
                                                  hT[e % 2][:, k, t * P:(t + 1) * P], w2[:, e, k, :],
                                                  start=(k == 0), stop=(k == FT - 1))
                        if t % 2 == 1:
                            mm.then_inc(S["y"], 1)

                def run(b):
                    hidden(b, 0)
                    for e in range(E):
                        if e + 1 < E:
                            hidden(b, e + 1)
                        outputs(b, e)
                run(0)
                with pe.Fori(1, BLOCKS) as b:
                    run(b)

            @block.scalar
            def _(act):
                act.wait_ge(S["weights"], 16)

                def run(b):
                    for e in range(E):
                        wait(act, S["y"], 2 * (E * b + e - 1))
                        for m in range(FT):
                            act.wait_ge(S["hidden"], FT * (E * b + e) + m + 1)
                            nc.scalar.activation(hT[e % 2][:, m, :], hp[m][:, :], ACT.Gelu,
                                                 bias=b1[:, e, m:m + 1]).then_inc(S["act"], 1)
                run(0)
                with act.Fori(1, BLOCKS) as b:
                    run(b)

            @block.vector
            def _(dve):
                def run(b):
                    wait(dve, S["added"], BT * E * b)
                    nc.vector.memset(keep["scratch"][:, 0:1], 0.0)
                    nc.vector.tensor_copy(share[:, :, :], keep["comb"][:, bass.ds(b * BT, BT), :]
                                          ).then_inc(S["share"], 1)
                    dve.wait_ge(S["share"], b + 1)
                    for e in range(E):
                        for t in range(BT):
                            if t % 2 == 0:
                                dve.wait_ge(S["y"], 2 * (E * b + e) + t // 2 + 1)
                            y = yp[2 * (e % 2) + t // 2][:, t % 2, :]
                            if e == 0:
                                wait(dve, S["moe_out"], 2 * b)
                                ins = nc.vector.tensor_scalar(acc[:, t, :], y, share[:, t, 0:1], None, ALU.mult)
                            else:
                                dve.wait_ge(S["added"], BT * (E * b + e - 1) + t + 1)
                                ins = nc.vector.scalar_tensor_tensor(out=acc[:, t, :], in0=y,
                                                                     scalar=share[:, t, e:e + 1],
                                                                     in1=acc[:, t, :], op0=ALU.mult, op1=ALU.add)
                            ins.then_inc(S["added"], 1)
                    dve.wait_ge(S["added"], BT * E * (b + 1))
                    nc.vector.scalar_tensor_tensor(out=flat(acc[:, :, :]), in0=flat(acc[:, :, :]), scalar=0.3,
                                                   in1=flat(keep["hs"][:, bass.ds(b * BT, BT), :]), op0=ALU.mult,
                                                   op1=ALU.add).then_inc(S["moe_out"], 1)
                    dve.wait_ge(S["moe_out"], 2 * b + 1)
                    xs = flat(keep["x"][:, bass.ds(b * BT, BT), :])
                    nc.vector.scalar_tensor_tensor(out=xs, in0=flat(acc[:, :, :]), scalar=keep["gate"][:, 1:2],
                                                   in1=xs, op0=ALU.mult, op1=ALU.add).then_inc(S["moe_out"], 1)
                run(0)
                with dve.Fori(1, BLOCKS) as b:
                    run(b)
    zero_semaphores(nc, S["all"])


def layer0_feed_forward(nc, keep, S, dram):
    with ExitStack() as ctx:
        keep = dict(keep, hs=ctx.enter_context(nc.sbuf_tensor("hs", [P, TILES, D], F32)),
                    mT=ctx.enter_context(nc.sbuf_tensor("mT", [P, KT, TOKENS], F32)),
                    comb=ctx.enter_context(nc.sbuf_tensor("comb", [P, TILES, 8], F32)))
        latent_attention(nc, keep, S, dram)
        experts_of_two(nc, keep, S, dram)


def cross_wide(nc, keep, S, dram, latents):
    VD, L = 64, "L3" if latents else "L1"
    H = 8 if latents else 16
    INNER = H * VD
    MT = INNER // P
    KEYS = 2 * SEQ if latents else SEQ
    CH = 4
    scale = VD ** -0.5
    kinds = [("h", 0)]
    if latents:
        kinds += [("c", 0)]
    kinds += [("q", m) for m in range(0, MT, 2)]
    for m in range(0, MT, 2):
        kinds += [("k", m)] + ([("kr", m)] if latents else [])
    if latents:
        kinds += [("kl", m) for m in range(0, MT, 2)]
    kinds += [("v", n) for n in range(0, H, CH)]
    if latents:
        kinds += [("vl", n) for n in range(0, H, CH)]
    NP, NE = len(kinds), MT // 2 + 1
    kinds_at = {k: i for i, k in enumerate(kinds)}

    def make(nc, keep, bufs, S, ctx):
        sb = bufs["sb"]
        wq, wkv = sb("wq", [P, KT, INNER]), sb("wkv", [P, KT, 2 * INNER])
        wo = sb("wo", [P, MT, D])
        gamma, beta = sb("gamma", [P, KT]), sb("beta", [P, KT])
        h, h2 = sb("h", [P, QT, D]), sb("h2", [P, QT, D])
        hT = sb("hT", [P, KT, SEQ])
        stream = [sb(f"stream{i}", [P, 2, SEQ]) for i in range(2)]
        qT = [sb(f"qT{i}", [P, MT, SEQ]) for i in range(2)]
        kT = [sb(f"kT{i}", [P, MT, KEYS]) for i in range(2)]
        v = [sb(f"v{i}", [P, KEYS // P, H, VD + 1]) for i in range(2)]
        oT = sb("oT", [P, MT, SEQ])
        bufs["stream"] = stream
        work, o = bufs["pro"], bufs["o"]
        weights = [(wq[:, :, :], dram[L + "wq"].rearrange("(k p) m -> p k m", p=P)),
                   (wkv[:, :, :], dram[L + "wkv"].rearrange("(k p) m -> p k m", p=P)),
                   (wo[:, :, :], dram[L + "wo"].rearrange("(k p) m -> p k m", p=P)),
                   (gamma[:, :], dram[L + "gamma"]), (beta[:, :], dram[L + "beta"])]
        bias = None
        if latents:
            wkr = sb("wkr", [P, KT, INNER])
            gammax, betax = sb("gammax", [P, KT]), sb("betax", [P, KT])
            cos, sin = sb("cos", [P, SEQ]), sb("sin", [P, SEQ])
            turned, mixed = sb("turned", [P, 2, SEQ]), sb("mixed", [P, 2, SEQ])
            ch, cT = sb("ch", [P, QT, D]), sb("cT", [P, KT, SEQ])
            weights += [(wkr[:, :, :], dram[L + "wkr"].rearrange("(k p) m -> p k m", p=P)),
                        (gammax[:, :], dram[L + "gammax"]), (betax[:, :], dram[L + "betax"]),
                        (cos[:, :], dram["cos64"]), (sin[:, :], dram["sin64"])]
        else:
            bo = sb("bo", [1, D])
            weights += [(bo[:, :], dram[L + "bo"])]
            bias = bo[0:1, :]

        def setup(dve):
            for i in range(2):
                ins = nc.vector.memset(v[i][:, :, :, VD:VD + 1], 1.0)
            ins.then_inc(S["setup"], 1)
            dve.wait_ge(S["setup"], 1)

        def norm(n, c, half, par):
            if n == 0:
                return x_norm(keep, h)(n, c, half, par)
            if n == 1:
                return (lambda t: h[:, t, :]), (lambda t: h2[:, t, :])
            return (lambda t: stream[par][:, t, :]), (lambda t: ch[:, t, :])

        def norm_wait(dve, n, c, half, par):
            if n == 1:
                dve.wait_ge(S["normed"], (3 if latents else 2) * c + 1)
            if n == 2:
                dve.wait_ge(S["stream"][par], 16 * (half + 1))

        def pro_fill(pe, j, c, half, par):
            kind, m = kinds[j]
            if kind in ("h", "c"):
                return turn(nc, keep, work, h2 if kind == "h" else ch)
            if kind == "q":
                return project(nc, work, wq, hT, (m, m + 1))
            if kind == "k":
                if not latents and m == 0:
                    pe.wait_ge(S["stream"][par], 16 * (half + 1))
                return project(nc, work, wkv, cT if latents else stream[par], (m, m + 1))
            if kind == "kr":
                return project(nc, work, wkr, cT, (m, m + 1))
            if kind == "kl":
                return project(nc, work, wkv, hT, (m, m + 1))
            src = hT if kind == "vl" else cT if latents else stream[par]
            return project_rows(nc, work, src, wkv, INNER + m * VD, CH * VD)

        def pro_copy(eng, j, c, half, par):
            kind, m = kinds[j]
            if kind in ("h", "c"):
                dst, g, b = (hT, gamma, beta) if kind == "h" else (cT, gammax, betax)
                for k in range(KT):
                    ins = nc.vector.tensor_scalar(dst[:, k, :], work[:, k * SEQ:(k + 1) * SEQ], g[:, k:k + 1],
                                                  b[:, k:k + 1], ALU.mult, ALU.add)
                return ins
            if kind == "q":
                return nc.scalar.mul(flat(qT[par][:, m:m + 2, :]), work[:, :], scale)
            if kind == "kl" or (kind == "k" and not latents):
                at = SEQ if kind == "kl" else 0
                return nc.scalar.copy(kT[par][:, m:m + 2, at:at + SEQ],
                                      work[:, :].rearrange("p (a b) -> p a b", a=2))
            if kind in ("v", "vl"):
                t0 = QT if kind == "vl" else 0
                for t in range(QT):
                    ins = nc.scalar.copy(v[par][:, t0 + t, m:m + CH, 0:VD],
                                         work[:, t * CH * VD:(t + 1) * CH * VD].rearrange("p (h v) -> p h v", h=CH))
                return ins
            to, table = (mixed, cos) if kind == "k" else (turned, sin)
            ins = nc.vector.tensor_tensor(to[:, :, :], work[:, :].rearrange("p (a b) -> p a b", a=2),
                                          table[:, :].unsqueeze(1).to_broadcast([P, 2, SEQ]), ALU.mult)
            if kind == "k":
                return ins
            ins.then_inc(S["rope"], 1)
            eng.wait_ge(S["rope"], (MT // 2) * c + m // 2 + 1)
            return nc.vector.tensor_tensor(kT[par][:, m:m + 2, 0:SEQ], mixed[:, :, :], turned[:, :, :], ALU.add)

        def epi_fill(pe, j, c, par):
            if j < NE - 1:
                return turn(nc, keep, work, o[par], slice(j * D, (j + 1) * D))
            return output_rows(nc, work, oT, wo, bias, keep, MT)

        def epi_copy(eng, j, c, half, par):
            if j < NE - 1:
                return nc.scalar.copy(flat(oT[:, 2 * j:2 * j + 2, :]), work[:, :])
            at = 6 if latents else 2
            return add_output(nc, eng, keep, work, keep["gate"][:, at:at + 1], c)

        def q_of(par, hh, t):
            r = 64 * (hh % 2)
            return qT[par][r:r + 64, hh // 2, t * P:(t + 1) * P]

        def k_of(par, hh):
            r = 64 * (hh % 2)
            return kT[par][r:r + 64, hh // 2, :]

        def row_max(dve, nmax, bank, c, hh, p):
            if latents:
                return nc.vector.tensor_reduce(nmax[:, p, 0:1], bank[:, :], AX.X, ALU.max, negate=True)
            return plain_max(nc, dve, nmax, bank, p)

        def exp(act, prob, nmax, bank, hh, p):
            if latents:
                return nc.scalar.activation(prob[:, :], bank[:, :], ACT.Exp, bias=nmax[:, p, 0:1])
            return plain_exp(nc, act, prob, nmax, bank, p)

        def pro_engine(j):
            return "dve" if kinds[j][0] in ("h", "c", "kr") or (latents and kinds[j][0] == "k") else "act"

        if latents:
            pro_at, epi_at = spread([6 + 0.5 * j for j in range(NP)]), spread([1.5, 2.5, 3.5])
        else:
            pro_at, epi_at = spread([7 + 0.5 * j for j in range(NP)]), spread([1, 2, 3, 4, 5])
        return dict(weights=weights, setup=setup, act_setup=lambda act: None, norm=norm,
                    norm_job=[None, 0, 1] if latents else [None, 0], norm_wait=norm_wait,
                    q=q_of, k=k_of, v=lambda par, hh, k: v[par][:, k, hh, :],
                    pro_fill=pro_fill, pro_copy=pro_copy,
                    pro_frees=[i for i, (k, m) in enumerate(kinds) if k not in ("h", "c")],
                    pro_engine=pro_engine, epi_fill=epi_fill, epi_copy=epi_copy,
                    epi_engine=lambda j: "act" if j < NE - 1 else "dve", pro_at=pro_at, epi_at=epi_at,
                    row_max=row_max, exp=exp)

    source = dram["ctx"] if latents else dram["ctxT"]
    attention_stage(nc, keep, S, dict(
        name=L, heads=H, vd=VD, group=2, wide=latents, narrow=False, n_pro=NP, n_epi=NE,
        n_norm=3 if latents else 2, pT_on_act=True,
        stream=lambda bufs, c, par: [(bufs["stream"][par][:, :, :],
                                      source[bass.ds(c, 1), :, :, :].rearrange("a p k s -> (a p) k s"))],
        make=make))


def relu_feed_forward(nc, keep, S, dram):
    F, N = 1024, 512
    FT, BT, BLOCKS = F // P, N // P, TOKENS // N
    L = "L2f"
    with ExitStack() as ctx:
        def sb(name, shape, dt=F32):
            return ctx.enter_context(nc.sbuf_tensor(L + name, shape, dt))
        w1, w2 = sb("w1", [P, KT, F]), sb("w2", [P, FT, D])
        b1, b2 = sb("b1", [P, FT]), sb("b2", [1, D])
        h, hT, aT = sb("h", [P, BT, D]), sb("hT", [P, KT, N]), sb("aT", [P, FT, N])
        st, mv, rstd = sb("st", [P, BT, 6]), sb("mv", [P, BT, 2]), sb("rstd", [P, BT])
        hp = [ctx.enter_context(nc.psum_tensor(f"{L}h{i}", [P, N], F32)) for i in range(4)]
        tp = [ctx.enter_context(nc.psum_tensor(f"{L}t{i}", [P, N], F32)) for i in range(KT)]
        yp = [ctx.enter_context(nc.psum_tensor(f"{L}y{i}", [P, 2, D], F32)) for i in range(2)]

        with nc.Block() as block:
            @block.sync
            def _(sp):
                sp.dma_start(w1[:, :, :], dram[L + "w1"].rearrange("(k p) f -> p k f", p=P)
                             ).then_inc(S["weights"], 16)
                sp.dma_start(w2[:, :, :], dram[L + "w2"].rearrange("(k p) f -> p k f", p=P)
                             ).then_inc(S["weights"], 16)
                sp.dma_start(b1[:, :], dram[L + "b1"]).then_inc(S["weights"], 16)
                sp.dma_start(b2[:, :], dram[L + "b2"]).then_inc(S["weights"], 16)

            @block.gpsimd
            def _(pool):
                def run(b):
                    pool.wait_ge(S["var"], b + 1)
                    nc.gpsimd.tensor_tensor(rstd[:, :], mv[:, :, 1], keep["eps"][:, :], ALU.add
                                            ).then_inc(S["vareps"], 1)
                    pool.wait_ge(S["vareps"], b + 1)
                    nc.gpsimd.tensor_tensor(rstd[:, :], rstd[:, :], keep["mhalf"][:, :], ALU.pow
                                            ).then_inc(S["rstd"], 1)
                run(0)
                with pool.Fori(1, BLOCKS) as b:
                    run(b)

            @block.vector
            def _(dve):
                def norm(b):
                    for t in range(BT):
                        ins = nc.vector.bn_stats(st[:, t, :],
                                                 keep["x"][:, bass.ds(b * BT + t, 1), :].rearrange("p a b -> p (a b)"))
                    ins.then_inc(S["stats"], 1)
                    dve.wait_ge(S["stats"], b + 1)
                    nc.vector.memset(keep["scratch"][:, 0:1], 0.0)
                    for t in range(BT):
                        ins = nc.vector.bn_aggr(mv[:, t, :], st[:, t, :])
                    ins.then_inc(S["var"], 1)
                    dve.wait_ge(S["rstd"], b + 1)
                    wait(dve, S["turned"], KT * b)
                    for t in range(BT):
                        ins = nc.vector.tensor_scalar(
                            h[:, t, :], keep["x"][:, bass.ds(b * BT + t, 1), :].rearrange("p a b -> p (a b)"),
                            mv[:, t, 0:1], rstd[:, t:t + 1], ALU.subtract, ALU.mult)
                    ins.then_inc(S["normed"], 1)

                def copy_turned(b):
                    for k in range(KT):
                        dve.wait_ge(S["turned"], KT * b + k + 1)
                        nc.vector.tensor_copy(hT[:, k, :], tp[k][:, :]).then_inc(S["turn_copied"], 1)

                def residual(b):
                    for i in range(2):
                        dve.wait_ge(S["y"], 2 * b + i + 1)
                        xs = flat(keep["x"][:, bass.ds(b * BT + 2 * i, 2), :])
                        nc.vector.scalar_tensor_tensor(out=xs, in0=flat(yp[i][:, :, :]), scalar=keep["gate"][:, 5:6],
                                                       in1=xs, op0=ALU.mult, op1=ALU.add).then_inc(S["added"], 1)

                def run(b, last=False):
                    if not last:
                        norm(b + 1)
                        copy_turned(b + 1)
                    residual(b)
                norm(0)
                copy_turned(0)
                run(0)
                with dve.Fori(1, BLOCKS - 1) as b:
                    run(b)
                run(BLOCKS - 1, last=True)

            @block.scalar
            def _(act):
                act.wait_ge(S["weights"], 64)

                def run(b):
                    wait(act, S["y"], 2 * b)
                    for m in range(FT):
                        act.wait_ge(S["hidden"], FT * b + m + 1)
                        nc.scalar.activation(aT[:, m, :], hp[m % 4][:, :], ACT.Relu, bias=b1[:, m:m + 1]
                                             ).then_inc(S["act"], 1)
                run(0)
                with act.Fori(1, BLOCKS) as b:
                    run(b)

            @block.tensor
            def _(pe):
                def turn_block(b):
                    pe.wait_ge(S["normed"], b + 1)
                    wait(pe, S["turn_copied"], KT * b)
                    for k in range(KT):
                        for t in range(BT):
                            mm = nc.tensor.transpose(tp[k][:, t * P:(t + 1) * P], h[:, t, k * P:(k + 1) * P],
                                                     keep["ident"][:, :])
                        mm.then_inc(S["turned"], 1)

                def run(b, last=False):
                    pe.wait_ge(S["turn_copied"], KT * (b + 1))
                    for m in range(FT):
                        wait(pe, S["act"], FT * b + m - 3)
                        for k in range(KT):
                            mm = nc.tensor.matmul(hp[m % 4][:, :], w1[:, k, m * P:(m + 1) * P], hT[:, k, :],
                                                  start=(k == 0), stop=(k == KT - 1))
                        mm.then_inc(S["hidden"], 1)
                    if not last:
                        turn_block(b + 1)
                    pe.wait_ge(S["act"], FT * (b + 1))
                    for t in range(BT):
                        if t % 2 == 0:
                            wait(pe, S["added"], 2 * (b - 1) + t // 2 + 1)
                        y = yp[t // 2][:, t % 2, :]
                        for k in range(FT):
                            nc.tensor.matmul(y, aT[:, k, t * P:(t + 1) * P], w2[:, k, :], start=(k == 0), stop=False)
                        mm = nc.tensor.matmul(y, keep["ones"][0:1, :], b2[0:1, :], start=False, stop=True)
                        if t % 2 == 1:
                            mm.then_inc(S["y"], 1)
                turn_block(0)
                pe.wait_ge(S["weights"], 64)
                run(0)
                with pe.Fori(1, BLOCKS - 1) as b:
                    run(b)
                run(BLOCKS - 1, last=True)
    zero_semaphores(nc, S["all"])


ROUND = 12582912.0
QMAX = 32767.0


def quantised_feed_forward(nc, keep, S, dram):
    F, N, W = 768, 512, 32
    FT, BT, BLOCKS = F // P, N // P, TOKENS // N
    L = "L3f"
    with ExitStack() as ctx:
        def sb(name, shape, dt=F32, ctx=ctx):
            return ctx.enter_context(nc.sbuf_tensor(L + name, shape, dt))
        wT = {n: sb(n + "T", [P, KT, F]) for n in ("up", "gate")}
        wT["down"] = sb("downT", [P, FT, D])
        hT = flat(keep["x"][:, :, :]).rearrange("p (k n) -> p k n", k=KT)
        peak, top, scale, inv = sb("peak", [P, TILES]), sb("top", [P, 8]), sb("scale", [P, 8]), sb("inv", [P, 8])

        def global_scale(dve, which, peaks, after):
            dve.wait_ge(S["peaks"], after)
            nc.vector.tensor_reduce(top[:, which:which + 1], peaks, AX.X, ALU.max).then_inc(S["local_top"], 1)
            dve.wait_ge(S["top"], 1)
            nc.vector.tensor_scalar(scale[:, which:which + 1], top[:, which:which + 1], 1.0 / QMAX, 1e-12,
                                    ALU.mult, ALU.max).then_inc(S["scale"], 1)
            dve.wait_ge(S["scale"], 1)
            nc.vector.reciprocal(inv[:, which:which + 1], scale[:, which:which + 1]).then_inc(S["inv"], 1)
            dve.wait_ge(S["inv"], 1)

        def global_top(pool, which):
            pool.wait_ge(S["local_top"], 1)
            nc.gpsimd.partition_all_reduce(top[:, which:which + 1], top[:, which:which + 1], P,
                                           bass.bass_isa.ReduceOp.max).then_inc(S["top"], 1)

        with ExitStack() as inner:
            raw = {n: sb(n, [P, FT * KT * P], ctx=inner) for n in ("up", "gate", "down")}
            amax, ws = sb("amax", [P, 3, 48], ctx=inner), sb("ws", [P, 3, 48], ctx=inner)
            wi = sb("wi", [P, 3, 48], ctx=inner)
            h = sb("h", [P, TILES, D], ctx=inner)
            st, mv = sb("st", [P, TILES, 6], ctx=inner), sb("mv", [P, TILES, 2], ctx=inner)
            rstd = sb("rstd", [P, TILES], ctx=inner)
            tp = [inner.enter_context(nc.psum_tensor(f"{L}t{i}", [P, 512], F32)) for i in range(4)]
            names = ("up", "gate", "down")
            WJ = 9
            LINKS = 7

            with nc.Block() as block:
                @block.sync
                def _(sp):
                    for n in names:
                        cols = D if n != "down" else F
                        sp.dma_start(raw[n][:, :].rearrange("p (a i) -> p a i", i=cols),
                                     dram[L + n].rearrange("(a p) i -> p a i", p=P)).then_inc(S["weights"], 16)
                    sp.dma_start(dram["x_spill"], keep["x"][:, :, :]).then_inc(S["stream"][0], 16)
                    sp.wait_ge(S["stream"][0], 16)

                @block.gpsimd
                def _(pool):
                    pool.wait_ge(S["var"], 1)
                    for q in range(TILES // BT):
                        nc.gpsimd.tensor_tensor(rstd[:, BT * q:BT * (q + 1)], mv[:, BT * q:BT * (q + 1), 1],
                                                keep["eps"][:, :], ALU.add).then_inc(S["vareps"], 1)
                    pool.wait_ge(S["vareps"], TILES // BT)
                    for q in range(TILES // BT):
                        nc.gpsimd.tensor_tensor(rstd[:, BT * q:BT * (q + 1)], rstd[:, BT * q:BT * (q + 1)],
                                                keep["mhalf"][:, :], ALU.pow).then_inc(S["rstd"], 1)
                    global_top(pool, 0)

                @block.vector
                def _(dve):
                    for t in range(TILES):
                        ins = nc.vector.bn_stats(st[:, t, :], keep["x"][:, t, :])
                    ins.then_inc(S["stats"], 1)
                    dve.wait_ge(S["stats"], 1)
                    for t in range(TILES):
                        ins = nc.vector.bn_aggr(mv[:, t, :], st[:, t, :])
                    ins.then_inc(S["var"], 1)
                    dve.wait_ge(S["weights"], 48)
                    done = [0]

                    def linked(ins):
                        done[0] += 1
                        ins.then_inc(S["route"], 1)
                        dve.wait_ge(S["route"], done[0])
                    for i, n in enumerate(names):
                        w = raw[n][:, :].rearrange("p (b w) -> p b w", w=W)
                        linked(nc.vector.tensor_reduce(amax[:, i, :], w, AX.X, ALU.max, apply_absolute_value=True))
                        linked(nc.vector.tensor_scalar(ws[:, i, :], amax[:, i, :], 1.0 / 7.0, 1e-12, ALU.mult,
                                                       ALU.max))
                        linked(nc.vector.reciprocal(wi[:, i, :], ws[:, i, :]))
                        linked(nc.vector.tensor_tensor(w, w, wi[:, i, :].unsqueeze(2).to_broadcast([P, 48, W]),
                                                       ALU.mult))
                        linked(nc.vector.tensor_scalar(w, w, ROUND, ROUND, ALU.add, ALU.subtract))
                        linked(nc.vector.tensor_scalar(w, w, -8.0, 7.0, ALU.max, ALU.min))
                        linked(nc.vector.tensor_tensor(w, w, ws[:, i, :].unsqueeze(2).to_broadcast([P, 48, W]),
                                                       ALU.mult))
                    assert done[0] == 3 * LINKS
                    dve.wait_ge(S["rstd"], TILES // BT)
                    for t in range(TILES):
                        ins = nc.vector.tensor_scalar(h[:, t, :], keep["x"][:, t, :], mv[:, t, 0:1], rstd[:, t:t + 1],
                                                      ALU.subtract, ALU.mult)
                    ins.then_inc(S["normed"], 1)
                    dve.wait_ge(S["normed"], 1)
                    nc.vector.tensor_reduce(peak[:, :], h[:, :, :], AX.X, ALU.max, apply_absolute_value=True
                                            ).then_inc(S["peaks"], 1)
                    global_scale(dve, 0, peak[:, :], 1)
                    QB = 8
                    for q in range(QB):
                        part = flat(h[:, q * TILES // QB:(q + 1) * TILES // QB, :])
                        nc.vector.tensor_scalar(part, part, inv[:, 0:1], ROUND, ALU.mult, ALU.add
                                                ).then_inc(S["rounded"], 1)
                    dve.wait_ge(S["rounded"], QB)
                    for q in range(QB):
                        part = flat(h[:, q * TILES // QB:(q + 1) * TILES // QB, :])
                        nc.vector.tensor_scalar(part, part, ROUND, scale[:, 0:1], ALU.subtract, ALU.mult
                                                ).then_inc(S["quantised"], 1)

                @block.tensor
                def _(pe):
                    n_bank = 0
                    for i, n in enumerate(names):
                        pe.wait_ge(S["route"], LINKS * (i + 1))
                        for j in range(3):
                            if n_bank >= 4:
                                pe.wait_ge(S["turn_copied"], n_bank - 3)
                            for q in range(4):
                                at = ((2 * j + q // 2) * D + (q % 2) * P) if n != "down" else (
                                    (q % 2) * F + (2 * j + q // 2) * P)
                                mm = nc.tensor.transpose(tp[n_bank % 4][:, q * P:(q + 1) * P], raw[n][:, at:at + P],
                                                         keep["ident"][:, :])
                            mm.then_inc(S["turned"], 1)
                            n_bank += 1
                    for b in range(BLOCKS):
                        pe.wait_ge(S["quantised"], b + 1)
                        for k in range(KT):
                            pe.wait_ge(S["turn_copied"], n_bank - 3)
                            for t in range(BT):
                                mm = nc.tensor.transpose(tp[n_bank % 4][:, t * P:(t + 1) * P],
                                                         h[:, BT * b + t, k * P:(k + 1) * P], keep["ident"][:, :])
                            mm.then_inc(S["turned"], 1)
                            n_bank += 1

                @block.scalar
                def _(act):
                    n_bank = 0
                    for n in names:
                        for j in range(3):
                            act.wait_ge(S["turned"], n_bank + 1)
                            src = tp[n_bank % 4][:, :]
                            if n == "down":
                                dst = flat(wT[n][:, 2 * j:2 * j + 2, :])
                            else:
                                src = src.rearrange("p (a k i) -> p k a i", a=2, k=KT)
                                dst = wT[n][:, :, 2 * j * P:(2 * j + 2) * P].rearrange("p k (a i) -> p k a i", a=2)
                            if n == "down":
                                nc.scalar.copy(dst, src).then_inc(S["turn_copied"], 1)
                            else:
                                nc.scalar.copy(dst[:, 0], src[:, 0])
                                nc.scalar.copy(dst[:, 1], src[:, 1]).then_inc(S["turn_copied"], 1)
                            n_bank += 1
                    act.wait_ge(S["stream"][0], 16)
                    act.wait_ge(S["normed"], 1)
                    for b in range(BLOCKS):
                        for k in range(KT):
                            act.wait_ge(S["turned"], n_bank + 1)
                            nc.scalar.copy(hT[:, k, b * N:(b + 1) * N], tp[n_bank % 4][:, :]
                                           ).then_inc(S["turn_copied"], 1)
                            n_bank += 1
            zero_semaphores(nc, S["all"])

        g = sb("g", [P, BLOCKS, FT * N])
        up = sb("upq", [P, BLOCKS, FT * N], I16)
        bank = [ctx.enter_context(nc.psum_tensor(f"{L}b{i}", [P, N], F32)) for i in range(6)]

        def project_all(which, quantise_up):
            with nc.Block() as block:
                @block.tensor
                def _(pe):
                    def run(b):
                        for m in range(FT):
                            wait(pe, S["copied"], FT * (b - 1) + m + 1)
                            for k in range(KT):
                                mm = nc.tensor.matmul(bank[m][:, :], wT[which][:, k, m * P:(m + 1) * P],
                                                      hT[:, k, bass.ds(b * N, N)], start=(k == 0), stop=(k == KT - 1))
                            mm.then_inc(S["hidden"], 1)
                    run(0)
                    with pe.Fori(1, BLOCKS) as b:
                        run(b)

                @block.scalar
                def _(act):
                    def run(b):
                        for m in range(FT):
                            if quantise_up:
                                act.wait_ge(S["quantised"], b + 1)
                            act.wait_ge(S["hidden"], FT * b + m + 1)
                            nc.scalar.copy(g[:, b, m * N:(m + 1) * N], bank[m][:, :]).then_inc(S["copied"], 1)
                    for b in range(BLOCKS):
                        run(b)

                @block.vector
                def _(dve):
                    def run(b):
                        if quantise_up:
                            g_b = g[:, bass.ds(b, 1), :].rearrange("p a b -> p (a b)")
                            nc.vector.tensor_scalar(g_b, g_b, inv[:, 1:2], ROUND, ALU.mult, ALU.add
                                                    ).then_inc(S["rounded"], 1)
                            dve.wait_ge(S["rounded"], b + 1)
                            nc.vector.tensor_scalar(up[:, bass.ds(b, 1), :].rearrange("p a b -> p (a b)"), g_b,
                                                    ROUND, None, ALU.subtract).then_inc(S["quantised"], 1)
                        wait(dve, S["peaks"], b)
                        dve.wait_ge(S["copied"], FT * (b + 1))
                        nc.vector.memset(keep["scratch"][:, 1:2], 0.0)
                        nc.vector.tensor_reduce(peaks[:, bass.ds(b, 1)],
                                                g[:, bass.ds(b, 1), :].rearrange("p a b -> p (a b)"), AX.X, ALU.max,
                                                apply_absolute_value=True).then_inc(S["peaks"], 1)
                    run(0)
                    with dve.Fori(1, BLOCKS) as b:
                        run(b)
                    global_scale(dve, 2 if quantise_up else 1, peaks[:, :], BLOCKS)

                @block.gpsimd
                def _(pool):
                    global_top(pool, 2 if quantise_up else 1)
            zero_semaphores(nc, S["all"])

        peaks = sb("peaks", [P, BLOCKS])
        project_all("up", False)
        project_all("gate", True)

        NP2 = 4
        HALF = FT * N // NP2
        sig = [sb(f"sig{i}", [P, HALF]) for i in range(2)]

        with nc.Block() as block:
            def part(i):
                return g[:, i // NP2, (i % NP2) * HALF:(i % NP2 + 1) * HALF]

            @block.vector
            def _(dve):
                n = BLOCKS * NP2

                def round_part(i, which):
                    nc.vector.tensor_scalar(part(i), part(i), inv[:, which:which + 1], ROUND, ALU.mult, ALU.add
                                            ).then_inc(S["rounded"], 1)

                def rescale_part(i, which, after):
                    dve.wait_ge(S["rounded"], after)
                    nc.vector.tensor_scalar(part(i), part(i), ROUND, scale[:, which:which + 1], ALU.subtract,
                                            ALU.mult).then_inc(S["quantised"], 1)

                def gated(i):
                    dve.wait_ge(S["act"], i + 1)
                    nc.vector.tensor_scalar(sig[i % 2][:, :], sig[i % 2][:, :], ROUND, 65535.0, ALU.subtract,
                                            ALU.min).then_inc(S["sig_clipped"], 1)
                    dve.wait_ge(S["sig_clipped"], i + 1)
                    nc.vector.scalar_tensor_tensor(out=part(i), in0=sig[i % 2][:, :], scalar=1.0 / 65536.0,
                                                   in1=part(i), op0=ALU.mult, op1=ALU.mult).then_inc(S["gated"], 1)
                    dve.wait_ge(S["gated"], i + 1)
                    nc.vector.tensor_reduce(peak[:, i:i + 1], part(i), AX.X, ALU.max, apply_absolute_value=True
                                            ).then_inc(S["peaks"], 1)
                round_part(0, 2)
                for i in range(n):
                    if i + 1 < n:
                        round_part(i + 1, 2)
                    rescale_part(i, 2, i + 1)
                    if i >= 1:
                        gated(i - 1)
                gated(n - 1)
                dve.wait_ge(S["peaks"], n)
                global_scale(dve, 3, peak[:, 0:n], n)

            @block.scalar
            def _(act):
                for i in range(BLOCKS * NP2):
                    act.wait_ge(S["quantised"], i + 1)
                    if i >= 2:
                        act.wait_ge(S["gated"], i - 1)
                    nc.scalar.activation(sig[i % 2][:, :], part(i), ACT.Sigmoid).then_inc(S["sigmoid"], 1)
                    act.wait_ge(S["sigmoid"], i + 1)
                    nc.scalar.activation(sig[i % 2][:, :], sig[i % 2][:, :], ACT.Copy, bias=ROUND, scale=65536.0
                                         ).then_inc(S["act"], 1)

            @block.gpsimd
            def _(pool):
                global_top(pool, 3)
        zero_semaphores(nc, S["all"])

        with nc.Block() as block:
            @block.vector
            def _(dve):
                n = BLOCKS * NP2

                def up_part(i):
                    return up[:, i // NP2, (i % NP2) * HALF:(i % NP2 + 1) * HALF]

                def round_part(i):
                    nc.vector.tensor_scalar(part(i), part(i), inv[:, 3:4], ROUND, ALU.mult, ALU.add
                                            ).then_inc(S["rounded"], 1)

                def multiply(i):
                    dve.wait_ge(S["rounded"], i + 1)
                    nc.vector.tensor_scalar(part(i), part(i), ROUND, scale[:, 3:4], ALU.subtract, ALU.mult
                                            ).then_inc(S["quantised"], 1)
                    dve.wait_ge(S["quantised"], i + 1)
                    nc.vector.scalar_tensor_tensor(out=part(i), in0=up_part(i), scalar=scale[:, 1:2], in1=part(i),
                                                   op0=ALU.mult, op1=ALU.mult).then_inc(S["gated"], 1)
                    dve.wait_ge(S["gated"], i + 1)
                    nc.vector.tensor_reduce(peak[:, i:i + 1], part(i), AX.X, ALU.max, apply_absolute_value=True
                                            ).then_inc(S["peaks"], 1)
                round_part(0)
                for i in range(n):
                    if i + 1 < n:
                        round_part(i + 1)
                    multiply(i)
                global_scale(dve, 4, peak[:, 0:n], n)

            @block.gpsimd
            def _(pool):
                global_top(pool, 4)
        zero_semaphores(nc, S["all"])

        if True:
            xo = [keep["x"][:, i, :] for i in range(2)]
            oq = [flat(keep["x"][:, 4 * i + 4:4 * i + 7, :]) for i in range(2)]
            yp = [bank[0], bank[1]]

            with nc.Block() as block:
                @block.vector
                def _(dve):
                    def quantise(b, q, par):
                        t = BT * b + q
                        src = g[:, bass.ds(b, 1), :].rearrange("p a (f n) -> p (a f) n", n=N)[:, :, q * P:(q + 1) * P]
                        dst = oq[par].rearrange("p (f n) -> p f n", n=P)
                        wait(dve, S["y"], t - 1)
                        nc.vector.tensor_scalar(dst, src, inv[:, 4:5], ROUND, ALU.mult, ALU.add
                                                ).then_inc(S["rounded"], 1)
                        dve.wait_ge(S["rounded"], t + 1)
                        nc.vector.tensor_scalar(oq[par], oq[par], ROUND, scale[:, 4:5], ALU.subtract,
                                                ALU.mult).then_inc(S["quantised"], 1)

                    def residual(b, q, par):
                        t = BT * b + q
                        dve.wait_ge(S["y"], t + 1)
                        dve.wait_ge(S["stream"][par], 16 * (2 * b + q // 2 + 1))
                        nc.vector.scalar_tensor_tensor(out=xo[par], in0=yp[par][:, 0:D],
                                                       scalar=keep["gate"][:, 7:8], in1=xo[par],
                                                       op0=ALU.mult, op1=ALU.add).then_inc(S["added"], 1)

                    def block_of(b, first=False):
                        for q in range(BT):
                            quantise(b, q, q % 2)
                            if q >= 1:
                                residual(b, q - 1, (q - 1) % 2)
                            elif not first:
                                residual(b - 1, BT - 1, 1)
                    block_of(0, first=True)
                    with dve.Fori(1, BLOCKS) as b:
                        block_of(b)
                    residual(BLOCKS - 1, BT - 1, 1)

                @block.tensor
                def _(pe):
                    def run(b):
                        for q in range(BT):
                            t = BT * b + q
                            pe.wait_ge(S["quantised"], t + 1)
                            wait(pe, S["added"], t - 1)
                            for k in range(FT):
                                mm = nc.tensor.matmul(yp[q % 2][:, 0:D], oq[q % 2][:, k * P:(k + 1) * P],
                                                      wT["down"][:, k, :], start=(k == 0), stop=(k == FT - 1))
                            mm.then_inc(S["y"], 1)
                    run(0)
                    with pe.Fori(1, BLOCKS) as b:
                        run(b)

                @block.sync
                def _(sp):
                    def load(i, par):
                        sp.dma_start(xo[par], dram["x_spill"][:, bass.ds(2 * i + par, 1), :].rearrange(
                            "p a d -> p (a d)")).then_inc(S["stream"][par], 16)

                    def store(i, par):
                        t = 2 * i + par
                        sp.wait_ge(S["added"], t + 1)
                        sp.dma_start(dram["out"][bass.ds(t * P, P), :], xo[par]).then_inc(S["stored"][par], 16)
                    load(0, 0)
                    load(0, 1)
                    with sp.Fori(0, TILES // 2 - 1) as i:
                        for par in range(2):
                            store(i, par)
                            sp.wait_ge(S["stored"][par], 16 * (i + 1))
                            load(i + 1, par)
                    for par in range(2):
                        store(TILES // 2 - 1, par)
                    for par in range(2):
                        sp.wait_ge(S["stored"][par], 16 * (TILES // 2))


def routed_experts(nc, keep, S, dram):
    E, K, CAP, F, L = 64, 8, 128, 192, "L1f"
    FH = F // 2
    SLOTS = E * CAP
    OUT_OF_RANGE = 65536.0
    AHEAD = 4
    with ExitStack() as ctx:
        def sb(name, shape, dt=F32, ctx=ctx):
            return ctx.enter_context(nc.sbuf_tensor(L + name, shape, dt))
        slots, share = sb("slots", [P, TILES, K], U32), sb("share", [P, TILES, K])

        def by_pairs(eng, run, tail=None):
            run(0, 0, 0)
            run(1, 0, 1)
            with eng.Fori(1, BATCH // 2) as i:
                run(2 * i, i + 0, 0)
                run(2 * i + 1, i + 0, 1)

        with ExitStack() as inner:
            def sbi(name, shape, dt=F32):
                return sb(name, shape, dt, ctx=inner)
            router = sbi("router", [P, KT, E])
            wsgu, wsd = sbi("wsgu", [P, KT, 2 * F]), sbi("wsd", [FH, 2, D])
            tri, iota = sbi("tri", [P, P]), sbi("iota", [P, E])
            h = [sbi(f"h{i}", [P, QT, D]) for i in range(2)]
            slot_of = [sbi(f"slot_of{i}", [P, QT, K], U32) for i in range(2)]
            hT = sbi("hT", [P, KT, SEQ])
            st, mv, rstd = sbi("st", [P, QT, 6]), sbi("mv", [P, QT, 2]), sbi("rstd", [P, QT])
            nm, tot, rtot = sbi("nm", [P, QT]), sbi("tot", [P, QT]), sbi("rtot", [P, QT])
            e, top, idx = sbi("e", [P, QT, E]), sbi("top", [P, QT, K]), sbi("idx", [P, QT, K], U32)
            idf, hit = sbi("idf", [P, QT, K]), sbi("hit", [P, QT, K, E])
            member, before = sbi("member", [P, QT, E]), sbi("before", [P, E])
            place, placed = sbi("place", [P, QT, K, E]), sbi("placed", [P, QT, K])
            late, slotf = sbi("late", [P, QT, K]), sbi("slotf", [P, QT, K])
            silu, act_h = sbi("silu", [FH, 2, SEQ]), sbi("act_h", [FH, 2, SEQ])
            zeros, tick = sbi("zeros", [P, 2048]), sbi("tick", [P, 2])
            turned = inner.enter_context(nc.psum_tensor(L + "pt", [P, 512], F32))
            logit = inner.enter_context(nc.psum_tensor(L + "pl", [P, 512], F32))
            posp = inner.enter_context(nc.psum_tensor(L + "pp", [P, 512], F32))
            gp = inner.enter_context(nc.psum_tensor(L + "pg", [FH, 512], F32))
            upp = inner.enter_context(nc.psum_tensor(L + "pu", [FH, 512], F32))
            yp = inner.enter_context(nc.psum_tensor(L + "py", [P, 512], F32))
            R = 18
            NW = 5

            with nc.Block() as block:
                @block.sync
                def _(sp):
                    sp.dma_start(router[:, :, :], dram[L + "router"].rearrange("(k p) m -> p k m", p=P)
                                 ).then_inc(S["weights"], 16)
                    sp.dma_start(wsgu[:, :, :], dram[L + "wsgu"].rearrange("(k p) m -> p k m", p=P)
                                 ).then_inc(S["weights"], 16)
                    sp.dma_start(wsd[:, :, :], dram[L + "wsd"].rearrange("(k p) m -> p k m", p=FH)
                                 ).then_inc(S["weights"], 16)
                    sp.dma_start(tri[:, :], dram["tri"]).then_inc(S["weights"], 16)
                    sp.dma_start(iota[:, :], dram["iota"]).then_inc(S["weights"], 16)
                    sp.wait_ge(S["setup"], 1)
                    for q in range(8):
                        sp.dma_start(dram["x_slots"][q * 1024:(q + 1) * 1024, :].rearrange("(p a) d -> p (a d)", p=P),
                                     zeros[:, :]).then_inc(S["zeroed"], 16)

                @block.gpsimd
                def _(pool):
                    pool.wait_ge(S["zeroed"], 128)

                    def rstds(c):
                        pool.wait_ge(S["var"], c + 1)
                        nc.gpsimd.tensor_tensor(rstd[:, :], mv[:, :, 1], keep["eps"][:, 0:QT], ALU.add
                                                ).then_inc(S["vareps"], 1)
                        pool.wait_ge(S["vareps"], c + 1)
                        nc.gpsimd.tensor_tensor(rstd[:, :], rstd[:, :], keep["mhalf"][:, 0:QT], ALU.pow
                                                ).then_inc(S["rstd"], 1)

                    def scatter(c, par):
                        wait(pool, S["tick"], c)
                        pool.wait_ge(S["slots"], c + 1)
                        nc.gpsimd.tensor_tensor(tick[:, 0:1], keep["eps"][:, 0:1], keep["eps"][:, 0:1], ALU.add
                                                ).then_inc(S["tick"], 1)
                        for t in range(QT):
                            for k in range(K):
                                nc.gpsimd.indirect_dma_start(
                                    dram["x_slots"], bass.IndirectOffsetOnAxis(slot_of[par][:, t, k:k + 1], 0),
                                    h[par][:, t, :], None, bounds_check=SLOTS - 1, oob_is_err=False
                                ).then_inc(S["scattered"][par], 16)
                    rstds(0)
                    rstds(1)
                    scatter(0, 0)
                    with pool.Fori(0, BATCH // 2 - 1) as i:
                        rstds(2 * i + 2)
                        scatter(2 * i + 1, 1)
                        rstds(2 * i + 3)
                        scatter(2 * i + 2, 0)
                    scatter(BATCH - 1, 1)
                    for par in range(2):
                        pool.wait_ge(S["scattered"][par], 16 * QT * K * BATCH // 2)

                @block.vector
                def _(dve):
                    nc.vector.memset(zeros[:, :], 0.0).then_inc(S["setup"], 1)
                    nc.vector.memset(before[:, :], 0.0).then_inc(S["counted"], 1)
                    dve.wait_ge(S["weights"], 16 * NW)

                    def run(c, half, par):
                        n = [0]

                        def linked(ins):
                            n[0] += 1
                            ins.then_inc(S["route"], 1)
                            dve.wait_ge(S["route"], R * c + n[0])

                        def take_wait():
                            nc.vector.memset(keep["scratch"][:, 2:3], 0.0)

                        def x_tile(t):
                            return keep["x"][:, bass.ds(c * QT + t, 1), :].rearrange("p a b -> p (a b)")

                        def per_token(ap, m):
                            return ap.unsqueeze(2).to_broadcast([P, QT, m])
                        for t in range(QT):
                            ins = nc.vector.bn_stats(st[:, t, :], x_tile(t))
                        linked(ins)
                        take_wait()
                        for t in range(QT):
                            ins = nc.vector.bn_aggr(mv[:, t, :], st[:, t, :])
                        ins.then_inc(S["var"], 1)
                        dve.wait_ge(S["rstd"], c + 1)
                        wait(dve, S["scattered"][par], 16 * QT * K * half)
                        wait(dve, S["turned"], c)
                        for t in range(QT):
                            ins = nc.vector.tensor_scalar(h[par][:, t, :], x_tile(t), mv[:, t, 0:1], rstd[:, t:t + 1],
                                                          ALU.subtract, ALU.mult)
                        ins.then_inc(S["normed"], 1)
                        dve.wait_ge(S["turned"], c + 1)
                        nc.vector.tensor_copy(flat(hT[:, :, :]), turned[:, :]).then_inc(S["turn_copied"], 1)
                        dve.wait_ge(S["logits"], c + 1)
                        nc.vector.tensor_reduce(nm[:, :], logit[:, 0:QT * E].rearrange("p (t e) -> p t e", t=QT),
                                                AX.X, ALU.max, negate=True).then_inc(S["route_max"], 1)
                        dve.wait_ge(S["route_exp"], c + 1)
                        linked(nc.vector.tensor_reduce(tot[:, :], e[:, :, :], AX.X, ALU.add))
                        linked(nc.vector.reciprocal(rtot[:, :], tot[:, :]))
                        linked(nc.vector.tensor_tensor(e[:, :, :], e[:, :, :], per_token(rtot[:, :], E), ALU.mult))
                        take_wait()
                        for t in range(QT):
                            ins = nc.vector.max(top[:, t, :], e[:, t, :])
                        linked(ins)
                        take_wait()
                        for t in range(QT):
                            ins = nc.vector.max_index(idx[:, t, :], top[:, t, :], e[:, t, :])
                        linked(ins)
                        linked(nc.vector.tensor_copy(idf[:, :, :], idx[:, :, :]))
                        linked(nc.vector.tensor_reduce(tot[:, :], top[:, :, :], AX.X, ALU.add))
                        linked(nc.vector.reciprocal(rtot[:, :], tot[:, :]))
                        nc.vector.tensor_tensor(top[:, :, :], top[:, :, :], per_token(rtot[:, :], K), ALU.mult)
                        for t in range(QT):
                            ins = nc.vector.tensor_tensor(
                                hit[:, t, :, :], iota[:, :].unsqueeze(1).to_broadcast([P, K, E]),
                                idf[:, t, :].unsqueeze(2).to_broadcast([P, K, E]), ALU.is_equal)
                        linked(ins)
                        for t in range(QT):
                            ins = nc.vector.tensor_reduce(member[:, t, :], hit[:, t, :, :].rearrange("p k e -> p e k"),
                                                          AX.X, ALU.add)
                        ins.then_inc(S["member"], 1)
                        dve.wait_ge(S["placed"], c + 1)
                        for t in range(QT):
                            ins = nc.vector.tensor_tensor(
                                place[:, t, :, :], hit[:, t, :, :],
                                posp[:, t * E:(t + 1) * E].unsqueeze(1).to_broadcast([P, K, E]), ALU.mult)
                        linked(ins)
                        linked(nc.vector.tensor_reduce(flat(placed[:, :, :]),
                                                       place[:, :, :, :].rearrange("p t k e -> p (t k) e"), AX.X,
                                                       ALU.add))
                        linked(nc.vector.tensor_tensor(before[:, :], before[:, :], member[:, 0, :], ALU.add))
                        nc.vector.tensor_tensor(before[:, :], before[:, :], member[:, 1, :], ALU.add
                                                ).then_inc(S["counted"], 1)
                        nc.vector.tensor_scalar(late[:, :, :], placed[:, :, :], float(CAP), OUT_OF_RANGE, ALU.is_ge,
                                                ALU.mult)
                        linked(nc.vector.scalar_tensor_tensor(out=flat(slotf[:, :, :]), in0=flat(idf[:, :, :]),
                                                              scalar=float(CAP), in1=flat(placed[:, :, :]),
                                                              op0=ALU.mult, op1=ALU.add))
                        linked(nc.vector.tensor_tensor(slotf[:, :, :], slotf[:, :, :], late[:, :, :], ALU.add))
                        nc.vector.tensor_copy(slot_of[par][:, :, :], slotf[:, :, :]).then_inc(S["slots"], 1)
                        linked(nc.vector.tensor_scalar(placed[:, :, :], placed[:, :, :], float(CAP), None, ALU.is_lt))
                        linked(nc.vector.tensor_tensor(top[:, :, :], top[:, :, :], placed[:, :, :], ALU.mult))
                        dve.wait_ge(S["slots"], c + 1)
                        nc.vector.tensor_scalar(keep["scratch"][:, 1:2], keep["eps"][:, 0:1], 0.0, None, ALU.mult)
                        nc.vector.tensor_copy(slots[:, bass.ds(c * QT, QT), :], slot_of[par][:, :, :])
                        linked(nc.vector.tensor_scalar(share[:, bass.ds(c * QT, QT), :], top[:, :, :],
                                                       keep["gate"][:, 3:4], None, ALU.mult))
                        assert n[0] == R, n[0]
                        dve.wait_ge(S["act"], c + 1)
                        dve.wait_ge(S["up"], c + 1)
                        nc.vector.tensor_tensor(flat(act_h[:, :, :]), flat(silu[:, :, :]), upp[:, :], ALU.mult
                                                ).then_inc(S["gated"], 1)
                        dve.wait_ge(S["y"], c + 1)
                        add_output(nc, dve, keep, yp, keep["gate"][:, 3:4], c).then_inc(S["added"], 1)
                    by_pairs(dve, run)

                @block.scalar
                def _(act):
                    def run(c, half, par):
                        act.wait_ge(S["route_max"], c + 1)
                        for t in range(QT):
                            ins = nc.scalar.activation(e[:, t, :], logit[:, t * E:(t + 1) * E], ACT.Exp,
                                                       bias=nm[:, t:t + 1])
                        ins.then_inc(S["route_exp"], 1)
                        act.wait_ge(S["up"], c + 1)
                        wait(act, S["gated"], c)
                        nc.scalar.activation(flat(silu[:, :, :]), gp[:, :], ACT.Silu).then_inc(S["act"], 1)
                    by_pairs(act, run)

                @block.tensor
                def _(pe):
                    pe.wait_ge(S["weights"], 16 * NW)

                    def run(c, half, par):
                        pe.wait_ge(S["normed"], c + 1)
                        wait(pe, S["turn_copied"], c)
                        turn(nc, keep, turned, h[par]).then_inc(S["turned"], 1)
                        pe.wait_ge(S["turn_copied"], c + 1)
                        wait(pe, S["route_exp"], c)
                        for t in range(QT):
                            for k in range(KT):
                                mm = nc.tensor.matmul(logit[:, t * E:(t + 1) * E], hT[:, k, t * P:(t + 1) * P],
                                                      router[:, k, :], start=(k == 0), stop=(k == KT - 1))
                        mm.then_inc(S["logits"], 1)
                        wait(pe, S["gated"], c)
                        for bank, at in ((gp, 0), (upp, F)):
                            for m in range(2):
                                for k in range(KT):
                                    mm = nc.tensor.matmul(bank[:, m * SEQ:(m + 1) * SEQ],
                                                          wsgu[:, k, at + m * FH:at + (m + 1) * FH], hT[:, k, :],
                                                          start=(k == 0), stop=(k == KT - 1))
                        mm.then_inc(S["up"], 1)
                        pe.wait_ge(S["member"], c + 1)
                        pe.wait_ge(S["counted"], c + 1)
                        for t in range(QT):
                            nc.tensor.matmul(posp[:, t * E:(t + 1) * E], tri[:, :], member[:, t, :],
                                             start=True, stop=False)
                            if t == 1:
                                nc.tensor.matmul(posp[:, t * E:(t + 1) * E], keep["ones"][:, :], member[:, 0, :],
                                                 start=False, stop=False)
                            mm = nc.tensor.matmul(posp[:, t * E:(t + 1) * E], keep["ones"][:, :], before[:, :],
                                                  start=False, stop=True)
                        mm.then_inc(S["placed"], 1)
                        pe.wait_ge(S["gated"], c + 1)
                        wait(pe, S["added"], c)
                        for t in range(QT):
                            for m in range(2):
                                mm = nc.tensor.matmul(yp[:, t * D:(t + 1) * D], act_h[:, m, t * P:(t + 1) * P],
                                                      wsd[:, m, :], start=(m == 0), stop=(m == 1))
                        mm.then_inc(S["y"], 1)
                    by_pairs(pe, run)
            zero_semaphores(nc, S["all"])

        with ExitStack() as inner:
            wgu = [sb(f"wgu{i}", [P, 2, KT, F], ctx=inner) for i in range(AHEAD)]
            wd = [sb(f"wd{i}", [FH, 2, D], ctx=inner) for i in range(AHEAD)]
            xs = [sb(f"xs{i}", [P, D], ctx=inner) for i in range(AHEAD)]
            xT = [sb(f"xT{i}", [P, KT, P], ctx=inner) for i in range(2)]
            silu = [sb(f"esilu{i}", [FH, 2, P], ctx=inner) for i in range(2)]
            act_h = [sb(f"eact{i}", [FH, 2, P], ctx=inner) for i in range(2)]
            y = [sb(f"y{i}", [P, D], ctx=inner) for i in range(2)]
            pt = [inner.enter_context(nc.psum_tensor(f"{L}et{i}", [P, KT * P], F32)) for i in range(2)]
            pg = inner.enter_context(nc.psum_tensor(L + "eg", [FH, 2, P], F32))
            pu = [inner.enter_context(nc.psum_tensor(f"{L}eu{i}", [FH, 2, P], F32)) for i in range(2)]
            py = [inner.enter_context(nc.psum_tensor(f"{L}ey{i}", [P, D], F32)) for i in range(2)]

            def first(e):
                return isinstance(e, int) and e == 0

            def by_experts(eng, run):
                for b in range(AHEAD):
                    run(b, 0, b, False)
                with eng.Fori(1, E // AHEAD - 1) as i:
                    for b in range(AHEAD):
                        run(AHEAD * i + b, i + 0, b, False)
                for b in range(AHEAD):
                    run(E - AHEAD + b, E // AHEAD - 1, b, b == AHEAD - 1)

            with nc.Block() as block:
                @block.sync
                def _(sp):
                    def run(e, quarter, b, last):
                        wait(sp, S["y"], e - AHEAD + 1)
                        for i, n in enumerate(("wg", "wu")):
                            sp.dma_start(wgu[b][:, i, :, :], dram[L + n][bass.ds(e, 1), :, :].rearrange(
                                "a (k p) f -> p (a k) f", p=P)).then_inc(S["stream"][b], 16)
                        sp.dma_start(wd[b][:, :, :], dram[L + "wd"][bass.ds(e, 1), :, :].rearrange(
                            "a (k p) f -> p (a k) f", p=FH)).then_inc(S["stream"][b], 16)
                        sp.dma_start(xs[b][:, :], dram["x_slots"][bass.ds(e * CAP, CAP), :]
                                     ).then_inc(S["stream"][b], 16)
                    by_experts(sp, run)

                @block.tensor
                def _(pe):
                    def turn_rows(e, quarter, b):
                        par = b % 2
                        pe.wait_ge(S["stream"][b], 64 * (quarter + 1))
                        wait(pe, S["turn_copied"], e - 1)
                        for k in range(KT):
                            mm = nc.tensor.transpose(pt[par][:, k * P:(k + 1) * P], xs[b][:, k * P:(k + 1) * P],
                                                     keep["ident"][:, :])
                        mm.then_inc(S["turned"], 1)

                    def hidden(e, b):
                        par = b % 2
                        pe.wait_ge(S["turn_copied"], e + 1)
                        for i, bank in ((0, pg), (1, pu[par])):
                            if i == 0:
                                wait(pe, S["act"], e)
                            else:
                                wait(pe, S["gated"], e - 1)
                            for m in range(2):
                                for k in range(KT):
                                    mm = nc.tensor.matmul(bank[:, m, :], wgu[b][:, i, k, m * FH:(m + 1) * FH],
                                                          xT[par][:, k, :], start=(k == 0), stop=(k == KT - 1))
                            mm.then_inc(S["hidden"], 1)

                    def outputs(e, b):
                        par = b % 2
                        pe.wait_ge(S["gated"], e + 1)
                        wait(pe, S["copied"], e - 1)
                        for m in range(2):
                            mm = nc.tensor.matmul(py[par][:, :], act_h[par][:, m, :], wd[b][:, m, :],
                                                  start=(m == 0), stop=(m == 1))
                        mm.then_inc(S["y"], 1)

                    def run(e, quarter, b, last):
                        hidden(e, b)
                        if not last:
                            turn_rows(e + 1, quarter + (b + 1) // AHEAD, (b + 1) % AHEAD)
                        if not first(e):
                            outputs(e - 1, (b - 1) % AHEAD)
                    turn_rows(0, 0, 0)
                    by_experts(pe, run)
                    outputs(E - 1, AHEAD - 1)

                @block.scalar
                def _(act):
                    def run(e, quarter, b, last):
                        par = b % 2
                        act.wait_ge(S["hidden"], 2 * e + 1)
                        wait(act, S["gated"], e - 1)
                        nc.scalar.activation(silu[par][:, :, :], pg[:, :, :], ACT.Silu).then_inc(S["act"], 1)
                        if not first(e):
                            if b:
                                store(e - 1, quarter, b - 1)
                            else:
                                store(e - 1, quarter - 1, AHEAD - 1)

                    def store(e, quarter, b):
                        par = b % 2
                        act.wait_ge(S["y"], e + 1)
                        wait(act, S["stored"][par], 16 * (2 * quarter + b // 2))
                        nc.scalar.copy(y[par][:, :], py[par][:, :]).then_inc(S["copied"], 1)
                        act.wait_ge(S["copied"], e + 1)
                        act.dma_start(dram["y_slots"][bass.ds(e * CAP, CAP), :], y[par][:, :]
                                      ).then_inc(S["stored"][par], 16)
                    by_experts(act, run)
                    store(E - 1, E // AHEAD - 1, AHEAD - 1)
                    for par in range(2):
                        act.wait_ge(S["stored"][par], 16 * E // 2)

                @block.vector
                def _(dve):
                    def run(e, quarter, b, last):
                        par = b % 2
                        dve.wait_ge(S["turned"], e + 1)
                        wait(dve, S["hidden"], 2 * (e - 1))
                        nc.vector.tensor_copy(flat(xT[par][:, :, :]), pt[par][:, :]).then_inc(S["turn_copied"], 1)

                    def gate(e, par):
                        dve.wait_ge(S["hidden"], 2 * e + 2)
                        dve.wait_ge(S["act"], e + 1)
                        wait(dve, S["y"], e - 1)
                        nc.vector.tensor_tensor(act_h[par][:, :, :], silu[par][:, :, :], pu[par][:, :, :], ALU.mult
                                                ).then_inc(S["gated"], 1)

                    def both(e, quarter, b, last):
                        gate(e, b % 2)
                        if not last:
                            run(e + 1, None, (b + 1) % AHEAD, False)
                    run(0, 0, 0, False)
                    by_experts(dve, both)
            zero_semaphores(nc, S["all"])

        with ExitStack() as inner:
            rows = [sb(f"rows{i}", [P, QT, K, D], ctx=inner) for i in range(2)]
            slot_of = [sb(f"gslot{i}", [P, QT, K], U32, ctx=inner) for i in range(2)]
            mine = [sb(f"mine{i}", [P, QT, K], ctx=inner) for i in range(2)]
            tick = sb("gtick", [P, 2], ctx=inner)

            with nc.Block() as block:
                @block.gpsimd
                def _(pool):
                    def run(c, half, par):
                        wait(pool, S["tick"], c)
                        pool.wait_ge(S["slots"], c + 1)
                        nc.gpsimd.tensor_tensor(tick[:, 0:1], keep["eps"][:, 0:1], keep["eps"][:, 0:1], ALU.add
                                                ).then_inc(S["tick"], 1)
                        for t in range(QT):
                            for k in range(K):
                                nc.gpsimd.indirect_dma_start(
                                    rows[par][:, t, k, :], None, dram["y_slots"],
                                    bass.IndirectOffsetOnAxis(slot_of[par][:, t, k:k + 1], 0),
                                    bounds_check=SLOTS - 1, oob_is_err=False).then_inc(S["gathered"][par], 16)
                    by_pairs(pool, run)

                @block.vector
                def _(dve):
                    for par in range(2):
                        nc.vector.memset(rows[par][:, :, :, :], 0.0)

                    def fetch(c, half, par):
                        wait(dve, S["added"], K * (c - 1))
                        wait(dve, S["slots"], c)
                        nc.vector.tensor_scalar(keep["scratch"][:, 1:2], keep["eps"][:, 0:1], 0.0, None, ALU.mult)
                        nc.vector.tensor_copy(mine[par][:, :, :], share[:, bass.ds(c * QT, QT), :])
                        nc.vector.tensor_copy(slot_of[par][:, :, :], slots[:, bass.ds(c * QT, QT), :]
                                              ).then_inc(S["slots"], 1)

                    def sums(c, half, par):
                        dve.wait_ge(S["gathered"][par], 16 * QT * K * (half + 1))
                        dve.wait_ge(S["slots"], c + 1)
                        for k in range(K):
                            if k:
                                dve.wait_ge(S["added"], K * c + k)
                            for t in range(QT):
                                xt = keep["x"][:, bass.ds(c * QT + t, 1), :].rearrange("p a b -> p (a b)")
                                ins = nc.vector.scalar_tensor_tensor(out=xt, in0=rows[par][:, t, k, :],
                                                                     scalar=mine[par][:, t, k:k + 1], in1=xt,
                                                                     op0=ALU.mult, op1=ALU.add)
                            ins.then_inc(S["added"], 1)
                    fetch(0, 0, 0)
                    fetch(1, 0, 1)
                    with dve.Fori(0, BATCH // 2 - 1) as i:
                        sums(2 * i, i + 0, 0)
                        fetch(2 * i + 2, None, 0)
                        sums(2 * i + 1, i + 0, 1)
                        fetch(2 * i + 3, None, 1)
                    sums(BATCH - 2, BATCH // 2 - 1, 0)
                    sums(BATCH - 1, BATCH // 2 - 1, 1)
            zero_semaphores(nc, S["all"])


def flamingo(nc, dram, out):
    with ExitStack() as ctx:
        def sb(name, shape, dt=F32):
            return ctx.enter_context(nc.sbuf_tensor(name, shape, dt))

        names = ["weights", "setup", "act_setup", "stats", "var", "vareps", "rstd", "normed", "pro_filled",
                 "pro_copied", "epi_filled", "epi_copied", "scores", "row_max", "exp", "pT", "pT_copied", "pv",
                 "rden", "hs_saved", "tick", "slots", "counted", "logits", "member", "placed", "zeroed", "up", "turned", "turn_copied", "peaks", "local_top", "top", "scale", "inv", "rounded", "quantised",
                 "copied", "sig_clipped", "gated", "sigmoid", "mT_saved", "route", "route_max", "route_exp", "hidden", "act", "y", "added", "share",
                 "moe_out", "o_ready", "raw", "back", "masked", "rope"] + []
        S = {n: ctx.enter_context(nc.semaphore(n)) for n in names}
        S["stream"] = [ctx.enter_context(nc.semaphore(f"stream{i}")) for i in range(4)]
        S["stored"] = [ctx.enter_context(nc.semaphore(f"stored{i}")) for i in range(2)]
        for n in ("scattered", "gathered"):
            S[n] = [ctx.enter_context(nc.semaphore(f"{n}{i}")) for i in range(2)]
        S["all"] = [S[n] for n in names] + S["stream"] + S["stored"] + S["scattered"] + S["gathered"]
        x_loaded = ctx.enter_context(nc.semaphore("x_loaded"))
        gates_loaded = ctx.enter_context(nc.semaphore("gates_loaded"))
        ready = ctx.enter_context(nc.semaphore("constants_ready"))
        tanh_done = ctx.enter_context(nc.semaphore("tanh_done"))

        keep = dict(x=sb("x", [P, TILES, D]), ident=sb("ident", [P, P]), ones=sb("ones", [P, P]),
                    mhalf=sb("mhalf", [P, 4]), eps=sb("eps", [P, 4]), scratch=sb("scratch", [P, 4]), gate=sb("gate", [P, 10]))

        with nc.Block() as block:
            @block.sync
            def _(sp):
                sp.dma_start(keep["gate"][:, 0:9], dram["gates"]).then_inc(gates_loaded, 16)
                sp.dma_start(keep["ident"][:, :], dram["ident"]).then_inc(gates_loaded, 16)
                for q in range(4):
                    n = TILES // 4
                    sp.dma_start(keep["x"][:, q * n:(q + 1) * n, :],
                                 dram["x"][q * n * P:(q + 1) * n * P, :].rearrange("(t p) d -> p t d", p=P)
                                 ).then_inc(x_loaded, 16)
                sp.wait_ge(x_loaded, 64)

            @block.vector
            def _(dve):
                nc.vector.memset(keep["ones"][:, :], 1.0)
                nc.vector.memset(keep["mhalf"][:, :], -0.5)
                nc.vector.memset(keep["eps"][:, :], EPS)
                dve.wait_ge(tanh_done, 1)
                nc.vector.tensor_tensor(keep["gate"][:, 2:3], keep["gate"][:, 2:3], keep["gate"][:, 8:9],
                                        ALU.mult).then_inc(ready, 1)

            @block.scalar
            def _(act):
                act.wait_ge(gates_loaded, 32)
                nc.scalar.activation(keep["gate"][:, 0:9], keep["gate"][:, 0:9], ACT.Tanh).then_inc(tanh_done, 1)

        stages = [lambda: cross_small(nc, keep, S, dram, rope=False),
                  lambda: layer0_feed_forward(nc, keep, S, dram),
                  lambda: cross_wide(nc, keep, S, dram, latents=False),
                  lambda: routed_experts(nc, keep, S, dram),
                  lambda: cross_small(nc, keep, S, dram, rope=True),
                  lambda: relu_feed_forward(nc, keep, S, dram),
                  lambda: cross_wide(nc, keep, S, dram, latents=True),
                  lambda: quantised_feed_forward(nc, keep, S, dram)]
        for stage in stages:
            stage()


def lay_out(inp):
    f = {k: np.asarray(v) for k, v in inp.items()}
    a = {}
    a["x"] = f["x"].reshape(TOKENS, D)
    a["ctxT"] = f["ctx_1024"].reshape(BATCH, SEQ, KT, P).transpose(0, 3, 2, 1)
    a["mask"] = f["mask_1x1xSxS2_fk1"].reshape(SEQ, SEQ)
    gates = np.stack([f["g_xattn"], f["g_ffn"]], axis=1).reshape(8)
    a["gates"] = np.broadcast_to(np.concatenate([gates, f["L1_xattn_gate"]]), (P, 9))
    a["ident"] = np.eye(P, dtype=np.float32)
    a["iota"] = np.broadcast_to(np.arange(64, dtype=np.float32), (P, 64))
    a["pick4"] = np.stack([(np.arange(P) // 8) % 4 == i for i in range(4)], axis=1).astype(np.float32)
    a["pick2"] = np.stack([(np.arange(P) // 16) % 2 == i for i in range(2)], axis=1).astype(np.float32)

    def col(b):
        return b.reshape(-1, P).T

    def rows(b):
        return np.broadcast_to(b, (P, b.size))
    a["L0wq"], a["L0wk"], a["L0wv"], a["L0wo"] = [f[f"L0_xattn_w{n}"] for n in "qkvo"]
    a["L0bq"], a["L0bk"] = col(f["L0_xattn_bq"]), col(f["L0_xattn_bk"])
    a["L0bv"], a["L0bo"] = rows(f["L0_xattn_bv"]), f["L0_xattn_bo"].reshape(1, D)
    a["L2wq"], a["L2wk"], a["L2wv"], a["L2wo"] = [f[f"L2_xattn_W{n}"].T for n in "qkvo"]
    a["L2bq"], a["L2bk"] = col(f["L2_xattn_bq"]), col(f["L2_xattn_bk"])
    a["L2bv"], a["L2bo"] = rows(f["L2_xattn_bv"]), f["L2_xattn_bo"].reshape(1, D)
    turn16 = (np.arange(D) // 16) * 16 + (np.arange(D) + 8) % 16
    a["L2wqr"], a["L2wkr"] = a["L2wq"][:, turn16], a["L2wk"][:, turn16]
    a["L2bqr"], a["L2bkr"] = col(f["L2_xattn_bq"][turn16]), col(f["L2_xattn_bk"][turn16])

    lat = (np.arange(16)[:, None] * 16 + np.arange(8)).reshape(-1)
    a["L0fwq"], a["L0fbq"] = f["L0_ffn_q_w"][:, lat], f["L0_ffn_q_b"][lat].reshape(P, 1)
    a["L0fwk"], a["L0fbk"] = f["L0_ffn_k_w"], f["L0_ffn_k_b"].reshape(P, 1)
    a["L0fwv"], a["L0fbv"] = f["L0_ffn_v_w"], rows(f["L0_ffn_v_b"])
    a["L0fwo"], a["L0fbo"] = f["L0_ffn_o_w"][:P], col(f["L0_ffn_o_b"])
    a["L0frouter"], a["L0fbr"] = f["L0_ffn_router_w"], f["L0_ffn_router_b"].reshape(1, 8)
    a["L0fw1"], a["L0fw2"], a["L0fb2"] = f["L0_ffn_w1"], f["L0_ffn_w2"], f["L0_ffn_b2"]
    a["L0fb1"] = f["L0_ffn_b1"].reshape(8, 4, P).transpose(2, 0, 1)

    a["L1wq"], a["L1wkv"], a["L1wo"] = f["L1_xattn_w_q"], f["L1_xattn_w_kv"], f["L1_xattn_w_out"]
    a["L1gamma"], a["L1beta"] = col(f["L1_xattn_ln_gamma"]), col(f["L1_xattn_ln_beta"])
    a["L1bo"] = f["L1_xattn_b_out"].reshape(1, D)
    a["L3wq"], a["L3wkv"], a["L3wo"] = f["L3_xattn_Wq"], f["L3_xattn_Wkv"], f["L3_xattn_Wo"]
    a["ctx"] = f["ctx_1024"].reshape(BATCH, QT, P, D).transpose(0, 2, 1, 3)
    turn64 = (np.arange(512) // 64) * 64 + (np.arange(512) + 32) % 64
    a["L3wkr"] = f["L3_xattn_Wkv"][:, turn64]
    a["L3gamma"], a["L3beta"] = col(f["L3_xattn_gamma_l"]), col(f["L3_xattn_beta_l"])
    a["L3gammax"], a["L3betax"] = col(f["L3_xattn_gamma_x"]), col(f["L3_xattn_beta_x"])

    a["L2fw1"], a["L2fw2"] = f["L2_ffn_W1"], f["L2_ffn_W2"]
    a["L2fb1"], a["L2fb2"] = col(f["L2_ffn_b1"]), f["L2_ffn_b2"].reshape(1, D)
    a["L3fup"], a["L3fgate"], a["L3fdown"] = f["L3_ffn_w_up"], f["L3_ffn_w_gate"], f["L3_ffn_w_down"]

    a["L1frouter"] = f["L1_ffn_router_w"].T
    a["L1fwg"], a["L1fwu"], a["L1fwd"] = f["L1_ffn_w_gate"], f["L1_ffn_w_up"], f["L1_ffn_w_down"]
    a["L1fwsgu"], a["L1fwsd"] = f["L1_ffn_ws_gate_up"], f["L1_ffn_ws_down"]
    a["tri"] = np.triu(np.ones((P, P), np.float32), 1)

    def rope_tables(dim):
        inv = (1.0 / 10000.0 ** (np.arange(0, dim, 2, dtype=np.float32) / np.float32(dim))).astype(np.float32)
        angle = np.arange(SEQ, dtype=np.float32)[:, None] * inv[None, :]
        cos, sin = np.cos(angle).T, np.sin(angle).T
        reps = P // dim
        return (np.tile(np.concatenate([cos, cos]), (reps, 1)).astype(np.float32),
                np.tile(np.concatenate([-sin, sin]), (reps, 1)).astype(np.float32))
    a["cos16"], a["sin16"] = rope_tables(16)
    a["cos64"], a["sin64"] = rope_tables(64)
    return {k: np.ascontiguousarray(v) for k, v in a.items()}


def kernel(**inputs):
    import concourse.bacc as bacc
    from concourse.bass_utils import run_bass_kernel_spmd

    arrays = lay_out(inputs)
    nc = bacc.Bacc("TRN2", target_bir_lowering=False, num_devices=1)
    dram = {k: nc.dram_tensor("in_" + k, list(v.shape), F32, kind="ExternalInput").ap()
            for k, v in arrays.items()}
    out = nc.dram_tensor("out_x", [TOKENS, D], F32, kind="ExternalOutput").ap()
    dram["out"] = out
    dram["x_spill"] = nc.dram_tensor("x_spill", [P, TILES, D], F32, kind="Internal").ap()
    for n in ("x_slots", "y_slots"):
        dram[n] = nc.dram_tensor(n, [64 * 128, D], F32, kind="Internal").ap()
    flamingo(nc, dram, out)
    r = run_bass_kernel_spmd(nc, [{"in_" + k: v for k, v in arrays.items()}], core_ids=[0])
    return r.results[0]["out_x"].reshape(BATCH, SEQ, D)
```

```python
from contextlib import ExitStack

import numpy as np

import concourse.bass as bass
from concourse import mybir

F32 = mybir.dt.float32
BF16 = mybir.dt.bfloat16
I16 = mybir.dt.int16
U32 = mybir.dt.uint32
ALU = mybir.AluOpType
ACT = mybir.ActivationFunctionType
AX = mybir.AxisListType

BATCH, SEQ, D = 16, 256, 256
TOKENS = BATCH * SEQ
P = 128
TILES = TOKENS // P
QT = SEQ // P
KT = D // P
EPS = 1e-5
BIG = 1.0e9


def wait(eng, sem, value):
    if isinstance(value, int) and value <= 0:
        return
    eng.wait_ge(sem, value)


def zero_semaphores(nc, sems):
    with nc.Block() as block:
        @block.gpsimd
        def _(pool):
            for s in sems:
                pool.sem_clear(s)


def attention_stage(nc, keep, S, cfg):
    UN = 16
    H, VD, G = cfg["heads"], cfg["vd"], cfg["group"]
    wide = cfg["wide"]
    NP, NE, NL = cfg["n_pro"], cfg["n_epi"], cfg["n_norm"]
    narrow = cfg["narrow"]
    VW = 32
    UG = G * (2 if wide else 1)
    NG = UN // UG
    pT_on_act = cfg["pT_on_act"]

    with ExitStack() as ctx:
        def sb(name, shape, dt=F32):
            return ctx.enter_context(nc.sbuf_tensor(cfg["name"] + name, shape, dt))

        def psum(name, shape):
            return ctx.enter_context(nc.psum_tensor(cfg["name"] + name, shape, F32))

        score = [psum(f"score{i}", [P, 512]) for i in range(4)]
        ptp = psum("ptp", [P, 512])
        pvp = [psum(f"pvp{i}", [P, 512]) for i in range(2)]
        work = psum("work", [P, 512])

        bufs = {}
        bufs["sb"], bufs["pro"], bufs["epi"] = sb, work, work
        prob = [sb(f"prob{i}", [P, 512]) for i in range(2)]
        pT = [sb(f"pT{i}", [P, 4, P]) for i in range(2)]
        nmax = sb("nmax", [P, 4, 2])
        if narrow:
            raw = [sb(f"raw{i}", [P, SEQ]) for i in range(2)]
            rden = sb("rden", [P, 2, 2, G])
            o = [sb(f"o{i}", [P, QT, H * VD]) for i in range(2)]
        else:
            sums, rden = sb("sums", [P, 4, 2]), sb("rden", [P, 4, 2])
            o = [sb(f"oT{i}", [P, H * VD // P, SEQ]) for i in range(2)]
        st = sb("st", [P, NL, QT, 6])
        mv = sb("mv", [P, NL, QT, 2])
        rstd = sb("rstd", [P, NL, QT])
        bufs.update(o=o, nmax=nmax)
        fns = cfg["make"](nc, keep, bufs, S, ctx)
        qT_of, kT_of, v_of = fns["q"], fns["k"], fns["v"]

        def for_batches(eng, head, body, tail):
            head()
            body(0, 0, 0, True, False)
            with eng.Fori(0, (BATCH - 2) // 2) as i:
                body(2 * i + 1, i + 0, 1, False, False)
                body(2 * i + 2, i + 1, 0, False, False)
            body(BATCH - 1, BATCH // 2 - 1, 1, False, True)
            tail()

        with nc.Block() as block:
            @block.sync
            def _(sp):
                for dst, src in fns["weights"]:
                    sp.dma_start(dst, src).then_inc(S["weights"], 16)
                if "stream" in cfg:
                    for c in range(2):
                        for dst, src in cfg["stream"](bufs, c, c):
                            sp.dma_start(dst, src).then_inc(S["stream"][c], 16)
                    with sp.Fori(0, BATCH // 2 - 1) as i:
                        for par in range(2):
                            sp.wait_ge(S["pro_filled"], NP * (2 * i + par + 1))
                            for dst, src in cfg["stream"](bufs, 2 * i + par + 2, par):
                                sp.dma_start(dst, src).then_inc(S["stream"][par], 16)

                if fns.get("sync_more"):
                    fns["sync_more"](sp)

            @block.gpsimd
            def _(pool):
                def rstds(c, half, par):
                    for n in range(NL):
                        pool.wait_ge(S["var"], NL * c + n + 1)
                        nc.gpsimd.tensor_tensor(rstd[:, n, :], mv[:, n, :, 1], keep["eps"][:, 0:QT],
                                                ALU.add).then_inc(S["vareps"], 1)
                        pool.wait_ge(S["vareps"], NL * c + n + 1)
                        nc.gpsimd.tensor_tensor(rstd[:, n, :], rstd[:, n, :], keep["mhalf"][:, 0:QT],
                                                ALU.pow).then_inc(S["rstd"], 1)
                    if fns.get("pool"):
                        fns["pool"](pool, c, half, par)
                rstds(0, 0, 0)
                with pool.Fori(1, BATCH) as c:
                    rstds(c, None, None)
                if fns.get("pool_tail"):
                    fns["pool_tail"](pool)

            @block.vector
            def _(dve):
                def norm(n, c, half, par):
                    src, dst = fns["norm"](n, c, half, par)
                    fns["norm_wait"](dve, n, c, half, par)
                    for t in range(QT):
                        ins = nc.vector.bn_stats(st[:, n, t, :], src(t))
                    ins.then_inc(S["stats"], 1)
                    dve.wait_ge(S["stats"], NL * c + n + 1)
                    nc.vector.memset(keep["scratch"][:, 0:1], 0.0)
                    for t in range(QT):
                        ins = nc.vector.bn_aggr(mv[:, n, t, :], st[:, n, t, :])
                    ins.then_inc(S["var"], 1)

                def normed(n, c, half, par):
                    src, dst = fns["norm"](n, c, half, par)
                    dve.wait_ge(S["rstd"], NL * c + n + 1)
                    if fns["norm_job"][n] is not None:
                        wait(dve, S["pro_filled"], NP * (c - 1) + fns["norm_job"][n] + 1)
                    for t in range(QT):
                        ins = nc.vector.tensor_scalar(dst(t), src(t), mv[:, n, t, 0:1],
                                                      rstd[:, n, t:t + 1], ALU.subtract, ALU.mult)
                    ins.then_inc(S["normed"], 1)

                def row_max(c, h, par):
                    p = h % 4
                    dve.wait_ge(S["scores"], UN * c + h + 1)
                    fns["row_max"](dve, nmax, score[p], c, h, p).then_inc(S["row_max"], 1)

                def copy_pT(c, h):
                    p = h % 2
                    dve.wait_ge(S["pT"], UN * c + h + 1)
                    wait(dve, S["pv"], UN * c + h - 1)
                    nc.vector.tensor_copy(pT[p][:, :, :].rearrange("p a b -> p (a b)"),
                                          ptp[:, :]).then_inc(S["pT_copied"], 1)

                def divide(c, h, par):
                    p, parts = h % 4, 1 if wide else QT
                    dve.wait_ge(S["exp"], UN * c + h + 1)
                    nc.vector.reciprocal(rden[:, p, 0:parts], sums[:, p, 0:parts]).then_inc(S["rden"], 1)
                    dve.wait_ge(S["rden"], UN * c + h + 1)
                    n = 512 // parts
                    for t in range(parts):
                        ins = nc.vector.tensor_scalar(prob[h % 2][:, t * n:(t + 1) * n],
                                                      prob[h % 2][:, t * n:(t + 1) * n],
                                                      rden[:, p, t:t + 1], None, ALU.mult)
                    ins.then_inc(S["scaled"], 1)

                def copy_out(c, g, par):
                    dve.wait_ge(S["pv"], UN * c + UG * (g + 1))
                    if g == 0:
                        wait(dve, S["epi_filled"], NE * (c - 1))
                    nc.vector.tensor_copy(o[par][:, g, :], pvp[g % 2][:, 0:SEQ]).then_inc(S["o_ready"], 1)

                def normalise(c, g, par):
                    p = g % 2
                    bank = pvp[1][:, 0:QT * G * VW].rearrange("p (t g v) -> p t g v", t=QT, g=G)
                    dve.wait_ge(S["back"], NG * c + g + 1)
                    nc.vector.reciprocal(rden[:, p, :, :], bank[:, :, :, VD]).then_inc(S["rden"], 1)
                    dve.wait_ge(S["rden"], NG * c + g + 1)
                    if g == 0:
                        wait(dve, S["epi_filled"], NE * (c - 1))
                    for t in range(QT):
                        r = rden[:, p, t, :].unsqueeze(2).to_broadcast([P, G, VD])
                        dst = o[par][:, t, g * G * VD:(g + 1) * G * VD].rearrange("p (g v) -> p g v", g=G)
                        ins = nc.vector.tensor_tensor(dst, bank[:, t, :, 0:VD], r, ALU.mult)
                    ins.then_inc(S["o_ready"], 1)

                def copy_raw(c, g):
                    dve.wait_ge(S["pv"], UN * c + UG * (g + 1))
                    wait(dve, S["back"], NG * c + g - 1)
                    nc.vector.tensor_copy(raw[g % 2][:, :], pvp[0][:, 0:SEQ]).then_inc(S["raw"], 1)

                def pro_copy(j, c, half, par):
                    if fns["pro_engine"](j) == "dve":
                        dve.wait_ge(S["pro_filled"], NP * c + j + 1)
                        if j in fns["pro_frees"]:
                            wait(dve, S["pv"], UN * (c - 1))
                        fns["pro_copy"](dve, j, c, half, par).then_inc(S["pro_copied"], 1)

                def epi_copy(j, c, half, par):
                    if fns["epi_engine"](j) == "dve":
                        dve.wait_ge(S["epi_filled"], NE * c + j + 1)
                        fns["epi_copy"](dve, j, c, half, par).then_inc(S["epi_copied"], 1)

                def prologue(c, half, par):
                    for n in range(NL):
                        norm(n, c, half, par)
                        normed(n, c, half, par)
                    for j in range(NP):
                        pro_copy(j, c, half, par)

                def head():
                    dve.wait_ge(S["weights"], 16 * len(fns["weights"]))
                    fns["setup"](dve)
                    prologue(0, 0, 0)
                    row_max(0, 0, 0)
                    row_max(0, 1, 0)
                    if not narrow:
                        divide(0, 0, 0)

                def body(c, half, par, first, last):
                    nxt = (c + 1, half + par, 1 - par)

                    def jobs(at):
                        if not first:
                            for j in fns["epi_at"](at):
                                epi_copy(j, c - 1, None, 1 - par)
                        if not last:
                            for j in fns["pro_at"](at):
                                pro_copy(j, *nxt)

                    for h in range(UN):
                        if h + 2 < UN:
                            row_max(c, h + 2, par)
                        elif not last:
                            row_max(c + 1, h + 2 - UN, 1 - par)
                        if narrow and h > UG and h % UG == 1:
                            normalise(c, h // UG - 1, par)
                        if narrow and h == 1 and not first:
                            normalise(c - 1, NG - 1, 1 - par)
                        if not narrow and h + 1 < UN:
                            divide(c, h + 1, par)
                        elif not narrow and not last:
                            divide(c + 1, 0, 1 - par)
                        jobs(h)
                        if not pT_on_act:
                            copy_pT(c, h)
                        if h >= 1 and h % UG == 0:
                            (copy_raw(c, h // UG - 1) if narrow else copy_out(c, h // UG - 1, par))
                        if h == 0 and not first:
                            (copy_raw(c - 1, NG - 1) if narrow else copy_out(c - 1, NG - 1, 1 - par))
                        jobs(h + 0.5)
                        if not last:
                            for n in range(NL):
                                if h == 2 * n:
                                    norm(n, *nxt)
                                if h == 2 * n + 1:
                                    normed(n, *nxt)

                def tail():
                    if narrow:
                        copy_raw(BATCH - 1, NG - 1)
                        normalise(BATCH - 1, NG - 1, 1)
                    else:
                        copy_out(BATCH - 1, NG - 1, 1)
                    for j in range(NE):
                        epi_copy(j, BATCH - 1, BATCH // 2 - 1, 1)

                for_batches(dve, head, body, tail)

            @block.scalar
            def _(act):
                def exp(c, h):
                    p = h % 2
                    act.wait_ge(S["row_max"], UN * c + h + 1)
                    wait(act, S["pT"], UN * c + h - 1)
                    if narrow:
                        ins = fns["exp"](act, prob[p], nmax, score[h % 4], h, h % 4)
                    else:
                        ins = fns["exp"](act, prob[p], nmax, score[h % 4], h, h % 4, sums)
                    ins.then_inc(S["exp"], 1)

                def copy_pT(c, h):
                    p = h % 2
                    act.wait_ge(S["pT"], UN * c + h + 1)
                    wait(act, S["pv"], UN * c + h - 1)
                    nc.scalar.copy(pT[p][:, :, :].rearrange("p a b -> p (a b)"),
                                   ptp[:, :]).then_inc(S["pT_copied"], 1)

                def pro_copy(j, c, half, par):
                    if fns["pro_engine"](j) == "act":
                        act.wait_ge(S["pro_filled"], NP * c + j + 1)
                        if j in fns["pro_frees"]:
                            wait(act, S["pv"], UN * (c - 1))
                        fns["pro_copy"](act, j, c, half, par).then_inc(S["pro_copied"], 1)

                def epi_copy(j, c, half, par):
                    if fns["epi_engine"](j) == "act":
                        act.wait_ge(S["epi_filled"], NE * c + j + 1)
                        fns["epi_copy"](act, j, c, half, par).then_inc(S["epi_copied"], 1)
                    if fns.get("epi_act"):
                        fns["epi_act"](act, j, c)

                def head():
                    act.wait_ge(S["weights"], 16 * len(fns["weights"]))
                    fns["act_setup"](act)
                    for j in range(NP):
                        pro_copy(j, 0, 0, 0)
                    exp(0, 0)

                def body(c, half, par, first, last):
                    nxt = (c + 1, half + par, 1 - par)

                    def jobs(at):
                        if not first:
                            for j in fns["epi_at"](at):
                                epi_copy(j, c - 1, None, 1 - par)
                        if not last:
                            for j in fns["pro_at"](at):
                                pro_copy(j, *nxt)

                    for h in range(UN):
                        if h + 1 < UN:
                            exp(c, h + 1)
                        elif not last:
                            exp(c + 1, 0)
                        jobs(h)
                        if pT_on_act:
                            copy_pT(c, h)
                        jobs(h + 0.5)

                def tail():
                    for j in range(NE):
                        epi_copy(j, BATCH - 1, BATCH // 2 - 1, 1)

                for_batches(act, head, body, tail)

            @block.tensor
            def _(pe):
                def scores(c, h, par):
                    p = h % 4
                    wait(pe, S["exp"], UN * c + h - 3)
                    if h == 0:
                        pe.wait_ge(S["pro_copied"], NP * (c + 1))
                    if wide:
                        head, t = h // 2, h % 2
                        mm = nc.tensor.matmul(score[p][:, :], qT_of(par, head, t), kT_of(par, head),
                                              start=True, stop=True)
                    else:
                        for t in range(QT):
                            mm = nc.tensor.matmul(score[p][:, t * SEQ:(t + 1) * SEQ], qT_of(par, h, t),
                                                  kT_of(par, h), start=True, stop=True)
                    mm.then_inc(S["scores"], 1)

                def transpose_probs(c, h):
                    p = h % 2
                    pe.wait_ge(S["exp" if narrow else "scaled"], UN * c + h + 1)
                    wait(pe, S["pT_copied"], UN * c + h)
                    for k in range(4):
                        to = k if wide else (k % 2) * 2 + k // 2
                        mm = nc.tensor.transpose(ptp[:, to * P:(to + 1) * P],
                                                 prob[p][:, k * P:(k + 1) * P], keep["ident"][:, :])
                    mm.then_inc(S["pT"], 1)

                def pv(c, h, par):
                    p = h % 2
                    g = h // UG
                    pe.wait_ge(S["pT_copied"], UN * c + h + 1)
                    if narrow:
                        if h % UG == 0:
                            wait(pe, S["raw"], NG * c + g)
                        r = 32 * (h % G)
                        for k in range(2):
                            mm = nc.tensor.matmul(pvp[0][r:r + 32, 0:SEQ], v_of(par, h, k),
                                                  pT[p][:, 2 * k:2 * k + 2, :], start=(k == 0), stop=(k == 1))
                        mm.then_inc(S["pv"], 1)
                        return
                    if h % UG == 0:
                        wait(pe, S["o_ready"], NG * c + g - 1)
                    r = 64 * ((h // 2 if wide else h) % 2)
                    if wide:
                        head, t = h // 2, h % 2
                        for k in range(4):
                            mm = nc.tensor.matmul(pvp[g % 2][r:r + 64, t * P:(t + 1) * P], v_of(par, head, k),
                                                  pT[p][:, k, :], start=(k == 0), stop=(k == 3))
                    else:
                        for k in range(2):
                            mm = nc.tensor.matmul(pvp[g % 2][r:r + 64, 0:SEQ], v_of(par, h, k),
                                                  pT[p][:, 2 * k:2 * k + 2, :], start=(k == 0), stop=(k == 1))
                    mm.then_inc(S["pv"], 1)

                def turn_back(c, g):
                    pe.wait_ge(S["raw"], NG * c + g + 1)
                    wait(pe, S["o_ready"], NG * c + g)
                    for t in range(QT):
                        mm = nc.tensor.transpose(pvp[1][:, t * P:(t + 1) * P], raw[g % 2][:, t * P:(t + 1) * P],
                                                 keep["ident"][:, :])
                    mm.then_inc(S["back"], 1)

                def pro_fill(j, c, half, par):
                    wait(pe, S["pro_copied"], NP * c + j)
                    if j == 0:
                        wait(pe, S["epi_copied"], NE * (c - 1))
                    if j in fns["norm_job"]:
                        pe.wait_ge(S["normed"], NL * c + fns["norm_job"].index(j) + 1)
                    fns["pro_fill"](pe, j, c, half, par).then_inc(S["pro_filled"], 1)

                def epi_fill(j, c, par):
                    wait(pe, S["epi_copied"], NE * c + j)
                    if j == 0:
                        pe.wait_ge(S["o_ready"], NG * (c + 1))
                    fns["epi_fill"](pe, j, c, par).then_inc(S["epi_filled"], 1)

                def head():
                    pe.wait_ge(S["weights"], 16 * len(fns["weights"]))
                    for j in range(NP):
                        pro_fill(j, 0, 0, 0)
                    scores(0, 0, 0)
                    scores(0, 1, 0)

                def body(c, half, par, first, last):
                    nxt = (c + 1, half + par, 1 - par)

                    def jobs(at):
                        if not first:
                            for j in fns["epi_at"](at):
                                epi_fill(j, c - 1, 1 - par)
                        if not last:
                            for j in fns["pro_at"](at):
                                pro_fill(j, *nxt)

                    for h in range(UN):
                        if h + 2 < UN:
                            scores(c, h + 2, par)
                        elif not last:
                            scores(c + 1, h + 2 - UN, 1 - par)
                        if h > 0:
                            pv(c, h - 1, par)
                        elif not first:
                            pv(c - 1, UN - 1, 1 - par)
                        if narrow and h > UG and h % UG == 1:
                            turn_back(c, h // UG - 1)
                        if narrow and h == 1 and not first:
                            turn_back(c - 1, NG - 1)
                        jobs(h)
                        transpose_probs(c, h)
                        jobs(h + 0.5)

                def tail():
                    pv(BATCH - 1, UN - 1, 1)
                    if narrow:
                        turn_back(BATCH - 1, NG - 1)
                    for j in range(NE):
                        epi_fill(j, BATCH - 1, 1)

                for_batches(pe, head, body, tail)
    zero_semaphores(nc, S["all"])


def spread(slots):
    return lambda h: [j for j, s in enumerate(slots) if s == h]


def plain_max(nc, dve, nmax, bank, p):
    return nc.vector.tensor_reduce(nmax[:, p, :], bank[:, :].rearrange("p (t k) -> p t k", t=QT), AX.X,
                                   ALU.max, negate=True)


def plain_exp(nc, act, prob, nmax, bank, p, scale=1.0):
    for t in range(QT):
        ins = nc.scalar.activation(prob[:, t * SEQ:(t + 1) * SEQ], bank[:, t * SEQ:(t + 1) * SEQ], ACT.Exp,
                                   bias=nmax[:, p, t:t + 1], scale=scale)
    return ins


def project(nc, bank, w, rhs, tiles, n=SEQ):
    for i, m in enumerate(tiles):
        for k in range(KT):
            mm = nc.tensor.matmul(bank[:, i * n:(i + 1) * n], w[:, k, m * P:(m + 1) * P], rhs[:, k, :],
                                  start=(k == 0), stop=(k == KT - 1))
    return mm


def project_rows(nc, bank, lhsT, w, cols, n):
    for t in range(QT):
        for k in range(KT):
            mm = nc.tensor.matmul(bank[:, t * n:(t + 1) * n], lhsT[:, k, t * P:(t + 1) * P],
                                  w[:, k, cols:cols + n], start=(k == 0), stop=(k == KT - 1))
    return mm


def turn(nc, keep, bank, rows, features=slice(0, D)):
    base = features.start
    for k in range(KT):
        for t in range(QT):
            mm = nc.tensor.transpose(bank[:, k * SEQ + t * P:k * SEQ + (t + 1) * P],
                                     rows[:, t, base + k * P:base + (k + 1) * P], keep["ident"][:, :])
    return mm


def output_rows(nc, bank, oT, w, bias, keep, parts):
    for t in range(QT):
        for k in range(parts):
            mm = nc.tensor.matmul(bank[:, t * D:(t + 1) * D], oT[:, k, t * P:(t + 1) * P], w[:, k, :],
                                  start=(k == 0), stop=(bias is None and k == parts - 1))
        if bias is not None:
            mm = nc.tensor.matmul(bank[:, t * D:(t + 1) * D], keep["ones"][0:1, :], bias,
                                  start=False, stop=True)
    return mm


def flat(ap):
    return ap.rearrange("p a b -> p (a b)")


def add_output(nc, dve, keep, bank, gate, c):
    xs = keep["x"][:, bass.ds(c * QT, QT), :]
    return nc.vector.scalar_tensor_tensor(out=flat(xs), in0=bank[:, :], scalar=gate, in1=flat(xs),
                                          op0=ALU.mult, op1=ALU.add)


def x_norm(keep, h):
    def norm(n, c, half, par):
        return (lambda t: keep["x"][:, bass.ds(c * QT + t, 1), :].rearrange("p a b -> p (a b)"),
                lambda t: h[:, t, :])
    return norm


def experts_of_two(nc, keep, S, dram):
    E, F, N = 8, 512, 512
    FT, BT, BLOCKS = F // P, N // P, TOKENS // N
    L = "L0f"
    with ExitStack() as ctx:
        def sb(name, shape, dt=F32):
            return ctx.enter_context(nc.sbuf_tensor("moe0" + name, shape, dt))
        w1, w2 = sb("w1", [P, E, KT, F]), sb("w2", [P, E, FT, D])
        b1 = sb("b1", [P, E, FT])
        hT = [sb(f"hT{i}", [P, FT, N]) for i in range(2)]
        share, acc = sb("share", [P, BT, E]), sb("acc", [P, BT, D])
        hp = [ctx.enter_context(nc.psum_tensor(f"moe0h{i}", [P, N], F32)) for i in range(FT)]
        yp = [ctx.enter_context(nc.psum_tensor(f"moe0y{i}", [P, 2, D], F32)) for i in range(4)]

        with nc.Block() as block:
            @block.sync
            def _(sp):
                sp.dma_start(b1[:, :, :], dram[L + "b1"]).then_inc(S["weights"], 16)
                for e in range(E):
                    sp.dma_start(w1[:, e, :, :], dram[L + "w1"][e].rearrange("(k p) f -> p k f", p=P)
                                 ).then_inc(S["expert_loaded"][e], 16)
                    sp.dma_start(w2[:, e, :, :], dram[L + "w2"][e].rearrange("(k p) f -> p k f", p=P)
                                 ).then_inc(S["expert_loaded"][e], 16)

            @block.tensor
            def _(pe):
                def hidden(b, e):
                    if isinstance(b, int):
                        pe.wait_ge(S["expert_loaded"][e], 32)
                    for m in range(FT):
                        wait(pe, S["act"], FT * (E * b + e - 1) + m + 1)
                        for k in range(KT):
                            mm = nc.tensor.matmul(hp[m][:, :], w1[:, e, k, m * P:(m + 1) * P],
                                                  keep["mT"][:, k, bass.ds(b * N, N)],
                                                  start=(k == 0), stop=(k == KT - 1))
                        mm.then_inc(S["hidden"], 1)

                def outputs(b, e):
                    pe.wait_ge(S["act"], FT * (E * b + e + 1))
                    for t in range(BT):
                        if t % 2 == 0:
                            wait(pe, S["added"], BT * (E * b + e - 2) + t + 2)
                        for k in range(FT):
                            mm = nc.tensor.matmul(yp[2 * (e % 2) + t // 2][:, t % 2, :],
                                                  hT[e % 2][:, k, t * P:(t + 1) * P], w2[:, e, k, :],
                                                  start=(k == 0), stop=(k == FT - 1))
                        if t % 2 == 1:
                            mm.then_inc(S["y"], 1)

                def run(b):
                    hidden(b, 0)
                    for e in range(E):
                        if e + 1 < E:
                            hidden(b, e + 1)
                        outputs(b, e)
                run(0)
                with pe.Fori(1, BLOCKS) as b:
                    run(b)

            @block.scalar
            def _(act):
                act.wait_ge(S["weights"], 16)

                def run(b):
                    for e in range(E):
                        wait(act, S["y"], 2 * (E * b + e - 1))
                        for m in range(FT):
                            act.wait_ge(S["hidden"], FT * (E * b + e) + m + 1)
                            nc.scalar.activation(hT[e % 2][:, m, :], hp[m][:, :], ACT.Gelu,
                                                 bias=b1[:, e, m:m + 1]).then_inc(S["act"], 1)
                run(0)
                with act.Fori(1, BLOCKS) as b:
                    run(b)

            @block.vector
            def _(dve):
                def run(b):
                    wait(dve, S["added"], BT * E * b)
                    nc.vector.memset(keep["scratch"][:, 0:1], 0.0)
                    nc.vector.tensor_copy(share[:, :, :], keep["comb"][:, bass.ds(b * BT, BT), :]
                                          ).then_inc(S["share"], 1)
                    dve.wait_ge(S["share"], b + 1)
                    for e in range(E):
                        for t in range(BT):
                            if t % 2 == 0:
                                dve.wait_ge(S["y"], 2 * (E * b + e) + t // 2 + 1)
                            y = yp[2 * (e % 2) + t // 2][:, t % 2, :]
                            if e == 0:
                                wait(dve, S["moe_out"], 2 * b)
                                ins = nc.vector.tensor_scalar(acc[:, t, :], y, share[:, t, 0:1], None, ALU.mult)
                            else:
                                dve.wait_ge(S["added"], BT * (E * b + e - 1) + t + 1)
                                ins = nc.vector.scalar_tensor_tensor(out=acc[:, t, :], in0=y,
                                                                     scalar=share[:, t, e:e + 1],
                                                                     in1=acc[:, t, :], op0=ALU.mult, op1=ALU.add)
                            ins.then_inc(S["added"], 1)
                    dve.wait_ge(S["added"], BT * E * (b + 1))
                    nc.vector.scalar_tensor_tensor(out=flat(acc[:, :, :]), in0=flat(acc[:, :, :]), scalar=0.3,
                                                   in1=flat(keep["hs"][:, bass.ds(b * BT, BT), :]), op0=ALU.mult,
                                                   op1=ALU.add).then_inc(S["moe_out"], 1)
                    dve.wait_ge(S["moe_out"], 2 * b + 1)
                    xs = flat(keep["x"][:, bass.ds(b * BT, BT), :])
                    nc.vector.scalar_tensor_tensor(out=xs, in0=flat(acc[:, :, :]), scalar=keep["gate"][:, 1:2],
                                                   in1=xs, op0=ALU.mult, op1=ALU.add).then_inc(S["moe_out"], 1)
                run(0)
                with dve.Fori(1, BLOCKS) as b:
                    run(b)
    zero_semaphores(nc, S["all"])


def layer0_feed_forward(nc, keep, S, dram):
    with ExitStack() as ctx:
        keep = dict(keep, hs=ctx.enter_context(nc.sbuf_tensor("hs", [P, TILES, D], F32)),
                    mT=ctx.enter_context(nc.sbuf_tensor("mT", [P, KT, TOKENS], F32)),
                    comb=ctx.enter_context(nc.sbuf_tensor("comb", [P, TILES, 8], F32)))
        latent_attention(nc, keep, S, dram)
        experts_of_two(nc, keep, S, dram)


def cross_wide(nc, keep, S, dram, latents):
    VD, L = 64, "L3" if latents else "L1"
    H = 8 if latents else 16
    INNER = H * VD
    MT = INNER // P
    KEYS = 2 * SEQ if latents else SEQ
    CH = 4
    scale = VD ** -0.5
    kinds = [("h", 0)]
    if latents:
        kinds += [("c", 0)]
    kinds += [("q", m) for m in range(0, MT, 2)]
    for m in range(0, MT, 2):
        kinds += [("k", m)] + ([("kr", m)] if latents else [])
    if latents:
        kinds += [("kl", m) for m in range(0, MT, 2)]
    kinds += [("v", n) for n in range(0, H, CH)]
    if latents:
        kinds += [("vl", n) for n in range(0, H, CH)]
    NP, NE = len(kinds), QT
    kinds_at = {k: i for i, k in enumerate(kinds)}

    def make(nc, keep, bufs, S, ctx):
        sb = bufs["sb"]
        wq, wkv = sb("wq", [P, KT, INNER]), sb("wkv", [P, KT, 2 * INNER])
        wo = sb("wo", [P, MT, D])
        gamma, beta = sb("gamma", [P, KT]), sb("beta", [P, KT])
        h, h2 = sb("h", [P, QT, D]), sb("h2", [P, QT, D])
        hT = sb("hT", [P, KT, SEQ])
        stream = [sb(f"stream{i}", [P, 2, SEQ]) for i in range(2)]
        qT = [sb(f"qT{i}", [P, MT, SEQ]) for i in range(2)]
        kT = [sb(f"kT{i}", [P, MT, KEYS]) for i in range(2)]
        v = [sb(f"v{i}", [P, KEYS // P, H, VD]) for i in range(2)]
        bufs["stream"] = stream
        work, o = bufs["pro"], bufs["o"]
        weights = [(wq[:, :, :], dram[L + "wq"].rearrange("(k p) m -> p k m", p=P)),
                   (wkv[:, :, :], dram[L + "wkv"].rearrange("(k p) m -> p k m", p=P)),
                   (wo[:, :, :], dram[L + "wo"].rearrange("(k p) m -> p k m", p=P)),
                   (gamma[:, :], dram[L + "gamma"]), (beta[:, :], dram[L + "beta"])]
        bias = None
        if latents:
            wkr = sb("wkr", [P, KT, INNER])
            gammax, betax = sb("gammax", [P, KT]), sb("betax", [P, KT])
            cos, sin = sb("cos", [P, SEQ]), sb("sin", [P, SEQ])
            turned, mixed = sb("turned", [P, 2, SEQ]), sb("mixed", [P, 2, SEQ])
            ch, cT = sb("ch", [P, QT, D]), sb("cT", [P, KT, SEQ])
            weights += [(wkr[:, :, :], dram[L + "wkr"].rearrange("(k p) m -> p k m", p=P)),
                        (gammax[:, :], dram[L + "gammax"]), (betax[:, :], dram[L + "betax"]),
                        (cos[:, :], dram["cos64"]), (sin[:, :], dram["sin64"])]
        else:
            bo = sb("bo", [1, D])
            weights += [(bo[:, :], dram[L + "bo"])]
            bias = bo[0:1, :]

        def setup(dve):
            pass

        def norm(n, c, half, par):
            if n == 0:
                return x_norm(keep, h)(n, c, half, par)
            if n == 1:
                return (lambda t: h[:, t, :]), (lambda t: h2[:, t, :])
            return (lambda t: stream[par][:, t, :]), (lambda t: ch[:, t, :])

        def norm_wait(dve, n, c, half, par):
            if n == 1:
                dve.wait_ge(S["normed"], (3 if latents else 2) * c + 1)
            if n == 2:
                dve.wait_ge(S["stream"][par], 16 * (half + 1))

        def pro_fill(pe, j, c, half, par):
            kind, m = kinds[j]
            if kind in ("h", "c"):
                return turn(nc, keep, work, h2 if kind == "h" else ch)
            if kind == "q":
                return project(nc, work, wq, hT, (m, m + 1))
            if kind == "k":
                if not latents and m == 0:
                    pe.wait_ge(S["stream"][par], 16 * (half + 1))
                return project(nc, work, wkv, cT if latents else stream[par], (m, m + 1))
            if kind == "kr":
                return project(nc, work, wkr, cT, (m, m + 1))
            if kind == "kl":
                return project(nc, work, wkv, hT, (m, m + 1))
            src = hT if kind == "vl" else cT if latents else stream[par]
            return project_rows(nc, work, src, wkv, INNER + m * VD, CH * VD)

        def pro_copy(eng, j, c, half, par):
            kind, m = kinds[j]
            if kind in ("h", "c"):
                dst, g, b = (hT, gamma, beta) if kind == "h" else (cT, gammax, betax)
                for k in range(KT):
                    ins = nc.vector.tensor_scalar(dst[:, k, :], work[:, k * SEQ:(k + 1) * SEQ], g[:, k:k + 1],
                                                  b[:, k:k + 1], ALU.mult, ALU.add)
                return ins
            if kind == "q":
                return nc.scalar.mul(flat(qT[par][:, m:m + 2, :]), work[:, :], scale)
            if kind == "kl" or (kind == "k" and not latents):
                at = SEQ if kind == "kl" else 0
                return nc.scalar.copy(kT[par][:, m:m + 2, at:at + SEQ],
                                      work[:, :].rearrange("p (a b) -> p a b", a=2))
            if kind in ("v", "vl"):
                t0 = QT if kind == "vl" else 0
                for t in range(QT):
                    ins = nc.scalar.copy(v[par][:, t0 + t, m:m + CH, 0:VD],
                                         work[:, t * CH * VD:(t + 1) * CH * VD].rearrange("p (h v) -> p h v", h=CH))
                return ins
            to, table = (mixed, cos) if kind == "k" else (turned, sin)
            ins = nc.vector.tensor_tensor(to[:, :, :], work[:, :].rearrange("p (a b) -> p a b", a=2),
                                          table[:, :].unsqueeze(1).to_broadcast([P, 2, SEQ]), ALU.mult)
            if kind == "k":
                return ins
            ins.then_inc(S["rope"], 1)
            eng.wait_ge(S["rope"], (MT // 2) * c + m // 2 + 1)
            return nc.vector.tensor_tensor(kT[par][:, m:m + 2, 0:SEQ], mixed[:, :, :], turned[:, :, :], ALU.add)

        def epi_fill(pe, j, c, par):
            for k in range(MT):
                mm = nc.tensor.matmul(work[:, 0:D], o[par][:, k, j * P:(j + 1) * P], wo[:, k, :],
                                      start=(k == 0), stop=(bias is None and k == MT - 1))
            if bias is not None:
                mm = nc.tensor.matmul(work[:, 0:D], keep["ones"][0:1, :], bias, start=False, stop=True)
            return mm

        def epi_copy(eng, j, c, half, par):
            at = 6 if latents else 2
            xs = keep["x"][:, bass.ds(c * QT + j, 1), :].rearrange("p a b -> p (a b)")
            return nc.vector.scalar_tensor_tensor(out=xs, in0=work[:, 0:D], scalar=keep["gate"][:, at:at + 1],
                                                  in1=xs, op0=ALU.mult, op1=ALU.add)

        def q_of(par, hh, t):
            r = 64 * (hh % 2)
            return qT[par][r:r + 64, hh // 2, t * P:(t + 1) * P]

        def k_of(par, hh):
            r = 64 * (hh % 2)
            return kT[par][r:r + 64, hh // 2, :]

        def row_max(dve, nmax, bank, c, hh, p):
            if latents:
                return nc.vector.tensor_reduce(nmax[:, p, 0:1], bank[:, :], AX.X, ALU.max, negate=True)
            return plain_max(nc, dve, nmax, bank, p)

        def exp(act, prob, nmax, bank, hh, p, sums):
            if latents:
                return nc.scalar.activation(prob[:, :], bank[:, :], ACT.Exp, bias=nmax[:, p, 0:1],
                                            accum_out=sums[:, p, 0:1])
            for t in range(QT):
                ins = nc.scalar.activation(prob[:, t * SEQ:(t + 1) * SEQ], bank[:, t * SEQ:(t + 1) * SEQ], ACT.Exp,
                                           bias=nmax[:, p, t:t + 1], accum_out=sums[:, p, t:t + 1])
            return ins

        def pro_engine(j):
            return "dve" if kinds[j][0] in ("h", "c", "kr") or (latents and kinds[j][0] == "k") else "act"

        if latents:
            pro_at, epi_at = spread([6 + 0.5 * j for j in range(NP)]), spread([2, 4])
        else:
            pro_at, epi_at = spread([7 + 0.5 * j for j in range(NP)]), spread([2, 4])
        return dict(weights=weights, setup=setup, act_setup=lambda act: None, norm=norm,
                    norm_job=[None, 0, 1] if latents else [None, 0], norm_wait=norm_wait,
                    q=q_of, k=k_of, v=lambda par, hh, k: v[par][:, k, hh, :],
                    pro_fill=pro_fill, pro_copy=pro_copy,
                    pro_frees=[i for i, (k, m) in enumerate(kinds) if k not in ("h", "c")],
                    pro_engine=pro_engine, epi_fill=epi_fill, epi_copy=epi_copy,
                    epi_engine=lambda j: "dve", pro_at=pro_at, epi_at=epi_at,
                    row_max=row_max, exp=exp)

    source = dram["ctx"] if latents else dram["ctxT"]
    attention_stage(nc, keep, S, dict(
        name=L, heads=H, vd=VD, group=2, wide=latents, narrow=False, n_pro=NP, n_epi=NE,
        n_norm=3 if latents else 2, pT_on_act=True,
        stream=lambda bufs, c, par: [(bufs["stream"][par][:, :, :],
                                      source[bass.ds(c, 1), :, :, :].rearrange("a p k s -> (a p) k s"))],
        make=make))


def relu_feed_forward(nc, keep, S, dram):
    F, N = 1024, 512
    FT, BT, BLOCKS = F // P, N // P, TOKENS // N
    L = "L2f"
    with ExitStack() as ctx:
        def sb(name, shape, dt=F32):
            return ctx.enter_context(nc.sbuf_tensor(L + name, shape, dt))
        w1, w2 = sb("w1", [P, KT, F]), sb("w2", [P, FT, D])
        b1, b2 = sb("b1", [P, FT]), sb("b2", [1, D])
        h, hT, aT = sb("h", [P, BT, D]), sb("hT", [P, KT, N]), sb("aT", [P, FT, N])
        st, mv, rstd = sb("st", [P, BT, 6]), sb("mv", [P, BT, 2]), sb("rstd", [P, BT])
        hp = [ctx.enter_context(nc.psum_tensor(f"{L}h{i}", [P, N], F32)) for i in range(4)]
        tp = [ctx.enter_context(nc.psum_tensor(f"{L}t{i}", [P, N], F32)) for i in range(KT)]
        yp = [ctx.enter_context(nc.psum_tensor(f"{L}y{i}", [P, 2, D], F32)) for i in range(2)]

        with nc.Block() as block:
            @block.sync
            def _(sp):
                sp.dma_start(w1[:, :, :], dram[L + "w1"].rearrange("(k p) f -> p k f", p=P)
                             ).then_inc(S["weights"], 16)
                sp.dma_start(w2[:, :, :], dram[L + "w2"].rearrange("(k p) f -> p k f", p=P)
                             ).then_inc(S["weights"], 16)
                sp.dma_start(b1[:, :], dram[L + "b1"]).then_inc(S["weights"], 16)
                sp.dma_start(b2[:, :], dram[L + "b2"]).then_inc(S["weights"], 16)

            @block.gpsimd
            def _(pool):
                def run(b):
                    pool.wait_ge(S["var"], b + 1)
                    nc.gpsimd.tensor_tensor(rstd[:, :], mv[:, :, 1], keep["eps"][:, :], ALU.add
                                            ).then_inc(S["vareps"], 1)
                    pool.wait_ge(S["vareps"], b + 1)
                    nc.gpsimd.tensor_tensor(rstd[:, :], rstd[:, :], keep["mhalf"][:, :], ALU.pow
                                            ).then_inc(S["rstd"], 1)
                run(0)
                with pool.Fori(1, BLOCKS) as b:
                    run(b)

            @block.vector
            def _(dve):
                def norm(b):
                    for t in range(BT):
                        ins = nc.vector.bn_stats(st[:, t, :],
                                                 keep["x"][:, bass.ds(b * BT + t, 1), :].rearrange("p a b -> p (a b)"))
                    ins.then_inc(S["stats"], 1)
                    dve.wait_ge(S["stats"], b + 1)
                    nc.vector.memset(keep["scratch"][:, 0:1], 0.0)
                    for t in range(BT):
                        ins = nc.vector.bn_aggr(mv[:, t, :], st[:, t, :])
                    ins.then_inc(S["var"], 1)
                    dve.wait_ge(S["rstd"], b + 1)
                    wait(dve, S["turned"], KT * b)
                    for t in range(BT):
                        ins = nc.vector.tensor_scalar(
                            h[:, t, :], keep["x"][:, bass.ds(b * BT + t, 1), :].rearrange("p a b -> p (a b)"),
                            mv[:, t, 0:1], rstd[:, t:t + 1], ALU.subtract, ALU.mult)
                    ins.then_inc(S["normed"], 1)

                def copy_turned(b):
                    for k in range(KT):
                        dve.wait_ge(S["turned"], KT * b + k + 1)
                        nc.vector.tensor_copy(hT[:, k, :], tp[k][:, :]).then_inc(S["turn_copied"], 1)

                def residual(b):
                    for i in range(2):
                        dve.wait_ge(S["y"], 2 * b + i + 1)
                        xs = flat(keep["x"][:, bass.ds(b * BT + 2 * i, 2), :])
                        nc.vector.scalar_tensor_tensor(out=xs, in0=flat(yp[i][:, :, :]), scalar=keep["gate"][:, 5:6],
                                                       in1=xs, op0=ALU.mult, op1=ALU.add).then_inc(S["added"], 1)

                def run(b, last=False):
                    if not last:
                        norm(b + 1)
                        copy_turned(b + 1)
                    residual(b)
                norm(0)
                copy_turned(0)
                run(0)
                with dve.Fori(1, BLOCKS - 1) as b:
                    run(b)
                run(BLOCKS - 1, last=True)

            @block.scalar
            def _(act):
                act.wait_ge(S["weights"], 64)

                def run(b):
                    wait(act, S["y"], 2 * b)
                    for m in range(FT):
                        act.wait_ge(S["hidden"], FT * b + m + 1)
                        nc.scalar.activation(aT[:, m, :], hp[m % 4][:, :], ACT.Relu, bias=b1[:, m:m + 1]
                                             ).then_inc(S["act"], 1)
                run(0)
                with act.Fori(1, BLOCKS) as b:
                    run(b)

            @block.tensor
            def _(pe):
                def turn_block(b):
                    pe.wait_ge(S["normed"], b + 1)
                    wait(pe, S["turn_copied"], KT * b)
                    for k in range(KT):
                        for t in range(BT):
                            mm = nc.tensor.transpose(tp[k][:, t * P:(t + 1) * P], h[:, t, k * P:(k + 1) * P],
                                                     keep["ident"][:, :])
                        mm.then_inc(S["turned"], 1)

                def run(b, last=False):
                    pe.wait_ge(S["turn_copied"], KT * (b + 1))
                    for m in range(FT):
                        wait(pe, S["act"], FT * b + m - 3)
                        for k in range(KT):
                            mm = nc.tensor.matmul(hp[m % 4][:, :], w1[:, k, m * P:(m + 1) * P], hT[:, k, :],
                                                  start=(k == 0), stop=(k == KT - 1))
                        mm.then_inc(S["hidden"], 1)
                    if not last:
                        turn_block(b + 1)
                    pe.wait_ge(S["act"], FT * (b + 1))
                    for t in range(BT):
                        if t % 2 == 0:
                            wait(pe, S["added"], 2 * (b - 1) + t // 2 + 1)
                        y = yp[t // 2][:, t % 2, :]
                        for k in range(FT):
                            nc.tensor.matmul(y, aT[:, k, t * P:(t + 1) * P], w2[:, k, :], start=(k == 0), stop=False)
                        mm = nc.tensor.matmul(y, keep["ones"][0:1, :], b2[0:1, :], start=False, stop=True)
                        if t % 2 == 1:
                            mm.then_inc(S["y"], 1)
                turn_block(0)
                pe.wait_ge(S["weights"], 64)
                run(0)
                with pe.Fori(1, BLOCKS - 1) as b:
                    run(b)
                run(BLOCKS - 1, last=True)
    zero_semaphores(nc, S["all"])


ROUND = 12582912.0
QMAX = 32767.0


def quantised_feed_forward(nc, keep, S, dram):
    F, N, W = 768, 512, 32
    FT, BT, BLOCKS = F // P, N // P, TOKENS // N
    L = "L3f"
    with ExitStack() as ctx:
        def sb(name, shape, dt=F32, ctx=ctx):
            return ctx.enter_context(nc.sbuf_tensor(L + name, shape, dt))
        wT = {n: sb(n + "T", [P, KT, F]) for n in ("up", "gate")}
        wT["down"] = sb("downT", [P, FT, D])
        hT = flat(keep["x"][:, :, :]).rearrange("p (k n) -> p k n", k=KT)
        peak, top, scale, inv = sb("peak", [P, TILES]), sb("top", [P, 8]), sb("scale", [P, 8]), sb("inv", [P, 8])

        def global_scale(dve, which, peaks, after):
            dve.wait_ge(S["peaks"], after)
            nc.vector.tensor_reduce(top[:, which:which + 1], peaks, AX.X, ALU.max).then_inc(S["local_top"], 1)
            dve.wait_ge(S["top"], 1)
            nc.vector.tensor_scalar(scale[:, which:which + 1], top[:, which:which + 1], 1.0 / QMAX, 1e-12,
                                    ALU.mult, ALU.max).then_inc(S["scale"], 1)
            dve.wait_ge(S["scale"], 1)
            nc.vector.reciprocal(inv[:, which:which + 1], scale[:, which:which + 1]).then_inc(S["inv"], 1)
            dve.wait_ge(S["inv"], 1)

        def global_top(pool, which):
            pool.wait_ge(S["local_top"], 1)
            nc.gpsimd.partition_all_reduce(top[:, which:which + 1], top[:, which:which + 1], P,
                                           bass.bass_isa.ReduceOp.max).then_inc(S["top"], 1)

        with ExitStack() as inner:
            raw = {n: sb(n, [P, FT * KT * P], ctx=inner) for n in ("up", "gate", "down")}
            amax, ws = sb("amax", [P, 3, 48], ctx=inner), sb("ws", [P, 3, 48], ctx=inner)
            wi = sb("wi", [P, 3, 48], ctx=inner)
            h = sb("h", [P, TILES, D], ctx=inner)
            st, mv = sb("st", [P, TILES, 6], ctx=inner), sb("mv", [P, TILES, 2], ctx=inner)
            rstd = sb("rstd", [P, TILES], ctx=inner)
            tp = [inner.enter_context(nc.psum_tensor(f"{L}t{i}", [P, 512], F32)) for i in range(4)]
            names = ("up", "gate", "down")
            WJ = 9
            LINKS = 7

            with nc.Block() as block:
                @block.sync
                def _(sp):
                    for n in names:
                        cols = D if n != "down" else F
                        sp.dma_start(raw[n][:, :].rearrange("p (a i) -> p a i", i=cols),
                                     dram[L + n].rearrange("(a p) i -> p a i", p=P)).then_inc(S["weights"], 16)
                    sp.dma_start(dram["x_spill"], keep["x"][:, :, :]).then_inc(S["stream"][0], 16)
                    sp.wait_ge(S["stream"][0], 16)

                @block.gpsimd
                def _(pool):
                    pool.wait_ge(S["var"], 1)
                    for q in range(TILES // BT):
                        nc.gpsimd.tensor_tensor(rstd[:, BT * q:BT * (q + 1)], mv[:, BT * q:BT * (q + 1), 1],
                                                keep["eps"][:, :], ALU.add).then_inc(S["vareps"], 1)
                    pool.wait_ge(S["vareps"], TILES // BT)
                    for q in range(TILES // BT):
                        nc.gpsimd.tensor_tensor(rstd[:, BT * q:BT * (q + 1)], rstd[:, BT * q:BT * (q + 1)],
                                                keep["mhalf"][:, :], ALU.pow).then_inc(S["rstd"], 1)
                    global_top(pool, 0)

                @block.vector
                def _(dve):
                    for t in range(TILES):
                        ins = nc.vector.bn_stats(st[:, t, :], keep["x"][:, t, :])
                    ins.then_inc(S["stats"], 1)
                    dve.wait_ge(S["stats"], 1)
                    for t in range(TILES):
                        ins = nc.vector.bn_aggr(mv[:, t, :], st[:, t, :])
                    ins.then_inc(S["var"], 1)
                    dve.wait_ge(S["weights"], 48)
                    done = [0]

                    def linked(ins):
                        done[0] += 1
                        ins.then_inc(S["route"], 1)
                        dve.wait_ge(S["route"], done[0])
                    for i, n in enumerate(names):
                        w = raw[n][:, :].rearrange("p (b w) -> p b w", w=W)
                        linked(nc.vector.tensor_reduce(amax[:, i, :], w, AX.X, ALU.max, apply_absolute_value=True))
                        linked(nc.vector.tensor_scalar(ws[:, i, :], amax[:, i, :], 1.0 / 7.0, 1e-12, ALU.mult,
                                                       ALU.max))
                        linked(nc.vector.reciprocal(wi[:, i, :], ws[:, i, :]))
                        linked(nc.vector.tensor_tensor(w, w, wi[:, i, :].unsqueeze(2).to_broadcast([P, 48, W]),
                                                       ALU.mult))
                        linked(nc.vector.tensor_scalar(w, w, ROUND, ROUND, ALU.add, ALU.subtract))
                        linked(nc.vector.tensor_scalar(w, w, -8.0, 7.0, ALU.max, ALU.min))
                        linked(nc.vector.tensor_tensor(w, w, ws[:, i, :].unsqueeze(2).to_broadcast([P, 48, W]),
                                                       ALU.mult))
                    assert done[0] == 3 * LINKS
                    dve.wait_ge(S["rstd"], TILES // BT)
                    for t in range(TILES):
                        ins = nc.vector.tensor_scalar(h[:, t, :], keep["x"][:, t, :], mv[:, t, 0:1], rstd[:, t:t + 1],
                                                      ALU.subtract, ALU.mult)
                    ins.then_inc(S["normed"], 1)
                    dve.wait_ge(S["normed"], 1)
                    nc.vector.tensor_reduce(peak[:, :], h[:, :, :], AX.X, ALU.max, apply_absolute_value=True
                                            ).then_inc(S["peaks"], 1)
                    global_scale(dve, 0, peak[:, :], 1)
                    QB = 8
                    for q in range(QB):
                        part = flat(h[:, q * TILES // QB:(q + 1) * TILES // QB, :])
                        nc.vector.tensor_scalar(part, part, inv[:, 0:1], ROUND, ALU.mult, ALU.add
                                                ).then_inc(S["rounded"], 1)
                    dve.wait_ge(S["rounded"], QB)
                    for q in range(QB):
                        part = flat(h[:, q * TILES // QB:(q + 1) * TILES // QB, :])
                        nc.vector.tensor_scalar(part, part, ROUND, scale[:, 0:1], ALU.subtract, ALU.mult
                                                ).then_inc(S["quantised"], 1)

                @block.tensor
                def _(pe):
                    n_bank = 0
                    for i, n in enumerate(names):
                        pe.wait_ge(S["route"], LINKS * (i + 1))
                        for j in range(3):
                            if n_bank >= 4:
                                pe.wait_ge(S["turn_copied"], n_bank - 3)
                            for q in range(4):
                                at = ((2 * j + q // 2) * D + (q % 2) * P) if n != "down" else (
                                    (q % 2) * F + (2 * j + q // 2) * P)
                                mm = nc.tensor.transpose(tp[n_bank % 4][:, q * P:(q + 1) * P], raw[n][:, at:at + P],
                                                         keep["ident"][:, :])
                            mm.then_inc(S["turned"], 1)
                            n_bank += 1
                    for b in range(BLOCKS):
                        pe.wait_ge(S["quantised"], b + 1)
                        for k in range(KT):
                            pe.wait_ge(S["turn_copied"], n_bank - 3)
                            for t in range(BT):
                                mm = nc.tensor.transpose(tp[n_bank % 4][:, t * P:(t + 1) * P],
                                                         h[:, BT * b + t, k * P:(k + 1) * P], keep["ident"][:, :])
                            mm.then_inc(S["turned"], 1)
                            n_bank += 1

                @block.scalar
                def _(act):
                    n_bank = 0
                    for n in names:
                        for j in range(3):
                            act.wait_ge(S["turned"], n_bank + 1)
                            src = tp[n_bank % 4][:, :]
                            if n == "down":
                                dst = flat(wT[n][:, 2 * j:2 * j + 2, :])
                            else:
                                src = src.rearrange("p (a k i) -> p k a i", a=2, k=KT)
                                dst = wT[n][:, :, 2 * j * P:(2 * j + 2) * P].rearrange("p k (a i) -> p k a i", a=2)
                            if n == "down":
                                nc.scalar.copy(dst, src).then_inc(S["turn_copied"], 1)
                            else:
                                nc.scalar.copy(dst[:, 0], src[:, 0])
                                nc.scalar.copy(dst[:, 1], src[:, 1]).then_inc(S["turn_copied"], 1)
                            n_bank += 1
                    act.wait_ge(S["stream"][0], 16)
                    act.wait_ge(S["normed"], 1)
                    for b in range(BLOCKS):
                        for k in range(KT):
                            act.wait_ge(S["turned"], n_bank + 1)
                            nc.scalar.copy(hT[:, k, b * N:(b + 1) * N], tp[n_bank % 4][:, :]
                                           ).then_inc(S["turn_copied"], 1)
                            n_bank += 1
            zero_semaphores(nc, S["all"])

        g = sb("g", [P, BLOCKS, FT * N])
        up = sb("upq", [P, BLOCKS, FT * N], I16)
        bank = [ctx.enter_context(nc.psum_tensor(f"{L}b{i}", [P, N], F32)) for i in range(6)]

        def project_all(which, quantise_up):
            with nc.Block() as block:
                @block.tensor
                def _(pe):
                    def run(b):
                        for m in range(FT):
                            wait(pe, S["copied"], FT * (b - 1) + m + 1)
                            for k in range(KT):
                                mm = nc.tensor.matmul(bank[m][:, :], wT[which][:, k, m * P:(m + 1) * P],
                                                      hT[:, k, bass.ds(b * N, N)], start=(k == 0), stop=(k == KT - 1))
                            mm.then_inc(S["hidden"], 1)
                    run(0)
                    with pe.Fori(1, BLOCKS) as b:
                        run(b)

                @block.scalar
                def _(act):
                    def run(b):
                        for m in range(FT):
                            if quantise_up:
                                act.wait_ge(S["quantised"], b + 1)
                            act.wait_ge(S["hidden"], FT * b + m + 1)
                            nc.scalar.copy(g[:, b, m * N:(m + 1) * N], bank[m][:, :]).then_inc(S["copied"], 1)
                    for b in range(BLOCKS):
                        run(b)

                @block.vector
                def _(dve):
                    def run(b):
                        if quantise_up:
                            g_b = g[:, bass.ds(b, 1), :].rearrange("p a b -> p (a b)")
                            nc.vector.tensor_scalar(g_b, g_b, inv[:, 1:2], ROUND, ALU.mult, ALU.add
                                                    ).then_inc(S["rounded"], 1)
                            dve.wait_ge(S["rounded"], b + 1)
                            nc.vector.tensor_scalar(up[:, bass.ds(b, 1), :].rearrange("p a b -> p (a b)"), g_b,
                                                    ROUND, None, ALU.subtract).then_inc(S["quantised"], 1)
                        wait(dve, S["peaks"], b)
                        dve.wait_ge(S["copied"], FT * (b + 1))
                        nc.vector.memset(keep["scratch"][:, 1:2], 0.0)
                        nc.vector.tensor_reduce(peaks[:, bass.ds(b, 1)],
                                                g[:, bass.ds(b, 1), :].rearrange("p a b -> p (a b)"), AX.X, ALU.max,
                                                apply_absolute_value=True).then_inc(S["peaks"], 1)
                    run(0)
                    with dve.Fori(1, BLOCKS) as b:
                        run(b)
                    global_scale(dve, 2 if quantise_up else 1, peaks[:, :], BLOCKS)

                @block.gpsimd
                def _(pool):
                    global_top(pool, 2 if quantise_up else 1)
            zero_semaphores(nc, S["all"])

        peaks = sb("peaks", [P, BLOCKS])
        project_all("up", False)
        project_all("gate", True)

        NP2 = 4
        HALF = FT * N // NP2
        sig = [sb(f"sig{i}", [P, HALF]) for i in range(2)]

        with nc.Block() as block:
            def part(i):
                return g[:, i // NP2, (i % NP2) * HALF:(i % NP2 + 1) * HALF]

            @block.vector
            def _(dve):
                n = BLOCKS * NP2

                def round_part(i, which):
                    nc.vector.tensor_scalar(part(i), part(i), inv[:, which:which + 1], ROUND, ALU.mult, ALU.add
                                            ).then_inc(S["rounded"], 1)

                def rescale_part(i, which, after):
                    dve.wait_ge(S["rounded"], after)
                    nc.vector.tensor_scalar(part(i), part(i), ROUND, scale[:, which:which + 1], ALU.subtract,
                                            ALU.mult).then_inc(S["quantised"], 1)

                def gated(i):
                    dve.wait_ge(S["act"], i + 1)
                    nc.vector.tensor_scalar(sig[i % 2][:, :], sig[i % 2][:, :], ROUND, 65535.0, ALU.subtract,
                                            ALU.min).then_inc(S["sig_clipped"], 1)
                    dve.wait_ge(S["sig_clipped"], i + 1)
                    nc.vector.scalar_tensor_tensor(out=part(i), in0=sig[i % 2][:, :], scalar=1.0 / 65536.0,
                                                   in1=part(i), op0=ALU.mult, op1=ALU.mult).then_inc(S["gated"], 1)
                    dve.wait_ge(S["gated"], i + 1)
                    nc.vector.tensor_reduce(peak[:, i:i + 1], part(i), AX.X, ALU.max, apply_absolute_value=True
                                            ).then_inc(S["peaks"], 1)
                round_part(0, 2)
                for i in range(n):
                    if i + 1 < n:
                        round_part(i + 1, 2)
                    rescale_part(i, 2, i + 1)
                    if i >= 1:
                        gated(i - 1)
                gated(n - 1)
                dve.wait_ge(S["peaks"], n)
                global_scale(dve, 3, peak[:, 0:n], n)

            @block.scalar
            def _(act):
                for i in range(BLOCKS * NP2):
                    act.wait_ge(S["quantised"], i + 1)
                    if i >= 2:
                        act.wait_ge(S["gated"], i - 1)
                    nc.scalar.activation(sig[i % 2][:, :], part(i), ACT.Sigmoid).then_inc(S["sigmoid"], 1)
                    act.wait_ge(S["sigmoid"], i + 1)
                    nc.scalar.activation(sig[i % 2][:, :], sig[i % 2][:, :], ACT.Copy, bias=ROUND, scale=65536.0
                                         ).then_inc(S["act"], 1)

            @block.gpsimd
            def _(pool):
                global_top(pool, 3)
        zero_semaphores(nc, S["all"])

        with nc.Block() as block:
            @block.vector
            def _(dve):
                n = BLOCKS * NP2

                def up_part(i):
                    return up[:, i // NP2, (i % NP2) * HALF:(i % NP2 + 1) * HALF]

                def round_part(i):
                    nc.vector.tensor_scalar(part(i), part(i), inv[:, 3:4], ROUND, ALU.mult, ALU.add
                                            ).then_inc(S["rounded"], 1)

                def multiply(i):
                    dve.wait_ge(S["rounded"], i + 1)
                    nc.vector.tensor_scalar(part(i), part(i), ROUND, scale[:, 3:4], ALU.subtract, ALU.mult
                                            ).then_inc(S["quantised"], 1)
                    dve.wait_ge(S["quantised"], i + 1)
                    nc.vector.scalar_tensor_tensor(out=part(i), in0=up_part(i), scalar=scale[:, 1:2], in1=part(i),
                                                   op0=ALU.mult, op1=ALU.mult).then_inc(S["gated"], 1)
                    dve.wait_ge(S["gated"], i + 1)
                    nc.vector.tensor_reduce(peak[:, i:i + 1], part(i), AX.X, ALU.max, apply_absolute_value=True
                                            ).then_inc(S["peaks"], 1)
                round_part(0)
                for i in range(n):
                    if i + 1 < n:
                        round_part(i + 1)
                    multiply(i)
                global_scale(dve, 4, peak[:, 0:n], n)

            @block.gpsimd
            def _(pool):
                global_top(pool, 4)
        zero_semaphores(nc, S["all"])

        if True:
            xo = [keep["x"][:, i, :] for i in range(2)]
            oq = [flat(keep["x"][:, 4 * i + 4:4 * i + 7, :]) for i in range(2)]
            yp = [bank[0], bank[1]]

            with nc.Block() as block:
                @block.vector
                def _(dve):
                    def quantise(b, q, par):
                        t = BT * b + q
                        src = g[:, bass.ds(b, 1), :].rearrange("p a (f n) -> p (a f) n", n=N)[:, :, q * P:(q + 1) * P]
                        dst = oq[par].rearrange("p (f n) -> p f n", n=P)
                        wait(dve, S["y"], t - 1)
                        nc.vector.tensor_scalar(dst, src, inv[:, 4:5], ROUND, ALU.mult, ALU.add
                                                ).then_inc(S["rounded"], 1)
                        dve.wait_ge(S["rounded"], t + 1)
                        nc.vector.tensor_scalar(oq[par], oq[par], ROUND, scale[:, 4:5], ALU.subtract,
                                                ALU.mult).then_inc(S["quantised"], 1)

                    def residual(b, q, par):
                        t = BT * b + q
                        dve.wait_ge(S["y"], t + 1)
                        dve.wait_ge(S["stream"][par], 16 * (2 * b + q // 2 + 1))
                        nc.vector.scalar_tensor_tensor(out=xo[par], in0=yp[par][:, 0:D],
                                                       scalar=keep["gate"][:, 7:8], in1=xo[par],
                                                       op0=ALU.mult, op1=ALU.add).then_inc(S["added"], 1)

                    def block_of(b, first=False):
                        for q in range(BT):
                            quantise(b, q, q % 2)
                            if q >= 1:
                                residual(b, q - 1, (q - 1) % 2)
                            elif not first:
                                residual(b - 1, BT - 1, 1)
                    block_of(0, first=True)
                    with dve.Fori(1, BLOCKS) as b:
                        block_of(b)
                    residual(BLOCKS - 1, BT - 1, 1)

                @block.tensor
                def _(pe):
                    def run(b):
                        for q in range(BT):
                            t = BT * b + q
                            pe.wait_ge(S["quantised"], t + 1)
                            wait(pe, S["added"], t - 1)
                            for k in range(FT):
                                mm = nc.tensor.matmul(yp[q % 2][:, 0:D], oq[q % 2][:, k * P:(k + 1) * P],
                                                      wT["down"][:, k, :], start=(k == 0), stop=(k == FT - 1))
                            mm.then_inc(S["y"], 1)
                    run(0)
                    with pe.Fori(1, BLOCKS) as b:
                        run(b)

                @block.sync
                def _(sp):
                    def load(i, par):
                        sp.dma_start(xo[par], dram["x_spill"][:, bass.ds(2 * i + par, 1), :].rearrange(
                            "p a d -> p (a d)")).then_inc(S["stream"][par], 16)

                    def store(i, par):
                        t = 2 * i + par
                        sp.wait_ge(S["added"], t + 1)
                        sp.dma_start(dram["out"][bass.ds(t * P, P), :], xo[par]).then_inc(S["stored"][par], 16)
                    load(0, 0)
                    load(0, 1)
                    with sp.Fori(0, TILES // 2 - 1) as i:
                        for par in range(2):
                            store(i, par)
                            sp.wait_ge(S["stored"][par], 16 * (i + 1))
                            load(i + 1, par)
                    for par in range(2):
                        store(TILES // 2 - 1, par)
                    for par in range(2):
                        sp.wait_ge(S["stored"][par], 16 * (TILES // 2))


def routed_experts(nc, keep, S, dram):
    E, K, CAP, F, L = 64, 8, 128, 192, "L1f"
    FH = F // 2
    SLOTS = E * CAP
    OUT_OF_RANGE = 65536.0
    AHEAD = 4
    with ExitStack() as ctx:
        def sb(name, shape, dt=F32, ctx=ctx):
            return ctx.enter_context(nc.sbuf_tensor(L + name, shape, dt))
        slots, share = sb("slots", [P, TILES, K], U32), sb("share", [P, TILES, K])

        def by_pairs(eng, run, tail=None):
            run(0, 0, 0)
            run(1, 0, 1)
            with eng.Fori(1, BATCH // 2) as i:
                run(2 * i, i + 0, 0)
                run(2 * i + 1, i + 0, 1)

        with ExitStack() as inner:
            def sbi(name, shape, dt=F32):
                return sb(name, shape, dt, ctx=inner)
            router = sbi("router", [P, KT, E])
            wsgu, wsd = sbi("wsgu", [P, KT, 2 * F]), sbi("wsd", [FH, 2, D])
            tri, iota = sbi("tri", [P, P]), sbi("iota", [P, E])
            h = [sbi(f"h{i}", [P, QT, D]) for i in range(2)]
            slot_of = [sbi(f"slot_of{i}", [P, QT, K], U32) for i in range(2)]
            hT = sbi("hT", [P, KT, SEQ])
            st, mv, rstd = sbi("st", [P, QT, 6]), sbi("mv", [P, QT, 2]), sbi("rstd", [P, QT])
            nm, tot, rtot = sbi("nm", [P, QT]), sbi("tot", [P, QT]), sbi("rtot", [P, QT])
            e, top, idx = sbi("e", [P, QT, E]), sbi("top", [P, QT, K]), sbi("idx", [P, QT, K], U32)
            idf, hit = sbi("idf", [P, QT, K]), sbi("hit", [P, QT, K, E])
            member, before = sbi("member", [P, QT, E]), sbi("before", [P, E])
            place, placed = sbi("place", [P, QT, K, E]), sbi("placed", [P, QT, K])
            late, slotf = sbi("late", [P, QT, K]), sbi("slotf", [P, QT, K])
            silu, act_h = sbi("silu", [FH, 2, SEQ]), sbi("act_h", [FH, 2, SEQ])
            zeros, tick = sbi("zeros", [P, 2048]), sbi("tick", [P, 2])
            turned = inner.enter_context(nc.psum_tensor(L + "pt", [P, 512], F32))
            logit = inner.enter_context(nc.psum_tensor(L + "pl", [P, 512], F32))
            posp = inner.enter_context(nc.psum_tensor(L + "pp", [P, 512], F32))
            gp = inner.enter_context(nc.psum_tensor(L + "pg", [FH, 512], F32))
            upp = inner.enter_context(nc.psum_tensor(L + "pu", [FH, 512], F32))
            yp = inner.enter_context(nc.psum_tensor(L + "py", [P, 512], F32))
            R = 18
            NW = 5

            with nc.Block() as block:
                @block.sync
                def _(sp):
                    sp.dma_start(router[:, :, :], dram[L + "router"].rearrange("(k p) m -> p k m", p=P)
                                 ).then_inc(S["weights"], 16)
                    sp.dma_start(wsgu[:, :, :], dram[L + "wsgu"].rearrange("(k p) m -> p k m", p=P)
                                 ).then_inc(S["weights"], 16)
                    sp.dma_start(wsd[:, :, :], dram[L + "wsd"].rearrange("(k p) m -> p k m", p=FH)
                                 ).then_inc(S["weights"], 16)
                    sp.dma_start(tri[:, :], dram["tri"]).then_inc(S["weights"], 16)
                    sp.dma_start(iota[:, :], dram["iota"]).then_inc(S["weights"], 16)
                    sp.wait_ge(S["setup"], 1)
                    for q in range(8):
                        sp.dma_start(dram["x_slots"][q * 1024:(q + 1) * 1024, :].rearrange("(p a) d -> p (a d)", p=P),
                                     zeros[:, :]).then_inc(S["zeroed"], 16)

                @block.gpsimd
                def _(pool):
                    pool.wait_ge(S["zeroed"], 128)

                    def rstds(c):
                        pool.wait_ge(S["var"], c + 1)
                        nc.gpsimd.tensor_tensor(rstd[:, :], mv[:, :, 1], keep["eps"][:, 0:QT], ALU.add
                                                ).then_inc(S["vareps"], 1)
                        pool.wait_ge(S["vareps"], c + 1)
                        nc.gpsimd.tensor_tensor(rstd[:, :], rstd[:, :], keep["mhalf"][:, 0:QT], ALU.pow
                                                ).then_inc(S["rstd"], 1)

                    def scatter(c, par):
                        wait(pool, S["tick"], c)
                        pool.wait_ge(S["slots"], c + 1)
                        nc.gpsimd.tensor_tensor(tick[:, 0:1], keep["eps"][:, 0:1], keep["eps"][:, 0:1], ALU.add
                                                ).then_inc(S["tick"], 1)
                        for t in range(QT):
                            for k in range(K):
                                nc.gpsimd.indirect_dma_start(
                                    dram["x_slots"], bass.IndirectOffsetOnAxis(slot_of[par][:, t, k:k + 1], 0),
                                    h[par][:, t, :], None, bounds_check=SLOTS - 1, oob_is_err=False
                                ).then_inc(S["scattered"][par], 16)
                    rstds(0)
                    rstds(1)
                    scatter(0, 0)
                    with pool.Fori(0, BATCH // 2 - 1) as i:
                        rstds(2 * i + 2)
                        scatter(2 * i + 1, 1)
                        rstds(2 * i + 3)
                        scatter(2 * i + 2, 0)
                    scatter(BATCH - 1, 1)
                    for par in range(2):
                        pool.wait_ge(S["scattered"][par], 16 * QT * K * BATCH // 2)

                @block.vector
                def _(dve):
                    nc.vector.memset(zeros[:, :], 0.0).then_inc(S["setup"], 1)
                    nc.vector.memset(before[:, :], 0.0).then_inc(S["counted"], 1)
                    dve.wait_ge(S["weights"], 16 * NW)

                    def run(c, half, par):
                        n = [0]

                        def linked(ins):
                            n[0] += 1
                            ins.then_inc(S["route"], 1)
                            dve.wait_ge(S["route"], R * c + n[0])

                        def take_wait():
                            nc.vector.memset(keep["scratch"][:, 2:3], 0.0)

                        def x_tile(t):
                            return keep["x"][:, bass.ds(c * QT + t, 1), :].rearrange("p a b -> p (a b)")

                        def per_token(ap, m):
                            return ap.unsqueeze(2).to_broadcast([P, QT, m])
                        for t in range(QT):
                            ins = nc.vector.bn_stats(st[:, t, :], x_tile(t))
                        linked(ins)
                        take_wait()
                        for t in range(QT):
                            ins = nc.vector.bn_aggr(mv[:, t, :], st[:, t, :])
                        ins.then_inc(S["var"], 1)
                        dve.wait_ge(S["rstd"], c + 1)
                        wait(dve, S["scattered"][par], 16 * QT * K * half)
                        wait(dve, S["turned"], c)
                        for t in range(QT):
                            ins = nc.vector.tensor_scalar(h[par][:, t, :], x_tile(t), mv[:, t, 0:1], rstd[:, t:t + 1],
                                                          ALU.subtract, ALU.mult)
                        ins.then_inc(S["normed"], 1)
                        dve.wait_ge(S["turned"], c + 1)
                        nc.vector.tensor_copy(flat(hT[:, :, :]), turned[:, :]).then_inc(S["turn_copied"], 1)
                        dve.wait_ge(S["logits"], c + 1)
                        nc.vector.tensor_reduce(nm[:, :], logit[:, 0:QT * E].rearrange("p (t e) -> p t e", t=QT),
                                                AX.X, ALU.max, negate=True).then_inc(S["route_max"], 1)
                        dve.wait_ge(S["route_exp"], c + 1)
                        linked(nc.vector.tensor_reduce(tot[:, :], e[:, :, :], AX.X, ALU.add))
                        linked(nc.vector.reciprocal(rtot[:, :], tot[:, :]))
                        linked(nc.vector.tensor_tensor(e[:, :, :], e[:, :, :], per_token(rtot[:, :], E), ALU.mult))
                        take_wait()
                        for t in range(QT):
                            ins = nc.vector.max(top[:, t, :], e[:, t, :])
                        linked(ins)
                        take_wait()
                        for t in range(QT):
                            ins = nc.vector.max_index(idx[:, t, :], top[:, t, :], e[:, t, :])
                        linked(ins)
                        linked(nc.vector.tensor_copy(idf[:, :, :], idx[:, :, :]))
                        linked(nc.vector.tensor_reduce(tot[:, :], top[:, :, :], AX.X, ALU.add))
                        linked(nc.vector.reciprocal(rtot[:, :], tot[:, :]))
                        nc.vector.tensor_tensor(top[:, :, :], top[:, :, :], per_token(rtot[:, :], K), ALU.mult)
                        for t in range(QT):
                            ins = nc.vector.tensor_tensor(
                                hit[:, t, :, :], iota[:, :].unsqueeze(1).to_broadcast([P, K, E]),
                                idf[:, t, :].unsqueeze(2).to_broadcast([P, K, E]), ALU.is_equal)
                        linked(ins)
                        for t in range(QT):
                            ins = nc.vector.tensor_reduce(member[:, t, :], hit[:, t, :, :].rearrange("p k e -> p e k"),
                                                          AX.X, ALU.add)
                        ins.then_inc(S["member"], 1)
                        dve.wait_ge(S["placed"], c + 1)
                        for t in range(QT):
                            ins = nc.vector.tensor_tensor(
                                place[:, t, :, :], hit[:, t, :, :],
                                posp[:, t * E:(t + 1) * E].unsqueeze(1).to_broadcast([P, K, E]), ALU.mult)
                        linked(ins)
                        linked(nc.vector.tensor_reduce(flat(placed[:, :, :]),
                                                       place[:, :, :, :].rearrange("p t k e -> p (t k) e"), AX.X,
                                                       ALU.add))
                        linked(nc.vector.tensor_tensor(before[:, :], before[:, :], member[:, 0, :], ALU.add))
                        nc.vector.tensor_tensor(before[:, :], before[:, :], member[:, 1, :], ALU.add
                                                ).then_inc(S["counted"], 1)
                        nc.vector.tensor_scalar(late[:, :, :], placed[:, :, :], float(CAP), OUT_OF_RANGE, ALU.is_ge,
                                                ALU.mult)
                        linked(nc.vector.scalar_tensor_tensor(out=flat(slotf[:, :, :]), in0=flat(idf[:, :, :]),
                                                              scalar=float(CAP), in1=flat(placed[:, :, :]),
                                                              op0=ALU.mult, op1=ALU.add))
                        linked(nc.vector.tensor_tensor(slotf[:, :, :], slotf[:, :, :], late[:, :, :], ALU.add))
                        nc.vector.tensor_copy(slot_of[par][:, :, :], slotf[:, :, :]).then_inc(S["slots"], 1)
                        linked(nc.vector.tensor_scalar(placed[:, :, :], placed[:, :, :], float(CAP), None, ALU.is_lt))
                        linked(nc.vector.tensor_tensor(top[:, :, :], top[:, :, :], placed[:, :, :], ALU.mult))
                        dve.wait_ge(S["slots"], c + 1)
                        nc.vector.tensor_scalar(keep["scratch"][:, 1:2], keep["eps"][:, 0:1], 0.0, None, ALU.mult)
                        nc.vector.tensor_copy(slots[:, bass.ds(c * QT, QT), :], slot_of[par][:, :, :])
                        linked(nc.vector.tensor_scalar(share[:, bass.ds(c * QT, QT), :], top[:, :, :],
                                                       keep["gate"][:, 3:4], None, ALU.mult))
                        assert n[0] == R, n[0]
                        dve.wait_ge(S["act"], c + 1)
                        dve.wait_ge(S["up"], c + 1)
                        nc.vector.tensor_tensor(flat(act_h[:, :, :]), flat(silu[:, :, :]), upp[:, :], ALU.mult
                                                ).then_inc(S["gated"], 1)
                        dve.wait_ge(S["y"], c + 1)
                        add_output(nc, dve, keep, yp, keep["gate"][:, 3:4], c).then_inc(S["added"], 1)
                    by_pairs(dve, run)

                @block.scalar
                def _(act):
                    def run(c, half, par):
                        act.wait_ge(S["route_max"], c + 1)
                        for t in range(QT):
                            ins = nc.scalar.activation(e[:, t, :], logit[:, t * E:(t + 1) * E], ACT.Exp,
                                                       bias=nm[:, t:t + 1])
                        ins.then_inc(S["route_exp"], 1)
                        act.wait_ge(S["up"], c + 1)
                        wait(act, S["gated"], c)
                        nc.scalar.activation(flat(silu[:, :, :]), gp[:, :], ACT.Silu).then_inc(S["act"], 1)
                    by_pairs(act, run)

                @block.tensor
                def _(pe):
                    pe.wait_ge(S["weights"], 16 * NW)

                    def run(c, half, par):
                        pe.wait_ge(S["normed"], c + 1)
                        wait(pe, S["turn_copied"], c)
                        turn(nc, keep, turned, h[par]).then_inc(S["turned"], 1)
                        pe.wait_ge(S["turn_copied"], c + 1)
                        wait(pe, S["route_exp"], c)
                        for t in range(QT):
                            for k in range(KT):
                                mm = nc.tensor.matmul(logit[:, t * E:(t + 1) * E], hT[:, k, t * P:(t + 1) * P],
                                                      router[:, k, :], start=(k == 0), stop=(k == KT - 1))
                        mm.then_inc(S["logits"], 1)
                        wait(pe, S["gated"], c)
                        for bank, at in ((gp, 0), (upp, F)):
                            for m in range(2):
                                for k in range(KT):
                                    mm = nc.tensor.matmul(bank[:, m * SEQ:(m + 1) * SEQ],
                                                          wsgu[:, k, at + m * FH:at + (m + 1) * FH], hT[:, k, :],
                                                          start=(k == 0), stop=(k == KT - 1))
                        mm.then_inc(S["up"], 1)
                        pe.wait_ge(S["member"], c + 1)
                        pe.wait_ge(S["counted"], c + 1)
                        for t in range(QT):
                            nc.tensor.matmul(posp[:, t * E:(t + 1) * E], tri[:, :], member[:, t, :],
                                             start=True, stop=False)
                            if t == 1:
                                nc.tensor.matmul(posp[:, t * E:(t + 1) * E], keep["ones"][:, :], member[:, 0, :],
                                                 start=False, stop=False)
                            mm = nc.tensor.matmul(posp[:, t * E:(t + 1) * E], keep["ones"][:, :], before[:, :],
                                                  start=False, stop=True)
                        mm.then_inc(S["placed"], 1)
                        pe.wait_ge(S["gated"], c + 1)
                        wait(pe, S["added"], c)
                        for t in range(QT):
                            for m in range(2):
                                mm = nc.tensor.matmul(yp[:, t * D:(t + 1) * D], act_h[:, m, t * P:(t + 1) * P],
                                                      wsd[:, m, :], start=(m == 0), stop=(m == 1))
                        mm.then_inc(S["y"], 1)
                    by_pairs(pe, run)
            zero_semaphores(nc, S["all"])

        with ExitStack() as inner:
            wgu = [sb(f"wgu{i}", [P, 2, KT, F], ctx=inner) for i in range(AHEAD)]
            wd = [sb(f"wd{i}", [FH, 2, D], ctx=inner) for i in range(AHEAD)]
            xs = [sb(f"xs{i}", [P, D], ctx=inner) for i in range(AHEAD)]
            xT = [sb(f"xT{i}", [P, KT, P], ctx=inner) for i in range(2)]
            silu = [sb(f"esilu{i}", [FH, 2, P], ctx=inner) for i in range(2)]
            act_h = [sb(f"eact{i}", [FH, 2, P], ctx=inner) for i in range(2)]
            y = [sb(f"y{i}", [P, D], ctx=inner) for i in range(2)]
            pt = [inner.enter_context(nc.psum_tensor(f"{L}et{i}", [P, KT * P], F32)) for i in range(2)]
            pg = inner.enter_context(nc.psum_tensor(L + "eg", [FH, 2, P], F32))
            pu = [inner.enter_context(nc.psum_tensor(f"{L}eu{i}", [FH, 2, P], F32)) for i in range(2)]
            py = [inner.enter_context(nc.psum_tensor(f"{L}ey{i}", [P, D], F32)) for i in range(2)]

            def first(e):
                return isinstance(e, int) and e == 0

            def by_experts(eng, run):
                for b in range(AHEAD):
                    run(b, 0, b, False)
                with eng.Fori(1, E // AHEAD - 1) as i:
                    for b in range(AHEAD):
                        run(AHEAD * i + b, i + 0, b, False)
                for b in range(AHEAD):
                    run(E - AHEAD + b, E // AHEAD - 1, b, b == AHEAD - 1)

            with nc.Block() as block:
                @block.sync
                def _(sp):
                    def run(e, quarter, b, last):
                        wait(sp, S["y"], e - AHEAD + 1)
                        for i, n in enumerate(("wg", "wu")):
                            sp.dma_start(wgu[b][:, i, :, :], dram[L + n][bass.ds(e, 1), :, :].rearrange(
                                "a (k p) f -> p (a k) f", p=P)).then_inc(S["stream"][b], 16)
                        sp.dma_start(wd[b][:, :, :], dram[L + "wd"][bass.ds(e, 1), :, :].rearrange(
                            "a (k p) f -> p (a k) f", p=FH)).then_inc(S["stream"][b], 16)
                        sp.dma_start(xs[b][:, :], dram["x_slots"][bass.ds(e * CAP, CAP), :]
                                     ).then_inc(S["stream"][b], 16)
                    by_experts(sp, run)

                @block.tensor
                def _(pe):
                    def turn_rows(e, quarter, b):
                        par = b % 2
                        pe.wait_ge(S["stream"][b], 64 * (quarter + 1))
                        wait(pe, S["turn_copied"], e - 1)
                        for k in range(KT):
                            mm = nc.tensor.transpose(pt[par][:, k * P:(k + 1) * P], xs[b][:, k * P:(k + 1) * P],
                                                     keep["ident"][:, :])
                        mm.then_inc(S["turned"], 1)

                    def hidden(e, b):
                        par = b % 2
                        pe.wait_ge(S["turn_copied"], e + 1)
                        for i, bank in ((0, pg), (1, pu[par])):
                            if i == 0:
                                wait(pe, S["act"], e)
                            else:
                                wait(pe, S["gated"], e - 1)
                            for m in range(2):
                                for k in range(KT):
                                    mm = nc.tensor.matmul(bank[:, m, :], wgu[b][:, i, k, m * FH:(m + 1) * FH],
                                                          xT[par][:, k, :], start=(k == 0), stop=(k == KT - 1))
                            mm.then_inc(S["hidden"], 1)

                    def outputs(e, b):
                        par = b % 2
                        pe.wait_ge(S["gated"], e + 1)
                        wait(pe, S["copied"], e - 1)
                        for m in range(2):
                            mm = nc.tensor.matmul(py[par][:, :], act_h[par][:, m, :], wd[b][:, m, :],
                                                  start=(m == 0), stop=(m == 1))
                        mm.then_inc(S["y"], 1)

                    def run(e, quarter, b, last):
                        hidden(e, b)
                        if not last:
                            turn_rows(e + 1, quarter + (b + 1) // AHEAD, (b + 1) % AHEAD)
                        if not first(e):
                            outputs(e - 1, (b - 1) % AHEAD)
                    turn_rows(0, 0, 0)
                    by_experts(pe, run)
                    outputs(E - 1, AHEAD - 1)

                @block.scalar
                def _(act):
                    def run(e, quarter, b, last):
                        par = b % 2
                        act.wait_ge(S["hidden"], 2 * e + 1)
                        wait(act, S["gated"], e - 1)
                        nc.scalar.activation(silu[par][:, :, :], pg[:, :, :], ACT.Silu).then_inc(S["act"], 1)
                        if not first(e):
                            if b:
                                store(e - 1, quarter, b - 1)
                            else:
                                store(e - 1, quarter - 1, AHEAD - 1)

                    def store(e, quarter, b):
                        par = b % 2
                        act.wait_ge(S["y"], e + 1)
                        wait(act, S["stored"][par], 16 * (2 * quarter + b // 2))
                        nc.scalar.copy(y[par][:, :], py[par][:, :]).then_inc(S["copied"], 1)
                        act.wait_ge(S["copied"], e + 1)
                        act.dma_start(dram["y_slots"][bass.ds(e * CAP, CAP), :], y[par][:, :]
                                      ).then_inc(S["stored"][par], 16)
                    by_experts(act, run)
                    store(E - 1, E // AHEAD - 1, AHEAD - 1)
                    for par in range(2):
                        act.wait_ge(S["stored"][par], 16 * E // 2)

                @block.vector
                def _(dve):
                    def run(e, quarter, b, last):
                        par = b % 2
                        dve.wait_ge(S["turned"], e + 1)
                        wait(dve, S["hidden"], 2 * (e - 1))
                        nc.vector.tensor_copy(flat(xT[par][:, :, :]), pt[par][:, :]).then_inc(S["turn_copied"], 1)

                    def gate(e, par):
                        dve.wait_ge(S["hidden"], 2 * e + 2)
                        dve.wait_ge(S["act"], e + 1)
                        wait(dve, S["y"], e - 1)
                        nc.vector.tensor_tensor(act_h[par][:, :, :], silu[par][:, :, :], pu[par][:, :, :], ALU.mult
                                                ).then_inc(S["gated"], 1)

                    def both(e, quarter, b, last):
                        gate(e, b % 2)
                        if not last:
                            run(e + 1, None, (b + 1) % AHEAD, False)
                    run(0, 0, 0, False)
                    by_experts(dve, both)
            zero_semaphores(nc, S["all"])

        with ExitStack() as inner:
            rows = [sb(f"rows{i}", [P, QT, K, D], ctx=inner) for i in range(2)]
            slot_of = [sb(f"gslot{i}", [P, QT, K], U32, ctx=inner) for i in range(2)]
            mine = [sb(f"mine{i}", [P, QT, K], ctx=inner) for i in range(2)]
            tick = sb("gtick", [P, 2], ctx=inner)

            with nc.Block() as block:
                @block.gpsimd
                def _(pool):
                    def run(c, half, par):
                        wait(pool, S["tick"], c)
                        pool.wait_ge(S["slots"], c + 1)
                        nc.gpsimd.tensor_tensor(tick[:, 0:1], keep["eps"][:, 0:1], keep["eps"][:, 0:1], ALU.add
                                                ).then_inc(S["tick"], 1)
                        for t in range(QT):
                            for k in range(K):
                                nc.gpsimd.indirect_dma_start(
                                    rows[par][:, t, k, :], None, dram["y_slots"],
                                    bass.IndirectOffsetOnAxis(slot_of[par][:, t, k:k + 1], 0),
                                    bounds_check=SLOTS - 1, oob_is_err=False).then_inc(S["gathered"][par], 16)
                    by_pairs(pool, run)

                @block.vector
                def _(dve):
                    for par in range(2):
                        nc.vector.memset(rows[par][:, :, :, :], 0.0)

                    def fetch(c, half, par):
                        wait(dve, S["added"], K * (c - 1))
                        wait(dve, S["slots"], c)
                        nc.vector.tensor_scalar(keep["scratch"][:, 1:2], keep["eps"][:, 0:1], 0.0, None, ALU.mult)
                        nc.vector.tensor_copy(mine[par][:, :, :], share[:, bass.ds(c * QT, QT), :])
                        nc.vector.tensor_copy(slot_of[par][:, :, :], slots[:, bass.ds(c * QT, QT), :]
                                              ).then_inc(S["slots"], 1)

                    def sums(c, half, par):
                        dve.wait_ge(S["gathered"][par], 16 * QT * K * (half + 1))
                        dve.wait_ge(S["slots"], c + 1)
                        for k in range(K):
                            if k:
                                dve.wait_ge(S["added"], K * c + k)
                            for t in range(QT):
                                xt = keep["x"][:, bass.ds(c * QT + t, 1), :].rearrange("p a b -> p (a b)")
                                ins = nc.vector.scalar_tensor_tensor(out=xt, in0=rows[par][:, t, k, :],
                                                                     scalar=mine[par][:, t, k:k + 1], in1=xt,
                                                                     op0=ALU.mult, op1=ALU.add)
                            ins.then_inc(S["added"], 1)
                    fetch(0, 0, 0)
                    fetch(1, 0, 1)
                    with dve.Fori(0, BATCH // 2 - 1) as i:
                        sums(2 * i, i + 0, 0)
                        fetch(2 * i + 2, None, 0)
                        sums(2 * i + 1, i + 0, 1)
                        fetch(2 * i + 3, None, 1)
                    sums(BATCH - 2, BATCH // 2 - 1, 0)
                    sums(BATCH - 1, BATCH // 2 - 1, 1)
            zero_semaphores(nc, S["all"])


def stacked_attention(nc, keep, S, dram, cfg):
    HD, H, G, NG, VW = cfg["dim"], 16, 4, 4, 32
    R = 6 * HD
    M0 = 96 if HD == 16 else 64
    KK = H * HD // P
    NP, NE = cfg["n_pro"], cfg["n_epi"]
    LOADS = 9
    name = cfg["name"]
    split_slots = cfg["split_slots"]
    turn_job = cfg["turn_job"]

    with ExitStack() as ctx:
        def sb(n, shape, dt=F32):
            return ctx.enter_context(nc.sbuf_tensor(name + n, shape, dt))

        def psum(n):
            return ctx.enter_context(nc.psum_tensor(name + n, [P, 512], F32))

        score, tscore = [psum(f"score{i}") for i in range(2)], [psum(f"tscore{i}") for i in range(2)]
        pvp, back, pro, epi = psum("pvp"), psum("back"), psum("pro"), psum("epi")
        qs = [sb(f"qs{i}", [M0 + 3, H, SEQ], BF16) for i in range(3)]
        ks = [sb(f"ks{i}", [M0 + 3, H, SEQ], BF16) for i in range(3)]
        nmax = [sb(f"nmax{i}", [P, QT, H]) for i in range(3)]
        mrow, mleft, mpart = sb("mrow", [8, SEQ]), sb("mleft", [8, SEQ]), sb("mpart", [8, 3, SEQ], BF16)
        probT = [sb(f"probT{i}", [P, 512]) for i in range(2)]
        raw = [sb(f"raw{i}", [P, SEQ]) for i in range(2)]
        rden = sb("rden", [P, QT, G])
        o = [sb(f"o{i}", [P, QT, H * HD]) for i in range(3)]
        v = [sb(f"v{i}", [P, QT, H, VW]) for i in range(3)]
        whole = {n: sb(n + "whole", [P, KK * SEQ]) for n in "qk"}
        left = {n: sb(n + "left", [P, KK * SEQ]) for n in "qk"}
        part = {n: sb(n + "part", [P, 3, KK * SEQ], BF16) for n in "qk"}
        zeros = sb("zeros", [P, KK * SEQ])
        st, mv, rstd = sb("st", [P, QT, 6]), sb("mv", [P, QT, 2]), sb("rstd", [P, QT])
        parts_dram = {n: dram[f"{n}_parts{HD}"] for n in "qk"}
        tops_dram = dram["top_parts"]
        bufs = dict(sb=sb, pro=pro, epi=epi, o=o, v=v, whole=whole)

        def split_step(r, eng, add, src, rest, dst, link, count, done):
            if r:
                eng.wait_ge(link, count + r)
            if r % 2 == 0:
                add(dst[r // 2], src if r == 0 else rest, zeros[0:src.shape[0], 0:src.shape[1]], ALU.add
                    ).then_inc(link, 1)
            elif r == 1:
                add(rest, src, dst[0], ALU.subtract).then_inc(link, 1)
            else:
                add(dst[2], rest, dst[1], ALU.subtract).then_inc(done, 1)

        def split_matrix(r, eng, add, which, n):
            if r == 0:
                eng.wait_ge(S[which + "_ready"], n + 1)
                wait(eng, S[which + "_stored"], 48 * n)
            split_step(r, eng, add, whole[which][:, :], left[which][:, :], [part[which][:, i, :] for i in range(3)],
                       S[which + "_link"], 3 * n, S[which + "_split"])
        fns = cfg["make"](nc, keep, bufs, S)
        schedule_pro, schedule_epi = cfg["pro_at"], cfg["epi_at"]

        mask = fns.get("mask")

        def batch(i, k):
            return 3 * i + k, i + k // 3, k % 3

        def iterations(eng, body):
            for c in range(3):
                body(0, c, True, True, c > 0)
            with eng.Fori(1, 4) as i:
                for k in range(3):
                    body(i, k, True, True, True)
            body(0, 12, True, True, True)
            body(0, 13, True, True, True)
            body(0, 14, True, False, True)
            body(0, 15, False, False, True)

        with nc.Block() as block:
            @block.sync
            def _(sp):
                for dst, src in fns["weights"]:
                    sp.dma_start(dst, src).then_inc(S["weights"], 16)

                def stream(b):
                    n, rnd, buf = b
                    if "stream" in fns:
                        wait(sp, S["pro_filled"], NP * (n - 2))
                        dst, src = fns["stream"](n, buf)
                        sp.dma_start(dst, src).then_inc(S["stream"][buf], 16)

                def store_parts(which, b):
                    n, rnd, buf = b
                    sp.wait_ge(S[which + "_split"], n + 1)
                    for r in range(3):
                        sp.dma_start(parts_dram[which][buf, r].rearrange("d (h k) s -> (d h) (k s)", k=KK),
                                     part[which][:, r, :]).then_inc(S[which + "_stored"], 16)

                def load_stack(which, b):
                    n, rnd, buf = b
                    sp.wait_ge(S[which + "_stored"], 48 * (n + 1))
                    if which == "q":
                        pieces = [(0, 0, 3), (3, 0, 2), (5, 0, 1)]
                    else:
                        pieces = [(0, 0, 1), (1, 0, 1), (2, 0, 1), (3, 1, 1), (4, 1, 1), (5, 2, 1)]
                    for at, r, m in pieces:
                        sp.dma_start((qs if which == "q" else ks)[buf][at * HD:(at + m) * HD, :, :],
                                     parts_dram[which][buf, r:r + m].rearrange("r d h s -> (r d) h s")
                                     ).then_inc(S["stacked"][buf], 16)

                def store_tops(g, b):
                    n, rnd, buf = b
                    sp.wait_ge(S["tops_split"], 2 * n + g + 1)
                    sp.dma_start(tops_dram[buf, g].rearrange("r h s -> h r s"), mpart[:, :, :]
                                 ).then_inc(S["tops_stored"], 16)

                def load_tops(g, b):
                    n, rnd, buf = b
                    sp.wait_ge(S["tops_stored"], 16 * (2 * n + g + 1))
                    sp.dma_start(qs[buf][M0:M0 + 3, 8 * g:8 * g + 8, :], tops_dram[buf, g]
                                 ).then_inc(S["tops_in"][buf], 16)

                def body(i, k, a, p, e):
                    store_tops(1, batch(i, k))
                    load_tops(1, batch(i, k))
                    if k + 3 < BATCH:
                        stream(batch(i, k + 3))
                    if p:
                        store_parts("k", batch(i, k + 2))
                        load_stack("k", batch(i, k + 2))
                    if a:
                        store_tops(0, batch(i, k + 1))
                        load_tops(0, batch(i, k + 1))
                    if p:
                        store_parts("q", batch(i, k + 2))
                        load_stack("q", batch(i, k + 2))
                    if fns.get("sync_more"):
                        fns["sync_more"](sp, 3 * i + k, k + 3 < BATCH, e)

                for k in range(3):
                    stream(batch(0, k))
                sp.wait_ge(S["setup"], 1)
                for k in range(2):
                    if fns.get("sync_head"):
                        fns["sync_head"](sp, k)
                    for which in "kq":
                        store_parts(which, batch(0, k))
                        load_stack(which, batch(0, k))
                store_tops(0, batch(0, 0))
                load_tops(0, batch(0, 0))
                iterations(sp, body)
                if fns.get("sync_tail"):
                    fns["sync_tail"](sp)

            @block.gpsimd
            def _(pool):
                add = nc.gpsimd.tensor_tensor

                def rstds(n):
                    pool.wait_ge(S["var"], n + 1)
                    add(rstd[:, :], mv[:, :, 1], keep["eps"][:, 0:QT], ALU.add).then_inc(S["vareps"], 1)
                    pool.wait_ge(S["vareps"], n + 1)
                    add(rstd[:, :], rstd[:, :], keep["mhalf"][:, 0:QT], ALU.pow).then_inc(S["rstd"], 1)

                def split_ready(which, n):
                    for r in range(4):
                        split_matrix(r, pool, add, which, n)

                def split_tops(g, n):
                    pool.wait_ge(S["tops_copied"], 2 * n + g + 1)
                    wait(pool, S["tops_stored"], 16 * (2 * n + g))
                    for r in range(4):
                        split_step(r, pool, add, mrow[:, :], mleft[:, :], [mpart[:, i, :] for i in range(3)],
                                   S["tops_link"], 3 * (2 * n + g), S["tops_split"])

                def body(i, k, a, p, e):
                    c = 3 * i + k
                    split_tops(1, c)
                    if p:
                        split_ready("k", c + 2)
                        if not split_slots:
                            split_ready("q", c + 2)
                    if a:
                        split_tops(0, c + 1)
                    if k + 3 < BATCH:
                        rstds(c + 3)
                pool.wait_ge(S["setup"], 1)
                for n in range(2):
                    rstds(n)
                    split_ready("k", n)
                    if not split_slots:
                        split_ready("q", n)
                rstds(2)
                split_tops(0, 0)
                iterations(pool, body)

            @block.vector
            def _(dve):
                def x_tile(n, t):
                    return keep["x"][:, bass.ds(n * QT + t, 1), :].rearrange("p a b -> p (a b)")

                def norm(n):
                    if fns.get("norm_wait"):
                        fns["norm_wait"](dve, n)
                    for t in range(QT):
                        ins = nc.vector.bn_stats(st[:, t, :], x_tile(n, t))
                    ins.then_inc(S["stats"], 1)
                    dve.wait_ge(S["stats"], n + 1)
                    nc.vector.memset(keep["scratch"][:, 0:1], 0.0)
                    for t in range(QT):
                        ins = nc.vector.bn_aggr(mv[:, t, :], st[:, t, :])
                    ins.then_inc(S["var"], 1)

                def normed(n):
                    dve.wait_ge(S["rstd"], n + 1)
                    wait(dve, S["pro_filled"], 0 if isinstance(n, int) and n == 0 else NP * (n - 1) + turn_job + 1)
                    for t in range(QT):
                        ins = nc.vector.tensor_scalar(fns["h"][:, t, :], x_tile(n, t), mv[:, t, 0:1],
                                                      rstd[:, t:t + 1], ALU.subtract, ALU.mult)
                    ins.then_inc(S["normed"], 1)

                def row_max(h, b):
                    n, rnd, buf = b
                    if h == 0:
                        wait(dve, S["tops_filled"], 2 * (n - 2))
                    dve.wait_ge(S["scores"], 16 * n + h + 1)
                    src = score[h % 2]
                    if mask:
                        src = mask["masked"][h % 2]
                        nc.vector.tensor_tensor(src[:, :], score[h % 2][:, :], mask["rows"][:, :], ALU.add
                                                ).then_inc(S["masked"], 1)
                        dve.wait_ge(S["masked"], 16 * n + h + 1)
                    nc.vector.tensor_reduce(nmax[buf][:, :, h], src[:, :].rearrange("p (t k) -> p t k", t=QT),
                                            AX.X, ALU.max, negate=True).then_inc(S["row_max"], 1)

                def normalise(g, b):
                    n, rnd, buf = b
                    bank = back[:, 0:QT * P].rearrange("p (t g v) -> p t g v", t=QT, g=G)
                    dve.wait_ge(S["back"], NG * n + g + 1)
                    nc.vector.reciprocal(rden[:, :, :], bank[:, :, :, HD]).then_inc(S["rden"], 1)
                    dve.wait_ge(S["rden"], NG * n + g + 1)
                    if g == 0:
                        wait(dve, S["epi_filled"], NE * (n - 2))
                    for t in range(QT):
                        dst = o[buf][:, t, g * G * HD:(g + 1) * G * HD].rearrange("p (g v) -> p g v", g=G)
                        ins = nc.vector.tensor_tensor(dst, bank[:, t, :, 0:HD],
                                                      rden[:, t, :].unsqueeze(2).to_broadcast([P, G, HD]), ALU.mult)
                    ins.then_inc(S["o_ready"], 1)

                def pro_copy(j, b):
                    n, rnd, buf = b
                    if fns["pro_engine"](j) == "dve":
                        dve.wait_ge(S["pro_filled"], NP * n + j + 1)
                        if j == NP - 1:
                            wait(dve, S["pv"], 16 * (n - 2))
                        fns["pro_copy"](dve, j, n, buf).then_inc(S["pro_copied"], 1)

                def epi_copy(j, n):
                    if fns["epi_engine"](j) == "dve":
                        dve.wait_ge(S["epi_filled"], NE * n + j + 1)
                        fns["epi_copy"](dve, j, n).then_inc(S["epi_copied"], 1)

                def body(i, k, a, p, e):
                    c = 3 * i + k
                    for h in range(16):
                        if a:
                            row_max(h, batch(i, k + 1))
                        if h > G and h % G == 1:
                            normalise(h // G - 1, batch(i, k))
                        if h == 1 and e:
                            normalise(NG - 1, batch(i, k - 1))
                        if p:
                            for j in schedule_pro(h):
                                pro_copy(j, batch(i, k + 2))
                            if h in split_slots:
                                split_matrix(h - split_slots[0], dve, nc.vector.tensor_tensor, "q", c + 2)
                        if e:
                            for j in schedule_epi(h):
                                epi_copy(j, c - 1)
                        if k + 3 < BATCH:
                            if h == 14:
                                norm(c + 3)
                            if h == 15:
                                normed(c + 3)

                nc.vector.memset(zeros[:, :], 0.0)
                for b in range(3):
                    if R < M0:
                        nc.vector.memset(qs[b][32:64, :, :], 0.0)
                        nc.vector.memset(ks[b][32:64, :, :], 0.0)
                    nc.vector.memset(v[b][:, :, :, HD:HD + 1], 1.0)
                    nc.vector.memset(v[b][:, :, :, HD + 1:VW], 0.0)
                    ins = nc.vector.memset(ks[b][M0:M0 + 3, :, :], 1.0)
                ins.then_inc(S["setup"], 1)
                dve.wait_ge(S["weights"], 16 * len(fns["weights"]))
                if mask:
                    fns["mask_setup"](dve)
                for n in range(2):
                    norm(n)
                    normed(n)
                    for j in range(NP):
                        pro_copy(j, batch(0, n))
                    for r in range(len(split_slots)):
                        split_matrix(r, dve, nc.vector.tensor_tensor, "q", n)
                norm(2)
                normed(2)
                for h in range(16):
                    row_max(h, batch(0, 0))
                iterations(dve, body)
                normalise(NG - 1, batch(0, BATCH - 1))
                for j in range(NE):
                    epi_copy(j, BATCH - 1)

            @block.scalar
            def _(act):
                def exp(h, b):
                    n, rnd, buf = b
                    act.wait_ge(S["tscores"], 16 * n + h + 1)
                    wait(act, S["pv"], 16 * n + h - 1)
                    nc.scalar.activation(probT[h % 2][:, :], tscore[h % 2][:, :], ACT.Exp).then_inc(S["exp"], 1)

                def copy_raw(g, n):
                    act.wait_ge(S["pv"], 16 * n + G * (g + 1))
                    wait(act, S["back"], NG * n + g - 1)
                    nc.scalar.copy(raw[g % 2][:, :], pvp[:, 0:SEQ]).then_inc(S["raw"], 1)

                def copy_tops(g, n):
                    act.wait_ge(S["tops_filled"], 2 * n + g + 1)
                    wait(act, S["tops_split"], 2 * n + g)
                    nc.scalar.copy(mrow[:, :], epi[0:8, 0:SEQ]).then_inc(S["tops_copied"], 1)

                def pro_copy(j, b):
                    n, rnd, buf = b
                    if fns["pro_engine"](j) == "act":
                        act.wait_ge(S["pro_filled"], NP * n + j + 1)
                        fns["pro_copy"](act, j, n, buf).then_inc(S["pro_copied"], 1)

                def epi_copy(j, n):
                    if fns["epi_engine"](j) == "act":
                        act.wait_ge(S["epi_filled"], NE * n + j + 1)
                        fns["epi_copy"](act, j, n).then_inc(S["epi_copied"], 1)
                    if fns.get("epi_act"):
                        fns["epi_act"](act, j, n)

                def body(i, k, a, p, e):
                    c = 3 * i + k
                    for h in range(16):
                        exp(h, batch(i, k))
                        if h == 0:
                            copy_tops(1, c)
                            if e:
                                copy_raw(NG - 1, c - 1)
                        elif h % G == 0:
                            copy_raw(h // G - 1, c)
                        if p:
                            for j in schedule_pro(h):
                                pro_copy(j, batch(i, k + 2))
                        if h == 8 and a:
                            copy_tops(0, c + 1)
                        if e:
                            for j in schedule_epi(h):
                                epi_copy(j, c - 1)

                act.wait_ge(S["weights"], 16 * len(fns["weights"]))
                for n in range(2):
                    for j in range(NP):
                        pro_copy(j, batch(0, n))
                copy_tops(0, 0)
                iterations(act, body)
                copy_raw(NG - 1, BATCH - 1)
                for j in range(NE):
                    epi_copy(j, BATCH - 1)

            @block.tensor
            def _(pe):
                def scores(h, b):
                    n, rnd, buf = b
                    if h == 0:
                        pe.wait_ge(S["stacked"][buf], 16 * LOADS * (rnd + 1))
                    wait(pe, S["row_max"], 16 * n + h - 1)
                    for t in range(QT):
                        mm = nc.tensor.matmul(score[h % 2][:, t * SEQ:(t + 1) * SEQ],
                                              qs[buf][0:R, h, t * P:(t + 1) * P], ks[buf][0:R, h, :],
                                              start=True, stop=True)
                    mm.then_inc(S["scores"], 1)

                def turned_scores(h, b):
                    n, rnd, buf = b
                    if h % 8 == 0:
                        pe.wait_ge(S["tops_in"][buf], 16 * (2 * rnd + h // 8 + 1))
                    wait(pe, S["exp"], 16 * n + h - 1)
                    for t in range(QT):
                        mm = nc.tensor.matmul(tscore[h % 2][:, t * SEQ:(t + 1) * SEQ],
                                              ks[buf][:, h, t * P:(t + 1) * P], qs[buf][:, h, :],
                                              start=True, stop=not mask)
                        for r in range(3 if mask else 0):
                            mm = nc.tensor.matmul(tscore[h % 2][:, t * SEQ:(t + 1) * SEQ], mask["ident"][:, :],
                                                  mask["parts"][:, r, t * SEQ:(t + 1) * SEQ],
                                                  start=False, stop=(r == 2))
                    mm.then_inc(S["tscores"], 1)

                def pv(h, b):
                    n, rnd, buf = b
                    g = h // G
                    if h == 0:
                        pe.wait_ge(S["pro_copied"], NP * (n + 1))
                    pe.wait_ge(S["exp"], 16 * n + h + 1)
                    if h % G == 0:
                        wait(pe, S["raw"], NG * n + g)
                    r = 32 * (h % G)
                    for t in range(QT):
                        mm = nc.tensor.matmul(pvp[r:r + 32, 0:SEQ], v[buf][:, t, h, :],
                                              probT[h % 2][:, t * SEQ:(t + 1) * SEQ], start=(t == 0), stop=(t == 1))
                    mm.then_inc(S["pv"], 1)

                def turn_back(g, n):
                    pe.wait_ge(S["raw"], NG * n + g + 1)
                    wait(pe, S["o_ready"], NG * n + g)
                    for t in range(QT):
                        mm = nc.tensor.transpose(back[:, t * P:(t + 1) * P], raw[g % 2][:, t * P:(t + 1) * P],
                                                 keep["ident"][:, :])
                    mm.then_inc(S["back"], 1)

                def turn_tops(g, b):
                    n, rnd, buf = b
                    pe.wait_ge(S["row_max"], 16 * n + 8 * (g + 1))
                    if g == 0:
                        wait(pe, S["tops_copied"], 2 * n)
                    elif isinstance(n, int) and n < 2:
                        pe.wait_ge(S["tops_copied"], 2 * n + 1)
                    else:
                        pe.wait_ge(S["epi_copied"], NE * (n - 1))
                    for t in range(QT):
                        mm = nc.tensor.transpose(epi[0:8, t * P:(t + 1) * P], nmax[buf][:, t, 8 * g:8 * g + 8],
                                                 keep["ident"][:, :])
                    mm.then_inc(S["tops_filled"], 1)

                def pro_fill(j, b):
                    n, rnd, buf = b
                    wait(pe, S["pro_copied"], NP * n + j)
                    if j == turn_job:
                        pe.wait_ge(S["normed"], n + 1)
                    fns["pro_fill"](pe, j, n, rnd, buf).then_inc(S["pro_filled"], 1)

                def epi_fill(j, b):
                    n, rnd, buf = b
                    wait(pe, S["epi_copied"], NE * n + j)
                    if j == 0:
                        pe.wait_ge(S["o_ready"], NG * (n + 1))
                        tops = 2 * n + 5
                        pe.wait_ge(S["tops_copied"], min(tops, 2 * BATCH) if isinstance(tops, int) else tops)
                    fns["epi_fill"](pe, j, n, buf).then_inc(S["epi_filled"], 1)

                def body(i, k, a, p, e):
                    c = 3 * i + k
                    for h in range(16):
                        if h < 15:
                            turned_scores(h + 1, batch(i, k))
                        if a:
                            scores(h, batch(i, k + 1))
                        if h > 0:
                            pv(h - 1, batch(i, k))
                        elif e:
                            pv(15, batch(i, k - 1))
                        if h == 0:
                            turn_tops(1, batch(i, k))
                        if h > G and h % G == 1:
                            turn_back(h // G - 1, c)
                        if h == 1 and e:
                            turn_back(NG - 1, c - 1)
                        if p:
                            for j in schedule_pro(h):
                                pro_fill(j, batch(i, k + 2))
                        if h == 8 and a:
                            turn_tops(0, batch(i, k + 1))
                        if e:
                            for j in schedule_epi(h):
                                epi_fill(j, batch(i, k - 1))
                        if h == 15 and a:
                            turned_scores(0, batch(i, k + 1))

                pe.wait_ge(S["weights"], 16 * len(fns["weights"]))
                if mask:
                    pe.wait_ge(S["mask_ready"], 5)
                for n in range(2):
                    for j in range(NP):
                        pro_fill(j, batch(0, n))
                for h in range(16):
                    scores(h, batch(0, 0))
                    if h == 8:
                        turn_tops(0, batch(0, 0))
                turned_scores(0, batch(0, 0))
                iterations(pe, body)
                pv(15, batch(0, BATCH - 1))
                turn_back(NG - 1, BATCH - 1)
                for j in range(NE):
                    epi_fill(j, batch(0, BATCH - 1))
    zero_semaphores(nc, S["all"])


def cross_rope(nc, keep, S, dram):
    H, HD, L = 16, 16, "L2"

    def make(nc, keep, bufs, S):
        sb, pro, epi = bufs["sb"], bufs["pro"], bufs["epi"]
        wq, wqr, wk, wkr, wv, wo = w = [sb(n, [P, KT, D]) for n in ("wq", "wqr", "wk", "wkr", "wv", "wo")]
        weights = [(w[i][:, :, :], dram[L + n].rearrange("(k p) m -> p k m", p=P))
                   for i, n in enumerate(("wq", "wqr", "wk", "wkr", "wv", "wo"))]
        biases = [sb(n, [P, 2]) for n in ("bq", "bqr", "bk", "bkr")]
        weights += [(b[:, :], dram[L + n]) for b, n in zip(biases, ("bq", "bqr", "bk", "bkr"))]
        bv, bo = sb("bv", [P, D]), sb("bo", [1, D])
        tables = [sb(n, [P, SEQ]) for n in ("cosq", "sinq", "cosk", "sink")]
        weights += [(t[:, :], dram[n]) for t, n in zip(tables, ("cosq", "sinq", "cosk", "sink"))]
        weights += [(bv[:, :], dram[L + "bv"]), (bo[:, :], dram[L + "bo"])]
        h, hT, oT = sb("h", [P, QT, D]), sb("hT", [P, KT, SEQ]), sb("oT", [P, KT, SEQ])
        cT = [sb(f"cT{i}", [P, KT, SEQ]) for i in range(3)]
        turned, mixed = sb("turned", [P, KT, SEQ]), sb("mixed", [P, KT, SEQ])

        def pro_fill(pe, j, n, rnd, buf):
            if j == 0:
                pe.wait_ge(S["stream"][buf], 16 * (rnd + 1))
            if j < 2:
                return project(nc, pro, (wk, wkr)[j], cT[buf], range(KT))
            if j == 2:
                return turn(nc, keep, pro, h)
            if j < 5:
                return project(nc, pro, (wq, wqr)[j - 3], hT, range(KT))
            return project_rows(nc, pro, cT[buf], wv, 0, D)

        def pro_copy(eng, j, n, buf):
            if j == 2:
                return nc.scalar.copy(flat(hT[:, :, :]), pro[:, :])
            if j == 5:
                return nc.vector.tensor_tensor(
                    bufs["v"][buf][:, :, :, 0:HD], pro[:, :].rearrange("p (t h v) -> p t h v", t=QT, h=H),
                    bv[:, :].rearrange("p (h v) -> p h v", h=H).unsqueeze(1).to_broadcast([P, QT, H, HD]), ALU.add)
            which, rotated = ("k", j == 1) if j < 2 else ("q", j == 4)
            at = (2 if which == "k" else 0) + rotated
            to = turned if rotated else mixed
            for k in range(KT):
                ins = nc.vector.scalar_tensor_tensor(out=to[:, k, :], in0=pro[:, k * SEQ:(k + 1) * SEQ],
                                                     scalar=biases[at][:, k:k + 1], in1=tables[at][:, :],
                                                     op0=ALU.add, op1=ALU.mult)
            if not rotated:
                return ins
            ins.then_inc(S["rope"], 1)
            eng.wait_ge(S["rope"], 2 * n + (1 if which == "k" else 2))
            wait(eng, S[which + "_split"], n)
            nc.vector.tensor_tensor(bufs["whole"][which][:, :], flat(mixed[:, :, :]), flat(turned[:, :, :]),
                                    ALU.add).then_inc(S[which + "_ready"], 1)
            eng.wait_ge(S[which + "_ready"], n + 1)
            return nc.vector.memset(keep["scratch"][:, 1:2], 0.0)

        def epi_fill(pe, j, n, buf):
            if j == 0:
                return turn(nc, keep, epi, bufs["o"][buf])
            return output_rows(nc, epi, oT, wo, bo[0:1, :], keep, KT)

        def epi_copy(eng, j, n):
            if j == 0:
                return nc.scalar.copy(flat(oT[:, :, :]), epi[:, :])
            return add_output(nc, eng, keep, epi, keep["gate"][:, 4:5], n)

        return dict(weights=weights, h=h, pro_fill=pro_fill, pro_copy=pro_copy, epi_fill=epi_fill, epi_copy=epi_copy,
                    pro_engine=lambda j: "act" if j == 2 else "dve", epi_engine=lambda j: "act" if j == 0 else "dve",
                    stream=lambda n, buf: (cT[buf][:, :, :],
                                           dram["ctxT"][bass.ds(n, 1), :, :, :].rearrange("a p k s -> (a p) k s")))

    stacked_attention(nc, keep, S, dram, dict(name=L, dim=HD, n_pro=6, n_epi=2, make=make,
                                              turn_job=2,
                                              split_slots=[7, 8, 9, 10], pro_at=spread([0, 1, 3, 4, 6, 9]),
                                              epi_at=spread([12, 14])))


def cross_masked(nc, keep, S, dram):
    H, HD, L = 16, 16, "L0"

    def make(nc, keep, bufs, S):
        sb, pro, epi = bufs["sb"], bufs["pro"], bufs["epi"]
        wq, wk, wv, wo = w = [sb(n, [P, KT, D]) for n in ("wq", "wk", "wv", "wo")]
        weights = [(w[i][:, :, :], dram[L + n].rearrange("(k p) m -> p k m", p=P))
                   for i, n in enumerate(("wq", "wk", "wv", "wo"))]
        bq, bk, bv, bo = sb("bq", [P, 2]), sb("bk", [P, 2]), sb("bv", [P, D]), sb("bo", [1, D])
        weights += [(b[:, :], dram[L + n]) for b, n in ((bq, "bq"), (bk, "bk"), (bv, "bv"), (bo, "bo"))]
        h, hT, oT = sb("h", [P, QT, D]), sb("hT", [P, KT, SEQ]), sb("oT", [P, KT, SEQ])
        cT = [sb(f"cT{i}", [P, KT, SEQ]) for i in range(3)]
        rows, turned = sb("maskrows", [P, 512]), sb("maskturned", [P, 512])
        rest, parts, ident = sb("maskrest", [P, 512]), sb("maskparts", [P, 3, 512], BF16), sb("ident", [P, P], BF16)
        masked = [sb(f"masked{i}", [P, 512]) for i in range(2)]
        weights += [(rows[:, :].rearrange("p (t k) -> p t k", t=QT), dram["mask"].rearrange("(t p) k -> p t k", p=P)),
                    (turned[:, :].rearrange("p (t k) -> p t k", t=QT),
                     dram["maskT"].rearrange("(t p) k -> p t k", p=P))]

        def mask_setup(dve):
            nc.vector.tensor_copy(ident[:, :], keep["ident"][:, :])
            nc.vector.tensor_scalar(rows[:, :], rows[:, :], -BIG, None, ALU.mult)
            nc.vector.tensor_scalar(turned[:, :], turned[:, :], -BIG, None, ALU.mult).then_inc(S["mask_ready"], 1)
            dve.wait_ge(S["mask_ready"], 1)
            nc.vector.tensor_copy(parts[:, 0, :], turned[:, :]).then_inc(S["mask_ready"], 1)
            dve.wait_ge(S["mask_ready"], 2)
            nc.vector.tensor_tensor(rest[:, :], turned[:, :], parts[:, 0, :], ALU.subtract).then_inc(S["mask_ready"], 1)
            dve.wait_ge(S["mask_ready"], 3)
            nc.vector.tensor_copy(parts[:, 1, :], rest[:, :]).then_inc(S["mask_ready"], 1)
            dve.wait_ge(S["mask_ready"], 4)
            nc.vector.tensor_tensor(parts[:, 2, :], rest[:, :], parts[:, 1, :], ALU.subtract
                                    ).then_inc(S["mask_ready"], 1)

        def pro_fill(pe, j, n, rnd, buf):
            if j == 0:
                pe.wait_ge(S["stream"][buf], 16 * (rnd + 1))
                return project(nc, pro, wk, cT[buf], range(KT))
            if j == 1:
                return turn(nc, keep, pro, h)
            if j == 2:
                return project(nc, pro, wq, hT, range(KT))
            return project_rows(nc, pro, cT[buf], wv, 0, D)

        def pro_copy(eng, j, n, buf):
            if j == 1:
                return nc.scalar.copy(flat(hT[:, :, :]), pro[:, :])
            if j == 3:
                return nc.vector.tensor_tensor(
                    bufs["v"][buf][:, :, :, 0:HD], pro[:, :].rearrange("p (t h v) -> p t h v", t=QT, h=H),
                    bv[:, :].rearrange("p (h v) -> p h v", h=H).unsqueeze(1).to_broadcast([P, QT, H, HD]), ALU.add)
            which, b, scale = ("k", bk, 1.0) if j == 0 else ("q", bq, 0.25)
            wait(eng, S[which + "_split"], n)
            for k in range(KT):
                ins = nc.vector.tensor_scalar(bufs["whole"][which][:, k * SEQ:(k + 1) * SEQ],
                                              pro[:, k * SEQ:(k + 1) * SEQ], b[:, k:k + 1], scale,
                                              ALU.add, ALU.mult)
            ins.then_inc(S[which + "_ready"], 1)
            eng.wait_ge(S[which + "_ready"], n + 1)
            return nc.vector.memset(keep["scratch"][:, 1:2], 0.0)

        def epi_fill(pe, j, n, buf):
            if j == 0:
                return turn(nc, keep, epi, bufs["o"][buf])
            return output_rows(nc, epi, oT, wo, bo[0:1, :], keep, KT)

        def epi_copy(eng, j, n):
            if j == 0:
                return nc.scalar.copy(flat(oT[:, :, :]), epi[:, :])
            return add_output(nc, eng, keep, epi, keep["gate"][:, 0:1], n)

        return dict(weights=weights, h=h, pro_fill=pro_fill, pro_copy=pro_copy, epi_fill=epi_fill, epi_copy=epi_copy,
                    mask=dict(rows=rows, parts=parts, ident=ident, masked=masked), mask_setup=mask_setup,
                    pro_engine=lambda j: "act" if j == 1 else "dve", epi_engine=lambda j: "act" if j == 0 else "dve",
                    stream=lambda n, buf: (cT[buf][:, :, :],
                                           dram["ctxT"][bass.ds(n, 1), :, :, :].rearrange("a p k s -> (a p) k s")))

    stacked_attention(nc, keep, S, dram, dict(name=L, dim=HD, n_pro=4, n_epi=2, make=make, turn_job=1,
                                              split_slots=[], pro_at=spread([0, 1, 3, 7]),
                                              epi_at=spread([11, 13])))


def latent_attention(nc, keep, S, dram):
    H, VD, L, E = 16, 8, "L0f", 8
    LAT = H * VD
    scale = float(np.float32(1.0) / np.sqrt(np.float32(VD)))
    R = 13

    def make(nc, keep, bufs, S):
        sb, pro, epi, o, v = [bufs[n] for n in ("sb", "pro", "epi", "o", "v")]
        wq, wk, wv = [sb(n, [P, KT, LAT]) for n in ("wq", "wk", "wv")]
        wo, router, b2 = sb("wo", [P, D]), sb("router", [P, KT, E]), sb("b2", [E, D])
        bq, bk, bo, br = sb("bq", [P, 1]), sb("bk", [P, 1]), sb("bo", [P, KT]), sb("br", [1, E])
        bv, iota = sb("bv", [P, LAT]), sb("iota", [P, E])
        h, hT = sb("h", [P, QT, D]), sb("hT", [P, KT, SEQ])
        oT, mT = sb("oT", [P, SEQ]), sb("mT", [P, KT, SEQ])
        nm, tot, rtot = sb("nm", [P, QT]), sb("tot", [P, QT]), sb("rtot", [P, QT])
        e, top, idx = sb("e", [P, QT, E]), sb("top", [P, QT, 8]), sb("idx", [P, QT, 8], U32)
        idf, comb, hit = sb("idf", [P, QT, 8]), sb("comb", [P, QT, E]), sb("hit", [P, QT, E])
        combT = sb("combT", [E, SEQ])

        weights = [(w[:, :, :], dram[L + n].rearrange("(k p) m -> p k m", p=P))
                   for w, n in ((wq, "wq"), (wk, "wk"), (wv, "wv"), (router, "router"))]
        weights += [(w[:, :], dram[L + n]) for w, n in ((wo, "wo"), (b2, "b2"), (bq, "bq"), (bk, "bk"), (bo, "bo"),
                                                        (br, "br"), (bv, "bv"))]
        weights += [(iota[:, :], dram["iota"][:, 0:E])]

        def norm_wait(dve, n):
            wait(dve, S["hs_saved"], 16 * n)
            nc.vector.memset(keep["scratch"][:, 1:2], 0.0)

        def pro_fill(pe, j, n, rnd, buf):
            if j == 0:
                return turn(nc, keep, pro, h)
            if j == 1:
                for i, w in enumerate((wq, wk)):
                    for k in range(KT):
                        mm = nc.tensor.matmul(pro[:, i * SEQ:(i + 1) * SEQ], w[:, k, :], hT[:, k, :],
                                              start=(k == 0), stop=(k == KT - 1))
                return mm
            return project_rows(nc, pro, hT, wv, 0, LAT)

        def pro_copy(eng, j, n, buf):
            if j == 0:
                return nc.scalar.copy(flat(hT[:, :, :]), pro[:, :])
            if j == 1:
                wait(eng, S["k_split"], n)
                nc.vector.tensor_scalar(bufs["whole"]["k"][:, :], pro[:, SEQ:2 * SEQ], bk[:, 0:1], None, ALU.add
                                        ).then_inc(S["k_ready"], 1)
                wait(eng, S["q_split"], n)
                nc.vector.tensor_scalar(bufs["whole"]["q"][:, :], pro[:, 0:SEQ], bq[:, 0:1], scale, ALU.add, ALU.mult
                                        ).then_inc(S["q_ready"], 1)
                eng.wait_ge(S["q_ready"], n + 1)
                return nc.vector.memset(keep["scratch"][:, 2:3], 0.0)
            return nc.vector.tensor_tensor(
                v[buf][:, :, :, 0:VD], pro[:, 0:QT * LAT].rearrange("p (t h v) -> p t h v", t=QT, h=H),
                bv[:, :].rearrange("p (h v) -> p h v", h=H).unsqueeze(1).to_broadcast([P, QT, H, VD]), ALU.add)

        def epi_fill(pe, j, c, buf):
            if j == 0:
                for t in range(QT):
                    mm = nc.tensor.transpose(epi[:, t * P:(t + 1) * P], o[buf][:, t, :], keep["ident"][:, :])
                return mm
            if j == 1:
                for m in range(KT):
                    mm = nc.tensor.matmul(epi[:, m * SEQ:(m + 1) * SEQ], wo[:, m * P:(m + 1) * P], oT[:, :],
                                          start=True, stop=True)
                return mm
            for t in range(QT):
                if j == 2:
                    for k in range(KT):
                        nc.tensor.matmul(epi[:, t * E:(t + 1) * E], mT[:, k, t * P:(t + 1) * P], router[:, k, :],
                                         start=(k == 0), stop=False)
                    mm = nc.tensor.matmul(epi[:, t * E:(t + 1) * E], keep["ones"][0:1, :], br[0:1, :],
                                          start=False, stop=True)
                if j == 3:
                    mm = nc.tensor.transpose(epi[0:E, t * P:(t + 1) * P], comb[:, t, :], keep["ident"][:, :])
                if j == 4:
                    mm = nc.tensor.matmul(epi[:, t * D:(t + 1) * D], combT[:, t * P:(t + 1) * P], b2[:, :],
                                          start=True, stop=True)
            return mm

        def route(dve, c):
            n = [0]

            def linked(ins):
                n[0] += 1
                ins.then_inc(S["route"], 1)
                dve.wait_ge(S["route"], R * c + n[0])

            def take_wait():
                nc.vector.memset(keep["scratch"][:, 2:3], 0.0)

            logits = epi[:, 0:QT * E].rearrange("p (t e) -> p t e", t=QT)
            nc.vector.tensor_reduce(nm[:, :], logits, AX.X, ALU.max, negate=True).then_inc(S["route_max"], 1)
            dve.wait_ge(S["route_exp"], c + 1)
            linked(nc.vector.tensor_reduce(tot[:, :], e[:, :, :], AX.X, ALU.add))
            linked(nc.vector.reciprocal(rtot[:, :], tot[:, :]))
            linked(nc.vector.tensor_tensor(e[:, :, :], e[:, :, :],
                                           rtot[:, :].unsqueeze(2).to_broadcast([P, QT, E]), ALU.mult))
            take_wait()
            for t in range(QT):
                ins = nc.vector.max(top[:, t, :], e[:, t, :])
            linked(ins)
            take_wait()
            for t in range(QT):
                ins = nc.vector.max_index(idx[:, t, :], top[:, t, :], e[:, t, :])
            linked(ins)
            linked(nc.vector.tensor_copy(idf[:, :, :], idx[:, :, :]))
            linked(nc.vector.tensor_tensor(tot[:, :], top[:, :, 0], top[:, :, 1], ALU.add))
            linked(nc.vector.tensor_scalar(tot[:, :], tot[:, :], 1e-8, None, ALU.add))
            linked(nc.vector.reciprocal(rtot[:, :], tot[:, :]))
            linked(nc.vector.tensor_tensor(top[:, :, 0:2], top[:, :, 0:2],
                                           rtot[:, :].unsqueeze(2).to_broadcast([P, QT, 2]), ALU.mult))
            for t in range(QT):
                nc.vector.tensor_scalar(comb[:, t, :], iota[:, :], idf[:, t, 0:1], top[:, t, 0:1],
                                        ALU.is_equal, ALU.mult)
                ins = nc.vector.tensor_scalar(hit[:, t, :], iota[:, :], idf[:, t, 1:2], top[:, t, 1:2],
                                              ALU.is_equal, ALU.mult)
            linked(ins)
            linked(nc.vector.tensor_tensor(comb[:, :, :], comb[:, :, :], hit[:, :, :], ALU.add))
            linked(nc.vector.tensor_scalar(keep["comb"][:, bass.ds(c * QT, QT), :], comb[:, :, :], 1.0, None,
                                           ALU.mult))
            assert n[0] == R
            return nc.vector.memset(keep["scratch"][:, 3:4], 0.0)

        def epi_copy(eng, j, c):
            if j == 0:
                return nc.scalar.copy(oT[:, :], epi[:, 0:SEQ])
            if j == 1:
                wait(eng, S["mT_saved"], 16 * c)
                for m in range(KT):
                    ins = nc.vector.tensor_scalar(mT[:, m, :], epi[:, m * SEQ:(m + 1) * SEQ], bo[:, m:m + 1], None,
                                                  ALU.add)
                return ins
            if j == 2:
                return route(eng, c)
            if j == 3:
                return nc.vector.tensor_copy(combT[:, :], epi[0:E, 0:SEQ])
            eng.wait_ge(S["hs_saved"], 16 * (c + 1))
            hs = flat(keep["hs"][:, bass.ds(c * QT, QT), :])
            return nc.vector.scalar_tensor_tensor(out=hs, in0=epi[:, :], scalar=0.3, in1=hs, op0=ALU.mult,
                                                  op1=ALU.add)

        def epi_act(act, j, c):
            if j == 2:
                act.wait_ge(S["route_max"], c + 1)
                for t in range(QT):
                    ins = nc.scalar.activation(e[:, t, :], epi[:, t * E:(t + 1) * E], ACT.Exp,
                                               bias=nm[:, t:t + 1])
                ins.then_inc(S["route_exp"], 1)

        def save(sp, c):
            sp.wait_ge(S["normed"], c + 1)
            sp.dma_start(keep["hs"][:, bass.ds(c * QT, QT), :], h[:, :, :]).then_inc(S["hs_saved"], 16)

        def save_m(eng, c):
            eng.wait_ge(S["epi_copied"], 5 * c + 2)
            eng.dma_start(keep["mT"][:, :, bass.ds(c * SEQ, SEQ)], mT[:, :, :]).then_inc(S["mT_saved"], 16)

        def sync_head(sp, k):
            save(sp, k)
            if k == 1:
                save(sp, 2)

        def sync_more(sp, c, more, e):
            if e:
                save_m(sp, c - 1)
            if more:
                save(sp, c + 3)

        def sync_tail(sp):
            save_m(sp, BATCH - 1)
            sp.wait_ge(S["mT_saved"], 16 * BATCH)

        return dict(weights=weights, h=h, norm_wait=norm_wait, pro_fill=pro_fill, pro_copy=pro_copy,
                    epi_fill=epi_fill, epi_copy=epi_copy, epi_act=epi_act,
                    pro_engine=lambda j: "act" if j == 0 else "dve",
                    epi_engine=lambda j: "act" if j == 0 else "dve",
                    sync_head=sync_head, sync_more=sync_more, sync_tail=sync_tail)

    stacked_attention(nc, keep, S, dram, dict(name=L, dim=VD, n_pro=3, n_epi=5, turn_job=0, make=make,
                                              split_slots=[4, 5, 6, 7], pro_at=spread([1, 3, 7]),
                                              epi_at=spread([9, 10, 11, 13, 14])))


def flamingo(nc, dram, out):
    with ExitStack() as ctx:
        def sb(name, shape, dt=F32):
            return ctx.enter_context(nc.sbuf_tensor(name, shape, dt))

        names = ["weights", "setup", "act_setup", "stats", "var", "vareps", "rstd", "normed", "pro_filled",
                 "pro_copied", "epi_filled", "epi_copied", "scores", "row_max", "exp", "pT", "pT_copied", "pv",
                 "rden", "hs_saved", "tick", "slots", "counted", "logits", "member", "placed", "zeroed", "up", "turned", "turn_copied", "peaks", "local_top", "top", "scale", "inv", "rounded", "quantised",
                 "tscores", "q_ready", "q_link", "q_split", "q_stored", "k_ready", "k_link", "k_split", "k_stored", "tops_filled",
                 "tops_copied", "tops_link", "tops_split", "tops_stored", "scaled", "mask_ready", "copied", "sig_clipped", "gated", "sigmoid", "mT_saved", "route", "route_max", "route_exp", "hidden", "act", "y", "added", "share",
                 "moe_out", "o_ready", "raw", "back", "masked", "rope"] + []
        S = {n: ctx.enter_context(nc.semaphore(n)) for n in names}
        S["stream"] = [ctx.enter_context(nc.semaphore(f"stream{i}")) for i in range(4)]
        S["stored"] = [ctx.enter_context(nc.semaphore(f"stored{i}")) for i in range(2)]
        S["expert_loaded"] = [ctx.enter_context(nc.semaphore(f"expert_loaded{i}")) for i in range(8)]
        for n in ("stacked", "tops_in"):
            S[n] = [ctx.enter_context(nc.semaphore(f"{n}{i}")) for i in range(3)]
        for n in ("scattered", "gathered"):
            S[n] = [ctx.enter_context(nc.semaphore(f"{n}{i}")) for i in range(2)]
        S["all"] = [S[n] for n in names] + S["expert_loaded"] + S["stacked"] + S["tops_in"] + S["stream"] + S["stored"] + S["scattered"] + S["gathered"]
        x_loaded = ctx.enter_context(nc.semaphore("x_loaded"))
        gates_loaded = ctx.enter_context(nc.semaphore("gates_loaded"))
        ready = ctx.enter_context(nc.semaphore("constants_ready"))
        tanh_done = ctx.enter_context(nc.semaphore("tanh_done"))

        keep = dict(x=sb("x", [P, TILES, D]), ident=sb("ident", [P, P]), ones=sb("ones", [P, P]),
                    mhalf=sb("mhalf", [P, 4]), eps=sb("eps", [P, 4]), scratch=sb("scratch", [P, 4]), gate=sb("gate", [P, 10]))

        with nc.Block() as block:
            @block.sync
            def _(sp):
                sp.dma_start(keep["gate"][:, 0:9], dram["gates"]).then_inc(gates_loaded, 16)
                sp.dma_start(keep["ident"][:, :], dram["ident"]).then_inc(gates_loaded, 16)
                for q in range(4):
                    n = TILES // 4
                    sp.dma_start(keep["x"][:, q * n:(q + 1) * n, :],
                                 dram["x"][q * n * P:(q + 1) * n * P, :].rearrange("(t p) d -> p t d", p=P)
                                 ).then_inc(x_loaded, 16)
                sp.wait_ge(x_loaded, 64)

            @block.vector
            def _(dve):
                nc.vector.memset(keep["ones"][:, :], 1.0)
                nc.vector.memset(keep["mhalf"][:, :], -0.5)
                nc.vector.memset(keep["eps"][:, :], EPS)
                dve.wait_ge(tanh_done, 1)
                nc.vector.tensor_tensor(keep["gate"][:, 2:3], keep["gate"][:, 2:3], keep["gate"][:, 8:9],
                                        ALU.mult).then_inc(ready, 1)

            @block.scalar
            def _(act):
                act.wait_ge(gates_loaded, 32)
                nc.scalar.activation(keep["gate"][:, 0:9], keep["gate"][:, 0:9], ACT.Tanh).then_inc(tanh_done, 1)

        stages = [lambda: cross_masked(nc, keep, S, dram),
                  lambda: layer0_feed_forward(nc, keep, S, dram),
                  lambda: cross_wide(nc, keep, S, dram, latents=False),
                  lambda: routed_experts(nc, keep, S, dram),
                  lambda: cross_rope(nc, keep, S, dram),
                  lambda: relu_feed_forward(nc, keep, S, dram),
                  lambda: cross_wide(nc, keep, S, dram, latents=True),
                  lambda: quantised_feed_forward(nc, keep, S, dram)]
        for stage in stages:
            stage()


def lay_out(inp):
    f = {k: np.asarray(v) for k, v in inp.items()}
    a = {}
    a["x"] = f["x"].reshape(TOKENS, D)
    a["ctxT"] = f["ctx_1024"].reshape(BATCH, SEQ, KT, P).transpose(0, 3, 2, 1)
    a["mask"] = f["mask_1x1xSxS2_fk1"].reshape(SEQ, SEQ)
    a["maskT"] = a["mask"].T
    gates = np.stack([f["g_xattn"], f["g_ffn"]], axis=1).reshape(8)
    a["gates"] = np.broadcast_to(np.concatenate([gates, f["L1_xattn_gate"]]), (P, 9))
    a["ident"] = np.eye(P, dtype=np.float32)
    a["iota"] = np.broadcast_to(np.arange(64, dtype=np.float32), (P, 64))

    def col(b):
        return b.reshape(-1, P).T

    def rows(b):
        return np.broadcast_to(b, (P, b.size))
    r = np.arange(D)
    lay16 = ((r % P) % 8 * 2 + r // P) * 16 + (r % P) // 8
    a["L0wq"], a["L0wk"] = f["L0_xattn_wq"][:, lay16], f["L0_xattn_wk"][:, lay16]
    a["L0wv"], a["L0wo"] = f["L0_xattn_wv"], f["L0_xattn_wo"]
    a["L0bq"], a["L0bk"] = col(f["L0_xattn_bq"][lay16]), col(f["L0_xattn_bk"][lay16])
    a["L0bv"], a["L0bo"] = rows(f["L0_xattn_bv"]), f["L0_xattn_bo"].reshape(1, D)
    turn16 = (lay16 // 16) * 16 + (lay16 + 8) % 16
    a["L2wv"], a["L2wo"] = [f[f"L2_xattn_W{n}"].T for n in "vo"]
    for n in "qk":
        a["L2w" + n], a["L2w" + n + "r"] = f["L2_xattn_W" + n].T[:, lay16], f["L2_xattn_W" + n].T[:, turn16]
        a["L2b" + n], a["L2b" + n + "r"] = col(f["L2_xattn_b" + n][lay16]), col(f["L2_xattn_b" + n][turn16])
    a["L2bv"], a["L2bo"] = rows(f["L2_xattn_bv"]), f["L2_xattn_bo"].reshape(1, D)

    r = np.arange(P)
    latq, latk = (r % 16) * 16 + r // 16, (r % 16) * 8 + r // 16
    a["L0fwq"], a["L0fbq"] = f["L0_ffn_q_w"][:, latq], f["L0_ffn_q_b"][latq].reshape(P, 1)
    a["L0fwk"], a["L0fbk"] = f["L0_ffn_k_w"][:, latk], f["L0_ffn_k_b"][latk].reshape(P, 1)
    a["L0fwv"], a["L0fbv"] = f["L0_ffn_v_w"], rows(f["L0_ffn_v_b"])
    a["L0fwo"], a["L0fbo"] = f["L0_ffn_o_w"][:P], col(f["L0_ffn_o_b"])
    a["L0frouter"], a["L0fbr"] = f["L0_ffn_router_w"], f["L0_ffn_router_b"].reshape(1, 8)
    a["L0fw1"], a["L0fw2"], a["L0fb2"] = f["L0_ffn_w1"], f["L0_ffn_w2"], f["L0_ffn_b2"]
    a["L0fb1"] = f["L0_ffn_b1"].reshape(8, 4, P).transpose(2, 0, 1)

    a["L1wq"], a["L1wkv"], a["L1wo"] = f["L1_xattn_w_q"], f["L1_xattn_w_kv"], f["L1_xattn_w_out"]
    a["L1gamma"], a["L1beta"] = col(f["L1_xattn_ln_gamma"]), col(f["L1_xattn_ln_beta"])
    a["L1bo"] = f["L1_xattn_b_out"].reshape(1, D)
    a["L3wq"], a["L3wkv"], a["L3wo"] = f["L3_xattn_Wq"], f["L3_xattn_Wkv"], f["L3_xattn_Wo"]
    a["ctx"] = f["ctx_1024"].reshape(BATCH, QT, P, D).transpose(0, 2, 1, 3)
    turn64 = (np.arange(512) // 64) * 64 + (np.arange(512) + 32) % 64
    a["L3wkr"] = f["L3_xattn_Wkv"][:, turn64]
    a["L3gamma"], a["L3beta"] = col(f["L3_xattn_gamma_l"]), col(f["L3_xattn_beta_l"])
    a["L3gammax"], a["L3betax"] = col(f["L3_xattn_gamma_x"]), col(f["L3_xattn_beta_x"])

    a["L2fw1"], a["L2fw2"] = f["L2_ffn_W1"], f["L2_ffn_W2"]
    a["L2fb1"], a["L2fb2"] = col(f["L2_ffn_b1"]), f["L2_ffn_b2"].reshape(1, D)
    a["L3fup"], a["L3fgate"], a["L3fdown"] = f["L3_ffn_w_up"], f["L3_ffn_w_gate"], f["L3_ffn_w_down"]

    a["L1frouter"] = f["L1_ffn_router_w"].T
    a["L1fwg"], a["L1fwu"], a["L1fwd"] = f["L1_ffn_w_gate"], f["L1_ffn_w_up"], f["L1_ffn_w_down"]
    a["L1fwsgu"], a["L1fwsd"] = f["L1_ffn_ws_gate_up"], f["L1_ffn_ws_down"]
    a["tri"] = np.triu(np.ones((P, P), np.float32), 1)

    def rope_tables(dim):
        inv = (1.0 / 10000.0 ** (np.arange(0, dim, 2, dtype=np.float32) / np.float32(dim))).astype(np.float32)
        angle = np.arange(SEQ, dtype=np.float32)[:, None] * inv[None, :]
        cos, sin = np.cos(angle).T, np.sin(angle).T
        reps = P // dim
        return (np.tile(np.concatenate([cos, cos]), (reps, 1)).astype(np.float32),
                np.tile(np.concatenate([-sin, sin]), (reps, 1)).astype(np.float32))
    cos16, sin16 = [t[np.arange(P) // 8] for t in rope_tables(16)]
    a["cosk"], a["sink"] = cos16, sin16
    a["cosq"], a["sinq"] = cos16 * np.float32(0.25), sin16 * np.float32(0.25)
    a["cos64"], a["sin64"] = rope_tables(64)
    return {k: np.ascontiguousarray(v) for k, v in a.items()}


def kernel(**inputs):
    import concourse.bacc as bacc
    from concourse.bass_utils import run_bass_kernel_spmd

    arrays = lay_out(inputs)
    nc = bacc.Bacc("TRN2", target_bir_lowering=False, num_devices=1)
    dram = {k: nc.dram_tensor("in_" + k, list(v.shape), F32, kind="ExternalInput").ap()
            for k, v in arrays.items()}
    out = nc.dram_tensor("out_x", [TOKENS, D], F32, kind="ExternalOutput").ap()
    dram["out"] = out
    dram["x_spill"] = nc.dram_tensor("x_spill", [P, TILES, D], F32, kind="Internal").ap()
    for n in "qk":
        for dim in (8, 16):
            dram[f"{n}_parts{dim}"] = nc.dram_tensor(f"{n}_parts{dim}", [3, 3, dim, 16, SEQ], BF16, kind="Internal").ap()
    dram["top_parts"] = nc.dram_tensor("top_parts", [3, 2, 3, 8, SEQ], BF16, kind="Internal").ap()
    for n in ("x_slots", "y_slots"):
        dram[n] = nc.dram_tensor(n, [64 * 128, D], F32, kind="Internal").ap()
    flamingo(nc, dram, out)
    r = run_bass_kernel_spmd(nc, [{"in_" + k: v for k, v in arrays.items()}], core_ids=[0])
    return r.results[0]["out_x"].reshape(BATCH, SEQ, D)
```

```python
from contextlib import ExitStack

import numpy as np

import concourse.bass as bass
from concourse import mybir

F32 = mybir.dt.float32
BF16 = mybir.dt.bfloat16
I16 = mybir.dt.int16
U32 = mybir.dt.uint32
ALU = mybir.AluOpType
ACT = mybir.ActivationFunctionType
AX = mybir.AxisListType

BATCH, SEQ, D = 16, 256, 256
TOKENS = BATCH * SEQ
P = 128
TILES = TOKENS // P
QT = SEQ // P
KT = D // P
EPS = 1e-5
SLOT_TILES = 72
BIG = 1.0e9


def wait(eng, sem, value):
    if isinstance(value, int) and value <= 0:
        return
    eng.wait_ge(sem, value)


def zero_semaphores(nc, sems):
    with nc.Block() as block:
        @block.gpsimd
        def _(pool):
            for s in sems:
                pool.sem_clear(s)


def attention_stage(nc, keep, S, cfg):
    UN = 16
    H, VD, G = cfg["heads"], cfg["vd"], cfg["group"]
    wide = cfg["wide"]
    NP, NE, NL = cfg["n_pro"], cfg["n_epi"], cfg["n_norm"]
    UG = G * (2 if wide else 1)
    NG = UN // UG

    with ExitStack() as ctx:
        def sb(name, shape, dt=F32):
            return ctx.enter_context(nc.sbuf_tensor(cfg["name"] + name, shape, dt))

        def psum(name, shape):
            return ctx.enter_context(nc.psum_tensor(cfg["name"] + name, shape, F32))

        score = [psum(f"score{i}", [P, 512]) for i in range(4)]
        ptp = psum("ptp", [P, 512])
        pvp = [psum(f"pvp{i}", [P, 512]) for i in range(2)]
        work = psum("work", [P, 512])

        bufs = {}
        bufs["sb"], bufs["pro"], bufs["epi"] = sb, work, work
        prob = [sb(f"prob{i}", [P, 512]) for i in range(2)]
        pT = [sb(f"pT{i}", [P, 4, P]) for i in range(2)]
        nmax = sb("nmax", [P, 4, 2])
        sums, rden = sb("sums", [P, 4, 2]), sb("rden", [P, 4, 2])
        o = [sb(f"oT{i}", [P, H * VD // P, SEQ]) for i in range(2)]
        st = sb("st", [P, NL, QT, 6])
        mv = sb("mv", [P, NL, QT, 2])
        rstd = sb("rstd", [P, NL, QT])
        bufs.update(o=o, nmax=nmax)
        fns = cfg["make"](nc, keep, bufs, S, ctx)
        qT_of, kT_of, v_of = fns["q"], fns["k"], fns["v"]

        def for_batches(eng, head, body, tail):
            head()
            body(0, 0, 0, True, False)
            with eng.Fori(0, (BATCH - 2) // 2) as i:
                body(2 * i + 1, i + 0, 1, False, False)
                body(2 * i + 2, i + 1, 0, False, False)
            body(BATCH - 1, BATCH // 2 - 1, 1, False, True)
            tail()

        with nc.Block() as block:
            @block.sync
            def _(sp):
                for dst, src in fns["weights"]:
                    sp.dma_start(dst, src).then_inc(S["weights"], 16)
                if "stream" in cfg:
                    for c in range(2):
                        for dst, src in cfg["stream"](bufs, c, c):
                            sp.dma_start(dst, src).then_inc(S["stream"][c], 16)
                    with sp.Fori(0, BATCH // 2 - 1) as i:
                        for par in range(2):
                            sp.wait_ge(S["pro_filled"], NP * (2 * i + par + 1))
                            for dst, src in cfg["stream"](bufs, 2 * i + par + 2, par):
                                sp.dma_start(dst, src).then_inc(S["stream"][par], 16)

            @block.gpsimd
            def _(pool):
                def rstds(c, half, par):
                    for n in range(NL):
                        pool.wait_ge(S["var"], NL * c + n + 1)
                        nc.gpsimd.tensor_tensor(rstd[:, n, :], mv[:, n, :, 1], keep["eps"][:, 0:QT],
                                                ALU.add).then_inc(S["vareps"], 1)
                        pool.wait_ge(S["vareps"], NL * c + n + 1)
                        nc.gpsimd.tensor_tensor(rstd[:, n, :], rstd[:, n, :], keep["mhalf"][:, 0:QT],
                                                ALU.pow).then_inc(S["rstd"], 1)
                rstds(0, 0, 0)
                with pool.Fori(1, BATCH) as c:
                    rstds(c, None, None)

            @block.vector
            def _(dve):
                def norm(n, c, half, par):
                    src, dst = fns["norm"](n, c, half, par)
                    fns["norm_wait"](dve, n, c, half, par)
                    for t in range(QT):
                        ins = nc.vector.bn_stats(st[:, n, t, :], src(t))
                    ins.then_inc(S["stats"], 1)
                    dve.wait_ge(S["stats"], NL * c + n + 1)
                    nc.vector.memset(keep["scratch"][:, 0:1], 0.0)
                    for t in range(QT):
                        ins = nc.vector.bn_aggr(mv[:, n, t, :], st[:, n, t, :])
                    ins.then_inc(S["var"], 1)

                def normed(n, c, half, par):
                    src, dst = fns["norm"](n, c, half, par)
                    dve.wait_ge(S["rstd"], NL * c + n + 1)
                    if fns["norm_job"][n] is not None:
                        wait(dve, S["pro_filled"], NP * (c - 1) + fns["norm_job"][n] + 1)
                    for t in range(QT):
                        ins = nc.vector.tensor_scalar(dst(t), src(t), mv[:, n, t, 0:1],
                                                      rstd[:, n, t:t + 1], ALU.subtract, ALU.mult)
                    ins.then_inc(S["normed"], 1)

                def row_max(c, h, par):
                    p = h % 4
                    dve.wait_ge(S["scores"], UN * c + h + 1)
                    fns["row_max"](dve, nmax, score[p], c, h, p).then_inc(S["row_max"], 1)

                def divide(c, h, par):
                    p, parts = h % 4, 1 if wide else QT
                    dve.wait_ge(S["exp"], UN * c + h + 1)
                    nc.vector.reciprocal(rden[:, p, 0:parts], sums[:, p, 0:parts]).then_inc(S["rden"], 1)
                    dve.wait_ge(S["rden"], UN * c + h + 1)
                    n = 512 // parts
                    for t in range(parts):
                        ins = nc.vector.tensor_scalar(prob[h % 2][:, t * n:(t + 1) * n],
                                                      prob[h % 2][:, t * n:(t + 1) * n],
                                                      rden[:, p, t:t + 1], None, ALU.mult)
                    ins.then_inc(S["scaled"], 1)

                def copy_out(c, g, par):
                    dve.wait_ge(S["pv"], UN * c + UG * (g + 1))
                    if g == 0:
                        wait(dve, S["epi_filled"], NE * (c - 1))
                    nc.vector.tensor_copy(o[par][:, g, :], pvp[g % 2][:, 0:SEQ]).then_inc(S["o_ready"], 1)

                def pro_copy(j, c, half, par):
                    if fns["pro_engine"](j) == "dve":
                        dve.wait_ge(S["pro_filled"], NP * c + j + 1)
                        if j in fns["pro_frees"]:
                            wait(dve, S["pv"], UN * (c - 1))
                        fns["pro_copy"](dve, j, c, half, par).then_inc(S["pro_copied"], 1)

                def epi_copy(j, c, half, par):
                    if fns["epi_engine"](j) == "dve":
                        dve.wait_ge(S["epi_filled"], NE * c + j + 1)
                        fns["epi_copy"](dve, j, c, half, par).then_inc(S["epi_copied"], 1)

                def prologue(c, half, par):
                    for n in range(NL):
                        norm(n, c, half, par)
                        normed(n, c, half, par)
                    for j in range(NP):
                        pro_copy(j, c, half, par)

                def head():
                    dve.wait_ge(S["weights"], 16 * len(fns["weights"]))
                    prologue(0, 0, 0)
                    row_max(0, 0, 0)
                    row_max(0, 1, 0)
                    divide(0, 0, 0)

                def body(c, half, par, first, last):
                    nxt = (c + 1, half + par, 1 - par)

                    def jobs(at):
                        if not first:
                            for j in fns["epi_at"](at):
                                epi_copy(j, c - 1, None, 1 - par)
                        if not last:
                            for j in fns["pro_at"](at):
                                pro_copy(j, *nxt)

                    for h in range(UN):
                        if h + 2 < UN:
                            row_max(c, h + 2, par)
                        elif not last:
                            row_max(c + 1, h + 2 - UN, 1 - par)
                        if h + 1 < UN:
                            divide(c, h + 1, par)
                        elif not last:
                            divide(c + 1, 0, 1 - par)
                        jobs(h)
                        if h >= 1 and h % UG == 0:
                            copy_out(c, h // UG - 1, par)
                        if h == 0 and not first:
                            copy_out(c - 1, NG - 1, 1 - par)
                        jobs(h + 0.5)
                        if not last:
                            for n in range(NL):
                                if h == 2 * n:
                                    norm(n, *nxt)
                                if h == 2 * n + 1:
                                    normed(n, *nxt)

                def tail():
                    copy_out(BATCH - 1, NG - 1, 1)
                    for j in range(NE):
                        epi_copy(j, BATCH - 1, BATCH // 2 - 1, 1)

                for_batches(dve, head, body, tail)

            @block.scalar
            def _(act):
                def exp(c, h):
                    p = h % 2
                    act.wait_ge(S["row_max"], UN * c + h + 1)
                    wait(act, S["pT"], UN * c + h - 1)
                    fns["exp"](act, prob[p], nmax, score[h % 4], h, h % 4, sums).then_inc(S["exp"], 1)

                def copy_pT(c, h):
                    p = h % 2
                    act.wait_ge(S["pT"], UN * c + h + 1)
                    wait(act, S["pv"], UN * c + h - 1)
                    nc.scalar.copy(pT[p][:, :, :].rearrange("p a b -> p (a b)"),
                                   ptp[:, :]).then_inc(S["pT_copied"], 1)

                def pro_copy(j, c, half, par):
                    if fns["pro_engine"](j) == "act":
                        act.wait_ge(S["pro_filled"], NP * c + j + 1)
                        if j in fns["pro_frees"]:
                            wait(act, S["pv"], UN * (c - 1))
                        fns["pro_copy"](act, j, c, half, par).then_inc(S["pro_copied"], 1)

                def epi_copy(j, c, half, par):
                    if fns["epi_engine"](j) == "act":
                        act.wait_ge(S["epi_filled"], NE * c + j + 1)
                        fns["epi_copy"](act, j, c, half, par).then_inc(S["epi_copied"], 1)

                def head():
                    act.wait_ge(S["weights"], 16 * len(fns["weights"]))
                    for j in range(NP):
                        pro_copy(j, 0, 0, 0)
                    exp(0, 0)

                def body(c, half, par, first, last):
                    nxt = (c + 1, half + par, 1 - par)

                    def jobs(at):
                        if not first:
                            for j in fns["epi_at"](at):
                                epi_copy(j, c - 1, None, 1 - par)
                        if not last:
                            for j in fns["pro_at"](at):
                                pro_copy(j, *nxt)

                    for h in range(UN):
                        if h + 1 < UN:
                            exp(c, h + 1)
                        elif not last:
                            exp(c + 1, 0)
                        jobs(h)
                        copy_pT(c, h)
                        jobs(h + 0.5)

                def tail():
                    for j in range(NE):
                        epi_copy(j, BATCH - 1, BATCH // 2 - 1, 1)

                for_batches(act, head, body, tail)

            @block.tensor
            def _(pe):
                def scores(c, h, par):
                    p = h % 4
                    wait(pe, S["exp"], UN * c + h - 3)
                    if h == 0:
                        pe.wait_ge(S["pro_copied"], NP * (c + 1))
                    if wide:
                        head, t = h // 2, h % 2
                        mm = nc.tensor.matmul(score[p][:, :], qT_of(par, head, t), kT_of(par, head),
                                              start=True, stop=True)
                    else:
                        for t in range(QT):
                            mm = nc.tensor.matmul(score[p][:, t * SEQ:(t + 1) * SEQ], qT_of(par, h, t),
                                                  kT_of(par, h), start=True, stop=True)
                    mm.then_inc(S["scores"], 1)

                def transpose_probs(c, h):
                    p = h % 2
                    pe.wait_ge(S["scaled"], UN * c + h + 1)
                    wait(pe, S["pT_copied"], UN * c + h)
                    for k in range(4):
                        to = k if wide else (k % 2) * 2 + k // 2
                        mm = nc.tensor.transpose(ptp[:, to * P:(to + 1) * P],
                                                 prob[p][:, k * P:(k + 1) * P], keep["ident"][:, :])
                    mm.then_inc(S["pT"], 1)

                def pv(c, h, par):
                    p = h % 2
                    g = h // UG
                    pe.wait_ge(S["pT_copied"], UN * c + h + 1)
                    if h % UG == 0:
                        wait(pe, S["o_ready"], NG * c + g - 1)
                    r = 64 * ((h // 2 if wide else h) % 2)
                    if wide:
                        head, t = h // 2, h % 2
                        for k in range(4):
                            mm = nc.tensor.matmul(pvp[g % 2][r:r + 64, t * P:(t + 1) * P], v_of(par, head, k),
                                                  pT[p][:, k, :], start=(k == 0), stop=(k == 3))
                    else:
                        for k in range(2):
                            mm = nc.tensor.matmul(pvp[g % 2][r:r + 64, 0:SEQ], v_of(par, h, k),
                                                  pT[p][:, 2 * k:2 * k + 2, :], start=(k == 0), stop=(k == 1))
                    mm.then_inc(S["pv"], 1)

                def pro_fill(j, c, half, par):
                    wait(pe, S["pro_copied"], NP * c + j)
                    if j == 0:
                        wait(pe, S["epi_copied"], NE * (c - 1))
                    if j in fns["norm_job"]:
                        pe.wait_ge(S["normed"], NL * c + fns["norm_job"].index(j) + 1)
                    fns["pro_fill"](pe, j, c, half, par).then_inc(S["pro_filled"], 1)

                def epi_fill(j, c, par):
                    wait(pe, S["epi_copied"], NE * c + j)
                    if j == 0:
                        pe.wait_ge(S["o_ready"], NG * (c + 1))
                    fns["epi_fill"](pe, j, c, par).then_inc(S["epi_filled"], 1)

                def head():
                    pe.wait_ge(S["weights"], 16 * len(fns["weights"]))
                    for j in range(NP):
                        pro_fill(j, 0, 0, 0)
                    scores(0, 0, 0)
                    scores(0, 1, 0)

                def body(c, half, par, first, last):
                    nxt = (c + 1, half + par, 1 - par)

                    def jobs(at):
                        if not first:
                            for j in fns["epi_at"](at):
                                epi_fill(j, c - 1, 1 - par)
                        if not last:
                            for j in fns["pro_at"](at):
                                pro_fill(j, *nxt)

                    for h in range(UN):
                        if h + 2 < UN:
                            scores(c, h + 2, par)
                        elif not last:
                            scores(c + 1, h + 2 - UN, 1 - par)
                        if h > 0:
                            pv(c, h - 1, par)
                        elif not first:
                            pv(c - 1, UN - 1, 1 - par)
                        jobs(h)
                        transpose_probs(c, h)
                        jobs(h + 0.5)

                def tail():
                    pv(BATCH - 1, UN - 1, 1)
                    for j in range(NE):
                        epi_fill(j, BATCH - 1, 1)

                for_batches(pe, head, body, tail)
    zero_semaphores(nc, S["all"])


def spread(slots):
    return lambda h: [j for j, s in enumerate(slots) if s == h]


def plain_max(nc, dve, nmax, bank, p):
    return nc.vector.tensor_reduce(nmax[:, p, :], bank[:, :].rearrange("p (t k) -> p t k", t=QT), AX.X,
                                   ALU.max, negate=True)


def project(nc, bank, w, rhs, tiles, n=SEQ):
    for i, m in enumerate(tiles):
        for k in range(KT):
            mm = nc.tensor.matmul(bank[:, i * n:(i + 1) * n], w[:, k, m * P:(m + 1) * P], rhs[:, k, :],
                                  start=(k == 0), stop=(k == KT - 1))
    return mm


def project_rows(nc, bank, lhsT, w, cols, n):
    for t in range(QT):
        for k in range(KT):
            mm = nc.tensor.matmul(bank[:, t * n:(t + 1) * n], lhsT[:, k, t * P:(t + 1) * P],
                                  w[:, k, cols:cols + n], start=(k == 0), stop=(k == KT - 1))
    return mm


def turn(nc, keep, bank, rows, features=slice(0, D)):
    base = features.start
    for k in range(KT):
        for t in range(QT):
            mm = nc.tensor.transpose(bank[:, k * SEQ + t * P:k * SEQ + (t + 1) * P],
                                     rows[:, t, base + k * P:base + (k + 1) * P], keep["ident"][:, :])
    return mm


def output_rows(nc, bank, oT, w, bias, keep, parts):
    for t in range(QT):
        for k in range(parts):
            mm = nc.tensor.matmul(bank[:, t * D:(t + 1) * D], oT[:, k, t * P:(t + 1) * P], w[:, k, :],
                                  start=(k == 0), stop=(bias is None and k == parts - 1))
        if bias is not None:
            mm = nc.tensor.matmul(bank[:, t * D:(t + 1) * D], keep["ones"][0:1, :], bias,
                                  start=False, stop=True)
    return mm


def flat(ap):
    return ap.rearrange("p a b -> p (a b)")


def add_output(nc, dve, keep, bank, gate, c):
    xs = keep["x"][:, bass.ds(c * QT, QT), :]
    return nc.vector.scalar_tensor_tensor(out=flat(xs), in0=bank[:, :], scalar=gate, in1=flat(xs),
                                          op0=ALU.mult, op1=ALU.add)


def x_norm(keep, h):
    def norm(n, c, half, par):
        return (lambda t: keep["x"][:, bass.ds(c * QT + t, 1), :].rearrange("p a b -> p (a b)"),
                lambda t: h[:, t, :])
    return norm


def dispatch_slots(nc, keep, S, dram):
    E, K, CH = 8, 2, TILES
    with ExitStack() as ctx:
        def sb(name, shape, dt=F32):
            return ctx.enter_context(nc.sbuf_tensor("slot" + name, shape, dt))
        tri, iota, upto = sb("tri", [P, P]), sb("iota", [P, 64]), sb("upto", [P, SLOT_TILES])
        hit, member = sb("hit", [P, CH, K, E]), sb("member", [P, CH, E])
        total = [sb(f"total{i}", [P, CH, E]) for i in range(2)]
        tiles, start = sb("tiles", [P, E]), sb("start", [P, E + 1])
        place, product = sb("place", [P, CH, E]), sb("product", [P, CH, K, E])
        slotf = sb("slotf", [P, CH, K])
        passed, owner = sb("passed", [1, SLOT_TILES, E]), sb("owner", [1, SLOT_TILES])
        within = ctx.enter_context(nc.psum_tensor("slotwithin", [P, CH * E], F32))
        totals = ctx.enter_context(nc.psum_tensor("slottotals", [P, CH * E], F32))

        with nc.Block() as block:
            @block.sync
            def _(sp):
                for dst, src in ((tri, "tri"), (iota, "iota"), (upto, "upto")):
                    sp.dma_start(dst[:, :], dram[src]).then_inc(S["weights"], 16)
                sp.dma_start(keep["b1"][:, :, :], dram["L0fb1"]).then_inc(S["experts_loaded"], 16)
                for e in range(E):
                    for n in ("w1", "w2"):
                        w = keep[n][:, e, :]
                        src = dram["L0f" + n][e]
                        sp.dma_start(w.rearrange("p (k f) -> p k f", f=src.shape[1]),
                                     src.rearrange("(k p) f -> p k f", p=P)).then_inc(S["experts_loaded"], 16)
                sp.wait_ge(S["experts_loaded"], 16 * (2 * E + 1))

            @block.tensor
            def _(pe):
                pe.wait_ge(S["member"], 1)
                nc.tensor.matmul(within[:, :], tri[:, :], flat(member[:, :, :]), start=True, stop=True)
                nc.tensor.matmul(totals[:, :], keep["ones"][:, :], flat(member[:, :, :]), start=True, stop=True
                                 ).then_inc(S["placed"], 1)

            @block.vector
            def _(dve):
                n = [0]

                def linked(ins):
                    n[0] += 1
                    ins.then_inc(S["route"], 1)
                    dve.wait_ge(S["route"], n[0])

                def over(ap, shape):
                    return ap.to_broadcast(shape)
                dve.wait_ge(S["weights"], 48)
                for k in range(K):
                    ins = nc.vector.tensor_tensor(hit[:, :, k, :], over(iota[:, 0:E].unsqueeze(1), [P, CH, E]),
                                                  over(keep["choice"][:, :, k].unsqueeze(2), [P, CH, E]),
                                                  ALU.is_equal)
                linked(ins)
                linked(nc.vector.tensor_tensor(member[:, :, :], hit[:, :, 0, :], hit[:, :, 1, :], ALU.add))
                nc.vector.memset(keep["scratch"][:, 0:1], 0.0).then_inc(S["member"], 1)
                dve.wait_ge(S["placed"], 1)
                linked(nc.vector.tensor_copy(flat(total[0][:, :, :]), totals[:, :]))
                at, step = 0, 1
                while step < CH:
                    nc.vector.tensor_copy(total[1 - at][:, 0:step, :], total[at][:, 0:step, :])
                    linked(nc.vector.tensor_tensor(total[1 - at][:, step:, :], total[at][:, step:, :],
                                                   total[at][:, 0:CH - step, :], ALU.add))
                    at, step = 1 - at, 2 * step
                total_up = total[at]
                linked(nc.vector.tensor_scalar(tiles[:, :], total_up[:, CH - 1, :], 63.5, 1.0 / P, ALU.add, ALU.mult))
                linked(nc.vector.tensor_scalar(tiles[:, :], tiles[:, :], 12582912.0, 12582912.0, ALU.add,
                                               ALU.subtract))
                linked(nc.vector.memset(start[:, 0:1], 0.0))
                for e in range(E):
                    linked(nc.vector.tensor_tensor(start[:, e + 1:e + 2], start[:, e:e + 1], tiles[:, e:e + 1],
                                                   ALU.add))
                linked(nc.vector.tensor_tensor(flat(place[:, :, :]), within[:, :], flat(total_up[:, :, :]), ALU.add))
                linked(nc.vector.tensor_tensor(flat(place[:, :, :]), flat(place[:, :, :]), totals[:, :],
                                               ALU.subtract))
                linked(nc.vector.tensor_scalar(tiles[:, :], start[:, 0:E], float(P), None, ALU.mult))
                linked(nc.vector.tensor_tensor(place[:, :, :], place[:, :, :],
                                               over(tiles[:, :].unsqueeze(1), [P, CH, E]), ALU.add))
                for k in range(K):
                    ins = nc.vector.tensor_tensor(product[:, :, k, :], hit[:, :, k, :], place[:, :, :], ALU.mult)
                linked(ins)
                linked(nc.vector.tensor_reduce(flat(slotf[:, :, :]), product[:, :, :, :].rearrange(
                    "p t k e -> p (t k) e"), AX.X, ALU.add))
                nc.vector.tensor_copy(keep["slot"][:, :, :], slotf[:, :, :]).then_inc(S["slots"], 1)
                linked(nc.vector.tensor_tensor(passed[:, :, :], over(upto[0:1, :].unsqueeze(2), [1, SLOT_TILES, E]),
                                               over(start[0:1, 1:E + 1].unsqueeze(1), [1, SLOT_TILES, E]),
                                               ALU.is_ge))
                linked(nc.vector.tensor_reduce(owner[:, :], passed[:, :, :], AX.X, ALU.add))
                linked(nc.vector.tensor_scalar(owner[:, :], owner[:, :], float(E - 1), None, ALU.min))
                nc.vector.tensor_copy(keep["tile_expert"][:, :], owner[:, :])

            @block.gpsimd
            def _(pool):
                pool.wait_ge(S["slots"], 1)
                for t in range(TILES):
                    for k in range(K):
                        nc.gpsimd.indirect_dma_start(
                            dram["m_slots"], bass.IndirectOffsetOnAxis(keep["slot"][:, t, k:k + 1], 0),
                            keep["m"][:, t, :], None, bounds_check=SLOT_TILES * P - 1, oob_is_err=False
                        ).then_inc(S["m_scattered"][0], 16)
                pool.wait_ge(S["m_scattered"][0], 16 * TILES * K)
    zero_semaphores(nc, S["all"])


def experts_of_two(nc, keep, S, dram):
    E, F, K = 8, 512, 2
    FT, L = F // P, "L0f"
    with ExitStack() as ctx:
        def sb(name, shape, dt=F32, ctx=ctx):
            return ctx.enter_context(nc.sbuf_tensor("moe0" + name, shape, dt))
        with ExitStack() as inner:
            w1, w2, b1 = keep["w1"], keep["w2"], keep["b1"]
            rows = [sb(f"rows{i}", [P, D], ctx=inner) for i in range(2)]
            mT = [sb(f"mT{i}", [P, D], ctx=inner) for i in range(2)]
            pre = [sb(f"pre{i}", [P, F], ctx=inner) for i in range(2)]
            hid = [sb(f"hid{i}", [P, F], ctx=inner) for i in range(2)]
            hT = [sb(f"hT{i}", [P, F], ctx=inner) for i in range(2)]
            y = [sb(f"y{i}", [P, D], ctx=inner) for i in range(2)]
            tp = inner.enter_context(nc.psum_tensor("moe0tp", [P, D], F32))
            hp = [inner.enter_context(nc.psum_tensor(f"moe0hp{i}", [P, F], F32)) for i in range(2)]
            htp = [inner.enter_context(nc.psum_tensor(f"moe0htp{i}", [P, F], F32)) for i in range(2)]
            yp = [inner.enter_context(nc.psum_tensor(f"moe0yp{i}", [P, D], F32)) for i in range(2)]

            def by_pairs(eng, run):
                for n in range(4):
                    run(n, n // 2, n % 2)
                with eng.Fori(2, SLOT_TILES // 2) as i:
                    run(2 * i, i + 0, 0)
                    run(2 * i + 1, i + 0, 1)

            with nc.Block() as block:
                @block.sync
                def _(sp):
                    def run(n, half, par):
                        wait(sp, S["turned"], n - 1)
                        sp.dma_start(rows[par][:, :], dram["m_slots"][bass.ds(n * P, P), :]
                                     ).then_inc(S["stream"][par], 16)
                    by_pairs(sp, run)

                @block.tensor
                def _(pe):
                    def turn_rows(n, half, par):
                        pe.wait_ge(S["stream"][par], 16 * (half + 1))
                        wait(pe, S["turn_copied"], n)
                        for k in range(KT):
                            mm = nc.tensor.transpose(tp[:, k * P:(k + 1) * P], rows[par][:, k * P:(k + 1) * P],
                                                     keep["ident"][:, :])
                        mm.then_inc(S["turned"], 1)

                    def hidden(n, par, e):
                        pe.wait_ge(S["turn_copied"], n + 1)
                        wait(pe, S["hidden_biased"], n - 1)
                        for k in range(KT):
                            mm = nc.tensor.matmul(hp[par][:, :], mT[par][:, k * P:(k + 1) * P],
                                                  w1[:, bass.ds(e, 1), k * F:(k + 1) * F].rearrange("p a f -> p (a f)"),
                                                  start=(k == 0), stop=(k == KT - 1))
                        mm.then_inc(S["hidden"], 1)

                    def turn_hidden(n, par):
                        pe.wait_ge(S["act"], n + 1)
                        wait(pe, S["raw"], n - 1)
                        for k in range(FT):
                            mm = nc.tensor.transpose(htp[par][:, k * P:(k + 1) * P], hid[par][:, k * P:(k + 1) * P],
                                                     keep["ident"][:, :])
                        mm.then_inc(S["back"], 1)

                    def outputs(n, par, e):
                        pe.wait_ge(S["raw"], n + 1)
                        wait(pe, S["copied"], n - 1)
                        for k in range(FT):
                            mm = nc.tensor.matmul(yp[par][:, :], hT[par][:, k * P:(k + 1) * P],
                                                  w2[:, bass.ds(e, 1), k * D:(k + 1) * D].rearrange("p a f -> p (a f)"),
                                                  start=(k == 0), stop=(k == FT - 1))
                        mm.then_inc(S["y"], 1)

                    def expert(n):
                        return pe.value_load(keep["tile_expert"][0:1, bass.ds(n, 1)], min_val=0, max_val=E - 1)

                    def run(n, half, par, more=True, lead=2):
                        hidden(n, par, expert(n))
                        if more:
                            turn_rows(n + 1, half + par, 1 - par)
                        if lead >= 1:
                            turn_hidden(n - 1, 1 - par)
                        if lead >= 2:
                            outputs(n - 2, par, expert(n - 2))
                    turn_rows(0, 0, 0)
                    for n in range(4):
                        run(n, n // 2, n % 2, lead=n)
                    with pe.Fori(2, SLOT_TILES // 2 - 1) as i:
                        run(2 * i, i + 0, 0)
                        run(2 * i + 1, i + 0, 1)
                    n = SLOT_TILES - 2
                    run(n, n // 2, 0)
                    run(n + 1, n // 2, 1, more=False)
                    turn_hidden(n + 1, 1)
                    outputs(n, 0, expert(n))
                    outputs(n + 1, 1, expert(n + 1))

                @block.vector
                def _(dve):
                    def bias(n, par, e):
                        dve.wait_ge(S["hidden"], n + 1)
                        wait(dve, S["act"], n - 1)
                        wait(dve, S["hidden_biased"], n)
                        nc.vector.memset(keep["scratch"][:, 0:1], 0.0)
                        nc.vector.tensor_tensor(pre[par][:, :], hp[par][:, :],
                                                b1[:, bass.ds(e, 1), :].rearrange("p a f -> p (a f)"), ALU.add
                                                ).then_inc(S["hidden_biased"], 1)

                    def copy_turned(n, par):
                        dve.wait_ge(S["turned"], n + 1)
                        wait(dve, S["hidden"], n - 1)
                        nc.vector.tensor_copy(mT[par][:, :], tp[:, :]).then_inc(S["turn_copied"], 1)

                    def copy_hidden(n, par):
                        dve.wait_ge(S["back"], n + 1)
                        wait(dve, S["y"], n - 1)
                        nc.vector.tensor_copy(hT[par][:, :], htp[par][:, :]).then_inc(S["raw"], 1)

                    def expert(n):
                        return dve.value_load(keep["tile_expert"][0:1, bass.ds(n, 1)], min_val=0, max_val=E - 1)

                    def run(n, par, more=True, lead=1):
                        e = expert(n)
                        if more:
                            copy_turned(n + 1, 1 - par)
                        bias(n, par, e)
                        if lead >= 1:
                            copy_hidden(n - 1, 1 - par)
                    copy_turned(0, 0)
                    for n in range(4):
                        run(n, n % 2, lead=n)
                    with dve.Fori(2, SLOT_TILES // 2 - 1) as i:
                        run(2 * i, 0)
                        run(2 * i + 1, 1)
                    n = SLOT_TILES - 2
                    run(n, 0)
                    run(n + 1, 1, more=False)
                    copy_hidden(n + 1, 1)

                @block.scalar
                def _(act):
                    def gelu(n, par):
                        act.wait_ge(S["hidden_biased"], n + 1)
                        wait(act, S["back"], n - 1)
                        nc.scalar.activation(hid[par][:, :], pre[par][:, :], ACT.Gelu).then_inc(S["act"], 1)

                    def store(n, half, par):
                        act.wait_ge(S["y"], n + 1)
                        wait(act, S["stored"][par], 16 * half)
                        nc.scalar.copy(y[par][:, :], yp[par][:, :]).then_inc(S["copied"], 1)
                        act.wait_ge(S["copied"], n + 1)
                        act.dma_start(dram["m_results"][bass.ds(n * P, P), :], y[par][:, :]
                                      ).then_inc(S["stored"][par], 16)
                    for n in range(4):
                        gelu(n, n % 2)
                        if n >= 2:
                            store(n - 2, 0, n % 2)
                    with act.Fori(2, SLOT_TILES // 2) as i:
                        for par in range(2):
                            gelu(2 * i + par, par)
                            store(2 * i + par - 2, i - 1, par)
                    for par in range(2):
                        store(SLOT_TILES - 2 + par, SLOT_TILES // 2 - 1, par)
                    for par in range(2):
                        act.wait_ge(S["stored"][par], 16 * SLOT_TILES // 2)
            zero_semaphores(nc, S["all"])

        AT = 4
        results = [sb(f"results{i}", [P, K, D]) for i in range(AT)]
        with nc.Block() as block:
            @block.gpsimd
            def _(pool):
                for t in range(TILES):
                    if t >= AT:
                        pool.wait_ge(S["added"], t - AT + 1)
                    for k in range(K):
                        nc.gpsimd.indirect_dma_start(
                            results[t % AT][:, k, :], None, dram["m_results"],
                            bass.IndirectOffsetOnAxis(keep["slot"][:, t, k:k + 1], 0),
                            bounds_check=SLOT_TILES * P - 1, oob_is_err=False).then_inc(S["m_gathered"][t % AT], 16)

            @block.vector
            def _(dve):
                for k in range(K):
                    ins = nc.vector.tensor_scalar(keep["share"][:, :, k], keep["share"][:, :, k], 0.3, None, ALU.mult)
                ins.then_inc(S["share"], 1)
                dve.wait_ge(S["share"], 1)
                for t in range(TILES):
                    dve.wait_ge(S["m_gathered"][t % AT], 16 * K * (t // AT + 1))
                    acc = keep["hs"][:, t, :]
                    for k in range(K):
                        nc.vector.scalar_tensor_tensor(out=acc, in0=results[t % AT][:, k, :],
                                                       scalar=keep["share"][:, t, k:k + 1], in1=acc, op0=ALU.mult,
                                                       op1=ALU.add).then_inc(S["moe_out"], 1)
                        dve.wait_ge(S["moe_out"], K * t + k + 1)
                    nc.vector.scalar_tensor_tensor(out=keep["x"][:, t, :], in0=acc, scalar=keep["gate"][:, 1:2],
                                                   in1=keep["x"][:, t, :], op0=ALU.mult, op1=ALU.add
                                                   ).then_inc(S["added"], 1)
    zero_semaphores(nc, S["all"])


def layer0_feed_forward(nc, keep, S, dram):
    with ExitStack() as ctx:
        def sb(name, shape, dt=F32, ctx=ctx):
            return ctx.enter_context(nc.sbuf_tensor(name, shape, dt))
        keep = dict(keep, hs=sb("hs", [P, TILES, D]), choice=sb("choice", [P, TILES, 2]),
                    share=sb("share", [P, TILES, 2]), slot=sb("slot", [P, TILES, 2], U32),
                    tile_expert=sb("tile_expert", [1, SLOT_TILES], U32))
        with ExitStack() as inner:
            keep["m"] = sb("m", [P, TILES, D], ctx=inner)
            latent_attention(nc, keep, S, dram)
            with ExitStack() as weights:
                E, F = 8, 512
                keep.update(w1=sb("moe0w1", [P, E, KT * F], ctx=weights), w2=sb("moe0w2", [P, E, F // P * D], ctx=weights),
                            b1=sb("moe0b1", [P, E, F], ctx=weights))
                dispatch_slots(nc, keep, S, dram)
                experts_of_two(nc, keep, S, dram)


def cross_wide(nc, keep, S, dram, latents):
    VD, L = 64, "L3" if latents else "L1"
    H = 8 if latents else 16
    INNER = H * VD
    MT = INNER // P
    KEYS = 2 * SEQ if latents else SEQ
    CH = 4
    scale = VD ** -0.5
    kinds = [("h", 0)]
    if latents:
        kinds += [("c", 0)]
    kinds += [("q", m) for m in range(0, MT, 2)]
    for m in range(0, MT, 2):
        kinds += [("k", m)] + ([("kr", m)] if latents else [])
    if latents:
        kinds += [("kl", m) for m in range(0, MT, 2)]
    kinds += [("v", n) for n in range(0, H, CH)]
    if latents:
        kinds += [("vl", n) for n in range(0, H, CH)]
    NP, NE = len(kinds), QT
    kinds_at = {k: i for i, k in enumerate(kinds)}

    def make(nc, keep, bufs, S, ctx):
        sb = bufs["sb"]
        wq, wkv = sb("wq", [P, KT, INNER]), sb("wkv", [P, KT, 2 * INNER])
        wo = sb("wo", [P, MT, D])
        gamma, beta = sb("gamma", [P, KT]), sb("beta", [P, KT])
        h, h2 = sb("h", [P, QT, D]), sb("h2", [P, QT, D])
        hT = sb("hT", [P, KT, SEQ])
        stream = [sb(f"stream{i}", [P, 2, SEQ]) for i in range(2)]
        qT = [sb(f"qT{i}", [P, MT, SEQ]) for i in range(2)]
        kT = [sb(f"kT{i}", [P, MT, KEYS]) for i in range(2)]
        v = [sb(f"v{i}", [P, KEYS // P, H, VD]) for i in range(2)]
        bufs["stream"] = stream
        work, o = bufs["pro"], bufs["o"]
        weights = [(wq[:, :, :], dram[L + "wq"].rearrange("(k p) m -> p k m", p=P)),
                   (wkv[:, :, :], dram[L + "wkv"].rearrange("(k p) m -> p k m", p=P)),
                   (wo[:, :, :], dram[L + "wo"].rearrange("(k p) m -> p k m", p=P)),
                   (gamma[:, :], dram[L + "gamma"]), (beta[:, :], dram[L + "beta"])]
        bias = None
        if latents:
            wkr = sb("wkr", [P, KT, INNER])
            gammax, betax = sb("gammax", [P, KT]), sb("betax", [P, KT])
            cos, sin = sb("cos", [P, SEQ]), sb("sin", [P, SEQ])
            turned, mixed = sb("turned", [P, 2, SEQ]), sb("mixed", [P, 2, SEQ])
            ch, cT = sb("ch", [P, QT, D]), sb("cT", [P, KT, SEQ])
            weights += [(wkr[:, :, :], dram[L + "wkr"].rearrange("(k p) m -> p k m", p=P)),
                        (gammax[:, :], dram[L + "gammax"]), (betax[:, :], dram[L + "betax"]),
                        (cos[:, :], dram["cos64"]), (sin[:, :], dram["sin64"])]
        else:
            bo = sb("bo", [1, D])
            weights += [(bo[:, :], dram[L + "bo"])]
            bias = bo[0:1, :]

        def norm(n, c, half, par):
            if n == 0:
                return x_norm(keep, h)(n, c, half, par)
            if n == 1:
                return (lambda t: h[:, t, :]), (lambda t: h2[:, t, :])
            return (lambda t: stream[par][:, t, :]), (lambda t: ch[:, t, :])

        def norm_wait(dve, n, c, half, par):
            if n == 1:
                dve.wait_ge(S["normed"], (3 if latents else 2) * c + 1)
            if n == 2:
                dve.wait_ge(S["stream"][par], 16 * (half + 1))

        def pro_fill(pe, j, c, half, par):
            kind, m = kinds[j]
            if kind in ("h", "c"):
                return turn(nc, keep, work, h2 if kind == "h" else ch)
            if kind == "q":
                return project(nc, work, wq, hT, (m, m + 1))
            if kind == "k":
                if not latents and m == 0:
                    pe.wait_ge(S["stream"][par], 16 * (half + 1))
                return project(nc, work, wkv, cT if latents else stream[par], (m, m + 1))
            if kind == "kr":
                return project(nc, work, wkr, cT, (m, m + 1))
            if kind == "kl":
                return project(nc, work, wkv, hT, (m, m + 1))
            src = hT if kind == "vl" else cT if latents else stream[par]
            return project_rows(nc, work, src, wkv, INNER + m * VD, CH * VD)

        def pro_copy(eng, j, c, half, par):
            kind, m = kinds[j]
            if kind in ("h", "c"):
                dst, g, b = (hT, gamma, beta) if kind == "h" else (cT, gammax, betax)
                for k in range(KT):
                    ins = nc.vector.tensor_scalar(dst[:, k, :], work[:, k * SEQ:(k + 1) * SEQ], g[:, k:k + 1],
                                                  b[:, k:k + 1], ALU.mult, ALU.add)
                return ins
            if kind == "q":
                return nc.scalar.mul(flat(qT[par][:, m:m + 2, :]), work[:, :], scale)
            if kind == "kl" or (kind == "k" and not latents):
                at = SEQ if kind == "kl" else 0
                return nc.scalar.copy(kT[par][:, m:m + 2, at:at + SEQ],
                                      work[:, :].rearrange("p (a b) -> p a b", a=2))
            if kind in ("v", "vl"):
                t0 = QT if kind == "vl" else 0
                for t in range(QT):
                    ins = nc.scalar.copy(v[par][:, t0 + t, m:m + CH, 0:VD],
                                         work[:, t * CH * VD:(t + 1) * CH * VD].rearrange("p (h v) -> p h v", h=CH))
                return ins
            to, table = (mixed, cos) if kind == "k" else (turned, sin)
            ins = nc.vector.tensor_tensor(to[:, :, :], work[:, :].rearrange("p (a b) -> p a b", a=2),
                                          table[:, :].unsqueeze(1).to_broadcast([P, 2, SEQ]), ALU.mult)
            if kind == "k":
                return ins
            ins.then_inc(S["rope"], 1)
            eng.wait_ge(S["rope"], (MT // 2) * c + m // 2 + 1)
            return nc.vector.tensor_tensor(kT[par][:, m:m + 2, 0:SEQ], mixed[:, :, :], turned[:, :, :], ALU.add)

        def epi_fill(pe, j, c, par):
            for k in range(MT):
                mm = nc.tensor.matmul(work[:, 0:D], o[par][:, k, j * P:(j + 1) * P], wo[:, k, :],
                                      start=(k == 0), stop=(bias is None and k == MT - 1))
            if bias is not None:
                mm = nc.tensor.matmul(work[:, 0:D], keep["ones"][0:1, :], bias, start=False, stop=True)
            return mm

        def epi_copy(eng, j, c, half, par):
            at = 6 if latents else 2
            xs = keep["x"][:, bass.ds(c * QT + j, 1), :].rearrange("p a b -> p (a b)")
            return nc.vector.scalar_tensor_tensor(out=xs, in0=work[:, 0:D], scalar=keep["gate"][:, at:at + 1],
                                                  in1=xs, op0=ALU.mult, op1=ALU.add)

        def q_of(par, hh, t):
            r = 64 * (hh % 2)
            return qT[par][r:r + 64, hh // 2, t * P:(t + 1) * P]

        def k_of(par, hh):
            r = 64 * (hh % 2)
            return kT[par][r:r + 64, hh // 2, :]

        def row_max(dve, nmax, bank, c, hh, p):
            if latents:
                return nc.vector.tensor_reduce(nmax[:, p, 0:1], bank[:, :], AX.X, ALU.max, negate=True)
            return plain_max(nc, dve, nmax, bank, p)

        def exp(act, prob, nmax, bank, hh, p, sums):
            if latents:
                return nc.scalar.activation(prob[:, :], bank[:, :], ACT.Exp, bias=nmax[:, p, 0:1],
                                            accum_out=sums[:, p, 0:1])
            for t in range(QT):
                ins = nc.scalar.activation(prob[:, t * SEQ:(t + 1) * SEQ], bank[:, t * SEQ:(t + 1) * SEQ], ACT.Exp,
                                           bias=nmax[:, p, t:t + 1], accum_out=sums[:, p, t:t + 1])
            return ins

        def pro_engine(j):
            return "dve" if kinds[j][0] in ("h", "c", "kr") or (latents and kinds[j][0] == "k") else "act"

        if latents:
            pro_at, epi_at = spread([6 + 0.5 * j for j in range(NP)]), spread([2, 4])
        else:
            pro_at, epi_at = spread([7 + 0.5 * j for j in range(NP)]), spread([2, 4])
        return dict(weights=weights, norm=norm,
                    norm_job=[None, 0, 1] if latents else [None, 0], norm_wait=norm_wait,
                    q=q_of, k=k_of, v=lambda par, hh, k: v[par][:, k, hh, :],
                    pro_fill=pro_fill, pro_copy=pro_copy,
                    pro_frees=[i for i, (k, m) in enumerate(kinds) if k not in ("h", "c")],
                    pro_engine=pro_engine, epi_fill=epi_fill, epi_copy=epi_copy,
                    epi_engine=lambda j: "dve", pro_at=pro_at, epi_at=epi_at,
                    row_max=row_max, exp=exp)

    source = dram["ctx"] if latents else dram["ctxT"]
    attention_stage(nc, keep, S, dict(
        name=L, heads=H, vd=VD, group=2, wide=latents, n_pro=NP, n_epi=NE,
        n_norm=3 if latents else 2,
        stream=lambda bufs, c, par: [(bufs["stream"][par][:, :, :],
                                      source[bass.ds(c, 1), :, :, :].rearrange("a p k s -> (a p) k s"))],
        make=make))


def relu_feed_forward(nc, keep, S, dram):
    F, N = 1024, 512
    FT, BT, BLOCKS = F // P, N // P, TOKENS // N
    L = "L2f"
    with ExitStack() as ctx:
        def sb(name, shape, dt=F32):
            return ctx.enter_context(nc.sbuf_tensor(L + name, shape, dt))
        w1, w2 = sb("w1", [P, KT, F]), sb("w2", [P, FT, D])
        b1, b2 = sb("b1", [P, FT]), sb("b2", [1, D])
        h, hT, aT = sb("h", [P, BT, D]), sb("hT", [P, KT, N]), sb("aT", [P, FT, N])
        st, mv, rstd = sb("st", [P, BT, 6]), sb("mv", [P, BT, 2]), sb("rstd", [P, BT])
        hp = [ctx.enter_context(nc.psum_tensor(f"{L}h{i}", [P, N], F32)) for i in range(4)]
        tp = [ctx.enter_context(nc.psum_tensor(f"{L}t{i}", [P, N], F32)) for i in range(KT)]
        yp = [ctx.enter_context(nc.psum_tensor(f"{L}y{i}", [P, 2, D], F32)) for i in range(2)]

        with nc.Block() as block:
            @block.sync
            def _(sp):
                sp.dma_start(w1[:, :, :], dram[L + "w1"].rearrange("(k p) f -> p k f", p=P)
                             ).then_inc(S["weights"], 16)
                sp.dma_start(w2[:, :, :], dram[L + "w2"].rearrange("(k p) f -> p k f", p=P)
                             ).then_inc(S["weights"], 16)
                sp.dma_start(b1[:, :], dram[L + "b1"]).then_inc(S["weights"], 16)
                sp.dma_start(b2[:, :], dram[L + "b2"]).then_inc(S["weights"], 16)

            @block.gpsimd
            def _(pool):
                def run(b):
                    pool.wait_ge(S["var"], b + 1)
                    nc.gpsimd.tensor_tensor(rstd[:, :], mv[:, :, 1], keep["eps"][:, :], ALU.add
                                            ).then_inc(S["vareps"], 1)
                    pool.wait_ge(S["vareps"], b + 1)
                    nc.gpsimd.tensor_tensor(rstd[:, :], rstd[:, :], keep["mhalf"][:, :], ALU.pow
                                            ).then_inc(S["rstd"], 1)
                run(0)
                with pool.Fori(1, BLOCKS) as b:
                    run(b)

            @block.vector
            def _(dve):
                def norm(b):
                    for t in range(BT):
                        ins = nc.vector.bn_stats(st[:, t, :],
                                                 keep["x"][:, bass.ds(b * BT + t, 1), :].rearrange("p a b -> p (a b)"))
                    ins.then_inc(S["stats"], 1)
                    dve.wait_ge(S["stats"], b + 1)
                    nc.vector.memset(keep["scratch"][:, 0:1], 0.0)
                    for t in range(BT):
                        ins = nc.vector.bn_aggr(mv[:, t, :], st[:, t, :])
                    ins.then_inc(S["var"], 1)
                    dve.wait_ge(S["rstd"], b + 1)
                    wait(dve, S["turned"], KT * b)
                    for t in range(BT):
                        ins = nc.vector.tensor_scalar(
                            h[:, t, :], keep["x"][:, bass.ds(b * BT + t, 1), :].rearrange("p a b -> p (a b)"),
                            mv[:, t, 0:1], rstd[:, t:t + 1], ALU.subtract, ALU.mult)
                    ins.then_inc(S["normed"], 1)

                def copy_turned(b):
                    for k in range(KT):
                        dve.wait_ge(S["turned"], KT * b + k + 1)
                        nc.vector.tensor_copy(hT[:, k, :], tp[k][:, :]).then_inc(S["turn_copied"], 1)

                def residual(b):
                    for i in range(2):
                        dve.wait_ge(S["y"], 2 * b + i + 1)
                        xs = flat(keep["x"][:, bass.ds(b * BT + 2 * i, 2), :])
                        nc.vector.scalar_tensor_tensor(out=xs, in0=flat(yp[i][:, :, :]), scalar=keep["gate"][:, 5:6],
                                                       in1=xs, op0=ALU.mult, op1=ALU.add).then_inc(S["added"], 1)

                def run(b, last=False):
                    if not last:
                        norm(b + 1)
                        copy_turned(b + 1)
                    residual(b)
                norm(0)
                copy_turned(0)
                run(0)
                with dve.Fori(1, BLOCKS - 1) as b:
                    run(b)
                run(BLOCKS - 1, last=True)

            @block.scalar
            def _(act):
                act.wait_ge(S["weights"], 64)

                def run(b):
                    wait(act, S["y"], 2 * b)
                    for m in range(FT):
                        act.wait_ge(S["hidden"], FT * b + m + 1)
                        nc.scalar.activation(aT[:, m, :], hp[m % 4][:, :], ACT.Relu, bias=b1[:, m:m + 1]
                                             ).then_inc(S["act"], 1)
                run(0)
                with act.Fori(1, BLOCKS) as b:
                    run(b)

            @block.tensor
            def _(pe):
                def turn_block(b):
                    pe.wait_ge(S["normed"], b + 1)
                    wait(pe, S["turn_copied"], KT * b)
                    for k in range(KT):
                        for t in range(BT):
                            mm = nc.tensor.transpose(tp[k][:, t * P:(t + 1) * P], h[:, t, k * P:(k + 1) * P],
                                                     keep["ident"][:, :])
                        mm.then_inc(S["turned"], 1)

                def run(b, last=False):
                    pe.wait_ge(S["turn_copied"], KT * (b + 1))
                    for m in range(FT):
                        wait(pe, S["act"], FT * b + m - 3)
                        for k in range(KT):
                            mm = nc.tensor.matmul(hp[m % 4][:, :], w1[:, k, m * P:(m + 1) * P], hT[:, k, :],
                                                  start=(k == 0), stop=(k == KT - 1))
                        mm.then_inc(S["hidden"], 1)
                    if not last:
                        turn_block(b + 1)
                    pe.wait_ge(S["act"], FT * (b + 1))
                    for t in range(BT):
                        if t % 2 == 0:
                            wait(pe, S["added"], 2 * (b - 1) + t // 2 + 1)
                        y = yp[t // 2][:, t % 2, :]
                        for k in range(FT):
                            nc.tensor.matmul(y, aT[:, k, t * P:(t + 1) * P], w2[:, k, :], start=(k == 0), stop=False)
                        mm = nc.tensor.matmul(y, keep["ones"][0:1, :], b2[0:1, :], start=False, stop=True)
                        if t % 2 == 1:
                            mm.then_inc(S["y"], 1)
                turn_block(0)
                pe.wait_ge(S["weights"], 64)
                run(0)
                with pe.Fori(1, BLOCKS - 1) as b:
                    run(b)
                run(BLOCKS - 1, last=True)
    zero_semaphores(nc, S["all"])


ROUND = 12582912.0
QMAX = 32767.0


def quantised_feed_forward(nc, keep, S, dram):
    F, N, W = 768, 512, 32
    FT, BT, BLOCKS = F // P, N // P, TOKENS // N
    L = "L3f"
    with ExitStack() as ctx:
        def sb(name, shape, dt=F32, ctx=ctx):
            return ctx.enter_context(nc.sbuf_tensor(L + name, shape, dt))
        wT = {n: sb(n + "T", [P, KT, F]) for n in ("up", "gate")}
        wT["down"] = sb("downT", [P, FT, D])
        hT = flat(keep["x"][:, :, :]).rearrange("p (k n) -> p k n", k=KT)
        peak, top, scale, inv = sb("peak", [P, TILES]), sb("top", [P, 8]), sb("scale", [P, 8]), sb("inv", [P, 8])

        def global_scale(dve, which, peaks, after):
            dve.wait_ge(S["peaks"], after)
            nc.vector.tensor_reduce(top[:, which:which + 1], peaks, AX.X, ALU.max).then_inc(S["local_top"], 1)
            dve.wait_ge(S["top"], 1)
            nc.vector.tensor_scalar(scale[:, which:which + 1], top[:, which:which + 1], 1.0 / QMAX, 1e-12,
                                    ALU.mult, ALU.max).then_inc(S["scale"], 1)
            dve.wait_ge(S["scale"], 1)
            nc.vector.reciprocal(inv[:, which:which + 1], scale[:, which:which + 1]).then_inc(S["inv"], 1)
            dve.wait_ge(S["inv"], 1)

        def global_top(pool, which):
            pool.wait_ge(S["local_top"], 1)
            nc.gpsimd.partition_all_reduce(top[:, which:which + 1], top[:, which:which + 1], P,
                                           bass.bass_isa.ReduceOp.max).then_inc(S["top"], 1)

        with ExitStack() as inner:
            raw = {n: sb(n, [P, FT * KT * P], ctx=inner) for n in ("up", "gate", "down")}
            amax, ws = sb("amax", [P, 3, 48], ctx=inner), sb("ws", [P, 3, 48], ctx=inner)
            wi = sb("wi", [P, 3, 48], ctx=inner)
            h = sb("h", [P, TILES, D], ctx=inner)
            st, mv = sb("st", [P, TILES, 6], ctx=inner), sb("mv", [P, TILES, 2], ctx=inner)
            rstd = sb("rstd", [P, TILES], ctx=inner)
            tp = [inner.enter_context(nc.psum_tensor(f"{L}t{i}", [P, 512], F32)) for i in range(4)]
            names = ("up", "gate", "down")
            WJ = 9
            LINKS = 7

            with nc.Block() as block:
                @block.sync
                def _(sp):
                    for n in names:
                        cols = D if n != "down" else F
                        sp.dma_start(raw[n][:, :].rearrange("p (a i) -> p a i", i=cols),
                                     dram[L + n].rearrange("(a p) i -> p a i", p=P)).then_inc(S["weights"], 16)
                    sp.dma_start(dram["x_spill"], keep["x"][:, :, :]).then_inc(S["stream"][0], 16)
                    sp.wait_ge(S["stream"][0], 16)

                @block.gpsimd
                def _(pool):
                    pool.wait_ge(S["var"], 1)
                    for q in range(TILES // BT):
                        nc.gpsimd.tensor_tensor(rstd[:, BT * q:BT * (q + 1)], mv[:, BT * q:BT * (q + 1), 1],
                                                keep["eps"][:, :], ALU.add).then_inc(S["vareps"], 1)
                    pool.wait_ge(S["vareps"], TILES // BT)
                    for q in range(TILES // BT):
                        nc.gpsimd.tensor_tensor(rstd[:, BT * q:BT * (q + 1)], rstd[:, BT * q:BT * (q + 1)],
                                                keep["mhalf"][:, :], ALU.pow).then_inc(S["rstd"], 1)
                    global_top(pool, 0)

                @block.vector
                def _(dve):
                    for t in range(TILES):
                        ins = nc.vector.bn_stats(st[:, t, :], keep["x"][:, t, :])
                    ins.then_inc(S["stats"], 1)
                    dve.wait_ge(S["stats"], 1)
                    for t in range(TILES):
                        ins = nc.vector.bn_aggr(mv[:, t, :], st[:, t, :])
                    ins.then_inc(S["var"], 1)
                    dve.wait_ge(S["weights"], 48)
                    done = [0]

                    def linked(ins):
                        done[0] += 1
                        ins.then_inc(S["route"], 1)
                        dve.wait_ge(S["route"], done[0])
                    for i, n in enumerate(names):
                        w = raw[n][:, :].rearrange("p (b w) -> p b w", w=W)
                        linked(nc.vector.tensor_reduce(amax[:, i, :], w, AX.X, ALU.max, apply_absolute_value=True))
                        linked(nc.vector.tensor_scalar(ws[:, i, :], amax[:, i, :], 1.0 / 7.0, 1e-12, ALU.mult,
                                                       ALU.max))
                        linked(nc.vector.reciprocal(wi[:, i, :], ws[:, i, :]))
                        linked(nc.vector.tensor_tensor(w, w, wi[:, i, :].unsqueeze(2).to_broadcast([P, 48, W]),
                                                       ALU.mult))
                        linked(nc.vector.tensor_scalar(w, w, ROUND, ROUND, ALU.add, ALU.subtract))
                        linked(nc.vector.tensor_scalar(w, w, -8.0, 7.0, ALU.max, ALU.min))
                        linked(nc.vector.tensor_tensor(w, w, ws[:, i, :].unsqueeze(2).to_broadcast([P, 48, W]),
                                                       ALU.mult))
                    assert done[0] == 3 * LINKS
                    dve.wait_ge(S["rstd"], TILES // BT)
                    for t in range(TILES):
                        ins = nc.vector.tensor_scalar(h[:, t, :], keep["x"][:, t, :], mv[:, t, 0:1], rstd[:, t:t + 1],
                                                      ALU.subtract, ALU.mult)
                    ins.then_inc(S["normed"], 1)
                    dve.wait_ge(S["normed"], 1)
                    nc.vector.tensor_reduce(peak[:, :], h[:, :, :], AX.X, ALU.max, apply_absolute_value=True
                                            ).then_inc(S["peaks"], 1)
                    global_scale(dve, 0, peak[:, :], 1)
                    QB = 8
                    for q in range(QB):
                        part = flat(h[:, q * TILES // QB:(q + 1) * TILES // QB, :])
                        nc.vector.tensor_scalar(part, part, inv[:, 0:1], ROUND, ALU.mult, ALU.add
                                                ).then_inc(S["rounded"], 1)
                    dve.wait_ge(S["rounded"], QB)
                    for q in range(QB):
                        part = flat(h[:, q * TILES // QB:(q + 1) * TILES // QB, :])
                        nc.vector.tensor_scalar(part, part, ROUND, scale[:, 0:1], ALU.subtract, ALU.mult
                                                ).then_inc(S["quantised"], 1)

                @block.tensor
                def _(pe):
                    n_bank = 0
                    for i, n in enumerate(names):
                        pe.wait_ge(S["route"], LINKS * (i + 1))
                        for j in range(3):
                            if n_bank >= 4:
                                pe.wait_ge(S["turn_copied"], n_bank - 3)
                            for q in range(4):
                                at = ((2 * j + q // 2) * D + (q % 2) * P) if n != "down" else (
                                    (q % 2) * F + (2 * j + q // 2) * P)
                                mm = nc.tensor.transpose(tp[n_bank % 4][:, q * P:(q + 1) * P], raw[n][:, at:at + P],
                                                         keep["ident"][:, :])
                            mm.then_inc(S["turned"], 1)
                            n_bank += 1
                    for b in range(BLOCKS):
                        pe.wait_ge(S["quantised"], b + 1)
                        for k in range(KT):
                            pe.wait_ge(S["turn_copied"], n_bank - 3)
                            for t in range(BT):
                                mm = nc.tensor.transpose(tp[n_bank % 4][:, t * P:(t + 1) * P],
                                                         h[:, BT * b + t, k * P:(k + 1) * P], keep["ident"][:, :])
                            mm.then_inc(S["turned"], 1)
                            n_bank += 1

                @block.scalar
                def _(act):
                    n_bank = 0
                    for n in names:
                        for j in range(3):
                            act.wait_ge(S["turned"], n_bank + 1)
                            src = tp[n_bank % 4][:, :]
                            if n == "down":
                                dst = flat(wT[n][:, 2 * j:2 * j + 2, :])
                            else:
                                src = src.rearrange("p (a k i) -> p k a i", a=2, k=KT)
                                dst = wT[n][:, :, 2 * j * P:(2 * j + 2) * P].rearrange("p k (a i) -> p k a i", a=2)
                            if n == "down":
                                nc.scalar.copy(dst, src).then_inc(S["turn_copied"], 1)
                            else:
                                nc.scalar.copy(dst[:, 0], src[:, 0])
                                nc.scalar.copy(dst[:, 1], src[:, 1]).then_inc(S["turn_copied"], 1)
                            n_bank += 1
                    act.wait_ge(S["stream"][0], 16)
                    act.wait_ge(S["normed"], 1)
                    for b in range(BLOCKS):
                        for k in range(KT):
                            act.wait_ge(S["turned"], n_bank + 1)
                            nc.scalar.copy(hT[:, k, b * N:(b + 1) * N], tp[n_bank % 4][:, :]
                                           ).then_inc(S["turn_copied"], 1)
                            n_bank += 1
            zero_semaphores(nc, S["all"])

        g = sb("g", [P, BLOCKS, FT * N])
        up = sb("upq", [P, BLOCKS, FT * N], I16)
        bank = [ctx.enter_context(nc.psum_tensor(f"{L}b{i}", [P, N], F32)) for i in range(6)]

        def project_all(which, quantise_up):
            with nc.Block() as block:
                @block.tensor
                def _(pe):
                    def run(b):
                        for m in range(FT):
                            wait(pe, S["copied"], FT * (b - 1) + m + 1)
                            for k in range(KT):
                                mm = nc.tensor.matmul(bank[m][:, :], wT[which][:, k, m * P:(m + 1) * P],
                                                      hT[:, k, bass.ds(b * N, N)], start=(k == 0), stop=(k == KT - 1))
                            mm.then_inc(S["hidden"], 1)
                    run(0)
                    with pe.Fori(1, BLOCKS) as b:
                        run(b)

                @block.scalar
                def _(act):
                    def run(b):
                        for m in range(FT):
                            if quantise_up:
                                act.wait_ge(S["quantised"], b + 1)
                            act.wait_ge(S["hidden"], FT * b + m + 1)
                            nc.scalar.copy(g[:, b, m * N:(m + 1) * N], bank[m][:, :]).then_inc(S["copied"], 1)
                    for b in range(BLOCKS):
                        run(b)

                @block.vector
                def _(dve):
                    def run(b):
                        if quantise_up:
                            g_b = g[:, bass.ds(b, 1), :].rearrange("p a b -> p (a b)")
                            nc.vector.tensor_scalar(g_b, g_b, inv[:, 1:2], ROUND, ALU.mult, ALU.add
                                                    ).then_inc(S["rounded"], 1)
                            dve.wait_ge(S["rounded"], b + 1)
                            nc.vector.tensor_scalar(up[:, bass.ds(b, 1), :].rearrange("p a b -> p (a b)"), g_b,
                                                    ROUND, None, ALU.subtract).then_inc(S["quantised"], 1)
                        wait(dve, S["peaks"], b)
                        dve.wait_ge(S["copied"], FT * (b + 1))
                        nc.vector.memset(keep["scratch"][:, 1:2], 0.0)
                        nc.vector.tensor_reduce(peaks[:, bass.ds(b, 1)],
                                                g[:, bass.ds(b, 1), :].rearrange("p a b -> p (a b)"), AX.X, ALU.max,
                                                apply_absolute_value=True).then_inc(S["peaks"], 1)
                    run(0)
                    with dve.Fori(1, BLOCKS) as b:
                        run(b)
                    global_scale(dve, 2 if quantise_up else 1, peaks[:, :], BLOCKS)

                @block.gpsimd
                def _(pool):
                    global_top(pool, 2 if quantise_up else 1)
            zero_semaphores(nc, S["all"])

        peaks = sb("peaks", [P, BLOCKS])
        project_all("up", False)
        project_all("gate", True)

        NP2 = 4
        HALF = FT * N // NP2
        AT = 3
        n = BLOCKS * NP2
        side = [sb(f"side{i}", [P, HALF]) for i in range(AT)]

        def part(i):
            return g[:, i // NP2, (i % NP2) * HALF:(i % NP2 + 1) * HALF]

        def up_part(i):
            return up[:, i // NP2, (i % NP2) * HALF:(i % NP2 + 1) * HALF]

        def round_part(i, which):
            nc.scalar.activation(part(i), part(i), ACT.Copy, bias=ROUND, scale=inv[:, which:which + 1]
                                 ).then_inc(S["rounded"], 1)

        def rescale_part(dve, i, factor):
            dve.wait_ge(S["rounded"], i + 1)
            nc.vector.tensor_scalar(part(i), part(i), ROUND, factor, ALU.subtract, ALU.mult
                                    ).then_inc(S["quantised"], 1)

        def peak_part(dve, i):
            dve.wait_ge(S["gated"], i + 1)
            nc.vector.tensor_reduce(peak[:, i:i + 1], part(i), AX.X, ALU.max, apply_absolute_value=True
                                    ).then_inc(S["peaks"], 1)

        def multiply_part(pool, i, ready):
            pool.wait_ge(ready, i + 1)
            nc.gpsimd.tensor_tensor(part(i), side[i % AT][:, :], part(i), ALU.mult).then_inc(S["gated"], 1)

        with nc.Block() as block:
            @block.vector
            def _(dve):
                nc.vector.tensor_scalar(scale[:, 5:6], scale[:, 2:3], 1.0 / 65536.0, None, ALU.mult
                                        ).then_inc(S["setup"], 1)
                dve.wait_ge(S["setup"], 1)
                for i in range(n + 2):
                    if i < n:
                        rescale_part(dve, i, scale[:, 5:6])
                    if 1 <= i <= n:
                        dve.wait_ge(S["act"], i)
                        nc.vector.tensor_scalar(side[(i - 1) % AT][:, :], side[(i - 1) % AT][:, :], ROUND, 65535.0,
                                                ALU.subtract, ALU.min).then_inc(S["sig_clipped"], 1)
                    if i >= 2:
                        peak_part(dve, i - 2)
                global_scale(dve, 3, peak[:, 0:n], n)

            @block.scalar
            def _(act):
                round_part(0, 2)
                for i in range(n):
                    if i + 1 < n:
                        round_part(i + 1, 2)
                    act.wait_ge(S["quantised"], i + 1)
                    if i >= AT:
                        act.wait_ge(S["gated"], i - AT + 1)
                    nc.scalar.activation(side[i % AT][:, :], part(i), ACT.Sigmoid, scale=65536.0
                                         ).then_inc(S["sigmoid"], 1)
                    act.wait_ge(S["sigmoid"], i + 1)
                    nc.scalar.activation(side[i % AT][:, :], side[i % AT][:, :], ACT.Copy, bias=ROUND, scale=65536.0
                                         ).then_inc(S["act"], 1)

            @block.gpsimd
            def _(pool):
                for i in range(n):
                    multiply_part(pool, i, S["sig_clipped"])
                global_top(pool, 3)
        zero_semaphores(nc, S["all"])

        with nc.Block() as block:
            @block.vector
            def _(dve):
                for i in range(n + 1):
                    if i < n:
                        rescale_part(dve, i, scale[:, 3:4])
                    if i >= 1:
                        peak_part(dve, i - 1)
                global_scale(dve, 4, peak[:, 0:n], n)

            @block.scalar
            def _(act):
                for i in range(n):
                    round_part(i, 3)
                    if i >= AT:
                        act.wait_ge(S["gated"], i - AT + 1)
                    nc.scalar.activation(side[i % AT][:, :], up_part(i), ACT.Copy, scale=scale[:, 1:2]
                                         ).then_inc(S["act"], 1)

            @block.gpsimd
            def _(pool):
                for i in range(n):
                    pool.wait_ge(S["act"], i + 1)
                    multiply_part(pool, i, S["quantised"])
                global_top(pool, 4)
        zero_semaphores(nc, S["all"])

        xo = [keep["x"][:, i, :] for i in range(2)]
        oq = [flat(keep["x"][:, 4 * i + 4:4 * i + 7, :]) for i in range(2)]
        yp = [bank[0], bank[1]]

        with nc.Block() as block:
            @block.vector
            def _(dve):
                def quantise(b, q, par):
                    t = BT * b + q
                    src = g[:, bass.ds(b, 1), :].rearrange("p a (f n) -> p (a f) n", n=N)[:, :, q * P:(q + 1) * P]
                    dst = oq[par].rearrange("p (f n) -> p f n", n=P)
                    wait(dve, S["y"], t - 1)
                    nc.vector.tensor_scalar(dst, src, inv[:, 4:5], ROUND, ALU.mult, ALU.add
                                            ).then_inc(S["rounded"], 1)
                    dve.wait_ge(S["rounded"], t + 1)
                    nc.vector.tensor_scalar(oq[par], oq[par], ROUND, scale[:, 4:5], ALU.subtract,
                                            ALU.mult).then_inc(S["quantised"], 1)

                def residual(b, q, par):
                    t = BT * b + q
                    dve.wait_ge(S["y"], t + 1)
                    dve.wait_ge(S["stream"][par], 16 * (2 * b + q // 2 + 1))
                    nc.vector.scalar_tensor_tensor(out=xo[par], in0=yp[par][:, 0:D],
                                                   scalar=keep["gate"][:, 7:8], in1=xo[par],
                                                   op0=ALU.mult, op1=ALU.add).then_inc(S["added"], 1)

                def block_of(b, first=False):
                    for q in range(BT):
                        quantise(b, q, q % 2)
                        if q >= 1:
                            residual(b, q - 1, (q - 1) % 2)
                        elif not first:
                            residual(b - 1, BT - 1, 1)
                block_of(0, first=True)
                with dve.Fori(1, BLOCKS) as b:
                    block_of(b)
                residual(BLOCKS - 1, BT - 1, 1)

            @block.tensor
            def _(pe):
                def run(b):
                    for q in range(BT):
                        t = BT * b + q
                        pe.wait_ge(S["quantised"], t + 1)
                        wait(pe, S["added"], t - 1)
                        for k in range(FT):
                            mm = nc.tensor.matmul(yp[q % 2][:, 0:D], oq[q % 2][:, k * P:(k + 1) * P],
                                                  wT["down"][:, k, :], start=(k == 0), stop=(k == FT - 1))
                        mm.then_inc(S["y"], 1)
                run(0)
                with pe.Fori(1, BLOCKS) as b:
                    run(b)

            @block.sync
            def _(sp):
                def load(i, par):
                    sp.dma_start(xo[par], dram["x_spill"][:, bass.ds(2 * i + par, 1), :].rearrange(
                        "p a d -> p (a d)")).then_inc(S["stream"][par], 16)

                def store(i, par):
                    t = 2 * i + par
                    sp.wait_ge(S["added"], t + 1)
                    sp.dma_start(dram["out"][bass.ds(t * P, P), :], xo[par]).then_inc(S["stored"][par], 16)
                load(0, 0)
                load(0, 1)
                with sp.Fori(0, TILES // 2 - 1) as i:
                    for par in range(2):
                        store(i, par)
                        sp.wait_ge(S["stored"][par], 16 * (i + 1))
                        load(i + 1, par)
                for par in range(2):
                    store(TILES // 2 - 1, par)
                for par in range(2):
                    sp.wait_ge(S["stored"][par], 16 * (TILES // 2))


def routed_experts(nc, keep, S, dram):
    E, K, CAP, F, L = 64, 8, 128, 192, "L1f"
    FH = F // 2
    SLOTS = E * CAP
    OUT_OF_RANGE = 65536.0
    AHEAD = 4
    with ExitStack() as ctx:
        def sb(name, shape, dt=F32, ctx=ctx):
            return ctx.enter_context(nc.sbuf_tensor(L + name, shape, dt))
        slots, share = sb("slots", [P, TILES, K], U32), sb("share", [P, TILES, K])

        def by_pairs(eng, run, tail=None):
            run(0, 0, 0)
            run(1, 0, 1)
            with eng.Fori(1, BATCH // 2) as i:
                run(2 * i, i + 0, 0)
                run(2 * i + 1, i + 0, 1)

        with ExitStack() as inner:
            def sbi(name, shape, dt=F32):
                return sb(name, shape, dt, ctx=inner)
            router = sbi("router", [P, KT, E])
            wsgu, wsd = sbi("wsgu", [P, KT, 2 * F]), sbi("wsd", [FH, 2, D])
            tri, iota = sbi("tri", [P, P]), sbi("iota", [P, E])
            h = [sbi(f"h{i}", [P, QT, D]) for i in range(2)]
            slot_of = [sbi(f"slot_of{i}", [P, QT, K], U32) for i in range(2)]
            hT = sbi("hT", [P, KT, SEQ])
            st, mv, rstd = sbi("st", [P, QT, 6]), sbi("mv", [P, QT, 2]), sbi("rstd", [P, QT])
            nm, tot, rtot = sbi("nm", [P, QT]), sbi("tot", [P, QT]), sbi("rtot", [P, QT])
            e, top, idx = sbi("e", [P, QT, E]), sbi("top", [P, QT, K]), sbi("idx", [P, QT, K], U32)
            idf, hit = sbi("idf", [P, QT, K]), sbi("hit", [P, QT, K, E])
            member, before = sbi("member", [P, QT, E]), sbi("before", [P, E])
            place, placed = sbi("place", [P, QT, K, E]), sbi("placed", [P, QT, K])
            late, slotf = sbi("late", [P, QT, K]), sbi("slotf", [P, QT, K])
            silu, act_h = sbi("silu", [FH, 2, SEQ]), sbi("act_h", [FH, 2, SEQ])
            zeros, tick = sbi("zeros", [P, 2048]), sbi("tick", [P, 2])
            turned = inner.enter_context(nc.psum_tensor(L + "pt", [P, 512], F32))
            logit = inner.enter_context(nc.psum_tensor(L + "pl", [P, 512], F32))
            posp = inner.enter_context(nc.psum_tensor(L + "pp", [P, 512], F32))
            gp = inner.enter_context(nc.psum_tensor(L + "pg", [FH, 512], F32))
            upp = inner.enter_context(nc.psum_tensor(L + "pu", [FH, 512], F32))
            yp = inner.enter_context(nc.psum_tensor(L + "py", [P, 512], F32))
            R = 18
            NW = 5

            with nc.Block() as block:
                @block.sync
                def _(sp):
                    sp.dma_start(router[:, :, :], dram[L + "router"].rearrange("(k p) m -> p k m", p=P)
                                 ).then_inc(S["weights"], 16)
                    sp.dma_start(wsgu[:, :, :], dram[L + "wsgu"].rearrange("(k p) m -> p k m", p=P)
                                 ).then_inc(S["weights"], 16)
                    sp.dma_start(wsd[:, :, :], dram[L + "wsd"].rearrange("(k p) m -> p k m", p=FH)
                                 ).then_inc(S["weights"], 16)
                    sp.dma_start(tri[:, :], dram["tri"]).then_inc(S["weights"], 16)
                    sp.dma_start(iota[:, :], dram["iota"]).then_inc(S["weights"], 16)
                    sp.wait_ge(S["setup"], 1)
                    for q in range(8):
                        sp.dma_start(dram["x_slots"][q * 1024:(q + 1) * 1024, :].rearrange("(p a) d -> p (a d)", p=P),
                                     zeros[:, :]).then_inc(S["zeroed"], 16)

                @block.gpsimd
                def _(pool):
                    pool.wait_ge(S["zeroed"], 128)

                    def rstds(c):
                        pool.wait_ge(S["var"], c + 1)
                        nc.gpsimd.tensor_tensor(rstd[:, :], mv[:, :, 1], keep["eps"][:, 0:QT], ALU.add
                                                ).then_inc(S["vareps"], 1)
                        pool.wait_ge(S["vareps"], c + 1)
                        nc.gpsimd.tensor_tensor(rstd[:, :], rstd[:, :], keep["mhalf"][:, 0:QT], ALU.pow
                                                ).then_inc(S["rstd"], 1)

                    def scatter(c, par):
                        wait(pool, S["tick"], c)
                        pool.wait_ge(S["slots"], c + 1)
                        nc.gpsimd.tensor_tensor(tick[:, 0:1], keep["eps"][:, 0:1], keep["eps"][:, 0:1], ALU.add
                                                ).then_inc(S["tick"], 1)
                        for t in range(QT):
                            for k in range(K):
                                nc.gpsimd.indirect_dma_start(
                                    dram["x_slots"], bass.IndirectOffsetOnAxis(slot_of[par][:, t, k:k + 1], 0),
                                    h[par][:, t, :], None, bounds_check=SLOTS - 1, oob_is_err=False
                                ).then_inc(S["scattered"][par], 16)
                    rstds(0)
                    rstds(1)
                    scatter(0, 0)
                    with pool.Fori(0, BATCH // 2 - 1) as i:
                        rstds(2 * i + 2)
                        scatter(2 * i + 1, 1)
                        rstds(2 * i + 3)
                        scatter(2 * i + 2, 0)
                    scatter(BATCH - 1, 1)
                    for par in range(2):
                        pool.wait_ge(S["scattered"][par], 16 * QT * K * BATCH // 2)

                @block.vector
                def _(dve):
                    nc.vector.memset(zeros[:, :], 0.0).then_inc(S["setup"], 1)
                    nc.vector.memset(before[:, :], 0.0).then_inc(S["counted"], 1)
                    dve.wait_ge(S["weights"], 16 * NW)

                    def add_shared(c):
                        dve.wait_ge(S["y"], c + 1)
                        add_output(nc, dve, keep, yp, keep["gate"][:, 3:4], c).then_inc(S["added"], 1)

                    def run(c, half, par):
                        n = [0]

                        def linked(ins):
                            n[0] += 1
                            ins.then_inc(S["route"], 1)
                            dve.wait_ge(S["route"], R * c + n[0])

                        def take_wait():
                            nc.vector.memset(keep["scratch"][:, 2:3], 0.0)

                        def x_tile(t):
                            return keep["x"][:, bass.ds(c * QT + t, 1), :].rearrange("p a b -> p (a b)")

                        def per_token(ap, m):
                            return ap.unsqueeze(2).to_broadcast([P, QT, m])
                        for t in range(QT):
                            ins = nc.vector.bn_stats(st[:, t, :], x_tile(t))
                        linked(ins)
                        take_wait()
                        for t in range(QT):
                            ins = nc.vector.bn_aggr(mv[:, t, :], st[:, t, :])
                        ins.then_inc(S["var"], 1)
                        dve.wait_ge(S["rstd"], c + 1)
                        wait(dve, S["scattered"][par], 16 * QT * K * half)
                        wait(dve, S["turned"], c)
                        for t in range(QT):
                            ins = nc.vector.tensor_scalar(h[par][:, t, :], x_tile(t), mv[:, t, 0:1], rstd[:, t:t + 1],
                                                          ALU.subtract, ALU.mult)
                        ins.then_inc(S["normed"], 1)
                        if not (isinstance(c, int) and c == 0):
                            add_shared(c - 1)
                        dve.wait_ge(S["turned"], c + 1)
                        nc.vector.tensor_copy(flat(hT[:, :, :]), turned[:, :]).then_inc(S["turn_copied"], 1)
                        dve.wait_ge(S["logits"], c + 1)
                        nc.vector.tensor_reduce(nm[:, :], logit[:, 0:QT * E].rearrange("p (t e) -> p t e", t=QT),
                                                AX.X, ALU.max, negate=True).then_inc(S["route_max"], 1)
                        dve.wait_ge(S["route_exp"], c + 1)
                        linked(nc.vector.tensor_reduce(tot[:, :], e[:, :, :], AX.X, ALU.add))
                        linked(nc.vector.reciprocal(rtot[:, :], tot[:, :]))
                        linked(nc.vector.tensor_tensor(e[:, :, :], e[:, :, :], per_token(rtot[:, :], E), ALU.mult))
                        take_wait()
                        for t in range(QT):
                            ins = nc.vector.max(top[:, t, :], e[:, t, :])
                        linked(ins)
                        take_wait()
                        for t in range(QT):
                            ins = nc.vector.max_index(idx[:, t, :], top[:, t, :], e[:, t, :])
                        linked(ins)
                        linked(nc.vector.tensor_copy(idf[:, :, :], idx[:, :, :]))
                        linked(nc.vector.tensor_reduce(tot[:, :], top[:, :, :], AX.X, ALU.add))
                        linked(nc.vector.reciprocal(rtot[:, :], tot[:, :]))
                        nc.vector.tensor_tensor(top[:, :, :], top[:, :, :], per_token(rtot[:, :], K), ALU.mult)
                        for t in range(QT):
                            ins = nc.vector.tensor_tensor(
                                hit[:, t, :, :], iota[:, :].unsqueeze(1).to_broadcast([P, K, E]),
                                idf[:, t, :].unsqueeze(2).to_broadcast([P, K, E]), ALU.is_equal)
                        linked(ins)
                        for t in range(QT):
                            ins = nc.vector.tensor_reduce(member[:, t, :], hit[:, t, :, :].rearrange("p k e -> p e k"),
                                                          AX.X, ALU.add)
                        ins.then_inc(S["member"], 1)
                        dve.wait_ge(S["act"], c + 1)
                        dve.wait_ge(S["up"], c + 1)
                        nc.vector.tensor_tensor(flat(act_h[:, :, :]), flat(silu[:, :, :]), upp[:, :], ALU.mult
                                                ).then_inc(S["gated"], 1)
                        dve.wait_ge(S["placed"], c + 1)
                        for t in range(QT):
                            ins = nc.vector.tensor_tensor(
                                place[:, t, :, :], hit[:, t, :, :],
                                posp[:, t * E:(t + 1) * E].unsqueeze(1).to_broadcast([P, K, E]), ALU.mult)
                        linked(ins)
                        linked(nc.vector.tensor_reduce(flat(placed[:, :, :]),
                                                       place[:, :, :, :].rearrange("p t k e -> p (t k) e"), AX.X,
                                                       ALU.add))
                        linked(nc.vector.tensor_tensor(before[:, :], before[:, :], member[:, 0, :], ALU.add))
                        nc.vector.tensor_tensor(before[:, :], before[:, :], member[:, 1, :], ALU.add
                                                ).then_inc(S["counted"], 1)
                        nc.vector.tensor_scalar(late[:, :, :], placed[:, :, :], float(CAP), OUT_OF_RANGE, ALU.is_ge,
                                                ALU.mult)
                        linked(nc.vector.scalar_tensor_tensor(out=flat(slotf[:, :, :]), in0=flat(idf[:, :, :]),
                                                              scalar=float(CAP), in1=flat(placed[:, :, :]),
                                                              op0=ALU.mult, op1=ALU.add))
                        linked(nc.vector.tensor_tensor(slotf[:, :, :], slotf[:, :, :], late[:, :, :], ALU.add))
                        nc.vector.tensor_copy(slot_of[par][:, :, :], slotf[:, :, :]).then_inc(S["slots"], 1)
                        linked(nc.vector.tensor_scalar(placed[:, :, :], placed[:, :, :], float(CAP), None, ALU.is_lt))
                        linked(nc.vector.tensor_tensor(top[:, :, :], top[:, :, :], placed[:, :, :], ALU.mult))
                        dve.wait_ge(S["slots"], c + 1)
                        nc.vector.tensor_scalar(keep["scratch"][:, 1:2], keep["eps"][:, 0:1], 0.0, None, ALU.mult)
                        nc.vector.tensor_copy(slots[:, bass.ds(c * QT, QT), :], slot_of[par][:, :, :])
                        linked(nc.vector.tensor_scalar(share[:, bass.ds(c * QT, QT), :], top[:, :, :],
                                                       keep["gate"][:, 3:4], None, ALU.mult))
                        assert n[0] == R, n[0]
                    by_pairs(dve, run)
                    add_shared(BATCH - 1)

                @block.scalar
                def _(act):
                    def run(c, half, par):
                        act.wait_ge(S["route_max"], c + 1)
                        for t in range(QT):
                            ins = nc.scalar.activation(e[:, t, :], logit[:, t * E:(t + 1) * E], ACT.Exp,
                                                       bias=nm[:, t:t + 1])
                        ins.then_inc(S["route_exp"], 1)
                        act.wait_ge(S["up"], c + 1)
                        wait(act, S["gated"], c)
                        nc.scalar.activation(flat(silu[:, :, :]), gp[:, :], ACT.Silu).then_inc(S["act"], 1)
                    by_pairs(act, run)

                @block.tensor
                def _(pe):
                    pe.wait_ge(S["weights"], 16 * NW)

                    def run(c, half, par):
                        pe.wait_ge(S["normed"], c + 1)
                        wait(pe, S["turn_copied"], c)
                        turn(nc, keep, turned, h[par]).then_inc(S["turned"], 1)
                        pe.wait_ge(S["turn_copied"], c + 1)
                        wait(pe, S["route_exp"], c)
                        for t in range(QT):
                            for k in range(KT):
                                mm = nc.tensor.matmul(logit[:, t * E:(t + 1) * E], hT[:, k, t * P:(t + 1) * P],
                                                      router[:, k, :], start=(k == 0), stop=(k == KT - 1))
                        mm.then_inc(S["logits"], 1)
                        wait(pe, S["gated"], c)
                        for bank, at in ((gp, 0), (upp, F)):
                            for m in range(2):
                                for k in range(KT):
                                    mm = nc.tensor.matmul(bank[:, m * SEQ:(m + 1) * SEQ],
                                                          wsgu[:, k, at + m * FH:at + (m + 1) * FH], hT[:, k, :],
                                                          start=(k == 0), stop=(k == KT - 1))
                        mm.then_inc(S["up"], 1)
                        pe.wait_ge(S["member"], c + 1)
                        pe.wait_ge(S["counted"], c + 1)
                        for t in range(QT):
                            nc.tensor.matmul(posp[:, t * E:(t + 1) * E], tri[:, :], member[:, t, :],
                                             start=True, stop=False)
                            if t == 1:
                                nc.tensor.matmul(posp[:, t * E:(t + 1) * E], keep["ones"][:, :], member[:, 0, :],
                                                 start=False, stop=False)
                            mm = nc.tensor.matmul(posp[:, t * E:(t + 1) * E], keep["ones"][:, :], before[:, :],
                                                  start=False, stop=True)
                        mm.then_inc(S["placed"], 1)
                        pe.wait_ge(S["gated"], c + 1)
                        wait(pe, S["added"], c)
                        for t in range(QT):
                            for m in range(2):
                                mm = nc.tensor.matmul(yp[:, t * D:(t + 1) * D], act_h[:, m, t * P:(t + 1) * P],
                                                      wsd[:, m, :], start=(m == 0), stop=(m == 1))
                        mm.then_inc(S["y"], 1)
                    by_pairs(pe, run)
            zero_semaphores(nc, S["all"])

        with ExitStack() as inner:
            wgu = [sb(f"wgu{i}", [P, 2, KT, F], ctx=inner) for i in range(AHEAD)]
            wd = [sb(f"wd{i}", [FH, 2, D], ctx=inner) for i in range(AHEAD)]
            xs = [sb(f"xs{i}", [P, D], ctx=inner) for i in range(AHEAD)]
            xT = [sb(f"xT{i}", [P, KT, P], ctx=inner) for i in range(2)]
            silu = [sb(f"esilu{i}", [FH, 2, P], ctx=inner) for i in range(2)]
            act_h = [sb(f"eact{i}", [FH, 2, P], ctx=inner) for i in range(2)]
            y = [sb(f"y{i}", [P, D], ctx=inner) for i in range(2)]
            pt = [inner.enter_context(nc.psum_tensor(f"{L}et{i}", [P, KT * P], F32)) for i in range(2)]
            pg = inner.enter_context(nc.psum_tensor(L + "eg", [FH, 2, P], F32))
            pu = [inner.enter_context(nc.psum_tensor(f"{L}eu{i}", [FH, 2, P], F32)) for i in range(2)]
            py = [inner.enter_context(nc.psum_tensor(f"{L}ey{i}", [P, D], F32)) for i in range(2)]

            def first(e):
                return isinstance(e, int) and e == 0

            def by_experts(eng, run):
                for b in range(AHEAD):
                    run(b, 0, b, False)
                with eng.Fori(1, E // AHEAD - 1) as i:
                    for b in range(AHEAD):
                        run(AHEAD * i + b, i + 0, b, False)
                for b in range(AHEAD):
                    run(E - AHEAD + b, E // AHEAD - 1, b, b == AHEAD - 1)

            with nc.Block() as block:
                @block.sync
                def _(sp):
                    def run(e, quarter, b, last):
                        wait(sp, S["y"], e - AHEAD + 1)
                        for i, n in enumerate(("wg", "wu")):
                            sp.dma_start(wgu[b][:, i, :, :], dram[L + n][bass.ds(e, 1), :, :].rearrange(
                                "a (k p) f -> p (a k) f", p=P)).then_inc(S["stream"][b], 16)
                        sp.dma_start(wd[b][:, :, :], dram[L + "wd"][bass.ds(e, 1), :, :].rearrange(
                            "a (k p) f -> p (a k) f", p=FH)).then_inc(S["stream"][b], 16)
                        sp.dma_start(xs[b][:, :], dram["x_slots"][bass.ds(e * CAP, CAP), :]
                                     ).then_inc(S["stream"][b], 16)
                    by_experts(sp, run)

                @block.tensor
                def _(pe):
                    def turn_rows(e, quarter, b):
                        par = b % 2
                        pe.wait_ge(S["stream"][b], 64 * (quarter + 1))
                        wait(pe, S["turn_copied"], e - 1)
                        for k in range(KT):
                            mm = nc.tensor.transpose(pt[par][:, k * P:(k + 1) * P], xs[b][:, k * P:(k + 1) * P],
                                                     keep["ident"][:, :])
                        mm.then_inc(S["turned"], 1)

                    def hidden(e, b):
                        par = b % 2
                        pe.wait_ge(S["turn_copied"], e + 1)
                        for i, bank in ((0, pg), (1, pu[par])):
                            if i == 0:
                                wait(pe, S["act"], e)
                            else:
                                wait(pe, S["gated"], e - 1)
                            for m in range(2):
                                for k in range(KT):
                                    mm = nc.tensor.matmul(bank[:, m, :], wgu[b][:, i, k, m * FH:(m + 1) * FH],
                                                          xT[par][:, k, :], start=(k == 0), stop=(k == KT - 1))
                            mm.then_inc(S["hidden"], 1)

                    def outputs(e, b):
                        par = b % 2
                        pe.wait_ge(S["gated"], e + 1)
                        wait(pe, S["copied"], e - 1)
                        for m in range(2):
                            mm = nc.tensor.matmul(py[par][:, :], act_h[par][:, m, :], wd[b][:, m, :],
                                                  start=(m == 0), stop=(m == 1))
                        mm.then_inc(S["y"], 1)

                    def run(e, quarter, b, last):
                        hidden(e, b)
                        if not last:
                            turn_rows(e + 1, quarter + (b + 1) // AHEAD, (b + 1) % AHEAD)
                        if not first(e):
                            outputs(e - 1, (b - 1) % AHEAD)
                    turn_rows(0, 0, 0)
                    by_experts(pe, run)
                    outputs(E - 1, AHEAD - 1)

                @block.scalar
                def _(act):
                    def run(e, quarter, b, last):
                        par = b % 2
                        act.wait_ge(S["hidden"], 2 * e + 1)
                        wait(act, S["gated"], e - 1)
                        nc.scalar.activation(silu[par][:, :, :], pg[:, :, :], ACT.Silu).then_inc(S["act"], 1)
                        if not first(e):
                            if b:
                                store(e - 1, quarter, b - 1)
                            else:
                                store(e - 1, quarter - 1, AHEAD - 1)

                    def store(e, quarter, b):
                        par = b % 2
                        act.wait_ge(S["y"], e + 1)
                        wait(act, S["stored"][par], 16 * (2 * quarter + b // 2))
                        nc.scalar.copy(y[par][:, :], py[par][:, :]).then_inc(S["copied"], 1)
                        act.wait_ge(S["copied"], e + 1)
                        act.dma_start(dram["y_slots"][bass.ds(e * CAP, CAP), :], y[par][:, :]
                                      ).then_inc(S["stored"][par], 16)
                    by_experts(act, run)
                    store(E - 1, E // AHEAD - 1, AHEAD - 1)
                    for par in range(2):
                        act.wait_ge(S["stored"][par], 16 * E // 2)

                @block.vector
                def _(dve):
                    def run(e, quarter, b, last):
                        par = b % 2
                        dve.wait_ge(S["turned"], e + 1)
                        wait(dve, S["hidden"], 2 * (e - 1))
                        nc.vector.tensor_copy(flat(xT[par][:, :, :]), pt[par][:, :]).then_inc(S["turn_copied"], 1)

                    def gate(e, par):
                        dve.wait_ge(S["hidden"], 2 * e + 2)
                        dve.wait_ge(S["act"], e + 1)
                        wait(dve, S["y"], e - 1)
                        nc.vector.tensor_tensor(act_h[par][:, :, :], silu[par][:, :, :], pu[par][:, :, :], ALU.mult
                                                ).then_inc(S["gated"], 1)

                    def both(e, quarter, b, last):
                        gate(e, b % 2)
                        if not last:
                            run(e + 1, None, (b + 1) % AHEAD, False)
                    run(0, 0, 0, False)
                    by_experts(dve, both)
            zero_semaphores(nc, S["all"])

        with ExitStack() as inner:
            rows = [sb(f"rows{i}", [P, QT, K, D], ctx=inner) for i in range(2)]
            slot_of = [sb(f"gslot{i}", [P, QT, K], U32, ctx=inner) for i in range(2)]
            mine = [sb(f"mine{i}", [P, QT, K], ctx=inner) for i in range(2)]
            tick = sb("gtick", [P, 2], ctx=inner)

            with nc.Block() as block:
                @block.gpsimd
                def _(pool):
                    def run(c, half, par):
                        wait(pool, S["tick"], c)
                        pool.wait_ge(S["slots"], c + 1)
                        nc.gpsimd.tensor_tensor(tick[:, 0:1], keep["eps"][:, 0:1], keep["eps"][:, 0:1], ALU.add
                                                ).then_inc(S["tick"], 1)
                        for t in range(QT):
                            for k in range(K):
                                nc.gpsimd.indirect_dma_start(
                                    rows[par][:, t, k, :], None, dram["y_slots"],
                                    bass.IndirectOffsetOnAxis(slot_of[par][:, t, k:k + 1], 0),
                                    bounds_check=SLOTS - 1, oob_is_err=False).then_inc(S["gathered"][par], 16)
                    by_pairs(pool, run)

                @block.vector
                def _(dve):
                    for par in range(2):
                        nc.vector.memset(rows[par][:, :, :, :], 0.0)

                    def fetch(c, half, par):
                        wait(dve, S["added"], K * (c - 1))
                        wait(dve, S["slots"], c)
                        nc.vector.tensor_scalar(keep["scratch"][:, 1:2], keep["eps"][:, 0:1], 0.0, None, ALU.mult)
                        nc.vector.tensor_copy(mine[par][:, :, :], share[:, bass.ds(c * QT, QT), :])
                        nc.vector.tensor_copy(slot_of[par][:, :, :], slots[:, bass.ds(c * QT, QT), :]
                                              ).then_inc(S["slots"], 1)

                    def sums(c, half, par):
                        dve.wait_ge(S["gathered"][par], 16 * QT * K * (half + 1))
                        dve.wait_ge(S["slots"], c + 1)
                        for k in range(K):
                            if k:
                                dve.wait_ge(S["added"], K * c + k)
                            for t in range(QT):
                                xt = keep["x"][:, bass.ds(c * QT + t, 1), :].rearrange("p a b -> p (a b)")
                                ins = nc.vector.scalar_tensor_tensor(out=xt, in0=rows[par][:, t, k, :],
                                                                     scalar=mine[par][:, t, k:k + 1], in1=xt,
                                                                     op0=ALU.mult, op1=ALU.add)
                            ins.then_inc(S["added"], 1)
                    fetch(0, 0, 0)
                    fetch(1, 0, 1)
                    with dve.Fori(0, BATCH // 2 - 1) as i:
                        sums(2 * i, i + 0, 0)
                        fetch(2 * i + 2, None, 0)
                        sums(2 * i + 1, i + 0, 1)
                        fetch(2 * i + 3, None, 1)
                    sums(BATCH - 2, BATCH // 2 - 1, 0)
                    sums(BATCH - 1, BATCH // 2 - 1, 1)
            zero_semaphores(nc, S["all"])


def stacked_attention(nc, keep, S, dram, cfg):
    HD, H, G, NG, VW = cfg["dim"], 16, 4, 4, 32
    R = 6 * HD
    M0 = 96 if HD == 16 else 64
    KK = H * HD // P
    NP, NE = cfg["n_pro"], cfg["n_epi"]
    LOADS = 9
    name = cfg["name"]
    split_slots = cfg["split_slots"]
    turn_job = cfg["turn_job"]

    with ExitStack() as ctx:
        def sb(n, shape, dt=F32):
            return ctx.enter_context(nc.sbuf_tensor(name + n, shape, dt))

        def psum(n):
            return ctx.enter_context(nc.psum_tensor(name + n, [P, 512], F32))

        score, tscore = [psum(f"score{i}") for i in range(2)], [psum(f"tscore{i}") for i in range(2)]
        pvp, back, pro, epi = psum("pvp"), psum("back"), psum("pro"), psum("epi")
        qs = [sb(f"qs{i}", [M0 + 3, H, SEQ], BF16) for i in range(3)]
        ks = [sb(f"ks{i}", [M0 + 3, H, SEQ], BF16) for i in range(3)]
        nmax = [sb(f"nmax{i}", [P, QT, H]) for i in range(3)]
        mrow, mleft, mpart = sb("mrow", [8, SEQ]), sb("mleft", [8, SEQ]), sb("mpart", [8, 3, SEQ], BF16)
        probT = [sb(f"probT{i}", [P, 512]) for i in range(2)]
        raw = [sb(f"raw{i}", [P, SEQ]) for i in range(2)]
        rden = sb("rden", [P, QT, G])
        o = [sb(f"o{i}", [P, QT, H * HD]) for i in range(3)]
        v = [sb(f"v{i}", [P, QT, H, VW]) for i in range(3)]
        whole = {n: sb(n + "whole", [P, KK * SEQ]) for n in "qk"}
        left = {n: sb(n + "left", [P, KK * SEQ]) for n in "qk"}
        part = {n: sb(n + "part", [P, 3, KK * SEQ], BF16) for n in "qk"}
        zeros = sb("zeros", [P, KK * SEQ])
        st, mv, rstd = sb("st", [P, QT, 6]), sb("mv", [P, QT, 2]), sb("rstd", [P, QT])
        parts_dram = {n: dram[f"{n}_parts{HD}"] for n in "qk"}
        tops_dram = dram["top_parts"]
        bufs = dict(sb=sb, pro=pro, epi=epi, o=o, v=v, whole=whole)

        def split_step(r, eng, add, src, rest, dst, link, count, done):
            if r:
                eng.wait_ge(link, count + r)
            if r % 2 == 0:
                add(dst[r // 2], src if r == 0 else rest, zeros[0:src.shape[0], 0:src.shape[1]], ALU.add
                    ).then_inc(link, 1)
            elif r == 1:
                add(rest, src, dst[0], ALU.subtract).then_inc(link, 1)
            else:
                add(dst[2], rest, dst[1], ALU.subtract).then_inc(done, 1)

        def split_matrix(r, eng, add, which, n):
            if r == 0:
                eng.wait_ge(S[which + "_ready"], n + 1)
                wait(eng, S[which + "_stored"], 48 * n)
            split_step(r, eng, add, whole[which][:, :], left[which][:, :], [part[which][:, i, :] for i in range(3)],
                       S[which + "_link"], 3 * n, S[which + "_split"])
        fns = cfg["make"](nc, keep, bufs, S)
        schedule_pro, schedule_epi = cfg["pro_at"], cfg["epi_at"]

        mask = fns.get("mask")

        def batch(i, k):
            return 3 * i + k, i + k // 3, k % 3

        def iterations(eng, body):
            for c in range(3):
                body(0, c, True, True, c > 0)
            with eng.Fori(1, 4) as i:
                for k in range(3):
                    body(i, k, True, True, True)
            body(0, 12, True, True, True)
            body(0, 13, True, True, True)
            body(0, 14, True, False, True)
            body(0, 15, False, False, True)

        with nc.Block() as block:
            @block.sync
            def _(sp):
                for dst, src in fns["weights"]:
                    sp.dma_start(dst, src).then_inc(S["weights"], 16)

                def stream(b):
                    n, rnd, buf = b
                    if "stream" in fns:
                        wait(sp, S["pro_filled"], NP * (n - 2))
                        dst, src = fns["stream"](n, buf)
                        sp.dma_start(dst, src).then_inc(S["stream"][buf], 16)

                def store_parts(which, b):
                    n, rnd, buf = b
                    sp.wait_ge(S[which + "_split"], n + 1)
                    for r in range(3):
                        sp.dma_start(parts_dram[which][buf, r].rearrange("d (h k) s -> (d h) (k s)", k=KK),
                                     part[which][:, r, :]).then_inc(S[which + "_stored"], 16)

                def load_stack(which, b):
                    n, rnd, buf = b
                    sp.wait_ge(S[which + "_stored"], 48 * (n + 1))
                    if which == "q":
                        pieces = [(0, 0, 3), (3, 0, 2), (5, 0, 1)]
                    else:
                        pieces = [(0, 0, 1), (1, 0, 1), (2, 0, 1), (3, 1, 1), (4, 1, 1), (5, 2, 1)]
                    for at, r, m in pieces:
                        sp.dma_start((qs if which == "q" else ks)[buf][at * HD:(at + m) * HD, :, :],
                                     parts_dram[which][buf, r:r + m].rearrange("r d h s -> (r d) h s")
                                     ).then_inc(S["stacked"][buf], 16)

                def store_tops(g, b):
                    n, rnd, buf = b
                    sp.wait_ge(S["tops_split"], 2 * n + g + 1)
                    sp.dma_start(tops_dram[buf, g].rearrange("r h s -> h r s"), mpart[:, :, :]
                                 ).then_inc(S["tops_stored"], 16)

                def load_tops(g, b):
                    n, rnd, buf = b
                    sp.wait_ge(S["tops_stored"], 16 * (2 * n + g + 1))
                    sp.dma_start(qs[buf][M0:M0 + 3, 8 * g:8 * g + 8, :], tops_dram[buf, g]
                                 ).then_inc(S["tops_in"][buf], 16)

                def body(i, k, a, p, e):
                    store_tops(1, batch(i, k))
                    load_tops(1, batch(i, k))
                    if k + 3 < BATCH:
                        stream(batch(i, k + 3))
                    if p:
                        store_parts("k", batch(i, k + 2))
                        load_stack("k", batch(i, k + 2))
                    if a:
                        store_tops(0, batch(i, k + 1))
                        load_tops(0, batch(i, k + 1))
                    if p:
                        store_parts("q", batch(i, k + 2))
                        load_stack("q", batch(i, k + 2))
                    if fns.get("sync_more"):
                        fns["sync_more"](sp, 3 * i + k, k + 3 < BATCH, e)

                for k in range(3):
                    stream(batch(0, k))
                sp.wait_ge(S["setup"], 1)
                for k in range(2):
                    if fns.get("sync_head"):
                        fns["sync_head"](sp, k)
                    for which in "kq":
                        store_parts(which, batch(0, k))
                        load_stack(which, batch(0, k))
                store_tops(0, batch(0, 0))
                load_tops(0, batch(0, 0))
                iterations(sp, body)
                if fns.get("sync_tail"):
                    fns["sync_tail"](sp)

            @block.gpsimd
            def _(pool):
                add = nc.gpsimd.tensor_tensor

                def rstds(n):
                    pool.wait_ge(S["var"], n + 1)
                    add(rstd[:, :], mv[:, :, 1], keep["eps"][:, 0:QT], ALU.add).then_inc(S["vareps"], 1)
                    pool.wait_ge(S["vareps"], n + 1)
                    add(rstd[:, :], rstd[:, :], keep["mhalf"][:, 0:QT], ALU.pow).then_inc(S["rstd"], 1)

                def split_ready(which, n):
                    for r in range(4):
                        split_matrix(r, pool, add, which, n)

                def split_tops(g, n):
                    pool.wait_ge(S["tops_copied"], 2 * n + g + 1)
                    wait(pool, S["tops_stored"], 16 * (2 * n + g))
                    for r in range(4):
                        split_step(r, pool, add, mrow[:, :], mleft[:, :], [mpart[:, i, :] for i in range(3)],
                                   S["tops_link"], 3 * (2 * n + g), S["tops_split"])

                def body(i, k, a, p, e):
                    c = 3 * i + k
                    split_tops(1, c)
                    if p:
                        split_ready("k", c + 2)
                        if not split_slots:
                            split_ready("q", c + 2)
                    if a:
                        split_tops(0, c + 1)
                    if k + 3 < BATCH:
                        rstds(c + 3)
                pool.wait_ge(S["setup"], 1)
                for n in range(2):
                    rstds(n)
                    split_ready("k", n)
                    if not split_slots:
                        split_ready("q", n)
                rstds(2)
                split_tops(0, 0)
                iterations(pool, body)

            @block.vector
            def _(dve):
                def x_tile(n, t):
                    return keep["x"][:, bass.ds(n * QT + t, 1), :].rearrange("p a b -> p (a b)")

                def norm(n):
                    if fns.get("norm_wait"):
                        fns["norm_wait"](dve, n)
                    for t in range(QT):
                        ins = nc.vector.bn_stats(st[:, t, :], x_tile(n, t))
                    ins.then_inc(S["stats"], 1)
                    dve.wait_ge(S["stats"], n + 1)
                    nc.vector.memset(keep["scratch"][:, 0:1], 0.0)
                    for t in range(QT):
                        ins = nc.vector.bn_aggr(mv[:, t, :], st[:, t, :])
                    ins.then_inc(S["var"], 1)

                def normed(n):
                    dve.wait_ge(S["rstd"], n + 1)
                    wait(dve, S["pro_filled"], 0 if isinstance(n, int) and n == 0 else NP * (n - 1) + turn_job + 1)
                    for t in range(QT):
                        ins = nc.vector.tensor_scalar(fns["h"][:, t, :], x_tile(n, t), mv[:, t, 0:1],
                                                      rstd[:, t:t + 1], ALU.subtract, ALU.mult)
                    ins.then_inc(S["normed"], 1)

                def row_max(h, b):
                    n, rnd, buf = b
                    if h == 0:
                        wait(dve, S["tops_filled"], 2 * (n - 2))
                    dve.wait_ge(S["scores"], 16 * n + h + 1)
                    src = score[h % 2]
                    if mask:
                        src = mask["masked"][h % 2]
                        nc.vector.tensor_tensor(src[:, :], score[h % 2][:, :], mask["rows"][:, :], ALU.add
                                                ).then_inc(S["masked"], 1)
                        dve.wait_ge(S["masked"], 16 * n + h + 1)
                    nc.vector.tensor_reduce(nmax[buf][:, :, h], src[:, :].rearrange("p (t k) -> p t k", t=QT),
                                            AX.X, ALU.max, negate=True).then_inc(S["row_max"], 1)

                def normalise(g, b):
                    n, rnd, buf = b
                    bank = back[:, 0:QT * P].rearrange("p (t g v) -> p t g v", t=QT, g=G)
                    dve.wait_ge(S["back"], NG * n + g + 1)
                    nc.vector.reciprocal(rden[:, :, :], bank[:, :, :, HD]).then_inc(S["rden"], 1)
                    dve.wait_ge(S["rden"], NG * n + g + 1)
                    if g == 0:
                        wait(dve, S["epi_filled"], NE * (n - 2))
                    for t in range(QT):
                        dst = o[buf][:, t, g * G * HD:(g + 1) * G * HD].rearrange("p (g v) -> p g v", g=G)
                        ins = nc.vector.tensor_tensor(dst, bank[:, t, :, 0:HD],
                                                      rden[:, t, :].unsqueeze(2).to_broadcast([P, G, HD]), ALU.mult)
                    ins.then_inc(S["o_ready"], 1)

                def pro_copy(j, b):
                    n, rnd, buf = b
                    if fns["pro_engine"](j) == "dve":
                        dve.wait_ge(S["pro_filled"], NP * n + j + 1)
                        if j == NP - 1:
                            wait(dve, S["pv"], 16 * (n - 2))
                        fns["pro_copy"](dve, j, n, buf).then_inc(S["pro_copied"], 1)

                def epi_copy(j, n):
                    if fns["epi_engine"](j) == "dve":
                        dve.wait_ge(S["epi_filled"], NE * n + j + 1)
                        fns["epi_copy"](dve, j, n).then_inc(S["epi_copied"], 1)

                def body(i, k, a, p, e):
                    c = 3 * i + k
                    for h in range(16):
                        if a:
                            row_max(h, batch(i, k + 1))
                        if h > G and h % G == 1:
                            normalise(h // G - 1, batch(i, k))
                        if h == 1 and e:
                            normalise(NG - 1, batch(i, k - 1))
                        if p:
                            for j in schedule_pro(h):
                                pro_copy(j, batch(i, k + 2))
                            if h in split_slots:
                                split_matrix(h - split_slots[0], dve, nc.vector.tensor_tensor, "q", c + 2)
                        if e:
                            for j in schedule_epi(h):
                                epi_copy(j, c - 1)
                        if k + 3 < BATCH:
                            if h == 14:
                                norm(c + 3)
                            if h == 15:
                                normed(c + 3)

                if fns.get("vector_setup"):
                    fns["vector_setup"](dve)
                nc.vector.memset(zeros[:, :], 0.0)
                for b in range(3):
                    if R < M0:
                        nc.vector.memset(qs[b][32:64, :, :], 0.0)
                        nc.vector.memset(ks[b][32:64, :, :], 0.0)
                    nc.vector.memset(v[b][:, :, :, HD:HD + 1], 1.0)
                    nc.vector.memset(v[b][:, :, :, HD + 1:VW], 0.0)
                    ins = nc.vector.memset(ks[b][M0:M0 + 3, :, :], 1.0)
                ins.then_inc(S["setup"], 1)
                dve.wait_ge(S["weights"], 16 * len(fns["weights"]))
                if mask:
                    fns["mask_setup"](dve)
                for n in range(2):
                    norm(n)
                    normed(n)
                    for j in range(NP):
                        pro_copy(j, batch(0, n))
                    for r in range(len(split_slots)):
                        split_matrix(r, dve, nc.vector.tensor_tensor, "q", n)
                norm(2)
                normed(2)
                for h in range(16):
                    row_max(h, batch(0, 0))
                iterations(dve, body)
                normalise(NG - 1, batch(0, BATCH - 1))
                for j in range(NE):
                    epi_copy(j, BATCH - 1)

            @block.scalar
            def _(act):
                def exp(h, b):
                    n, rnd, buf = b
                    act.wait_ge(S["tscores"], 16 * n + h + 1)
                    wait(act, S["pv"], 16 * n + h - 1)
                    nc.scalar.activation(probT[h % 2][:, :], tscore[h % 2][:, :], ACT.Exp).then_inc(S["exp"], 1)

                def copy_raw(g, n):
                    act.wait_ge(S["pv"], 16 * n + G * (g + 1))
                    wait(act, S["back"], NG * n + g - 1)
                    nc.scalar.copy(raw[g % 2][:, :], pvp[:, 0:SEQ]).then_inc(S["raw"], 1)

                def copy_tops(g, n):
                    act.wait_ge(S["tops_filled"], 2 * n + g + 1)
                    wait(act, S["tops_split"], 2 * n + g)
                    nc.scalar.copy(mrow[:, :], epi[0:8, 0:SEQ]).then_inc(S["tops_copied"], 1)

                def pro_copy(j, b):
                    n, rnd, buf = b
                    if fns["pro_engine"](j) == "act":
                        act.wait_ge(S["pro_filled"], NP * n + j + 1)
                        fns["pro_copy"](act, j, n, buf).then_inc(S["pro_copied"], 1)

                def epi_copy(j, n):
                    if fns["epi_engine"](j) == "act":
                        act.wait_ge(S["epi_filled"], NE * n + j + 1)
                        fns["epi_copy"](act, j, n).then_inc(S["epi_copied"], 1)
                    if fns.get("epi_act"):
                        fns["epi_act"](act, j, n)

                def body(i, k, a, p, e):
                    c = 3 * i + k
                    for h in range(16):
                        exp(h, batch(i, k))
                        if h == 0:
                            copy_tops(1, c)
                            if e:
                                copy_raw(NG - 1, c - 1)
                        elif h % G == 0:
                            copy_raw(h // G - 1, c)
                        if p:
                            for j in schedule_pro(h):
                                pro_copy(j, batch(i, k + 2))
                        if h == 8 and a:
                            copy_tops(0, c + 1)
                        if e:
                            for j in schedule_epi(h):
                                epi_copy(j, c - 1)

                act.wait_ge(S["weights"], 16 * len(fns["weights"]))
                for n in range(2):
                    for j in range(NP):
                        pro_copy(j, batch(0, n))
                copy_tops(0, 0)
                iterations(act, body)
                copy_raw(NG - 1, BATCH - 1)
                for j in range(NE):
                    epi_copy(j, BATCH - 1)

            @block.tensor
            def _(pe):
                def scores(h, b):
                    n, rnd, buf = b
                    if h == 0:
                        pe.wait_ge(S["stacked"][buf], 16 * LOADS * (rnd + 1))
                    wait(pe, S["row_max"], 16 * n + h - 1)
                    for t in range(QT):
                        mm = nc.tensor.matmul(score[h % 2][:, t * SEQ:(t + 1) * SEQ],
                                              qs[buf][0:R, h, t * P:(t + 1) * P], ks[buf][0:R, h, :],
                                              start=True, stop=True)
                    mm.then_inc(S["scores"], 1)

                def turned_scores(h, b):
                    n, rnd, buf = b
                    if h % 8 == 0:
                        pe.wait_ge(S["tops_in"][buf], 16 * (2 * rnd + h // 8 + 1))
                    wait(pe, S["exp"], 16 * n + h - 1)
                    for t in range(QT):
                        mm = nc.tensor.matmul(tscore[h % 2][:, t * SEQ:(t + 1) * SEQ],
                                              ks[buf][:, h, t * P:(t + 1) * P], qs[buf][:, h, :],
                                              start=True, stop=not mask)
                        for r in range(3 if mask else 0):
                            mm = nc.tensor.matmul(tscore[h % 2][:, t * SEQ:(t + 1) * SEQ], mask["ident"][:, :],
                                                  mask["parts"][:, r, t * SEQ:(t + 1) * SEQ],
                                                  start=False, stop=(r == 2))
                    mm.then_inc(S["tscores"], 1)

                def pv(h, b):
                    n, rnd, buf = b
                    g = h // G
                    if h == 0:
                        pe.wait_ge(S["pro_copied"], NP * (n + 1))
                    pe.wait_ge(S["exp"], 16 * n + h + 1)
                    if h % G == 0:
                        wait(pe, S["raw"], NG * n + g)
                    r = 32 * (h % G)
                    for t in range(QT):
                        mm = nc.tensor.matmul(pvp[r:r + 32, 0:SEQ], v[buf][:, t, h, :],
                                              probT[h % 2][:, t * SEQ:(t + 1) * SEQ], start=(t == 0), stop=(t == 1))
                    mm.then_inc(S["pv"], 1)

                def turn_back(g, n):
                    pe.wait_ge(S["raw"], NG * n + g + 1)
                    wait(pe, S["o_ready"], NG * n + g)
                    for t in range(QT):
                        mm = nc.tensor.transpose(back[:, t * P:(t + 1) * P], raw[g % 2][:, t * P:(t + 1) * P],
                                                 keep["ident"][:, :])
                    mm.then_inc(S["back"], 1)

                def turn_tops(g, b):
                    n, rnd, buf = b
                    pe.wait_ge(S["row_max"], 16 * n + 8 * (g + 1))
                    if g == 0:
                        wait(pe, S["tops_copied"], 2 * n)
                    elif isinstance(n, int) and n < 2:
                        pe.wait_ge(S["tops_copied"], 2 * n + 1)
                    else:
                        pe.wait_ge(S["epi_copied"], NE * (n - 1))
                    for t in range(QT):
                        mm = nc.tensor.transpose(epi[0:8, t * P:(t + 1) * P], nmax[buf][:, t, 8 * g:8 * g + 8],
                                                 keep["ident"][:, :])
                    mm.then_inc(S["tops_filled"], 1)

                def pro_fill(j, b):
                    n, rnd, buf = b
                    wait(pe, S["pro_copied"], NP * n + j)
                    if j == turn_job:
                        pe.wait_ge(S["normed"], n + 1)
                    fns["pro_fill"](pe, j, n, rnd, buf).then_inc(S["pro_filled"], 1)

                def epi_fill(j, b):
                    n, rnd, buf = b
                    wait(pe, S["epi_copied"], NE * n + j)
                    if j == 0:
                        pe.wait_ge(S["o_ready"], NG * (n + 1))
                        tops = 2 * n + 5
                        pe.wait_ge(S["tops_copied"], min(tops, 2 * BATCH) if isinstance(tops, int) else tops)
                    fns["epi_fill"](pe, j, n, buf).then_inc(S["epi_filled"], 1)

                def body(i, k, a, p, e):
                    c = 3 * i + k
                    for h in range(16):
                        if h < 15:
                            turned_scores(h + 1, batch(i, k))
                        if a:
                            scores(h, batch(i, k + 1))
                        if h > 0:
                            pv(h - 1, batch(i, k))
                        elif e:
                            pv(15, batch(i, k - 1))
                        if h == 0:
                            turn_tops(1, batch(i, k))
                        if h > G and h % G == 1:
                            turn_back(h // G - 1, c)
                        if h == 1 and e:
                            turn_back(NG - 1, c - 1)
                        if p:
                            for j in schedule_pro(h):
                                pro_fill(j, batch(i, k + 2))
                        if h == 8 and a:
                            turn_tops(0, batch(i, k + 1))
                        if e:
                            for j in schedule_epi(h):
                                epi_fill(j, batch(i, k - 1))
                        if h == 15 and a:
                            turned_scores(0, batch(i, k + 1))

                pe.wait_ge(S["weights"], 16 * len(fns["weights"]))
                if mask:
                    pe.wait_ge(S["mask_ready"], 5)
                for n in range(2):
                    for j in range(NP):
                        pro_fill(j, batch(0, n))
                for h in range(16):
                    scores(h, batch(0, 0))
                    if h == 8:
                        turn_tops(0, batch(0, 0))
                turned_scores(0, batch(0, 0))
                iterations(pe, body)
                pv(15, batch(0, BATCH - 1))
                turn_back(NG - 1, BATCH - 1)
                for j in range(NE):
                    epi_fill(j, batch(0, BATCH - 1))
    zero_semaphores(nc, S["all"])


def cross_rope(nc, keep, S, dram):
    H, HD, L = 16, 16, "L2"

    def make(nc, keep, bufs, S):
        sb, pro, epi = bufs["sb"], bufs["pro"], bufs["epi"]
        wq, wqr, wk, wkr, wv, wo = w = [sb(n, [P, KT, D]) for n in ("wq", "wqr", "wk", "wkr", "wv", "wo")]
        weights = [(w[i][:, :, :], dram[L + n].rearrange("(k p) m -> p k m", p=P))
                   for i, n in enumerate(("wq", "wqr", "wk", "wkr", "wv", "wo"))]
        biases = [sb(n, [P, 2]) for n in ("bq", "bqr", "bk", "bkr")]
        weights += [(b[:, :], dram[L + n]) for b, n in zip(biases, ("bq", "bqr", "bk", "bkr"))]
        bv, bo = sb("bv", [P, D]), sb("bo", [1, D])
        tables = [sb(n, [P, SEQ]) for n in ("cosq", "sinq", "cosk", "sink")]
        weights += [(t[:, :], dram[n]) for t, n in zip(tables, ("cosq", "sinq", "cosk", "sink"))]
        weights += [(bv[:, :], dram[L + "bv"]), (bo[:, :], dram[L + "bo"])]
        h, hT, oT = sb("h", [P, QT, D]), sb("hT", [P, KT, SEQ]), sb("oT", [P, KT, SEQ])
        cT = [sb(f"cT{i}", [P, KT, SEQ]) for i in range(3)]
        turned, mixed = sb("turned", [P, KT, SEQ]), sb("mixed", [P, KT, SEQ])

        def pro_fill(pe, j, n, rnd, buf):
            if j == 0:
                pe.wait_ge(S["stream"][buf], 16 * (rnd + 1))
            if j < 2:
                return project(nc, pro, (wk, wkr)[j], cT[buf], range(KT))
            if j == 2:
                return turn(nc, keep, pro, h)
            if j < 5:
                return project(nc, pro, (wq, wqr)[j - 3], hT, range(KT))
            return project_rows(nc, pro, cT[buf], wv, 0, D)

        def pro_copy(eng, j, n, buf):
            if j == 2:
                return nc.scalar.copy(flat(hT[:, :, :]), pro[:, :])
            if j == 5:
                return nc.vector.tensor_tensor(
                    bufs["v"][buf][:, :, :, 0:HD], pro[:, :].rearrange("p (t h v) -> p t h v", t=QT, h=H),
                    bv[:, :].rearrange("p (h v) -> p h v", h=H).unsqueeze(1).to_broadcast([P, QT, H, HD]), ALU.add)
            which, rotated = ("k", j == 1) if j < 2 else ("q", j == 4)
            at = (2 if which == "k" else 0) + rotated
            to = turned if rotated else mixed
            for k in range(KT):
                ins = nc.vector.scalar_tensor_tensor(out=to[:, k, :], in0=pro[:, k * SEQ:(k + 1) * SEQ],
                                                     scalar=biases[at][:, k:k + 1], in1=tables[at][:, :],
                                                     op0=ALU.add, op1=ALU.mult)
            if not rotated:
                return ins
            ins.then_inc(S["rope"], 1)
            eng.wait_ge(S["rope"], 2 * n + (1 if which == "k" else 2))
            wait(eng, S[which + "_split"], n)
            nc.vector.tensor_tensor(bufs["whole"][which][:, :], flat(mixed[:, :, :]), flat(turned[:, :, :]),
                                    ALU.add).then_inc(S[which + "_ready"], 1)
            eng.wait_ge(S[which + "_ready"], n + 1)
            return nc.vector.memset(keep["scratch"][:, 1:2], 0.0)

        def epi_fill(pe, j, n, buf):
            if j == 0:
                return turn(nc, keep, epi, bufs["o"][buf])
            return output_rows(nc, epi, oT, wo, bo[0:1, :], keep, KT)

        def epi_copy(eng, j, n):
            if j == 0:
                return nc.scalar.copy(flat(oT[:, :, :]), epi[:, :])
            return add_output(nc, eng, keep, epi, keep["gate"][:, 4:5], n)

        return dict(weights=weights, h=h, pro_fill=pro_fill, pro_copy=pro_copy, epi_fill=epi_fill, epi_copy=epi_copy,
                    pro_engine=lambda j: "act" if j == 2 else "dve", epi_engine=lambda j: "act" if j == 0 else "dve",
                    stream=lambda n, buf: (cT[buf][:, :, :],
                                           dram["ctxT"][bass.ds(n, 1), :, :, :].rearrange("a p k s -> (a p) k s")))

    stacked_attention(nc, keep, S, dram, dict(name=L, dim=HD, n_pro=6, n_epi=2, make=make,
                                              turn_job=2,
                                              split_slots=[7, 8, 9, 10], pro_at=spread([0, 1, 3, 4, 6, 9]),
                                              epi_at=spread([12, 14])))


def cross_masked(nc, keep, S, dram):
    H, HD, L = 16, 16, "L0"

    def make(nc, keep, bufs, S):
        sb, pro, epi = bufs["sb"], bufs["pro"], bufs["epi"]
        wq, wk, wv, wo = w = [sb(n, [P, KT, D]) for n in ("wq", "wk", "wv", "wo")]
        weights = [(w[i][:, :, :], dram[L + n].rearrange("(k p) m -> p k m", p=P))
                   for i, n in enumerate(("wq", "wk", "wv", "wo"))]
        bq, bk, bv, bo = sb("bq", [P, 2]), sb("bk", [P, 2]), sb("bv", [P, D]), sb("bo", [1, D])
        weights += [(b[:, :], dram[L + n]) for b, n in ((bq, "bq"), (bk, "bk"), (bv, "bv"), (bo, "bo"))]
        h, hT, oT = sb("h", [P, QT, D]), sb("hT", [P, KT, SEQ]), sb("oT", [P, KT, SEQ])
        cT = [sb(f"cT{i}", [P, KT, SEQ]) for i in range(3)]
        rows, turned = sb("maskrows", [P, 512]), sb("maskturned", [P, 512])
        rest, parts, ident = sb("maskrest", [P, 512]), sb("maskparts", [P, 3, 512], BF16), sb("ident", [P, P], BF16)
        masked = [sb(f"masked{i}", [P, 512]) for i in range(2)]
        weights += [(rows[:, :].rearrange("p (t k) -> p t k", t=QT), dram["mask"].rearrange("(t p) k -> p t k", p=P)),
                    (turned[:, :].rearrange("p (t k) -> p t k", t=QT),
                     dram["maskT"].rearrange("(t p) k -> p t k", p=P))]

        def mask_setup(dve):
            nc.vector.tensor_copy(ident[:, :], keep["ident"][:, :])
            nc.vector.tensor_scalar(rows[:, :], rows[:, :], -BIG, None, ALU.mult)
            nc.vector.tensor_scalar(turned[:, :], turned[:, :], -BIG, None, ALU.mult).then_inc(S["mask_ready"], 1)
            dve.wait_ge(S["mask_ready"], 1)
            nc.vector.tensor_copy(parts[:, 0, :], turned[:, :]).then_inc(S["mask_ready"], 1)
            dve.wait_ge(S["mask_ready"], 2)
            nc.vector.tensor_tensor(rest[:, :], turned[:, :], parts[:, 0, :], ALU.subtract).then_inc(S["mask_ready"], 1)
            dve.wait_ge(S["mask_ready"], 3)
            nc.vector.tensor_copy(parts[:, 1, :], rest[:, :]).then_inc(S["mask_ready"], 1)
            dve.wait_ge(S["mask_ready"], 4)
            nc.vector.tensor_tensor(parts[:, 2, :], rest[:, :], parts[:, 1, :], ALU.subtract
                                    ).then_inc(S["mask_ready"], 1)

        def pro_fill(pe, j, n, rnd, buf):
            if j == 0:
                pe.wait_ge(S["stream"][buf], 16 * (rnd + 1))
                return project(nc, pro, wk, cT[buf], range(KT))
            if j == 1:
                return turn(nc, keep, pro, h)
            if j == 2:
                return project(nc, pro, wq, hT, range(KT))
            return project_rows(nc, pro, cT[buf], wv, 0, D)

        def pro_copy(eng, j, n, buf):
            if j == 1:
                return nc.scalar.copy(flat(hT[:, :, :]), pro[:, :])
            if j == 3:
                return nc.vector.tensor_tensor(
                    bufs["v"][buf][:, :, :, 0:HD], pro[:, :].rearrange("p (t h v) -> p t h v", t=QT, h=H),
                    bv[:, :].rearrange("p (h v) -> p h v", h=H).unsqueeze(1).to_broadcast([P, QT, H, HD]), ALU.add)
            which, b, scale = ("k", bk, 1.0) if j == 0 else ("q", bq, 0.25)
            wait(eng, S[which + "_split"], n)
            for k in range(KT):
                ins = nc.vector.tensor_scalar(bufs["whole"][which][:, k * SEQ:(k + 1) * SEQ],
                                              pro[:, k * SEQ:(k + 1) * SEQ], b[:, k:k + 1], scale,
                                              ALU.add, ALU.mult)
            ins.then_inc(S[which + "_ready"], 1)
            eng.wait_ge(S[which + "_ready"], n + 1)
            return nc.vector.memset(keep["scratch"][:, 1:2], 0.0)

        def epi_fill(pe, j, n, buf):
            if j == 0:
                return turn(nc, keep, epi, bufs["o"][buf])
            return output_rows(nc, epi, oT, wo, bo[0:1, :], keep, KT)

        def epi_copy(eng, j, n):
            if j == 0:
                return nc.scalar.copy(flat(oT[:, :, :]), epi[:, :])
            return add_output(nc, eng, keep, epi, keep["gate"][:, 0:1], n)

        return dict(weights=weights, h=h, pro_fill=pro_fill, pro_copy=pro_copy, epi_fill=epi_fill, epi_copy=epi_copy,
                    mask=dict(rows=rows, parts=parts, ident=ident, masked=masked), mask_setup=mask_setup,
                    pro_engine=lambda j: "act" if j == 1 else "dve", epi_engine=lambda j: "act" if j == 0 else "dve",
                    stream=lambda n, buf: (cT[buf][:, :, :],
                                           dram["ctxT"][bass.ds(n, 1), :, :, :].rearrange("a p k s -> (a p) k s")))

    stacked_attention(nc, keep, S, dram, dict(name=L, dim=HD, n_pro=4, n_epi=2, make=make, turn_job=1,
                                              split_slots=[], pro_at=spread([0, 1, 3, 7]),
                                              epi_at=spread([11, 13])))


def latent_attention(nc, keep, S, dram):
    H, VD, L, E = 16, 8, "L0f", 8
    LAT = H * VD
    scale = float(np.float32(1.0) / np.sqrt(np.float32(VD)))
    R = 13

    def make(nc, keep, bufs, S):
        sb, pro, epi, o, v = [bufs[n] for n in ("sb", "pro", "epi", "o", "v")]
        wq, wk, wv = [sb(n, [P, KT, LAT]) for n in ("wq", "wk", "wv")]
        wo, router, b2 = sb("wo", [P, D]), sb("router", [P, KT, E]), sb("b2", [E, D])
        bq, bk, bo, br = sb("bq", [P, 1]), sb("bk", [P, 1]), sb("bo", [P, KT]), sb("br", [1, E])
        borow, nothing = sb("borow", [P, D]), sb("nothing", [P, 2048])
        bv, iota = sb("bv", [P, LAT]), sb("iota", [P, E])
        h, hT = sb("h", [P, QT, D]), sb("hT", [P, KT, SEQ])
        oT, mT = sb("oT", [P, SEQ]), sb("mT", [P, KT, SEQ])
        nm, tot, rtot = sb("nm", [P, QT]), sb("tot", [P, QT]), sb("rtot", [P, QT])
        e, top, idx = sb("e", [P, QT, E]), sb("top", [P, QT, 8]), sb("idx", [P, QT, 8], U32)
        idf, comb, hit = sb("idf", [P, QT, 8]), sb("comb", [P, QT, E]), sb("hit", [P, QT, E])
        combT = sb("combT", [E, SEQ])

        weights = [(w[:, :, :], dram[L + n].rearrange("(k p) m -> p k m", p=P))
                   for w, n in ((wq, "wq"), (wk, "wk"), (wv, "wv"), (router, "router"))]
        weights += [(w[:, :], dram[L + n]) for w, n in ((wo, "wo"), (b2, "b2"), (bq, "bq"), (bk, "bk"), (bo, "bo"),
                                                        (br, "br"), (bv, "bv"))]
        weights += [(iota[:, :], dram["iota"][:, 0:E]), (borow[:, :], dram[L + "borow"])]

        def norm_wait(dve, n):
            wait(dve, S["hs_saved"], 16 * n)
            nc.vector.memset(keep["scratch"][:, 1:2], 0.0)

        def pro_fill(pe, j, n, rnd, buf):
            if j == 0:
                return turn(nc, keep, pro, h)
            if j == 1:
                for i, w in enumerate((wq, wk)):
                    for k in range(KT):
                        mm = nc.tensor.matmul(pro[:, i * SEQ:(i + 1) * SEQ], w[:, k, :], hT[:, k, :],
                                              start=(k == 0), stop=(k == KT - 1))
                return mm
            return project_rows(nc, pro, hT, wv, 0, LAT)

        def pro_copy(eng, j, n, buf):
            if j == 0:
                return nc.scalar.copy(flat(hT[:, :, :]), pro[:, :])
            if j == 1:
                wait(eng, S["k_split"], n)
                nc.vector.tensor_scalar(bufs["whole"]["k"][:, :], pro[:, SEQ:2 * SEQ], bk[:, 0:1], None, ALU.add
                                        ).then_inc(S["k_ready"], 1)
                wait(eng, S["q_split"], n)
                nc.vector.tensor_scalar(bufs["whole"]["q"][:, :], pro[:, 0:SEQ], bq[:, 0:1], scale, ALU.add, ALU.mult
                                        ).then_inc(S["q_ready"], 1)
                eng.wait_ge(S["q_ready"], n + 1)
                return nc.vector.memset(keep["scratch"][:, 2:3], 0.0)
            return nc.vector.tensor_tensor(
                v[buf][:, :, :, 0:VD], pro[:, 0:QT * LAT].rearrange("p (t h v) -> p t h v", t=QT, h=H),
                bv[:, :].rearrange("p (h v) -> p h v", h=H).unsqueeze(1).to_broadcast([P, QT, H, VD]), ALU.add)

        def epi_fill(pe, j, c, buf):
            if j == 0:
                for t in range(QT):
                    mm = nc.tensor.transpose(epi[:, t * P:(t + 1) * P], o[buf][:, t, :], keep["ident"][:, :])
                return mm
            if j == 1:
                for m in range(KT):
                    mm = nc.tensor.matmul(epi[:, m * SEQ:(m + 1) * SEQ], wo[:, m * P:(m + 1) * P], oT[:, :],
                                          start=True, stop=True)
                return mm
            for t in range(QT):
                if j == 2:
                    for k in range(KT):
                        nc.tensor.matmul(epi[:, t * E:(t + 1) * E], mT[:, k, t * P:(t + 1) * P], router[:, k, :],
                                         start=(k == 0), stop=False)
                    mm = nc.tensor.matmul(epi[:, t * E:(t + 1) * E], keep["ones"][0:1, :], br[0:1, :],
                                          start=False, stop=True)
                if j == 3:
                    mm = nc.tensor.transpose(epi[0:E, t * P:(t + 1) * P], comb[:, t, :], keep["ident"][:, :])
                if j == 5:
                    mm = nc.tensor.matmul(epi[:, t * D:(t + 1) * D], oT[:, t * P:(t + 1) * P], wo[:, :],
                                          start=True, stop=True)
                if j == 4:
                    mm = nc.tensor.matmul(epi[:, t * D:(t + 1) * D], combT[:, t * P:(t + 1) * P], b2[:, :],
                                          start=True, stop=True)
            return mm

        def route(dve, c):
            n = [0]

            def linked(ins):
                n[0] += 1
                ins.then_inc(S["route"], 1)
                dve.wait_ge(S["route"], R * c + n[0])

            def take_wait():
                nc.vector.memset(keep["scratch"][:, 2:3], 0.0)

            logits = epi[:, 0:QT * E].rearrange("p (t e) -> p t e", t=QT)
            nc.vector.tensor_reduce(nm[:, :], logits, AX.X, ALU.max, negate=True).then_inc(S["route_max"], 1)
            dve.wait_ge(S["route_exp"], c + 1)
            linked(nc.vector.tensor_reduce(tot[:, :], e[:, :, :], AX.X, ALU.add))
            linked(nc.vector.reciprocal(rtot[:, :], tot[:, :]))
            linked(nc.vector.tensor_tensor(e[:, :, :], e[:, :, :],
                                           rtot[:, :].unsqueeze(2).to_broadcast([P, QT, E]), ALU.mult))
            take_wait()
            for t in range(QT):
                ins = nc.vector.max(top[:, t, :], e[:, t, :])
            linked(ins)
            take_wait()
            for t in range(QT):
                ins = nc.vector.max_index(idx[:, t, :], top[:, t, :], e[:, t, :])
            linked(ins)
            linked(nc.vector.tensor_copy(idf[:, :, :], idx[:, :, :]))
            linked(nc.vector.tensor_tensor(tot[:, :], top[:, :, 0], top[:, :, 1], ALU.add))
            linked(nc.vector.tensor_scalar(tot[:, :], tot[:, :], 1e-8, None, ALU.add))
            linked(nc.vector.reciprocal(rtot[:, :], tot[:, :]))
            linked(nc.vector.tensor_tensor(top[:, :, 0:2], top[:, :, 0:2],
                                           rtot[:, :].unsqueeze(2).to_broadcast([P, QT, 2]), ALU.mult))
            for t in range(QT):
                nc.vector.tensor_scalar(comb[:, t, :], iota[:, :], idf[:, t, 0:1], top[:, t, 0:1],
                                        ALU.is_equal, ALU.mult)
                ins = nc.vector.tensor_scalar(hit[:, t, :], iota[:, :], idf[:, t, 1:2], top[:, t, 1:2],
                                              ALU.is_equal, ALU.mult)
            linked(ins)
            linked(nc.vector.tensor_tensor(comb[:, :, :], comb[:, :, :], hit[:, :, :], ALU.add))
            nc.vector.tensor_scalar(keep["choice"][:, bass.ds(c * QT, QT), :], idf[:, :, 0:2], 1.0, None, ALU.mult)
            linked(nc.vector.tensor_scalar(keep["share"][:, bass.ds(c * QT, QT), :], top[:, :, 0:2], 1.0, None,
                                           ALU.mult))
            assert n[0] == R
            return nc.vector.memset(keep["scratch"][:, 3:4], 0.0)

        def epi_copy(eng, j, c):
            if j == 0:
                return nc.scalar.copy(oT[:, :], epi[:, 0:SEQ])
            if j == 1:
                for m in range(KT):
                    ins = nc.vector.tensor_scalar(mT[:, m, :], epi[:, m * SEQ:(m + 1) * SEQ], bo[:, m:m + 1], None,
                                                  ALU.add)
                return ins
            if j == 2:
                return route(eng, c)
            if j == 3:
                return nc.vector.tensor_copy(combT[:, :], epi[0:E, 0:SEQ])
            if j == 5:
                return nc.vector.tensor_tensor(keep["m"][:, bass.ds(c * QT, QT), :],
                                               epi[:, :].rearrange("p (t d) -> p t d", t=QT),
                                               borow[:, :].unsqueeze(1).to_broadcast([P, QT, D]), ALU.add)
            eng.wait_ge(S["hs_saved"], 16 * (c + 1))
            hs = flat(keep["hs"][:, bass.ds(c * QT, QT), :])
            return nc.vector.scalar_tensor_tensor(out=hs, in0=epi[:, :], scalar=0.3, in1=hs, op0=ALU.mult,
                                                  op1=ALU.add)

        def epi_act(act, j, c):
            if j == 2:
                act.wait_ge(S["route_max"], c + 1)
                for t in range(QT):
                    ins = nc.scalar.activation(e[:, t, :], epi[:, t * E:(t + 1) * E], ACT.Exp,
                                               bias=nm[:, t:t + 1])
                ins.then_inc(S["route_exp"], 1)

        def save(sp, c):
            sp.wait_ge(S["normed"], c + 1)
            sp.dma_start(keep["hs"][:, bass.ds(c * QT, QT), :], h[:, :, :]).then_inc(S["hs_saved"], 16)

        def sync_head(sp, k):
            save(sp, k)
            if k == 1:
                save(sp, 2)
                for q in range(SLOT_TILES * P // 1024):
                    sp.dma_start(dram["m_slots"][q * 1024:(q + 1) * 1024, :].rearrange("(p a) d -> p (a d)", p=P),
                                 nothing[:, :]).then_inc(S["zeroed"], 16)

        def sync_more(sp, c, more, e):
            if more:
                save(sp, c + 3)

        def sync_tail(sp):
            sp.wait_ge(S["zeroed"], 16 * (SLOT_TILES * P // 1024))
            sp.wait_ge(S["hs_saved"], 16 * BATCH)

        def vector_setup(dve):
            nc.vector.memset(nothing[:, :], 0.0)

        return dict(weights=weights, h=h, vector_setup=vector_setup, norm_wait=norm_wait, pro_fill=pro_fill, pro_copy=pro_copy,
                    epi_fill=epi_fill, epi_copy=epi_copy, epi_act=epi_act,
                    pro_engine=lambda j: "act" if j == 0 else "dve",
                    epi_engine=lambda j: "act" if j == 0 else "dve",
                    sync_head=sync_head, sync_more=sync_more, sync_tail=sync_tail)

    stacked_attention(nc, keep, S, dram, dict(name=L, dim=VD, n_pro=3, n_epi=6, turn_job=0, make=make,
                                              split_slots=[3, 4, 5, 6], pro_at=spread([0, 2, 4]),
                                              epi_at=spread([9, 10, 11, 13, 14, 15])))


def flamingo(nc, dram, out):
    with ExitStack() as ctx:
        def sb(name, shape, dt=F32):
            return ctx.enter_context(nc.sbuf_tensor(name, shape, dt))

        names = ["weights", "setup", "stats", "var", "vareps", "rstd", "normed", "pro_filled", "pro_copied", "epi_filled",
                 "epi_copied", "scores", "row_max", "exp", "pT", "pT_copied", "pv", "rden", "hs_saved",
                 "tick", "slots", "counted", "logits", "member", "placed", "zeroed", "up", "turned",
                 "turn_copied", "peaks", "local_top", "top", "scale", "inv", "rounded", "quantised",
                 "tscores", "q_ready", "q_link", "q_split", "q_stored", "k_ready", "k_link", "k_split",
                 "k_stored", "tops_filled", "tops_copied", "tops_link", "tops_split", "tops_stored",
                 "experts_loaded", "scaled", "hidden_biased", "mask_ready", "copied", "sig_clipped",
                 "gated", "sigmoid", "route", "route_max", "route_exp", "hidden", "act", "y", "added",
                 "share", "moe_out", "o_ready", "raw", "back", "masked", "rope"]
        S = {n: ctx.enter_context(nc.semaphore(n)) for n in names}
        S["stream"] = [ctx.enter_context(nc.semaphore(f"stream{i}")) for i in range(4)]
        S["stored"] = [ctx.enter_context(nc.semaphore(f"stored{i}")) for i in range(2)]
        for n in ("stacked", "tops_in"):
            S[n] = [ctx.enter_context(nc.semaphore(f"{n}{i}")) for i in range(3)]
        for n in ("scattered", "gathered", "m_scattered", "m_gathered"):
            S[n] = [ctx.enter_context(nc.semaphore(f"{n}{i}")) for i in range(4)]
        S["all"] = [S[n] for n in names] + S["stacked"] + S["tops_in"] + S["stream"] + S["stored"]
        x_loaded = ctx.enter_context(nc.semaphore("x_loaded"))
        gates_loaded = ctx.enter_context(nc.semaphore("gates_loaded"))
        ready = ctx.enter_context(nc.semaphore("constants_ready"))
        tanh_done = ctx.enter_context(nc.semaphore("tanh_done"))

        keep = dict(x=sb("x", [P, TILES, D]), ident=sb("ident", [P, P]), ones=sb("ones", [P, P]),
                    mhalf=sb("mhalf", [P, 4]), eps=sb("eps", [P, 4]), scratch=sb("scratch", [P, 4]), gate=sb("gate", [P, 10]))

        with nc.Block() as block:
            @block.sync
            def _(sp):
                sp.dma_start(keep["gate"][:, 0:9], dram["gates"]).then_inc(gates_loaded, 16)
                sp.dma_start(keep["ident"][:, :], dram["ident"]).then_inc(gates_loaded, 16)
                for q in range(4):
                    n = TILES // 4
                    sp.dma_start(keep["x"][:, q * n:(q + 1) * n, :],
                                 dram["x"][q * n * P:(q + 1) * n * P, :].rearrange("(t p) d -> p t d", p=P)
                                 ).then_inc(x_loaded, 16)
                sp.wait_ge(x_loaded, 64)

            @block.vector
            def _(dve):
                nc.vector.memset(keep["ones"][:, :], 1.0)
                nc.vector.memset(keep["mhalf"][:, :], -0.5)
                nc.vector.memset(keep["eps"][:, :], EPS)
                dve.wait_ge(tanh_done, 1)
                nc.vector.tensor_tensor(keep["gate"][:, 2:3], keep["gate"][:, 2:3], keep["gate"][:, 8:9],
                                        ALU.mult).then_inc(ready, 1)

            @block.scalar
            def _(act):
                act.wait_ge(gates_loaded, 32)
                nc.scalar.activation(keep["gate"][:, 0:9], keep["gate"][:, 0:9], ACT.Tanh).then_inc(tanh_done, 1)

        stages = [lambda: cross_masked(nc, keep, S, dram),
                  lambda: layer0_feed_forward(nc, keep, S, dram),
                  lambda: cross_wide(nc, keep, S, dram, latents=False),
                  lambda: routed_experts(nc, keep, S, dram),
                  lambda: cross_rope(nc, keep, S, dram),
                  lambda: relu_feed_forward(nc, keep, S, dram),
                  lambda: cross_wide(nc, keep, S, dram, latents=True),
                  lambda: quantised_feed_forward(nc, keep, S, dram)]
        for stage in stages:
            stage()


def lay_out(inp):
    f = {k: np.asarray(v) for k, v in inp.items()}
    a = {}
    a["x"] = f["x"].reshape(TOKENS, D)
    a["ctxT"] = f["ctx_1024"].reshape(BATCH, SEQ, KT, P).transpose(0, 3, 2, 1)
    a["mask"] = f["mask_1x1xSxS2_fk1"].reshape(SEQ, SEQ)
    a["maskT"] = a["mask"].T
    gates = np.stack([f["g_xattn"], f["g_ffn"]], axis=1).reshape(8)
    a["gates"] = np.broadcast_to(np.concatenate([gates, f["L1_xattn_gate"]]), (P, 9))
    a["ident"] = np.eye(P, dtype=np.float32)
    a["iota"] = np.broadcast_to(np.arange(64, dtype=np.float32), (P, 64))

    def col(b):
        return b.reshape(-1, P).T

    def rows(b):
        return np.broadcast_to(b, (P, b.size))
    r = np.arange(D)
    lay16 = ((r % P) % 8 * 2 + r // P) * 16 + (r % P) // 8
    a["L0wq"], a["L0wk"] = f["L0_xattn_wq"][:, lay16], f["L0_xattn_wk"][:, lay16]
    a["L0wv"], a["L0wo"] = f["L0_xattn_wv"], f["L0_xattn_wo"]
    a["L0bq"], a["L0bk"] = col(f["L0_xattn_bq"][lay16]), col(f["L0_xattn_bk"][lay16])
    a["L0bv"], a["L0bo"] = rows(f["L0_xattn_bv"]), f["L0_xattn_bo"].reshape(1, D)
    turn16 = (lay16 // 16) * 16 + (lay16 + 8) % 16
    a["L2wv"], a["L2wo"] = [f[f"L2_xattn_W{n}"].T for n in "vo"]
    for n in "qk":
        a["L2w" + n], a["L2w" + n + "r"] = f["L2_xattn_W" + n].T[:, lay16], f["L2_xattn_W" + n].T[:, turn16]
        a["L2b" + n], a["L2b" + n + "r"] = col(f["L2_xattn_b" + n][lay16]), col(f["L2_xattn_b" + n][turn16])
    a["L2bv"], a["L2bo"] = rows(f["L2_xattn_bv"]), f["L2_xattn_bo"].reshape(1, D)

    r = np.arange(P)
    latq, latk = (r % 16) * 16 + r // 16, (r % 16) * 8 + r // 16
    a["L0fwq"], a["L0fbq"] = f["L0_ffn_q_w"][:, latq], f["L0_ffn_q_b"][latq].reshape(P, 1)
    a["L0fwk"], a["L0fbk"] = f["L0_ffn_k_w"][:, latk], f["L0_ffn_k_b"][latk].reshape(P, 1)
    a["L0fwv"], a["L0fbv"] = f["L0_ffn_v_w"], rows(f["L0_ffn_v_b"])
    a["L0fwo"], a["L0fbo"] = f["L0_ffn_o_w"][:P], col(f["L0_ffn_o_b"])
    a["L0frouter"], a["L0fbr"] = f["L0_ffn_router_w"], f["L0_ffn_router_b"].reshape(1, 8)
    a["L0fw1"], a["L0fw2"], a["L0fb2"] = f["L0_ffn_w1"], f["L0_ffn_w2"], f["L0_ffn_b2"]
    a["L0fb1"] = np.broadcast_to(f["L0_ffn_b1"], (P, 8, 512))
    a["L0fborow"] = rows(f["L0_ffn_o_b"])
    a["upto"] = np.broadcast_to(np.arange(SLOT_TILES, dtype=np.float32), (P, SLOT_TILES))

    a["L1wq"], a["L1wkv"], a["L1wo"] = f["L1_xattn_w_q"], f["L1_xattn_w_kv"], f["L1_xattn_w_out"]
    a["L1gamma"], a["L1beta"] = col(f["L1_xattn_ln_gamma"]), col(f["L1_xattn_ln_beta"])
    a["L1bo"] = f["L1_xattn_b_out"].reshape(1, D)
    a["L3wq"], a["L3wkv"], a["L3wo"] = f["L3_xattn_Wq"], f["L3_xattn_Wkv"], f["L3_xattn_Wo"]
    a["ctx"] = f["ctx_1024"].reshape(BATCH, QT, P, D).transpose(0, 2, 1, 3)
    turn64 = (np.arange(512) // 64) * 64 + (np.arange(512) + 32) % 64
    a["L3wkr"] = f["L3_xattn_Wkv"][:, turn64]
    a["L3gamma"], a["L3beta"] = col(f["L3_xattn_gamma_l"]), col(f["L3_xattn_beta_l"])
    a["L3gammax"], a["L3betax"] = col(f["L3_xattn_gamma_x"]), col(f["L3_xattn_beta_x"])

    a["L2fw1"], a["L2fw2"] = f["L2_ffn_W1"], f["L2_ffn_W2"]
    a["L2fb1"], a["L2fb2"] = col(f["L2_ffn_b1"]), f["L2_ffn_b2"].reshape(1, D)
    a["L3fup"], a["L3fgate"], a["L3fdown"] = f["L3_ffn_w_up"], f["L3_ffn_w_gate"], f["L3_ffn_w_down"]

    a["L1frouter"] = f["L1_ffn_router_w"].T
    a["L1fwg"], a["L1fwu"], a["L1fwd"] = f["L1_ffn_w_gate"], f["L1_ffn_w_up"], f["L1_ffn_w_down"]
    a["L1fwsgu"], a["L1fwsd"] = f["L1_ffn_ws_gate_up"], f["L1_ffn_ws_down"]
    a["tri"] = np.triu(np.ones((P, P), np.float32), 1)

    def rope_tables(dim):
        inv = (1.0 / 10000.0 ** (np.arange(0, dim, 2, dtype=np.float32) / np.float32(dim))).astype(np.float32)
        angle = np.arange(SEQ, dtype=np.float32)[:, None] * inv[None, :]
        cos, sin = np.cos(angle).T, np.sin(angle).T
        reps = P // dim
        return (np.tile(np.concatenate([cos, cos]), (reps, 1)).astype(np.float32),
                np.tile(np.concatenate([-sin, sin]), (reps, 1)).astype(np.float32))
    cos16, sin16 = [t[np.arange(P) // 8] for t in rope_tables(16)]
    a["cosk"], a["sink"] = cos16, sin16
    a["cosq"], a["sinq"] = cos16 * np.float32(0.25), sin16 * np.float32(0.25)
    a["cos64"], a["sin64"] = rope_tables(64)
    return {k: np.ascontiguousarray(v) for k, v in a.items()}


def kernel(**inputs):
    import concourse.bacc as bacc
    from concourse.bass_utils import run_bass_kernel_spmd

    arrays = lay_out(inputs)
    nc = bacc.Bacc("TRN2", target_bir_lowering=False, num_devices=1)
    dram = {k: nc.dram_tensor("in_" + k, list(v.shape), F32, kind="ExternalInput").ap()
            for k, v in arrays.items()}
    out = nc.dram_tensor("out_x", [TOKENS, D], F32, kind="ExternalOutput").ap()
    dram["out"] = out
    dram["x_spill"] = nc.dram_tensor("x_spill", [P, TILES, D], F32, kind="Internal").ap()
    for n in "qk":
        for dim in (8, 16):
            dram[f"{n}_parts{dim}"] = nc.dram_tensor(f"{n}_parts{dim}", [3, 3, dim, 16, SEQ], BF16, kind="Internal").ap()
    dram["top_parts"] = nc.dram_tensor("top_parts", [3, 2, 3, 8, SEQ], BF16, kind="Internal").ap()
    for n in ("m_slots", "m_results"):
        dram[n] = nc.dram_tensor(n, [SLOT_TILES * P, D], F32, kind="Internal").ap()
    for n in ("x_slots", "y_slots"):
        dram[n] = nc.dram_tensor(n, [64 * 128, D], F32, kind="Internal").ap()
    flamingo(nc, dram, out)
    r = run_bass_kernel_spmd(nc, [{"in_" + k: v for k, v in arrays.items()}], core_ids=[0])
    return r.results[0]["out_x"].reshape(BATCH, SEQ, D)
```
